# Optimizing a Trainium2 kernel written in Bass

```python
import numpy as np
import jax
import jax.numpy as jnp

def _softmax(x, axis=-1):
    return jax.nn.softmax(x, axis=axis)

def _gelu(x):
    return jax.nn.gelu(x, approximate=True)

def _silu(x):
    return jax.nn.silu(x)

def _sigmoid(x):
    return jax.nn.sigmoid(x)

def _layernorm(x, axis=-1, eps=1e-05):
    m = jnp.mean(x, axis=axis, keepdims=True)
    v = jnp.var(x, axis=axis, keepdims=True)
    return (x - m) / jnp.sqrt(v + eps)

def _scatter_add(tgt, idx, src, axis=0):
    return tgt.at[idx].add(src)

def _segment_sum(src, seg, n):
    return jax.ops.segment_sum(src, seg, n)
kernel_name = 'mk_lm_tower_d2_tok_ids1024_r4_88ba91'

def setup_inputs(seed: int=0):
    np.random.seed(seed)
    _w = jnp.asarray

    def _rec_inputs():
        import jax
        import jax.numpy as jnp
        _rk = jax.random.key(seed)
        x = jax.random.randint(jax.random.fold_in(_rk, 1), (2, 1024), 0, 31993, jnp.int32)
        return x
    x = _rec_inputs()

    def _L0_tok_setup():
        import jax, jax.numpy as jnp
        import numpy as np
        EPS = 1e-05

        def layernorm(x, s, b):
            m = jnp.mean(x, axis=-1, keepdims=True)
            v = jnp.mean(jnp.square(x - m), axis=-1, keepdims=True)
            return (x - m) * jax.lax.rsqrt(v + EPS) * s + b

        def ssm(x, a_diag, Bm, Cm, Dm):
            a = jax.nn.sigmoid(a_diag)
            u = jnp.einsum('btd,ds->bts', x, Bm)

            def step(h, u_t):
                h = a * h + u_t
                return (h, h)
            h0 = jnp.zeros((x.shape[0], a.shape[0]), x.dtype)
            _, H = jax.lax.scan(step, h0, jnp.swapaxes(u, 0, 1))
            H = jnp.swapaxes(H, 0, 1)
            return jnp.einsum('bts,sd->btd', H, Cm) + jnp.einsum('btd,de->bte', x, Dm)
        key = jax.random.key(seed)
        ks = jax.random.split(key, 12)
        Bn, T = (4, 512)
        V, Dm, S, L, F = (8000, 256, 64, 4, 1024)

        def xavier(k, shape):
            fan_in, fan_out = (shape[-2], shape[-1])
            lim = float(np.sqrt(6.0 / (fan_in + fan_out)))
            return jax.random.uniform(k, shape, jnp.float32, -lim, lim)
        return {'tokens': jax.random.randint(ks[0], (Bn, T), 0, V), 'emb': jax.random.normal(ks[1], (V, Dm), jnp.float32), 'pos_emb': jax.random.normal(ks[2], (1024, Dm), jnp.float32), 'A_diag': jax.random.uniform(ks[3], (L, S), jnp.float32, -0.5, 0.5), 'B': xavier(ks[4], (L, Dm, S)), 'C': xavier(ks[5], (L, S, Dm)), 'D': xavier(ks[6], (L, Dm, Dm)) * 0.1, 'w1': xavier(ks[7], (L, Dm, F)), 'b1': jnp.zeros((L, F), jnp.float32), 'w2': xavier(ks[8], (L, F, Dm)), 'b2': jnp.zeros((L, Dm), jnp.float32), 'ln1_s': jnp.ones((L, Dm), jnp.float32), 'ln1_b': jnp.zeros((L, Dm), jnp.float32), 'ln2_s': jnp.ones((L, Dm), jnp.float32), 'ln2_b': jnp.zeros((L, Dm), jnp.float32), 'lnf_s': jnp.ones((Dm,), jnp.float32), 'lnf_b': jnp.zeros((Dm,), jnp.float32)}
    _L0_tok_all = _L0_tok_setup()
    _L0_tok_in = {k: v for k, v in _L0_tok_all.items() if k in ('emb', 'pos_emb', 'A_diag', 'B', 'C', 'D', 'w1', 'b1', 'w2', 'b2', 'ln1_s', 'ln1_b', 'ln2_s', 'ln2_b', 'lnf_s', 'lnf_b')}
    del _L0_tok_all

    def _L0_attn_setup():
        import jax, jax.numpy as jnp
        import numpy as np
        DIM = 256
        NUM_HEADS = 16
        HEAD_DIM = DIM // NUM_HEADS
        EPS = 1e-06

        def layer_norm(x, gamma, beta):
            mu = jnp.mean(x, axis=-1, keepdims=True)
            var = jnp.mean(jnp.square(x - mu), axis=-1, keepdims=True)
            return (x - mu) / jnp.sqrt(var + EPS) * gamma + beta

        def apply_rope(q, k):
            seq_len, head_dim = (q.shape[1], q.shape[3])
            half = head_dim // 2
            freq_range = jnp.arange(half, dtype=jnp.float32) / half
            inv_freq = 1.0 / 10000.0 ** freq_range
            t = jnp.arange(seq_len, dtype=jnp.float32)
            freqs = jnp.outer(t, inv_freq)
            emb = jnp.concatenate([freqs, freqs], axis=-1)
            cos = jnp.cos(emb)[None, :, None, :]
            sin = jnp.sin(emb)[None, :, None, :]

            def rotate_half(x):
                x1, x2 = (x[..., :half], x[..., half:])
                return jnp.concatenate([-x2, x1], axis=-1)
            return (q * cos + rotate_half(q) * sin, k * cos + rotate_half(k) * sin)
        key = jax.random.key(seed)
        ks = jax.random.split(key, 4)
        B, S = (2, 512)
        x = jax.random.normal(ks[0], (B, S, DIM), dtype=jnp.float32)
        lim_qkv = float(np.sqrt(6.0 / (DIM + 3 * DIM)))
        w_qkv = jax.random.uniform(ks[1], (3 * DIM, DIM), dtype=jnp.float32, minval=-lim_qkv, maxval=lim_qkv)
        lim_p = float(np.sqrt(6.0 / (DIM + DIM)))
        w_proj = jax.random.uniform(ks[2], (DIM, DIM), dtype=jnp.float32, minval=-lim_p, maxval=lim_p)
        b_proj = jnp.zeros((DIM,), dtype=jnp.float32)
        q_gamma = jnp.ones((HEAD_DIM,), dtype=jnp.float32)
        q_beta = jnp.zeros((HEAD_DIM,), dtype=jnp.float32)
        k_gamma = jnp.ones((HEAD_DIM,), dtype=jnp.float32)
        k_beta = jnp.zeros((HEAD_DIM,), dtype=jnp.float32)
        return {'x': x, 'w_qkv': w_qkv, 'w_proj': w_proj, 'b_proj': b_proj, 'q_gamma': q_gamma, 'q_beta': q_beta, 'k_gamma': k_gamma, 'k_beta': k_beta}
    _L0_attn_all = _L0_attn_setup()
    _L0_attn_in = {k: v for k, v in _L0_attn_all.items() if k in ('w_qkv', 'w_proj', 'b_proj', 'q_gamma', 'q_beta', 'k_gamma', 'k_beta')}
    del _L0_attn_all

    def _L0_ffn_setup():
        import jax, jax.numpy as jnp
        import numpy as np
        B, S, H = (4, 1024, 256)
        I = 512
        E = 16
        K = 2
        key = jax.random.key(seed)
        ks = jax.random.split(key, 5)
        scale = 0.02
        return {'hidden_states': jax.random.normal(ks[0], (B, S, H), dtype=jnp.float32), 'w_gate': jax.random.normal(ks[1], (H, E), dtype=jnp.float32) * scale, 'w_gate_proj': jax.random.normal(ks[2], (E, H, I), dtype=jnp.float32) * scale, 'w_up_proj': jax.random.normal(ks[3], (E, H, I), dtype=jnp.float32) * scale, 'w_down_proj': jax.random.normal(ks[4], (E, I, H), dtype=jnp.float32) * scale}
    _L0_ffn_all = _L0_ffn_setup()
    _L0_ffn_in = {k: v for k, v in _L0_ffn_all.items() if k in ('w_gate', 'w_gate_proj', 'w_up_proj', 'w_down_proj')}
    del _L0_ffn_all

    def _L1_attn_setup():
        import jax, jax.numpy as jnp
        import numpy as np
        EPS = 1e-05

        def xpos_rotate(x, offset=0, conjugate=False):
            b, s, h, dh = x.shape
            expoent = jnp.arange(0, dh, 2, dtype=jnp.float32) / dh
            angle = 10.0 ** (-4.0 * expoent)
            if conjugate:
                angle = -angle
            pos = jnp.arange(offset, s + offset, dtype=jnp.float32)
            nangle = pos[:, None] * angle[None, :]
            sin = jnp.sin(nangle)[None, :, None, :]
            cos = jnp.cos(nangle)[None, :, None, :]
            x0 = x[..., 0::2]
            x1 = x[..., 1::2]
            rot = jnp.stack([x0 * cos - x1 * sin, x0 * sin + x1 * cos], axis=-1)
            return rot.reshape(b, s, h, dh)

        def decay_mask(nseq, scale):
            idx = jnp.arange(nseq)
            diff = idx[:, None] - idx[None, :]
            mask = (diff >= 0).astype(scale.dtype)
            diff_c = jnp.maximum(diff, 0).astype(scale.dtype)
            logd = diff_c[None, :, :] * jnp.log(scale)[:, None, None]
            return jnp.exp(logd) * mask[None, :, :]

        def group_norm(R, gamma, beta, nheads):
            b, s, d = R.shape
            dh = d // nheads
            Rg = R.reshape(b, s, nheads, dh)
            mu = jnp.mean(Rg, axis=-1, keepdims=True)
            var = jnp.var(Rg, axis=-1, keepdims=True)
            Rn = (Rg - mu) * jax.lax.rsqrt(var + EPS)
            Rn = Rn * gamma.reshape(1, 1, nheads, dh) + beta.reshape(1, 1, nheads, dh)
            return Rn.reshape(b, s, d)
        key = jax.random.key(seed)
        ks = jax.random.split(key, 7)
        b, s, d, h = (2, 512, 256, 16)
        dh = d // h
        x = jax.random.normal(ks[0], (b, s, d), dtype=jnp.float32)
        std_qkv = float(np.sqrt(2.0 / (dh + d)))
        std_o = float(np.sqrt(2.0 / (d + d)))
        WQ = jax.random.normal(ks[1], (h, dh, d), dtype=jnp.float32) * std_qkv
        WK = jax.random.normal(ks[2], (h, dh, d), dtype=jnp.float32) * std_qkv
        WV = jax.random.normal(ks[3], (h, dh, d), dtype=jnp.float32) * std_qkv
        WO = jax.random.normal(ks[4], (d, d), dtype=jnp.float32) * std_o
        gamma = jnp.ones((d,), dtype=jnp.float32)
        beta = jnp.zeros((d,), dtype=jnp.float32)
        return {'x': x, 'WQ': WQ, 'WK': WK, 'WV': WV, 'WO': WO, 'gamma': gamma, 'beta': beta}
    _L1_attn_all = _L1_attn_setup()
    _L1_attn_in = {k: v for k, v in _L1_attn_all.items() if k in ('WQ', 'WK', 'WV', 'WO', 'gamma', 'beta')}
    del _L1_attn_all

    def _L1_ffn_setup():
        import jax, jax.numpy as jnp
        import numpy as np
        B, S, D, H, E = (4, 512, 256, 1024, 8)
        THRESHOLD = 0.5
        key = jax.random.key(seed)
        ks = jax.random.split(key, 7)
        s_in = 1.0 / np.sqrt(D)
        s_h = 1.0 / np.sqrt(H)
        return {'x': jax.random.normal(ks[0], (B, S, D), dtype=jnp.float32), 'Wg': jax.random.uniform(ks[1], (D, E), jnp.float32, -s_in, s_in), 'bg': jax.random.uniform(ks[2], (E,), jnp.float32, -s_in, s_in), 'W1': jax.random.uniform(ks[3], (E, D, H), jnp.float32, -s_in, s_in), 'b1': jax.random.uniform(ks[4], (E, H), jnp.float32, -s_in, s_in), 'W2': jax.random.uniform(ks[5], (E, H, D), jnp.float32, -s_h, s_h), 'b2': jax.random.uniform(ks[6], (E, D), jnp.float32, -s_h, s_h)}
    _L1_ffn_all = _L1_ffn_setup()
    _L1_ffn_in = {k: v for k, v in _L1_ffn_all.items() if k in ('Wg', 'bg', 'W1', 'b1', 'W2', 'b2')}
    del _L1_ffn_all
    return {'x': x, 'L0_tok_emb': _L0_tok_in['emb'], 'L0_tok_pos_emb': _L0_tok_in['pos_emb'], 'L0_tok_A_diag': _L0_tok_in['A_diag'], 'L0_tok_B': _L0_tok_in['B'], 'L0_tok_C': _L0_tok_in['C'], 'L0_tok_D': _L0_tok_in['D'], 'L0_tok_w1': _L0_tok_in['w1'], 'L0_tok_b1': _L0_tok_in['b1'], 'L0_tok_w2': _L0_tok_in['w2'], 'L0_tok_b2': _L0_tok_in['b2'], 'L0_tok_ln1_s': _L0_tok_in['ln1_s'], 'L0_tok_ln1_b': _L0_tok_in['ln1_b'], 'L0_tok_ln2_s': _L0_tok_in['ln2_s'], 'L0_tok_ln2_b': _L0_tok_in['ln2_b'], 'L0_tok_lnf_s': _L0_tok_in['lnf_s'], 'L0_tok_lnf_b': _L0_tok_in['lnf_b'], 'L0_attn_w_qkv': _L0_attn_in['w_qkv'], 'L0_attn_w_proj': _L0_attn_in['w_proj'], 'L0_attn_b_proj': _L0_attn_in['b_proj'], 'L0_attn_q_gamma': _L0_attn_in['q_gamma'], 'L0_attn_q_beta': _L0_attn_in['q_beta'], 'L0_attn_k_gamma': _L0_attn_in['k_gamma'], 'L0_attn_k_beta': _L0_attn_in['k_beta'], 'L0_ffn_w_gate': _L0_ffn_in['w_gate'], 'L0_ffn_w_gate_proj': _L0_ffn_in['w_gate_proj'], 'L0_ffn_w_up_proj': _L0_ffn_in['w_up_proj'], 'L0_ffn_w_down_proj': _L0_ffn_in['w_down_proj'], 'L1_attn_WQ': _L1_attn_in['WQ'], 'L1_attn_WK': _L1_attn_in['WK'], 'L1_attn_WV': _L1_attn_in['WV'], 'L1_attn_WO': _L1_attn_in['WO'], 'L1_attn_gamma': _L1_attn_in['gamma'], 'L1_attn_beta': _L1_attn_in['beta'], 'L1_ffn_Wg': _L1_ffn_in['Wg'], 'L1_ffn_bg': _L1_ffn_in['bg'], 'L1_ffn_W1': _L1_ffn_in['W1'], 'L1_ffn_b1': _L1_ffn_in['b1'], 'L1_ffn_W2': _L1_ffn_in['W2'], 'L1_ffn_b2': _L1_ffn_in['b2']}

def reference(x, L0_tok_emb, L0_tok_pos_emb, L0_tok_A_diag, L0_tok_B, L0_tok_C, L0_tok_D, L0_tok_w1, L0_tok_b1, L0_tok_w2, L0_tok_b2, L0_tok_ln1_s, L0_tok_ln1_b, L0_tok_ln2_s, L0_tok_ln2_b, L0_tok_lnf_s, L0_tok_lnf_b, L0_attn_w_qkv, L0_attn_w_proj, L0_attn_b_proj, L0_attn_q_gamma, L0_attn_q_beta, L0_attn_k_gamma, L0_attn_k_beta, L0_ffn_w_gate, L0_ffn_w_gate_proj, L0_ffn_w_up_proj, L0_ffn_w_down_proj, L1_attn_WQ, L1_attn_WK, L1_attn_WV, L1_attn_WO, L1_attn_gamma, L1_attn_beta, L1_ffn_Wg, L1_ffn_bg, L1_ffn_W1, L1_ffn_b1, L1_ffn_W2, L1_ffn_b2):
    import jax
    import jax.numpy as jnp

    def _L0_tok_ref(tokens, emb, pos_emb, A_diag, B, C, D, w1, b1, w2, b2, ln1_s, ln1_b, ln2_s, ln2_b, lnf_s, lnf_b):
        import jax, jax.numpy as jnp
        import numpy as np
        EPS = 1e-05

        def layernorm(x, s, b):
            m = jnp.mean(x, axis=-1, keepdims=True)
            v = jnp.mean(jnp.square(x - m), axis=-1, keepdims=True)
            return (x - m) * jax.lax.rsqrt(v + EPS) * s + b

        def ssm(x, a_diag, Bm, Cm, Dm):
            a = jax.nn.sigmoid(a_diag)
            u = jnp.einsum('btd,ds->bts', x, Bm)

            def step(h, u_t):
                h = a * h + u_t
                return (h, h)
            h0 = jnp.zeros((x.shape[0], a.shape[0]), x.dtype)
            _, H = jax.lax.scan(step, h0, jnp.swapaxes(u, 0, 1))
            H = jnp.swapaxes(H, 0, 1)
            return jnp.einsum('bts,sd->btd', H, Cm) + jnp.einsum('btd,de->bte', x, Dm)
        T = tokens.shape[1]
        x = emb[tokens] + pos_emb[:T][None]
        L = A_diag.shape[0]
        for l in range(L):
            x = x + ssm(layernorm(x, ln1_s[l], ln1_b[l]), A_diag[l], B[l], C[l], D[l])
            h = layernorm(x, ln2_s[l], ln2_b[l])
            h = jax.nn.gelu(jnp.einsum('btd,df->btf', h, w1[l]) + b1[l], approximate=False)
            x = x + jnp.einsum('btf,fd->btd', h, w2[l]) + b2[l]
        return layernorm(x, lnf_s, lnf_b)

    def _L0_attn_ref(x, w_qkv, w_proj, b_proj, q_gamma, q_beta, k_gamma, k_beta):
        import jax, jax.numpy as jnp
        import numpy as np
        DIM = 256
        NUM_HEADS = 16
        HEAD_DIM = DIM // NUM_HEADS
        EPS = 1e-06

        def layer_norm(x, gamma, beta):
            mu = jnp.mean(x, axis=-1, keepdims=True)
            var = jnp.mean(jnp.square(x - mu), axis=-1, keepdims=True)
            return (x - mu) / jnp.sqrt(var + EPS) * gamma + beta

        def apply_rope(q, k):
            seq_len, head_dim = (q.shape[1], q.shape[3])
            half = head_dim // 2
            freq_range = jnp.arange(half, dtype=jnp.float32) / half
            inv_freq = 1.0 / 10000.0 ** freq_range
            t = jnp.arange(seq_len, dtype=jnp.float32)
            freqs = jnp.outer(t, inv_freq)
            emb = jnp.concatenate([freqs, freqs], axis=-1)
            cos = jnp.cos(emb)[None, :, None, :]
            sin = jnp.sin(emb)[None, :, None, :]

            def rotate_half(x):
                x1, x2 = (x[..., :half], x[..., half:])
                return jnp.concatenate([-x2, x1], axis=-1)
            return (q * cos + rotate_half(q) * sin, k * cos + rotate_half(k) * sin)
        B, S, C = x.shape
        H, D = (NUM_HEADS, HEAD_DIM)
        qkv = jnp.einsum('bsc,oc->bso', x, w_qkv).reshape(B, S, 3, H, D)
        q = layer_norm(qkv[:, :, 0], q_gamma, q_beta)
        k = layer_norm(qkv[:, :, 1], k_gamma, k_beta)
        v = qkv[:, :, 2]
        q, k = apply_rope(q, k)
        scale = D ** (-0.5)
        q = q.astype(jnp.float32) * scale
        k = k.astype(jnp.float32)
        v = v.astype(jnp.float32)
        attn = jnp.einsum('bqhd,bkhd->bhqk', q, k)
        attn = jax.nn.softmax(attn, axis=-1)
        out = jnp.einsum('bhqk,bkhd->bqhd', attn, v).reshape(B, S, C)
        out = jnp.einsum('bsc,oc->bso', out, w_proj) + b_proj
        return out

    def _L0_ffn_ref(hidden_states, w_gate, w_gate_proj, w_up_proj, w_down_proj):
        import jax, jax.numpy as jnp
        import numpy as np
        B, S, H = (4, 1024, 256)
        I = 512
        E = 16
        K = 2
        b, s, h = hidden_states.shape
        x = hidden_states.reshape(-1, h)
        probs = jax.nn.softmax(x @ w_gate, axis=-1)
        topk_vals, topk_idx = jax.lax.top_k(probs, K)
        routing_weights = topk_vals / jnp.sum(topk_vals, axis=-1, keepdims=True)
        out = jnp.zeros_like(x)
        for e in range(E):
            we = jnp.sum(jnp.where(topk_idx == e, routing_weights, 0.0), axis=-1)
            g = x @ w_gate_proj[e]
            u = x @ w_up_proj[e]
            y = u * jax.nn.silu(g) @ w_down_proj[e]
            out = out + we[:, None] * y
        return out.reshape(b, s, h)

    def _L1_attn_ref(x, WQ, WK, WV, WO, gamma, beta):
        import jax, jax.numpy as jnp
        import numpy as np
        EPS = 1e-05

        def xpos_rotate(x, offset=0, conjugate=False):
            b, s, h, dh = x.shape
            expoent = jnp.arange(0, dh, 2, dtype=jnp.float32) / dh
            angle = 10.0 ** (-4.0 * expoent)
            if conjugate:
                angle = -angle
            pos = jnp.arange(offset, s + offset, dtype=jnp.float32)
            nangle = pos[:, None] * angle[None, :]
            sin = jnp.sin(nangle)[None, :, None, :]
            cos = jnp.cos(nangle)[None, :, None, :]
            x0 = x[..., 0::2]
            x1 = x[..., 1::2]
            rot = jnp.stack([x0 * cos - x1 * sin, x0 * sin + x1 * cos], axis=-1)
            return rot.reshape(b, s, h, dh)

        def decay_mask(nseq, scale):
            idx = jnp.arange(nseq)
            diff = idx[:, None] - idx[None, :]
            mask = (diff >= 0).astype(scale.dtype)
            diff_c = jnp.maximum(diff, 0).astype(scale.dtype)
            logd = diff_c[None, :, :] * jnp.log(scale)[:, None, None]
            return jnp.exp(logd) * mask[None, :, :]

        def group_norm(R, gamma, beta, nheads):
            b, s, d = R.shape
            dh = d // nheads
            Rg = R.reshape(b, s, nheads, dh)
            mu = jnp.mean(Rg, axis=-1, keepdims=True)
            var = jnp.var(Rg, axis=-1, keepdims=True)
            Rn = (Rg - mu) * jax.lax.rsqrt(var + EPS)
            Rn = Rn * gamma.reshape(1, 1, nheads, dh) + beta.reshape(1, 1, nheads, dh)
            return Rn.reshape(b, s, d)
        b, s, d = x.shape
        h, dh, _ = WQ.shape
        Q = jnp.einsum('bsd,hud->bshu', x, WQ)
        K = jnp.einsum('bsd,hud->bshu', x, WK)
        V = jnp.einsum('bsd,hud->bshu', x, WV)
        Q = xpos_rotate(Q)
        K = xpos_rotate(K)
        QK = jnp.einsum('bihd,bjhd->bhij', Q, K)
        scale = 1.0 - 2.0 ** (-5.0 - jnp.arange(h, dtype=jnp.float32))
        D = decay_mask(s, scale)
        QKD = QK * D[None]
        R = jnp.einsum('bhij,bjhd->bihd', QKD, V)
        R = R.reshape(b, s, d)
        R = group_norm(R, gamma, beta, h)
        y = R @ WO
        return y

    def _L1_ffn_ref(x, Wg, bg, W1, b1, W2, b2):
        import jax, jax.numpy as jnp
        import numpy as np
        B, S, D, H, E = (4, 512, 256, 1024, 8)
        THRESHOLD = 0.5
        b, s, d = x.shape
        x_flat = x.reshape(-1, d)
        probs = jax.nn.sigmoid(x_flat @ Wg + bg)
        mask = (probs > THRESHOLD).astype(x_flat.dtype)
        weights = probs * mask
        h = jax.nn.relu(jnp.einsum('td,edh->eth', x_flat, W1) + b1[:, None, :])
        expert_out = jnp.einsum('eth,ehd->etd', h, W2) + b2[:, None, :]
        combined = jnp.einsum('te,etd->td', weights, expert_out)
        return combined.reshape(b, s, d)
    h = _L0_tok_ref(x, L0_tok_emb, L0_tok_pos_emb, L0_tok_A_diag, L0_tok_B, L0_tok_C, L0_tok_D, L0_tok_w1, L0_tok_b1, L0_tok_w2, L0_tok_b2, L0_tok_ln1_s, L0_tok_ln1_b, L0_tok_ln2_s, L0_tok_ln2_b, L0_tok_lnf_s, L0_tok_lnf_b)
    h = h + _L0_attn_ref(_layernorm(h, axis=-1), L0_attn_w_qkv, L0_attn_w_proj, L0_attn_b_proj, L0_attn_q_gamma, L0_attn_q_beta, L0_attn_k_gamma, L0_attn_k_beta)
    h = h + _L0_ffn_ref(_layernorm(h, axis=-1), L0_ffn_w_gate, L0_ffn_w_gate_proj, L0_ffn_w_up_proj, L0_ffn_w_down_proj)
    h = h + _L1_attn_ref(_layernorm(h, axis=-1), L1_attn_WQ, L1_attn_WK, L1_attn_WV, L1_attn_WO, L1_attn_gamma, L1_attn_beta)
    h = h + _L1_ffn_ref(_layernorm(h, axis=-1), L1_ffn_Wg, L1_ffn_bg, L1_ffn_W1, L1_ffn_b1, L1_ffn_W2, L1_ffn_b2)
    return h

_drawn_inputs = setup_inputs


def setup_inputs(seed=0):
    import zlib

    import numpy as np

    out = dict(_drawn_inputs(seed))
    spreads = {'L0_tok_b1': (0.0, 0.1),
     'L0_tok_b2': (0.0, 0.1),
     'L0_tok_ln1_s': (1.0, 0.2),
     'L0_tok_ln1_b': (0.0, 0.1),
     'L0_tok_ln2_s': (1.0, 0.2),
     'L0_tok_ln2_b': (0.0, 0.1),
     'L0_tok_lnf_s': (1.0, 0.2),
     'L0_tok_lnf_b': (0.0, 0.1),
     'L0_attn_b_proj': (0.0, 0.1),
     'L0_attn_q_gamma': (1.0, 0.2),
     'L0_attn_q_beta': (0.0, 0.536),
     'L0_attn_k_gamma': (1.0, 0.6),
     'L0_attn_k_beta': (0.0, 0.744),
     'L1_attn_gamma': (1.0, 0.2),
     'L1_attn_beta': (0.0, 0.1)}
    factors = {'L1_ffn_b1': 5.077, 'L1_ffn_b2': 4.128}
    for name, (base, spread) in spreads.items():
        noise = np.random.default_rng([zlib.crc32(name.encode()), seed]).standard_normal(out[name].shape)
        drawn = base * np.exp(spread * noise) if base else spread * noise
        out[name] = jnp.asarray(drawn.astype(out[name].dtype))
    for name, factor in factors.items():
        out[name] = (out[name] * factor).astype(out[name].dtype)
    return out
```

```python
from contextlib import ExitStack

import numpy as np
import concourse.bass as bass
from concourse import mybir

F32 = mybir.dt.float32
F16 = mybir.dt.float16
I32 = mybir.dt.int32
U32 = mybir.dt.uint32
ACT = mybir.ActivationFunctionType
ALU = mybir.AluOpType
AX = mybir.AxisListType

P = 128
BATCH, SEQ, D = 2, 1024, 256
N = BATCH * SEQ
NT = N // P
KD = D // P
GT = 4
GN = GT * P
NG = N // GN
WS = 64.0


class Store:

    def __init__(self, nc, ctx, phase):
        self.nc, self.ctx, self.phase, self.sems = nc, ctx, phase, []
        ctx.callback(self.close)

    def sb(self, name, shape, dt=F32):
        return self.ctx.enter_context(self.nc.sbuf_tensor(self.phase + name, shape, dt))

    def ps(self, name, shape, dt=F32):
        return self.ctx.enter_context(self.nc.psum_tensor(self.phase + name, shape, dt))

    def sem(self, name):
        self.sems.append(self.nc.alloc_semaphore(self.phase + name))
        return self.sems[-1]

    def close(self):
        self.nc.clear_and_free_semaphores(self.sems)
        self.nc.all_engine_barrier()


def wait_apart(eng, passed, sem, value):
    eng.wait_ge(sem, value)
    eng.sem_inc(passed, 1)


def layer_stats(dve, passed, x, stats, mv, stats_done, before):
    for t in range(GT):
        ins = dve.bn_stats(stats[:, t, :], x[:, t, :])
    ins.then_inc(stats_done, 1)
    wait_apart(dve, passed, stats_done, before + 1)
    for t in range(GT):
        ins = dve.bn_aggr(mv[:, t, :], stats[:, t, :])
    return ins


def embed(nc, a, X):
    V = a["L0_tok_emb"].shape[0]
    with ExitStack() as ctx:
        s = Store(nc, ctx, "emb_")
        tok = s.sb("tok", [P, NT], I32)
        tokf = s.sb("tokf", [P, NT])
        wrap = s.sb("wrap", [P, NT])
        idx = s.sb("idx", [P, NT], U32)
        pos = s.sb("pos", [P, SEQ // P, D])
        tok_in, pos_in, rows_in = s.sem("tok_in"), s.sem("pos_in"), s.sem("rows_in")
        idx_step = s.sem("idx_step")
        added = s.sem("pos_added")
        passed = s.sem("passed")
        block = ctx.enter_context(nc.Block())

        @block.sync
        def _(sp):
            with nc.allow_non_contiguous_dma(reason="2048 token ids"):
                sp.dma_start(tok[:], a["x"].rearrange("b (t p) -> p (b t)", p=P)).then_inc(tok_in, 16)
            sp.dma_start(pos[:], a["L0_tok_pos_emb"][0:SEQ, :].rearrange("(t p) d -> p t d", p=P)).then_inc(pos_in, 16)

        @block.gpsimd
        def _(pool):
            pool.wait_ge(idx_step, 5)
            for t in range(NT):
                pool.indirect_dma_start(X[:, t, :], None, a["L0_tok_emb"],
                                        bass.IndirectOffsetOnAxis(idx[:, t:t + 1], 0)).then_inc(rows_in, 16)

        @block.vector
        def _(dve):
            dve.wait_ge(tok_in, 16)
            dve.tensor_copy(tokf[:], tok[:]).then_inc(idx_step, 1)
            dve.wait_ge(idx_step, 1)
            dve.tensor_scalar(wrap[:], tokf[:], 0.0, float(V), ALU.is_lt, ALU.mult).then_inc(idx_step, 1)
            dve.wait_ge(idx_step, 2)
            dve.tensor_tensor(tokf[:], tokf[:], wrap[:], ALU.add).then_inc(idx_step, 1)
            dve.wait_ge(idx_step, 3)
            dve.tensor_scalar(tokf[:], tokf[:], 0.0, float(V - 1), ALU.max, ALU.min).then_inc(idx_step, 1)
            dve.wait_ge(idx_step, 4)
            dve.tensor_copy(idx[:], tokf[:]).then_inc(idx_step, 1)
            dve.wait_ge(pos_in, 16)
            dve.wait_ge(rows_in, 16 * NT)
            for b in range(BATCH):
                xb = X[:, b * NT // BATCH:(b + 1) * NT // BATCH, :]
                dve.tensor_tensor(xb, xb, pos[:], ALU.add).then_inc(added, 1)
            dve.wait_ge(added, BATCH)


def trunk(nc, a, X, ident):
    L, S = a["L0_tok_A_diag"].shape
    F = a["L0_tok_w1"].shape[2]
    FT = F // P
    SS = 8.0
    assert SS * SS == WS
    K = 2 * NG
    EPS = 1e-5
    W1, W2, WD, WB, WC, WB2, WE = np.cumsum([0, KD * F, FT * D, KD * D, KD * S, D, D]).tolist()
    PIECES = 16
    PW = WB // PIECES
    with ExitStack() as ctx:
        s = Store(nc, ctx, "trunk_")
        raw = s.sb("w_raw", [P, WE])
        whi = [s.sb(f"w_hi{j}", [P, WE], F16) for j in range(2)]
        wlo = [s.sb(f"w_lo{j}", [P, WE], F16) for j in range(2)]
        b1 = [s.sb(f"b1_{j}", [P, FT]) for j in range(2)]
        aff = [s.sb(f"aff{j}", [P, 2, 2, KD]) for j in range(2)]
        a_raw = s.sb("a_raw", [S, L])
        a_e = s.sb("a_e", [S, L])
        a_sig = s.sb("a_sig", [S, L])
        a_row = [s.sb(f"a_row{j}", [S, GN]) for j in range(2)]
        ones32 = s.sb("ones32", [S, GN])
        ones16 = s.sb("ones16", [1, P], F16)
        mhalf = s.sb("mhalf", [P, GT])
        stats = s.sb("stats", [P, 2, GT, 6])
        mv = s.sb("mv", [P, 2, GT, 2])
        var = s.sb("var", [P, 2, GT])
        rstd = s.sb("rstd", [P, 2, GT])
        xn = s.sb("xn", [P, 2, GT, D])
        xT = s.sb("xT", [P, 2, KD, GN])
        xhi = s.sb("xhi", [P, 2, KD, GN], F16)
        xlo = s.sb("xlo", [P, 2, KD, GN], F16)
        hst = s.sb("hst", [S, 2, GN])
        hst_hi = s.sb("hst_hi", [S, GN], F16)
        hst_lo = s.sb("hst_lo", [S, GN], F16)
        NH = 3
        hf = s.sb("hf", [P, NH, GN])
        hhi = s.sb("hhi", [P, FT, GN], F16)
        hlo = s.sb("hlo", [P, FT, GN], F16)
        pT = [s.ps(f"pT{j}", [P, KD, GN]) for j in range(2)]
        pH = s.ps("pH", [P, 2, GN])
        pY = s.ps("pY", [P, GT, D])
        pU = pT[0][0:S, 0, :]

        w_in, small_in, a_in = s.sem("w_in"), [s.sem(f"small_in{j}") for j in range(2)], s.sem("a_in")
        split_step, w_ready = s.sem("split_step"), s.sem("w_ready")
        layer_free = s.sem("layer_free")
        consts = s.sem("consts")
        a_step = s.sem("a_step")
        arow_ready = s.sem("arow_ready")
        st_done = [s.sem(f"st_done{j}") for j in range(2)]
        mv_done = [s.sem(f"mv_done{j}") for j in range(2)]
        var_done = [s.sem(f"var_done{j}") for j in range(2)]
        rstd_done = [s.sem(f"rstd_done{j}") for j in range(2)]
        xn_done = [s.sem(f"xn_done{j}") for j in range(2)]
        turned = [s.sem(f"turned{j}") for j in range(2)]
        xT_done = [s.sem(f"xT_done{j}") for j in range(2)]
        xhi_done = [s.sem(f"xhi_done{j}") for j in range(2)]
        xlo_done = [s.sem(f"xlo_done{j}") for j in range(2)]
        u_done, scan_done, hsthi_done, hstlo_done = (s.sem(n) for n in ("u_done", "scan_done", "hsthi_done", "hstlo_done"))
        ys_done, ys_added = s.sem("ys_done"), s.sem("ys_added")
        h_done, gelu_done, hhi_done, hlo_done = (s.sem(n) for n in ("h_done", "gelu_done", "hhi_done", "hlo_done"))
        yf_done, yf_added = s.sem("yf_done"), s.sem("yf_added")
        passed, sp_passed = s.sem("passed"), s.sem("sp_passed")
        block = ctx.enter_context(nc.Block())

        def w1v(w, c, f):
            return w[:, W1 + c * F + f * P:W1 + c * F + (f + 1) * P]

        def w2v(w, f):
            return w[:, W2 + f * D:W2 + (f + 1) * D]

        def wdv(w, c):
            return w[:, WD + c * D:WD + (c + 1) * D]

        def wbv(w, c):
            return w[:, WB + c * S:WB + (c + 1) * S]

        def seen(i, k, each, plus=0):
            return i * (K * each) + (k * each + plus)

        @block.sync
        def _(sp):
            with nc.allow_non_contiguous_dma(reason="small parameters"):
                sp.dma_start(a_raw[:], a["L0_tok_A_diag"].rearrange("l s -> s l")).then_inc(a_in, 16)
            with sp.Fori(0, L // 2) as i:
                for j in range(2):
                    l = i * 2 + j
                    sp.wait_ge(layer_free, i * 2 + (j + 1))

                    def row(name):
                        return a[name][bass.ds(l, 1)]
                    for dst, src in (
                        (raw[:, W1:W2].rearrange("p (c f) -> p c f", c=KD), row("L0_tok_w1").rearrange("o (c p) f -> p (o c) f", p=P)),
                        (raw[:, W2:WD].rearrange("p (c d) -> p c d", c=FT), row("L0_tok_w2").rearrange("o (c p) d -> p (o c) d", p=P)),
                        (raw[:, WD:WB].rearrange("p (c d) -> p c d", c=KD), row("L0_tok_D").rearrange("o (c p) d -> p (o c) d", p=P)),
                        (raw[:, WB:WC].rearrange("p (c d) -> p c d", c=KD), row("L0_tok_B").rearrange("o (c p) d -> p (o c) d", p=P)),
                        (raw[0:S, WC:WB2], row("L0_tok_C").rearrange("o s d -> (o s) d")),
                        (raw[0:1, WB2:WE], row("L0_tok_b2")),
                    ):
                        sp.dma_start(dst, src).then_inc(w_in, 16)
                    with nc.allow_non_contiguous_dma(reason="small parameters"):
                        sp.dma_start(b1[j][:], row("L0_tok_b1").rearrange("o (c p) -> p (o c)", p=P)).then_inc(small_in[j], 16)
                        for n, name in enumerate(("ln1_s", "ln1_b", "ln2_s", "ln2_b")):
                            sp.dma_start(aff[j][:, n // 2, n % 2, :],
                                         row("L0_tok_" + name).rearrange("o (c p) -> p (o c)", p=P)).then_inc(small_in[j], 16)
                    wait_apart(sp, sp_passed, w_ready, i * 2 + (j + 1))

        NWD, NSD = 6, 5
        NSPLIT = 3 * (PIECES + 3)

        @block.gpsimd
        def _(pool):
            pool.memset(ones32[:], 1.0).then_inc(consts, 1)
            pool.memset(ones16[:], 1.0).then_inc(consts, 1)
            pool.memset(mhalf[:], -0.5).then_inc(consts, 1)

            def split(i, j, part, hi, lo, scale, n):
                base = i * (2 * NSPLIT) + (j * NSPLIT + 3 * n)
                pool.tensor_scalar(part, part, scale, None, ALU.mult).then_inc(split_step, 1)
                wait_apart(pool, passed, split_step, base + 1)
                pool.tensor_copy(hi, part).then_inc(split_step, 1)
                pool.wait_ge(split_step, base + 2)
                pool.tensor_tensor(lo, part, hi, ALU.subtract).then_inc(split_step, 1)

            def split_piece(i, j, n):
                if n == 0:
                    wait_apart(pool, passed, w_in, i * (2 * NWD * 16) + (j + 1) * NWD * 16)
                c = slice(n * PW, (n + 1) * PW)
                split(i, j, raw[:, c], whi[j][:, c], wlo[j][:, c], WS, n)
                if n == PIECES - 1:
                    for m, (rows, c, scale) in enumerate(((P, slice(WB, WC), SS), (S, slice(WC, WB2), SS), (1, slice(WB2, WE), WS))):
                        split(i, j, raw[0:rows, c], whi[j][0:rows, c], wlo[j][0:rows, c], scale, PIECES + m)
                    pool.wait_ge(split_step, i * (2 * NSPLIT) + (j + 1) * NSPLIT)
                    pool.sem_inc(w_ready, 1)

            def rsqrt(i, k, j):
                wait_apart(pool, passed, mv_done[j], seen(i, k, 1, 1))
                pool.tensor_scalar(var[:, j, :], mv[:, j, :, 1], EPS, None, ALU.add).then_inc(var_done[j], 1)
                pool.wait_ge(var_done[j], seen(i, k, 1, 1))
                pool.tensor_tensor(rstd[:, j, :], var[:, j, :], mhalf[:], ALU.pow).then_inc(rstd_done[j], 1)

            pool.wait_ge(consts, 3)
            with pool.Fori(0, L // 2) as i:
                for n in range(PIECES):
                    split_piece(i, 0, n)
                rsqrt(i, 0, 0)
                for k in range(K):
                    if k + 1 < K:
                        rsqrt(i, k + 1, 0)
                    for n in range(4 if k < 4 else 0):
                        split_piece(i, 1, 4 * k + n)
                    rsqrt(i, k, 1)

        @block.scalar
        def _(act):
            act.wait_ge(a_in, 16)
            act.activation(a_sig[:], a_raw[:], ACT.Sigmoid).then_inc(a_step, 1)

            def affine(i, k, j):
                lj = k // NG
                act.wait_ge(turned[j], seen(i, k, 1, 1))
                if k % NG == 0:
                    act.wait_ge(small_in[lj], i * (NSD * 16) + NSD * 16)
                for c in range(KD):
                    ins = act.activation(xT[:, j, c, :], pT[j][:, c, :], ACT.Identity,
                                         bias=aff[lj][:, j, 1, c:c + 1], scale=aff[lj][:, j, 0, c:c + 1])
                ins.then_inc(xT_done[j], 1)
                act.wait_ge(xT_done[j], seen(i, k, 1, 1))
                for c in range(KD):
                    ins = act.activation(xhi[:, j, c, :], xT[:, j, c, :], ACT.Copy)
                ins.then_inc(xhi_done[j], 1)

            def gelu(i, k, f):
                lj = k // NG
                act.wait_ge(h_done, seen(i, k, FT, f + 1))
                act.activation(hf[:, f % NH, :], pH[:, f % 2, :], ACT.Gelu, bias=b1[lj][:, f:f + 1],
                               scale=1.0 / WS).then_inc(gelu_done, 1)
                act.wait_ge(gelu_done, seen(i, k, FT, f + 1))
                act.activation(hhi[:, f, :], hf[:, f % NH, :], ACT.Copy).then_inc(hhi_done, 1)

            with act.Fori(0, L // 2) as i:
                affine(i, 0, 0)
                for k in range(K + 1):
                    if k:
                        if k > 1:
                            act.wait_ge(yf_done, seen(i, k - 1, 2))
                            act.wait_ge(hlo_done, seen(i, k - 1, FT))
                        for f in range(FT // 2):
                            if f >= NH:
                                act.wait_ge(hlo_done, seen(i, k - 1, FT, f - NH + 1))
                            gelu(i, k - 1, f)
                    if k < K:
                        act.wait_ge(scan_done, seen(i, k, 1, 1))
                        act.activation(hst_hi[:], hst[:, k % 2, :], ACT.Copy).then_inc(hsthi_done, 1)
                    if k:
                        for f in range(FT // 2, FT):
                            act.wait_ge(hlo_done, seen(i, k - 1, FT, f - NH + 1))
                            gelu(i, k - 1, f)
                    if k < K:
                        affine(i, k, 1)
                    if k + 1 < K:
                        affine(i, k + 1, 0)

        @block.vector
        def _(dve):
            def decay_row(i, j):
                dve.tensor_scalar(a_row[j][:], ones32[:], a_sig[:, bass.ds(i * 2 + j, 1)], None, ALU.mult).then_inc(arow_ready, 1)
                dve.wait_ge(arow_ready, i * 2 + (j + 1))

            def norm_stats(i, k, j):
                g = k % NG
                if j == 0:
                    if k >= NG:
                        dve.wait_ge(yf_added, seen(i, k - NG, 2, 2))
                else:
                    dve.wait_ge(ys_added, seen(i, k, 2, 2))
                layer_stats(dve, passed, X[:, g * GT:(g + 1) * GT, :], stats[:, j], mv[:, j], st_done[j],
                            seen(i, k, 1)).then_inc(mv_done[j], 1)

            def norm(i, k, j):
                g = k % NG
                dve.wait_ge(rstd_done[j], seen(i, k, 1, 1))
                if k:
                    dve.wait_ge(turned[j], seen(i, k, 1))
                for t in range(GT):
                    ins = dve.tensor_scalar(xn[:, j, t, :], X[:, g * GT + t, :], mv[:, j, t, 0:1],
                                            rstd[:, j, t:t + 1], ALU.subtract, ALU.mult)
                ins.then_inc(xn_done[j], 1)

            def low(i, k, j):
                dve.wait_ge(xhi_done[j], seen(i, k, 1, 1))
                for c in range(KD):
                    ins = dve.tensor_tensor(xlo[:, j, c, :], xT[:, j, c, :], xhi[:, j, c, :], ALU.subtract)
                ins.then_inc(xlo_done[j], 1)

            def h_low(i, k, f):
                dve.wait_ge(hhi_done, seen(i, k, FT, f + 1))
                dve.tensor_tensor(hlo[:, f, :], hf[:, f % NH, :], hhi[:, f, :], ALU.subtract).then_inc(hlo_done, 1)

            def add(i, k, half, done, added):
                g = k % NG
                dve.wait_ge(done, seen(i, k, 2, half + 1))
                x = X[:, g * GT + 2 * half:g * GT + 2 * half + 2, :]
                dve.scalar_tensor_tensor(out=x, in0=pY[:, 2 * half:2 * half + 2, :], scalar=1.0 / WS, in1=x,
                                         op0=ALU.mult, op1=ALU.add).then_inc(added, 1)

            def scan(i, k):
                dve.wait_ge(u_done, seen(i, k, 1, 1))
                if k >= 1:
                    dve.wait_ge(scan_done, seen(i, k, 1))
                start = 0.0 if k % 2 == 0 else hst[:, (k - 1) % 2, GN - 1:GN]
                dve.tensor_tensor_scan(hst[:, k % 2, :], a_row[k // NG][:], pU, start, ALU.mult, ALU.add).then_inc(scan_done, 1)
                dve.wait_ge(hsthi_done, seen(i, k, 1, 1))
                dve.tensor_tensor(hst_lo[:], hst[:, k % 2, :], hst_hi[:], ALU.subtract).then_inc(hstlo_done, 1)

            dve.sem_inc(layer_free, 2)
            dve.wait_ge(a_step, 1)
            dve.wait_ge(consts, 3)
            with dve.Fori(0, L // 2) as i:
                decay_row(i, 0)
                decay_row(i, 1)
                norm_stats(i, 0, 0)
                norm(i, 0, 0)
                low(i, 0, 0)
                for k in range(K + 1):
                    if k + 1 < K:
                        norm_stats(i, k + 1, 0)
                        norm(i, k + 1, 0)
                    if k:
                        for f in range(FT // 2):
                            h_low(i, k - 1, f)
                    if k < K:
                        scan(i, k)
                    if k:
                        for f in range(FT // 2, FT):
                            h_low(i, k - 1, f)
                    if k < K:
                        add(i, k, 0, ys_done, ys_added)
                        add(i, k, 1, ys_done, ys_added)
                        norm_stats(i, k, 1)
                        norm(i, k, 1)
                    if k:
                        add(i, k - 1, 0, yf_done, yf_added)
                    if k < K:
                        low(i, k, 1)
                    if k + 1 < K:
                        low(i, k + 1, 0)
                    if k:
                        add(i, k - 1, 1, yf_done, yf_added)
                    if k == NG or k == K:
                        dve.wait_ge(yf_added, seen(i, k, 2))
                        dve.sem_inc(layer_free, 1)
                for j in range(2):
                    dve.wait_ge(turned[j], seen(i, K, 1))

        @block.tensor
        def _(pe):
            def turn(i, k, j):
                pe.wait_ge(xn_done[j], seen(i, k, 1, 1))
                if k:
                    pe.wait_ge(xhi_done[j], seen(i, k, 1))
                    if j == 0:
                        pe.wait_ge(scan_done, seen(i, k, 1))
                for c in range(KD):
                    for t in range(GT):
                        ins = pe.transpose(pT[j][:, c, t * P:(t + 1) * P], xn[:, j, t, c * P:(c + 1) * P], ident[:])
                ins.then_inc(turned[j], 1)

            def three(out, hi, lo, whi_, wlo_, start, stop):
                pe.matmul(out, hi, whi_, start=start, stop=False)
                pe.matmul(out, hi, wlo_, start=False, stop=False)
                return pe.matmul(out, lo, whi_, start=False, stop=stop)

            def hidden(i, k, f):
                lj = k // NG
                if f >= 2:
                    pe.wait_ge(gelu_done, seen(i, k, FT, f - 1))
                for c in range(KD):
                    x_hi, x_lo = xhi[:, 1, c, :], xlo[:, 1, c, :]
                    pe.matmul(pH[:, f % 2, :], w1v(whi[lj], c, f), x_hi, start=(c == 0), stop=False)
                    pe.matmul(pH[:, f % 2, :], w1v(whi[lj], c, f), x_lo, start=False, stop=False)
                    ins = pe.matmul(pH[:, f % 2, :], w1v(wlo[lj], c, f), x_hi, start=False, stop=(c == KD - 1))
                ins.then_inc(h_done, 1)

            def u(i, k):
                lj = k // NG
                pe.wait_ge(xlo_done[0], seen(i, k, 1, 1))
                for c in range(KD):
                    x_hi, x_lo = xhi[:, 0, c, :], xlo[:, 0, c, :]
                    pe.matmul(pU, wbv(whi[lj], c), x_hi, start=(c == 0), stop=False)
                    pe.matmul(pU, wbv(whi[lj], c), x_lo, start=False, stop=False)
                    ins = pe.matmul(pU, wbv(wlo[lj], c), x_hi, start=False, stop=(c == KD - 1))
                ins.then_inc(u_done, 1)

            def y_state(i, k):
                lj = k // NG
                pe.wait_ge(hstlo_done, seen(i, k, 1, 1))
                for t in range(GT):
                    tok = slice(t * P, (t + 1) * P)
                    if t % 2 == 0 and k >= 2:
                        pe.wait_ge(yf_added, seen(i, k - 2, 2, t // 2 + 1))
                    for c in range(KD):
                        three(pY[:, t, :], xhi[:, 0, c, tok], xlo[:, 0, c, tok], wdv(whi[lj], c), wdv(wlo[lj], c), c == 0, False)
                    ins = three(pY[:, t, :], hst_hi[:, tok], hst_lo[:, tok], whi[lj][0:S, WC:WB2], wlo[lj][0:S, WC:WB2], False, True)
                    if t % 2 == 1:
                        ins.then_inc(ys_done, 1)

            def y_ff(i, k, t):
                lj = k // NG
                tok = slice(t * P, (t + 1) * P)
                if t == 0:
                    pe.wait_ge(hlo_done, seen(i, k, FT, FT))
                if t % 2 == 0:
                    pe.wait_ge(ys_added, seen(i, min(k + 1, K - 1), 2, t // 2 + 1))
                pe.matmul(pY[:, t, :], ones16[:], whi[lj][0:1, WB2:WE], start=True, stop=False)
                pe.matmul(pY[:, t, :], ones16[:], wlo[lj][0:1, WB2:WE], start=False, stop=False)
                for f in range(FT):
                    ins = three(pY[:, t, :], hhi[:, f, tok], hlo[:, f, tok], w2v(whi[lj], f), w2v(wlo[lj], f), False, f == FT - 1)
                if t % 2 == 1:
                    ins.then_inc(yf_done, 1)

            pe.wait_ge(consts, 3)
            with pe.Fori(0, L // 2) as i:
                turn(i, 0, 0)
                for k in range(K + 1):
                    if k % NG == 0 and k < K:
                        pe.wait_ge(w_ready, i * 2 + (k // NG + 1))
                    if k:
                        pe.wait_ge(xlo_done[1], seen(i, k, 1))
                        for f in range(FT // 2):
                            hidden(i, k - 1, f)
                    if k < K:
                        u(i, k)
                    if k:
                        for f in range(FT // 2, FT):
                            hidden(i, k - 1, f)
                    if k < K:
                        y_state(i, k)
                    if k:
                        for t in range(GT - 1):
                            y_ff(i, k - 1, t)
                    if k < K:
                        turn(i, k, 1)
                    if k + 1 < K:
                        turn(i, k + 1, 0)
                    if k:
                        y_ff(i, k - 1, GT - 1)
                for j in range(2):
                    pe.wait_ge(xhi_done[j], seen(i, K, 1))
                pe.wait_ge(scan_done, seen(i, K, 1))
                pe.wait_ge(yf_added, seen(i, K, 2))


def norm_group(dve, x, mv, rstd, out):
    for t in range(GT):
        ins = dve.tensor_scalar(out[:, t, :], x[:, t, :], mv[:, t, 0:1], rstd[:, t:t + 1], ALU.subtract, ALU.mult)
    return ins


def rotary_attention(nc, a, X, ident, ident16):
    H, HD = 16, D // 16
    PAIRS = H // 2
    T = SEQ // P
    FOUR = 4
    QUADS = H // FOUR
    MU = T * FOUR
    EU = 2 * FOUR * T
    G2 = T // GT
    QH = SEQ // GN
    E1, E2, E3 = 1e-5, 1e-5, 1e-6
    AW = 4 * HD
    MX = 3 * HD
    HK = 2 * H
    LAG = 2
    M_LAST = EU // 2 + LAG - 1
    M_SPLIT = M_LAST - (M_LAST + 1) // 3 + 1
    with ExitStack() as ctx:
        s = Store(nc, ctx, "attn_")
        w_raw = s.sb("w_raw", [P, 3 * D // P + KD, D])
        wq_raw, wp_raw = w_raw[:, 0:3 * D // P, :], w_raw[:, 3 * D // P:, :]
        WQ, WPJ, WBI, WE = np.cumsum([0, KD * 3 * D, KD * D, D]).tolist()
        wT = s.sb("wT", [P, WE])
        wThi = s.sb("wThi", [P, WE], F16)
        wTlo = s.sb("wTlo", [P, WE], F16)
        lnf = s.sb("lnf", [P, 2, D])
        gb = s.sb("gb", [P, 2, 2, HD])
        cos = s.sb("cos", [P, T, HD])
        sin = s.sb("sin", [P, T, HD])
        ones16 = s.sb("ones16", [1, P], F16)
        mhalf = s.sb("mhalf", [P, HK])
        stats = s.sb("stats", [P, GT, 6])
        mv = s.sb("mv", [P, GT, 2])
        var = s.sb("var", [P, GT])
        rstd = s.sb("rstd", [P, GT])
        xn = s.sb("xn", [P, GT, D])
        xhi = s.sb("xhi", [P, KD, GN], F16)
        xlo = s.sb("xlo", [P, KD, GN], F16)
        R = 5
        qk = s.sb("qk", [P, R, HK, HD])
        work = s.sb("work", [P, 2, HK, HD])
        rot = s.sb("rot", [P, HK, HD])
        hsum = s.sb("hsum", [P, R, HK])
        hrs = s.sb("hrs", [P, R, HK])
        qa = s.sb("qa", [P, T, H, 4, HD], F16)
        ka = s.sb("ka", [P, 2, H, 4, HD], F16)
        v1 = s.sb("v1", [P, T, H, P])
        qT = s.sb("qT", [P, H, SEQ], F16)
        kT = s.sb("kT", [P, PAIRS, SEQ], F16)
        mx = s.sb("mx", [P, 2, T, FOUR])
        NP_ = 4
        prob = wT[:, 0:NP_ * GN].rearrange("p (n q) -> p n q", n=NP_)
        rden = s.sb("rden", [P, GN])
        attn = w_raw[:].rearrange("p w d -> p (w d)").rearrange("p (c t) -> p c t", c=KD)
        pairs = [s.ps(f"pair{n}", [P, 2, GN]) for n in range(2)]
        bank = [pairs[n // 2][:, n % 2, :] for n in range(4)] + [s.ps(f"bank{n}", [P, GN])[:] for n in range(4, 8)]
        bank16 = [b.bitcast(F16) for b in bank]

        w_in, c_in = s.sem("w_in"), s.sem("c_in")
        consts, w_turned, w_copied, w_step, w_ready = (s.sem(n) for n in ("consts", "w_turned", "w_copied", "w_step", "w_ready"))
        names = ("st1 mv1 va1 rs1 n1 af1 st2 mv2 va2 rs2 xn_done turned xhi_done xlo_done qkv_done qk_copied "
                 "v_copied sum_done cen_done sq_done sum2_done hvar_done hrs_done scaled gam_done bet_done rope1 rope_done hi_done "
                 "lo_done turn2 kT_done qT_done m_done mx_done qmx_done mturn mq_done sT_done exp_done av_done o_done rd_done "
                 "ahi_done alo_done y_done y_added").split()
        m = {n: s.sem(n) for n in names}
        passed = s.sem("passed")
        block = ctx.enter_context(nc.Block())

        def v_view(t, parity, ones):
            half = 64 * (parity ^ ones)
            w = H * P
            return bass.AP(v1, t * w + parity * FOUR * P + half, [[T * w, P], [2 * FOUR * P, 2], [P + HD, FOUR], [1, HD]])

        def seen(i, each, n):
            return i * each + n

        NW = 3 * D // P + KD

        @block.sync
        def _(sp):
            sp.dma_start(wq_raw, a["L0_attn_w_qkv"].rearrange("(t p) c -> p t c", p=P)).then_inc(w_in, 16)
            sp.dma_start(wp_raw, a["L0_attn_w_proj"].rearrange("(t p) c -> p t c", p=P)).then_inc(w_in, 16)
            sp.dma_start(wT[0:1, WBI:WE], a["L0_attn_b_proj"].rearrange("(o d) -> o d", o=1)).then_inc(w_in, 16)
            sp.dma_start(lnf[:, 0, :], a["L0_tok_lnf_s"].partition_broadcast(P)).then_inc(c_in, 16)
            sp.dma_start(lnf[:, 1, :], a["L0_tok_lnf_b"].partition_broadcast(P)).then_inc(c_in, 16)
            for n, name in enumerate(("q_gamma", "q_beta", "k_gamma", "k_beta")):
                sp.dma_start(gb[:, n % 2, n // 2, :], a["L0_attn_" + name].partition_broadcast(P)).then_inc(c_in, 16)
            sp.dma_start(cos[:], a["c_cos0"].rearrange("(t p) f -> p t f", p=P)).then_inc(c_in, 16)
            sp.dma_start(sin[:], a["c_sin0"].rearrange("(t p) f -> p t f", p=P)).then_inc(c_in, 16)

        @block.gpsimd
        def _(pool):
            pool.memset(ones16[:], 1.0).then_inc(consts, 1)
            pool.memset(mhalf[:], -0.5).then_inc(consts, 1)
            pool.memset(v1[:], 0.0).then_inc(consts, 1)
            pool.memset(qT[:], 0.0).then_inc(consts, 1)
            pool.wait_ge(consts, 4)
            for t in range(T):
                for parity in range(2):
                    ins = pool.memset(v_view(t, parity, 1), 1.0)
            ins.then_inc(consts, 1)
            pool.memset(qa[:, :, :, 3, :], 0.0).then_inc(consts, 1)
            pool.memset(ka[:, :, :, 3, 1:HD], 0.0).then_inc(consts, 1)
            pool.memset(ka[:, :, :, 3, 0:1], 1.0).then_inc(consts, 1)
            wait_apart(pool, passed, c_in, 16 * 8)
            pool.tensor_scalar(gb[:, :, 0, :], gb[:, :, 0, :], float(HD) ** -0.5, None, ALU.mult).then_inc(consts, 1)
            pool.wait_ge(consts, 9)
            pool.wait_ge(w_copied, NW)
            wait_apart(pool, passed, w_in, 48)
            pool.tensor_scalar(wT[0:1, WBI:WE], wT[0:1, WBI:WE], WS, None, ALU.mult).then_inc(w_step, 1)
            wait_apart(pool, passed, w_step, 1)
            for rows, c in ((P, slice(WQ, WBI)), (1, slice(WBI, WE))):
                pool.tensor_copy(wThi[0:rows, c], wT[0:rows, c]).then_inc(w_step, 1)
            pool.wait_ge(w_step, 3)
            for rows, c in ((P, slice(WQ, WBI)), (1, slice(WBI, WE))):
                pool.tensor_tensor(wTlo[0:rows, c], wT[0:rows, c], wThi[0:rows, c], ALU.subtract).then_inc(w_ready, 1)

            def rsqrt(i, n, eps, mv_done, va, rs):
                wait_apart(pool, passed, m[mv_done], seen(i, G2, n + 1))
                pool.tensor_scalar(var[:], mv[:, :, 1], eps, None, ALU.add).then_inc(m[va], 1)
                pool.wait_ge(m[va], seen(i, G2, n + 1))
                pool.tensor_tensor(rstd[:], var[:], mhalf[:, 0:GT], ALU.pow).then_inc(m[rs], 1)

            with pool.Fori(0, BATCH) as i:
                for g in range(G2):
                    rsqrt(i, g, E1, "mv1", "va1", "rs1")
                    rsqrt(i, g, E2, "mv2", "va2", "rs2")
                    for st in range(GT + 3):
                        if 1 <= st < GT + 1:
                            t = g * GT + st - 1
                            wait_apart(pool, passed, m["sum2_done"], seen(i, T, t + 1))
                            pool.tensor_scalar(hsum[:, t % R, :], hsum[:, t % R, :], 1.0 / HD, E3, ALU.mult, ALU.add).then_inc(m["hvar_done"], 1)
                            pool.wait_ge(m["hvar_done"], seen(i, T, t + 1))
                            pool.tensor_tensor(hrs[:, t % R, :], hsum[:, t % R, :], mhalf[:], ALU.pow).then_inc(m["hrs_done"], 1)
                        if 2 <= st < GT + 2:
                            t = g * GT + st - 2
                            pool.wait_ge(m["scaled"], seen(i, T, t + 1))
                            for n, step in enumerate(("gam_done", "bet_done")):
                                for j in range(2):
                                    part = qk[:, t % R, j * H:(j + 1) * H, :]
                                    by = gb[:, n, j, :].unsqueeze(1).to_broadcast([P, H, HD])
                                    pool.tensor_tensor(part, part, by, ALU.add if n else ALU.mult).then_inc(m[step], 1)
                                pool.wait_ge(m[step], seen(i, 2 * T, 2 * t + 2))

        @block.scalar
        def _(act):
            for n in range(NW):
                act.wait_ge(w_turned, n + 1)
                to = wT[:, WQ:WPJ].rearrange("p (c o) -> p c o", c=KD) if n < NW - KD else \
                    wT[:, WPJ:WBI].rearrange("p (c o) -> p c o", c=KD)
                at = (n if n < NW - KD else n - (NW - KD)) * P
                act.activation(to[:, :, at:at + P], bank[n % 2][:, 0:KD * P].rearrange("p (c o) -> p c o", c=KD),
                               ACT.Copy, scale=WS).then_inc(w_copied, 1)

            def exp(i, n):
                act.wait_ge(m["sT_done"], seen(i, QUADS * EU, n + 1))
                if n >= NP_:
                    act.wait_ge(m["av_done"], seen(i, QUADS * EU, n - NP_ + 1))
                act.activation(prob[:, n % NP_, :], bank[4 + n % 2][:], ACT.Exp).then_inc(m["exp_done"], 1)

            act.wait_ge(consts, 9)
            act.wait_ge(w_ready, 2)
            with act.Fori(0, BATCH) as i:
                for g in range(G2):
                    act.wait_ge(m["turned"], seen(i, G2, g + 1))
                    if g:
                        act.wait_ge(m["qkv_done"], seen(i, T, g * GT))
                    for c in range(KD):
                        ins = act.activation(xhi[:, c, :], bank[c][:], ACT.Copy)
                    ins.then_inc(m["xhi_done"], 1)
                    for st in range(GT + 5):
                        if st < GT:
                            t = g * GT + st
                            act.wait_ge(m["qkv_done"], seen(i, T, t + 1))
                            if t >= R:
                                act.wait_ge(m["lo_done"], seen(i, T, t - R + 1))
                            act.activation(qk[:, t % R, :, :], bank[2 + t % 2][:].rearrange("p (h f) -> p h f", h=HK), ACT.Copy,
                                           scale=1.0 / WS).then_inc(m["qk_copied"], 1)
                            for parity in range(2):
                                src = bank[4][:, 0:D].rearrange("p (a b j f) -> p b a j f", a=2, b=2, j=FOUR)[:, parity]
                                ins = act.activation(v_view(t, parity, 0), src, ACT.Copy, scale=1.0 / WS)
                            ins.then_inc(m["v_copied"], 1)
                        if 1 <= st < GT + 1:
                            t = g * GT + st - 1
                            act.wait_ge(m["cen_done"], seen(i, T, t + 1))
                            act.activation(work[:, t % 2], qk[:, t % R], ACT.Square).then_inc(m["sq_done"], 1)
                        if 3 <= st < GT + 3:
                            t = g * GT + st - 3
                            act.wait_ge(m["rope_done"], seen(i, T, t + 1))
                            if t >= 2:
                                act.wait_ge(m["turn2"], seen(i, 2 * T, 2 * (t - 1)))
                            for n in (0, 2):
                                act.activation(qa[:, t, :, n, :], qk[:, t % R, 0:H, :], ACT.Copy)
                            for n in (0, 1):
                                ins = act.activation(ka[:, t % 2, :, n, :], qk[:, t % R, H:HK, :], ACT.Copy)
                            ins.then_inc(m["hi_done"], 1)
                        if 5 <= st < GT + 5:
                            t = g * GT + st - 5
                            act.wait_ge(m["turn2"], seen(i, 2 * T, 2 * t + 1))
                            act.activation(kT[:, :, t * P:(t + 1) * P], bank16[5].rearrange("p (h t) -> p h t", h=PAIRS),
                                           ACT.Copy).then_inc(m["kT_done"], 1)
                for d in range(QUADS):
                    for p in range(2 * d, 2 * d + 2):
                        act.wait_ge(m["mturn"], seen(i, PAIRS, p + 1))
                        for h in range(2):
                            r = slice(h * AW, (h + 1) * AW)
                            ins = act.activation(qT[r, 2 * p + h, :], bank16[6][r, :], ACT.Copy)
                        ins.then_inc(m["mq_done"], 1)
                    for v in range(EU):
                        exp(i, d * EU + v)
                for g in range(G2):
                    act.wait_ge(m["o_done"], seen(i, 2 * QUADS, 2 * QUADS))
                    if g:
                        act.wait_ge(m["y_done"], seen(i, 2 * G2, 2 * g))
                    for c in range(KD):
                        ins = act.activation(xhi[:, c, :], attn[:, c, g * GN:(g + 1) * GN], ACT.Copy)
                    ins.then_inc(m["ahi_done"], 1)
                act.wait_ge(m["y_done"], seen(i, 2 * G2, 2 * G2))

        @block.vector
        def _(dve):
            def query_max(i, d, n):
                dve.wait_ge(m["m_done"], seen(i, QUADS * MU, d * MU + n + 1))
                dve.tensor_reduce(mx[:, d % 2, n // FOUR, n % FOUR:n % FOUR + 1], pairs[n % 2][:], AX.XY, ALU.max).then_inc(m["mx_done"], 1)

            dve.wait_ge(consts, 9)
            dve.wait_ge(c_in, 16 * 8)
            with dve.Fori(0, BATCH) as i:
                for g in range(G2):
                    xg = X[:, bass.ds(i * T + g * GT, GT), :]

                    def xt(t):
                        return X[:, bass.ds(i * T + (g * GT + t), 1), :]

                    def stats_of(st, n):
                        for t in range(GT):
                            ins = dve.bn_stats(stats[:, t, :], xt(t))
                        ins.then_inc(m[st], 1)
                        wait_apart(dve, passed, m[st], seen(i, G2, g + 1))
                        for t in range(GT):
                            ins = dve.bn_aggr(mv[:, t, :], stats[:, t, :])
                        ins.then_inc(m[n], 1)

                    stats_of("st1", "mv1")
                    dve.wait_ge(m["rs1"], seen(i, G2, g + 1))
                    for t in range(GT):
                        ins = dve.tensor_scalar(xt(t), xt(t), mv[:, t, 0:1], rstd[:, t:t + 1], ALU.subtract, ALU.mult)
                    ins.then_inc(m["n1"], 1)
                    dve.wait_ge(m["n1"], seen(i, G2, g + 1))
                    for n, op in ((0, ALU.mult), (1, ALU.add)):
                        dve.tensor_tensor(xg, xg, lnf[:, n, :].unsqueeze(1).to_broadcast([P, GT, D]), op).then_inc(m["af1"], 1)
                        wait_apart(dve, passed, m["af1"], seen(i, 2 * G2, 2 * g + n + 1))
                    stats_of("st2", "mv2")
                    dve.wait_ge(m["rs2"], seen(i, G2, g + 1))
                    if g:
                        dve.wait_ge(m["turned"], seen(i, G2, g))
                    for t in range(GT):
                        ins = dve.tensor_scalar(xn[:, t, :], xt(t), mv[:, t, 0:1], rstd[:, t:t + 1], ALU.subtract, ALU.mult)
                    ins.then_inc(m["xn_done"], 1)
                    dve.wait_ge(m["xhi_done"], seen(i, G2, g + 1))
                    for c in range(KD):
                        ins = dve.tensor_tensor(xlo[:, c, :], bank[c][:], xhi[:, c, :], ALU.subtract)
                    ins.then_inc(m["xlo_done"], 1)
                    for st in range(GT + 5):
                        if st < GT:
                            t = g * GT + st
                            q = qk[:, t % R]
                            dve.wait_ge(m["qk_copied"], seen(i, T, t + 1))
                            dve.tensor_reduce(hsum[:, t % R, :], q, AX.X, ALU.add).then_inc(m["sum_done"], 1)
                            dve.wait_ge(m["sum_done"], seen(i, 2 * T, 2 * t + 1))
                            dve.tensor_scalar(hsum[:, t % R, :], hsum[:, t % R, :], 1.0 / HD, None, ALU.mult).then_inc(m["sum_done"], 1)
                            dve.wait_ge(m["sum_done"], seen(i, 2 * T, 2 * t + 2))
                            dve.tensor_tensor(q, q, hsum[:, t % R, :].unsqueeze(2).to_broadcast([P, HK, HD]), ALU.subtract).then_inc(m["cen_done"], 1)
                        if 1 <= st < GT + 1:
                            t = g * GT + st - 1
                            dve.wait_ge(m["sq_done"], seen(i, T, t + 1))
                            dve.tensor_reduce(hsum[:, t % R, :], work[:, t % 2], AX.X, ALU.add).then_inc(m["sum2_done"], 1)
                        if 2 <= st < GT + 2:
                            t = g * GT + st - 2
                            q = qk[:, t % R]
                            dve.wait_ge(m["hrs_done"], seen(i, T, t + 1))
                            dve.tensor_tensor(q, q, hrs[:, t % R, :].unsqueeze(2).to_broadcast([P, HK, HD]), ALU.mult).then_inc(m["scaled"], 1)
                        if 3 <= st < GT + 3:
                            t = g * GT + st - 3
                            q = qk[:, t % R]
                            dve.wait_ge(m["bet_done"], seen(i, 2 * T, 2 * t + 2))
                            if t:
                                dve.wait_ge(m["rope_done"], seen(i, T, t))
                            half = HD // 2
                            for n in range(2):
                                to, frm = slice(n * half, (n + 1) * half), slice((1 - n) * half, (2 - n) * half)
                                ins = dve.tensor_tensor(rot[:, :, to], q[:, :, frm], sin[:, t, to].unsqueeze(1).to_broadcast([P, HK, half]), ALU.mult)
                            ins.then_inc(m["rope1"], 1)
                            dve.wait_ge(m["rope1"], seen(i, 2 * T, 2 * t + 1))
                            dve.tensor_tensor(q, q, cos[:, t, :].unsqueeze(1).to_broadcast([P, HK, HD]), ALU.mult).then_inc(m["rope1"], 1)
                            dve.wait_ge(m["rope1"], seen(i, 2 * T, 2 * t + 2))
                            dve.tensor_tensor(q, q, rot[:], ALU.add).then_inc(m["rope_done"], 1)
                        if 4 <= st < GT + 4:
                            t = g * GT + st - 4
                            dve.wait_ge(m["hi_done"], seen(i, T, t + 1))
                            dve.tensor_tensor(qa[:, t, :, 1, :], qk[:, t % R, 0:H, :], qa[:, t, :, 0, :], ALU.subtract)
                            dve.tensor_tensor(ka[:, t % 2, :, 2, :], qk[:, t % R, H:HK, :], ka[:, t % 2, :, 0, :], ALU.subtract).then_inc(m["lo_done"], 1)
                        if 5 <= st < GT + 5:
                            t = g * GT + st - 5
                            dve.wait_ge(m["turn2"], seen(i, 2 * T, 2 * t + 2))
                            for h in range(2):
                                r = slice(h * AW, (h + 1) * AW)
                                ins = dve.tensor_copy(qT[r, h::2, t * P:(t + 1) * P], bank16[6][r, :].rearrange("p (h t) -> p h t", h=PAIRS))
                            ins.then_inc(m["qT_done"], 1)

                def new_rows(d):
                    dve.wait_ge(m["mx_done"], seen(i, QUADS * MU, (d + 1) * MU))
                    dve.tensor_scalar(qa[:, :, FOUR * d:FOUR * (d + 1), 3, 0], mx[:, d % 2], -1.0, None, ALU.mult).then_inc(m["qmx_done"], 1)

                for n in range(MU):
                    query_max(i, 0, n)
                new_rows(0)
                for d in range(QUADS):
                    for half in range(2):
                        if d + 1 < QUADS:
                            for n in (range(M_SPLIT) if half == 0 else range(M_SPLIT, MU)):
                                query_max(i, d + 1, n)
                            if half == 1:
                                new_rows(d + 1)
                        n = 2 * d + half
                        dve.wait_ge(m["av_done"], seen(i, QUADS * EU, (n + 1) * EU // 2))
                        val, den = slice(64 * (d % 2), 64 * (d % 2) + 64), slice(64 * (1 - d % 2), 64 * (1 - d % 2) + 64)
                        dve.reciprocal(rden[val, :], bank[7][den, :]).then_inc(m["rd_done"], 1)
                        dve.wait_ge(m["rd_done"], seen(i, 2 * QUADS, n + 1))
                        dve.tensor_tensor(attn[val, d // 2, half * GN:(half + 1) * GN], bank[7][val, :], rden[val, :], ALU.mult).then_inc(m["o_done"], 1)
                for g in range(G2):
                    dve.wait_ge(m["ahi_done"], seen(i, G2, g + 1))
                    for c in range(KD):
                        ins = dve.tensor_tensor(xlo[:, c, :], attn[:, c, g * GN:(g + 1) * GN], xhi[:, c, :], ALU.subtract)
                    ins.then_inc(m["alo_done"], 1)
                    for half in range(2):
                        dve.wait_ge(m["y_done"], seen(i, 2 * G2, 2 * g + half + 1))
                        x = X[:, bass.ds(i * T + (g * GT + 2 * half), 2), :]
                        dve.scalar_tensor_tensor(out=x, in0=bank[2 + half][:].rearrange("p (t d) -> p t d", t=2), scalar=1.0 / WS, in1=x,
                                                 op0=ALU.mult, op1=ALU.add).then_inc(m["y_added"], 1)

        @block.tensor
        def _(pe):
            pe.wait_ge(w_in, 48)
            for n in range(NW):
                src = wq_raw[:, n, :] if n < NW - KD else wp_raw[:, n - (NW - KD), :]
                if n >= 2:
                    pe.wait_ge(w_copied, n - 1)
                for c in range(KD):
                    ins = pe.transpose(bank[n % 2][:, c * P:(c + 1) * P], src[:, c * P:(c + 1) * P], ident[:])
                ins.then_inc(w_turned, 1)
            pe.wait_ge(consts, 9)
            pe.wait_ge(w_ready, 2)
            wq_h = wThi[:, WQ:WPJ].rearrange("p (c o) -> p c o", c=KD)
            wq_l = wTlo[:, WQ:WPJ].rearrange("p (c o) -> p c o", c=KD)
            wp_h = wThi[:, WPJ:WBI].rearrange("p (c o) -> p c o", c=KD)
            wp_l = wTlo[:, WPJ:WBI].rearrange("p (c o) -> p c o", c=KD)

            def dense(out, tok, w_h, w_l, cols, start=True):
                for c in range(KD):
                    pe.matmul(out, xhi[:, c, tok], w_h[:, c, cols], start=start and c == 0, stop=False)
                    pe.matmul(out, xhi[:, c, tok], w_l[:, c, cols], start=False, stop=False)
                    ins = pe.matmul(out, xlo[:, c, tok], w_h[:, c, cols], start=False, stop=c == KD - 1)
                return ins

            def max_scores(i, d, n):
                t, h = n // FOUR, FOUR * d + n % FOUR
                if d or n >= 2:
                    pe.wait_ge(m["mx_done"], seen(i, QUADS * MU, d * MU + n - 1))
                for half in range(2):
                    ins = pe.matmul(pairs[n % 2][:, half, :], qT[:, h, t * P:(t + 1) * P], kT[:, h // 2, half * GN:(half + 1) * GN],
                                    start=True, stop=True)
                ins.then_inc(m["m_done"], 1)

            def turn_q(i, d):
                pe.wait_ge(m["qmx_done"], seen(i, QUADS, d + 1))
                for p in range(2 * d, 2 * d + 2):
                    if p:
                        pe.wait_ge(m["mq_done"], seen(i, PAIRS, p))
                    for t in range(T):
                        ins = pe.transpose(bank16[6][:, t * P:(t + 1) * P], qa[:, t, 2 * p:2 * p + 2, :, :].rearrange("p h a f -> p (h a f)"), ident16[:])
                    ins.then_inc(m["mturn"], 1)

            def scores(i, n):
                d, half, h, kt = n // EU, n // (EU // 2) % 2, n // T % FOUR, n % T
                h += FOUR * d
                if n >= 2:
                    pe.wait_ge(m["exp_done"], seen(i, QUADS * EU, n - 1))
                pe.matmul(bank[4 + n % 2], kT[:, h // 2, kt * P:(kt + 1) * P], qT[:, h, half * GN:(half + 1) * GN],
                          start=True, stop=True).then_inc(m["sT_done"], 1)

            def values(i, n):
                d, h, kt = n // EU, n // T % FOUR, n % T
                first, last = n % (EU // 2) == 0, n % (EU // 2) == EU // 2 - 1
                if first and n:
                    pe.wait_ge(m["o_done"], seen(i, 2 * QUADS, n // (EU // 2)))
                pe.wait_ge(m["exp_done"], seen(i, QUADS * EU, n + 1))
                pe.matmul(bank[7], v1[:, kt, FOUR * d + h, :], prob[:, n % NP_, :], start=first, stop=last).then_inc(m["av_done"], 1)

            with pe.Fori(0, BATCH) as i:
                for g in range(G2):
                    pe.wait_ge(m["xn_done"], seen(i, G2, g + 1))
                    if g:
                        pe.wait_ge(m["xlo_done"], seen(i, G2, g))
                    for c in range(KD):
                        for t in range(GT):
                            ins = pe.transpose(bank[c][:, t * P:(t + 1) * P], xn[:, t, c * P:(c + 1) * P], ident[:])
                    ins.then_inc(m["turned"], 1)
                    pe.wait_ge(m["xlo_done"], seen(i, G2, g + 1))
                    for st in range(GT + 4):
                        if st < GT:
                            t = g * GT + st
                            if t >= 2:
                                pe.wait_ge(m["qk_copied"], seen(i, T, t - 1))
                            tok = slice(st * P, (st + 1) * P)
                            dense(bank[2 + t % 2], tok, wq_h, wq_l, slice(0, 2 * D))
                            if t:
                                pe.wait_ge(m["v_copied"], seen(i, T, t))
                            dense(bank[4][:, 0:D], tok, wq_h, wq_l, slice(2 * D, 3 * D)).then_inc(m["qkv_done"], 1)
                        if 4 <= st:
                            t = g * GT + st - 4
                            pe.wait_ge(m["lo_done"], seen(i, T, t + 1))
                            if t:
                                pe.wait_ge(m["kT_done"], seen(i, T, t))
                                pe.wait_ge(m["qT_done"], seen(i, T, t))
                            for src, b in ((ka[:, t % 2], 5), (qa[:, t], 6)):
                                for p in range(PAIRS):
                                    ins = pe.transpose(bank16[b][:, p * P:(p + 1) * P], src[:, 2 * p:2 * p + 2, :, :].rearrange("p h a f -> p (h a f)"), ident16[:])
                                ins.then_inc(m["turn2"], 1)
                pe.wait_ge(m["v_copied"], seen(i, T, T))
                pe.wait_ge(m["kT_done"], seen(i, T, T))
                pe.wait_ge(m["qT_done"], seen(i, T, T))
                for n in range(MU):
                    max_scores(i, 0, n)
                turn_q(i, 0)
                for d in range(QUADS):
                    pe.wait_ge(m["mq_done"], seen(i, PAIRS, 2 * d + 2))
                    for v in range(EU):
                        scores(i, d * EU + v)
                        if d + 1 < QUADS and v < 3 * MU // 2 and v % 3 != 2:
                            max_scores(i, d + 1, v - (v + 1) // 3)
                        if v >= LAG:
                            values(i, d * EU + v - LAG)
                    for v in range(EU - LAG, EU):
                        values(i, d * EU + v)
                    if d + 1 < QUADS:
                        turn_q(i, d + 1)
                for g in range(G2):
                    pe.wait_ge(m["alo_done"], seen(i, G2, g + 1))
                    for t in range(GT):
                        y = bank[2 + t // 2][:, (t % 2) * D:(t % 2 + 1) * D]
                        if g and t % 2 == 0:
                            pe.wait_ge(m["y_added"], seen(i, 2 * G2, 2 * (g - 1) + t // 2 + 1))
                        pe.matmul(y, ones16[:], wThi[0:1, WBI:WE], start=True, stop=False)
                        pe.matmul(y, ones16[:], wTlo[0:1, WBI:WE], start=False, stop=False)
                        ins = dense(y, slice(t * P, (t + 1) * P), wp_h, wp_l, slice(0, D), start=False)
                        if t % 2:
                            ins.then_inc(m["y_done"], 1)
                pe.wait_ge(m["y_added"], seen(i, 2 * G2, 2 * G2))


def experts(nc, a, X, ident, L1):
    if L1:
        gate, E, F = a["L1_ffn_Wg"], a["L1_ffn_W1"].shape[0], a["L1_ffn_W1"].shape[2]
    else:
        gate, E, F = a["L0_ffn_w_gate"], a["L0_ffn_w_gate_proj"].shape[0], a["L0_ffn_w_gate_proj"].shape[2]
    FT = F // P
    UP = 1 if L1 else 2
    EPS = 1e-5
    WU, WDN, WE = np.cumsum([0, UP * KD * F, FT * D]).tolist()
    QC = WE // NG
    HALF = 2.0 ** -23
    out_scale = 1.0 / WS if L1 else 1.0 / WS / WS
    with ExitStack() as ctx:
        s = Store(nc, ctx, "moe1_" if L1 else "moe0_")
        raw = s.sb("e_raw", [P, WE])
        whi = [s.sb(f"e_hi{j}", [P, WE], F16) for j in range(2)]
        wlo = [s.sb(f"e_lo{j}", [P, WE], F16) for j in range(2)]
        g_raw = s.sb("g_raw", [P, KD, E])
        g_hi = s.sb("g_hi", [P, KD, E], F16)
        g_lo = s.sb("g_lo", [P, KD, E], F16)
        bg = s.sb("bg", [P, E])
        iota = s.sb("iota", [P, E])
        stats = s.sb("stats", [P, GT, 6])
        mv = s.sb("mv", [P, GT, 2])
        var = s.sb("var", [P, GT])
        rstd = s.sb("rstd", [P, GT])
        mhalf = s.sb("mhalf", [P, GT])
        xn = s.sb("xn", [P, 2, GT, D])
        xhi = s.sb("xhi", [P, KD, N], F16)
        xlo = s.sb("xlo", [P, KD, N], F16)
        logit = s.sb("logit", [P, NT, E])
        prob = s.sb("prob", [P, NT, E])
        red = s.sb("red", [P, NT])
        top = s.sb("top", [P, NT, 8])
        topi = s.sb("topi", [P, NT, 8], U32)
        topf = s.sb("topf", [P, NT, 2])
        we = s.sb("we", [P, NT, E])
        b1 = s.sb("b1", [P, E, FT])
        b2r = s.sb("b2r", [P, E, D])
        b2s = s.sb("b2s", [P, E, D], F16)
        sel = s.sb("sel", [P, P], F16)
        NH = 3
        act1 = s.sb("act1", [P, NH, GN])
        hf = s.sb("hf", [P, NH, GN])
        hhi = s.sb("hhi", [P, 2, FT, GN], F16)
        hlo = s.sb("hlo", [P, 2, FT, GN], F16)
        pH = s.ps("pH", [P, 2, UP, GN])
        pT = s.ps("pT", [P, KD, GN])
        pY = s.ps("pY", [P, GT, D])
        pL = pY[:, 0:2, :].rearrange("p t d -> p (t d)")[:, 0:NT * E].rearrange("p (t e) -> p t e", e=E)

        names = ("w_in c_in g_in consts st mvd va rs xn_done turned xhi_done xlo_done g_split logits pre_w steps asteps we_ready "
                 "whi_done wlo_done h_done a_done hf_done hhi_done hlo_done y_done y_added bias_done").split()
        m = {n: s.sem(n) for n in names}
        passed = s.sem("passed")
        block = ctx.enter_context(nc.Block())
        K = 2 * NG
        NWD = 2 if L1 else 3

        def seen(i, k, each, plus=0):
            return i * (K * each) + (k * each + plus)

        def loop(eng, body):
            with eng.Fori(0, E // 2 - 1) as i:
                body(i, False)
            body(E // 2 - 1, True)

        @block.sync
        def _(sp):
            def load(e):
                def row(name):
                    return a[name][bass.ds(e, 1)]
                if L1:
                    parts = ((WU, KD, F, "L1_ffn_W1"), (WDN, FT, D, "L1_ffn_W2"))
                else:
                    parts = ((WU, KD, F, "L0_ffn_w_gate_proj"), (WU + KD * F, KD, F, "L0_ffn_w_up_proj"), (WDN, FT, D, "L0_ffn_w_down_proj"))
                for at, c, f, name in parts:
                    sp.dma_start(raw[:, at:at + c * f].rearrange("p (c f) -> p c f", c=c),
                                 row(name).rearrange("o (c p) f -> p (o c) f", p=P)).then_inc(m["w_in"], 16)

            with nc.allow_non_contiguous_dma(reason="small parameters"):
                sp.dma_start(g_raw[:], gate.rearrange("(c p) e -> p c e", p=P)).then_inc(m["g_in"], 16)
                if L1:
                    sp.dma_start(bg[:], a["L1_ffn_bg"].partition_broadcast(P)).then_inc(m["c_in"], 16)
                    sp.dma_start(b1[:], a["L1_ffn_b1"].rearrange("e (c p) -> p e c", p=P)).then_inc(m["c_in"], 16)
                    for r in (0, 32):
                        sp.dma_start(b2r[r:r + 1], a["L1_ffn_b2"].rearrange("(o e) d -> o e d", o=1)).then_inc(m["c_in"], 16)
                else:
                    sp.dma_start(iota[:], a["c_iota"].partition_broadcast(P)).then_inc(m["c_in"], 16)
            load(0)
            sp.wait_ge(m["wlo_done"], NG)
            load(1)

            def body(i, last):
                for j in range(0 if last else 2):
                    sp.wait_ge(m["wlo_done"], i * (2 * NG) + (j + 2) * NG)
                    load(i * 2 + (j + 2))
            loop(sp, body)

        @block.gpsimd
        def _(pool):
            pool.memset(mhalf[:], -0.5).then_inc(m["consts"], 1)
            pool.memset(sel[:], 0.0).then_inc(m["consts"], 1)
            pool.memset(b2s[:], 0.0).then_inc(m["consts"], 1)
            pool.wait_ge(m["consts"], 3)
            for r in (0, 32):
                ins = pool.memset(sel[r:r + 1, :], 1.0)
            ins.then_inc(m["consts"], 1)
            pool.wait_ge(m["consts"], 4)
            for g in range(NG):
                wait_apart(pool, passed, m["mvd"], g + 1)
                pool.tensor_scalar(var[:], mv[:, :, 1], EPS, None, ALU.add).then_inc(m["va"], 1)
                pool.wait_ge(m["va"], g + 1)
                pool.tensor_tensor(rstd[:], var[:], mhalf[:], ALU.pow).then_inc(m["rs"], 1)

        @block.scalar
        def _(act):
            def split_hi(e_at, j, q):
                act.wait_ge(m["w_in"], e_at[0])
                act.activation(whi[j][:, q * QC:(q + 1) * QC], raw[:, q * QC:(q + 1) * QC], ACT.Copy, scale=WS).then_inc(m["whi_done"], 1)

            for q in range(NG):
                split_hi((16 * NWD,), 0, q)
            act.wait_ge(m["g_in"], 16)
            act.activation(g_hi[:], g_raw[:], ACT.Copy, scale=WS).then_inc(m["g_split"], 1)
            for g in range(NG):
                act.wait_ge(m["turned"], g + 1)
                for c in range(KD):
                    ins = act.activation(xhi[:, c, g * GN:(g + 1) * GN], pT[:, c, :], ACT.Copy)
                ins.then_inc(m["xhi_done"], 1)
            act.wait_ge(m["pre_w"], 1)
            act.activation(prob[:], logit[:], ACT.Sigmoid if L1 else ACT.Exp).then_inc(m["asteps"], 1)

            def body(i, last):
                for k in range(K):
                    e, g, n = k // NG, k % NG, k % 2
                    for f in range(FT):
                        act.wait_ge(m["h_done"], seen(i, k, FT, f + 1))
                        if L1:
                            if k or f >= NH:
                                wait_apart(act, passed, m["hlo_done"], seen(i, k, FT, max(f - NH + 1, 0)))
                            else:
                                act.sem_inc(passed, 1)
                            act.activation(hf[:, f % NH, :], pH[:, f % 2, 0, :], ACT.Relu, scale=1.0 / WS,
                                           bias=b1[:, bass.ds(i * 2 + e, 1), f]).then_inc(m["hf_done"], 1)
                        else:
                            if f >= NH:
                                act.wait_ge(m["hf_done"], seen(i, k, FT, f - NH + 1))
                            act.activation(act1[:, f % NH, :], pH[:, f % 2, 0, :], ACT.Silu, scale=1.0 / WS).then_inc(m["a_done"], 1)
                        if f == 0 and not (last and e):
                            split_hi((i * (2 * 16 * NWD) + (e + 2) * 16 * NWD,), (e + 1) % 2, g)
                        act.wait_ge(m["hf_done"], seen(i, k, FT, f + 1))
                        if f == 0:
                            if k >= 2:
                                act.wait_ge(m["y_done"], seen(i, k - 1, 2))
                        act.activation(hhi[:, n, f, :], hf[:, f % NH, :], ACT.Copy).then_inc(m["hhi_done"], 1)
                act.wait_ge(m["hlo_done"], seen(i, K, FT))
                act.wait_ge(m["y_done"], seen(i, K, 2))
            loop(act, body)

        @block.vector
        def _(dve):
            def split_lo(at, j, q):
                dve.wait_ge(m["whi_done"], at)
                c = slice(q * QC, (q + 1) * QC)
                dve.scalar_tensor_tensor(out=wlo[j][:, c], in0=raw[:, c], scalar=WS, in1=whi[j][:, c], op0=ALU.mult,
                                         op1=ALU.subtract).then_inc(m["wlo_done"], 1)

            dve.wait_ge(m["consts"], 4)
            for g in range(NG):
                layer_stats(dve, passed, X[:, g * GT:(g + 1) * GT, :], stats, mv, m["st"], g).then_inc(m["mvd"], 1)
                dve.wait_ge(m["rs"], g + 1)
                if g >= 2:
                    dve.wait_ge(m["turned"], g - 1)
                norm_group(dve, X[:, g * GT:(g + 1) * GT, :], mv, rstd, xn[:, g % 2]).then_inc(m["xn_done"], 1)
                dve.wait_ge(m["xhi_done"], g + 1)
                for c in range(KD):
                    t = slice(g * GN, (g + 1) * GN)
                    ins = dve.tensor_tensor(xlo[:, c, t], pT[:, c, :], xhi[:, c, t], ALU.subtract)
                ins.then_inc(m["xlo_done"], 1)
            for q in range(NG):
                split_lo(q + 1, 0, q)
            dve.wait_ge(m["g_split"], 1)
            dve.scalar_tensor_tensor(out=g_lo[:], in0=g_raw[:], scalar=WS, in1=g_hi[:], op0=ALU.mult,
                                     op1=ALU.subtract).then_inc(m["g_split"], 1)
            count = [0]

            def step(ins):
                count[0] += 1
                ins.then_inc(m["steps"], 1)
                dve.wait_ge(m["steps"], count[0])

            dve.wait_ge(m["logits"], 1)
            dve.wait_ge(m["c_in"], 64 if L1 else 16)
            step(dve.tensor_scalar(logit[:], pL, 1.0 / WS, None, ALU.mult))
            if L1:
                dve.tensor_tensor(logit[:], logit[:], bg[:].unsqueeze(1).to_broadcast([P, NT, E]), ALU.add).then_inc(m["pre_w"], 1)
                dve.wait_ge(m["asteps"], 1)
                step(dve.scalar_tensor_tensor(out=we[:], in0=logit[:], scalar=HALF, in1=prob[:], op0=ALU.is_gt, op1=ALU.mult))
                for r in (0, 32):
                    ins = dve.tensor_scalar(b2r[r:r + 1], b2r[r:r + 1], WS, None, ALU.mult)
                step(ins)
                for r in (0, 32):
                    ins = dve.tensor_copy(b2s[r:r + 1], b2r[r:r + 1])
                step(ins)
                dve.tensor_tensor(b2s[32:33], b2r[32:33], b2s[32:33], ALU.subtract).then_inc(m["bias_done"], 1)
            else:
                step(dve.tensor_reduce(red[:], logit[:], AX.X, ALU.max))
                dve.tensor_tensor(logit[:], logit[:], red[:].unsqueeze(2).to_broadcast([P, NT, E]), ALU.subtract).then_inc(m["pre_w"], 1)
                dve.wait_ge(m["asteps"], 1)
                step(dve.tensor_reduce(red[:], prob[:], AX.X, ALU.add))
                step(dve.reciprocal(red[:], red[:]))
                step(dve.tensor_tensor(prob[:], prob[:], red[:].unsqueeze(2).to_broadcast([P, NT, E]), ALU.mult))
                for t in range(NT):
                    ins = dve.max(top[:, t, :], prob[:, t, :])
                step(ins)
                for t in range(NT):
                    ins = dve.max_index(topi[:, t, :], top[:, t, :], prob[:, t, :])
                step(ins)
                step(dve.tensor_copy(topf[:], topi[:, :, 0:2]))
                step(dve.tensor_tensor(red[:], top[:, :, 0], top[:, :, 1], ALU.add))
                step(dve.reciprocal(red[:], red[:]))
                step(dve.tensor_tensor(top[:, :, 0:2], top[:, :, 0:2], red[:].unsqueeze(2).to_broadcast([P, NT, 2]), ALU.mult))
                for t in range(NT):
                    dve.tensor_scalar(we[:, t, :], iota[:], topf[:, t, 0:1], top[:, t, 0:1], ALU.is_equal, ALU.mult)
                    ins = dve.tensor_scalar(logit[:, t, :], iota[:], topf[:, t, 1:2], top[:, t, 1:2], ALU.is_equal, ALU.mult)
                step(ins)
                step(dve.tensor_tensor(we[:], we[:], logit[:], ALU.add))
            step(dve.tensor_scalar(we[:], we[:], out_scale, None, ALU.mult))

            def body(i, last):
                def add(k):
                    e, g = k // NG, k % NG
                    for t in range(GT):
                        if t % 2 == 0:
                            dve.wait_ge(m["y_done"], seen(i, k, 2, t // 2 + 1))
                        x = X[:, g * GT + t, :]
                        ins = dve.scalar_tensor_tensor(out=x, in0=pY[:, t, :], scalar=we[:, g * GT + t, bass.ds(i * 2 + e, 1)], in1=x,
                                                       op0=ALU.mult, op1=ALU.add)
                        if t % 2 == 1:
                            ins.then_inc(m["y_added"], 1)

                for k in range(K):
                    e, g, n = k // NG, k % NG, k % 2
                    for f in range(FT):
                        if not L1:
                            dve.wait_ge(m["a_done"], seen(i, k, FT, f + 1))
                            if k or f >= NH:
                                dve.wait_ge(m["hlo_done"], seen(i, k, FT, max(f - NH + 1, 0)))
                            dve.tensor_tensor(hf[:, f % NH, :], pH[:, f % 2, 1, :], act1[:, f % NH, :], ALU.mult).then_inc(m["hf_done"], 1)
                        if f == 0 and k:
                            add(k - 1)
                        if f == 1 and not (last and e):
                            split_lo(i * (2 * NG) + (e + 1) * NG + g + 1, (e + 1) % 2, g)
                        dve.wait_ge(m["hhi_done"], seen(i, k, FT, f + 1))
                        dve.tensor_tensor(hlo[:, n, f, :], hf[:, f % NH, :], hhi[:, n, f, :], ALU.subtract).then_inc(m["hlo_done"], 1)
                add(K - 1)
                dve.wait_ge(m["hlo_done"], seen(i, K, FT))
            loop(dve, body)

        @block.tensor
        def _(pe):
            pe.wait_ge(m["consts"], 4)
            for g in range(NG):
                pe.wait_ge(m["xn_done"], g + 1)
                if g:
                    pe.wait_ge(m["xlo_done"], g)
                for c in range(KD):
                    for t in range(GT):
                        ins = pe.transpose(pT[:, c, t * P:(t + 1) * P], xn[:, g % 2, t, c * P:(c + 1) * P], ident[:])
                ins.then_inc(m["turned"], 1)
            pe.wait_ge(m["xlo_done"], NG)
            pe.wait_ge(m["g_split"], 2)
            for t in range(NT):
                tok = slice(t * P, (t + 1) * P)
                for c in range(KD):
                    pe.matmul(pL[:, t, :], xhi[:, c, tok], g_hi[:, c, :], start=(c == 0), stop=False)
                    pe.matmul(pL[:, t, :], xhi[:, c, tok], g_lo[:, c, :], start=False, stop=False)
                    ins = pe.matmul(pL[:, t, :], xlo[:, c, tok], g_hi[:, c, :], start=False, stop=(c == KD - 1))
            ins.then_inc(m["logits"], 1)
            pe.wait_ge(m["pre_w"], 1)
            if L1:
                pe.wait_ge(m["bias_done"], 1)

            def body(i, last):
                for k in range(K):
                    e, g, n = k // NG, k % NG, k % 2
                    if g == 0:
                        pe.wait_ge(m["wlo_done"], i * (2 * NG) + (e + 1) * NG)
                    tok = slice(g * GN, (g + 1) * GN)
                    for f in range(FT):
                        if k or f >= 2:
                            pe.wait_ge(m["hf_done"], seen(i, k, FT, max(f - 1, 0)))
                        for u in range(UP):
                            out = pH[:, f % 2, u, :]
                            for c in range(KD):
                                at = WU + u * KD * F + c * F + f * P
                                w_h, w_l = whi[e][:, at:at + P], wlo[e][:, at:at + P]
                                pe.matmul(out, w_h, xhi[:, c, tok], start=(c == 0), stop=False)
                                pe.matmul(out, w_h, xlo[:, c, tok], start=False, stop=False)
                                ins = pe.matmul(out, w_l, xhi[:, c, tok], start=False, stop=(c == KD - 1))
                        ins.then_inc(m["h_done"], 1)
                    if k:
                        pe.wait_ge(m["y_added"], seen(i, k, 2))
                    if L1:
                        for t in range(GT):
                            pe.matmul(pY[:, t, :], sel[:], b2s[:, bass.ds(i * 2 + e, 1), :].rearrange("p o d -> p (o d)"),
                                      start=(t % 2 == 0), stop=False, skip_group_check=True)
                    for f in range(FT):
                        pe.wait_ge(m["hlo_done"], seen(i, k, FT, f + 1))
                        w = slice(WDN + f * D, WDN + (f + 1) * D)
                        for t in range(GT):
                            ts = slice(t * P, (t + 1) * P)
                            pe.matmul(pY[:, t, :], hhi[:, n, f, ts], whi[e][:, w], start=(f == 0 and t % 2 == 0 and not L1), stop=False,
                                      skip_group_check=True)
                            pe.matmul(pY[:, t, :], hhi[:, n, f, ts], wlo[e][:, w], start=False, stop=False, skip_group_check=True)
                            ins = pe.matmul(pY[:, t, :], hlo[:, n, f, ts], whi[e][:, w], start=False, stop=(f == FT - 1 and t % 2 == 1),
                                            skip_group_check=True)
                            if f == FT - 1 and t % 2 == 1:
                                ins.then_inc(m["y_done"], 1)
                pe.wait_ge(m["hf_done"], seen(i, K, FT))
                pe.wait_ge(m["y_added"], seen(i, K, 2))
            loop(pe, body)


def retention(nc, a, X, ident, ident16):
    H, HD = 16, D // 16
    PAIRS = H // 2
    OCT = 2
    T = SEQ // P
    G2 = T // GT
    EPS = 1e-5
    AW = 4 * HD
    HK = 2 * H
    LAST = 11
    with ExitStack() as ctx:
        s = Store(nc, ctx, "ret_")
        w_raw = s.sb("w_raw", [P, 3 * KD, D])
        WQ, WO, WE = np.cumsum([0, KD * 3 * D, KD * D]).tolist()
        wT = s.sb("wT", [P, WE])
        wThi = s.sb("wThi", [P, WE], F16)
        wTlo = s.sb("wTlo", [P, WE], F16)
        gnp = s.sb("gnp", [P, 2, D])
        cos = s.sb("cos", [P, T, HD])
        sin = s.sb("sin", [P, T, HD])
        dmask = s.sb("dmask", [P, H, P])
        dq = s.sb("dq", [P, H])
        dk = s.sb("dk", [P, H])
        dstate = s.sb("dstate", [P, OCT])
        blocks = s.sb("blocks", [P, P])
        mhalf = s.sb("mhalf", [P, HK])
        stats = s.sb("stats", [P, GT, 6])
        mv = s.sb("mv", [P, GT, 2])
        var = s.sb("var", [P, GT])
        rstd = s.sb("rstd", [P, GT])
        xn = s.sb("xn", [P, GT, D])
        xhi = s.sb("xhi", [P, KD, SEQ], F16)
        xlo = s.sb("xlo", [P, KD, SEQ], F16)
        qk = s.sb("qk", [P, 4, HK, HD])
        rot = s.sb("rot", [P, HK, HD])
        v = s.sb("v", [P, 3, D])
        vhi = s.sb("vhi", [P, 8, D], F16)
        vlo = s.sb("vlo", [P, 8, D], F16)
        qd = s.sb("qd", [P, 3, H, HD])
        kd = s.sb("kd", [P, 3, H, HD])
        kdhi = s.sb("kdhi", [P, 6, D], F16)
        kdlo = s.sb("kdlo", [P, 6, D], F16)
        qa = s.sb("qa", [P, 2, H, 4, HD], F16)
        ka = s.sb("ka", [P, 2, H, 4, HD], F16)
        kT = s.sb("kT", [P, 2, PAIRS, P], F16)
        qT = s.sb("qT", [P, 2, H, P], F16)
        qdhi = s.sb("qdhi", [P, 4, OCT, P], F16)
        qdlo = s.sb("qdlo", [P, 4, OCT, P], F16)
        am = s.sb("am", [P, H, P])
        ahi = s.sb("ahi", [P, 3, H, P], F16)
        alo = s.sb("alo", [P, 3, H, P], F16)
        st = s.sb("st", [P, OCT, P])
        stx = s.sb("stx", [P, OCT, P])
        sthi = s.sb("sthi", [P, OCT, P], F16)
        stlo = s.sb("stlo", [P, OCT, P], F16)
        r = s.sb("r", [P, 4, H, HD])
        rsq = s.sb("rsq", [P, 2, H, HD])
        hsum = s.sb("hsum", [P, 2, H])
        hsq = s.sb("hsq", [P, 2, H])
        hvar = s.sb("hvar", [P, 2, H])
        rhi = s.sb("rhi", [P, 2, OCT, P], F16)
        rlo = s.sb("rlo", [P, 2, OCT, P], F16)
        bank = [s.ps(f"bank{n}", [P, GN])[:] for n in range(8)]
        bank16 = [b.bitcast(F16) for b in bank]
        QK, VY, KA, QA, SC, QD, RO = 0, 1, 2, 3, 4, 6, 7

        w_in, wo_in, c_in = s.sem("w_in"), s.sem("wo_in"), s.sem("c_in")
        consts, w_turned, w_copied, w_ready = (s.sem(n) for n in ("consts", "w_turned", "w_copied", "w_ready"))
        names = ("stx mvd va rs xn_done turned xhi_done xlo_done qkv_done qk_copied v_copied vhi_done vlo_done rot_done cos_done "
                 "rope_done qd_done kd_done hi_done kdhi_done kdlo_done lo_done ka_turned qa_turned qd_turned kT_done qT_done "
                 "qdhi_done qdlo_done sc_done am_done ahi_done alo_done out_done s1 s2 sthi_done stlo_done r_copied sum_done mean_done "
                 "cen_done sq_done sum2_done hvar_done hrs_done scaled gam_done bet_done r_turned rhi_done rlo_done y_done y_added").split()
        m = {n: s.sem(n) for n in names}
        passed = s.sem("passed")
        block = ctx.enter_context(nc.Block())
        NW = 3 * D // P
        SR = 4

        def after(eng, i, name, t, each=1, part=None):
            eng.wait_ge(m[name], i * (T * each) + (t * each + (each if part is None else part)))

        def parts(s_, lag):
            return s_ - lag if 0 <= s_ - lag < T else None

        @block.sync
        def _(sp):
            for n, name in enumerate(("WQ", "WK", "WV")):
                w = a["L1_attn_" + name].rearrange("h u d -> (h u) d")
                sp.dma_start(w_raw[:, n * KD:(n + 1) * KD, :], w.rearrange("(t p) c -> p t c", p=P)).then_inc(w_in, 16)
            sp.dma_start(wT[:, WO:WE].rearrange("p (c d) -> p c d", c=KD), a["L1_attn_WO"].rearrange("(c p) d -> p c d", p=P)).then_inc(wo_in, 16)
            sp.dma_start(gnp[:, 0, :], a["L1_attn_gamma"].partition_broadcast(P)).then_inc(c_in, 16)
            sp.dma_start(gnp[:, 1, :], a["L1_attn_beta"].partition_broadcast(P)).then_inc(c_in, 16)
            for dst, name in ((cos, "c_cos1"), (sin, "c_sin1")):
                sp.dma_start(dst[:], a[name].rearrange("(t p) f -> p t f", p=P)).then_inc(c_in, 16)
            for dst, name in ((dmask, "c_dmask"), (dq, "c_dq"), (dk, "c_dk"), (dstate, "c_dstate"), (blocks, "c_blocks")):
                sp.dma_start(dst[:], a[name]).then_inc(c_in, 16)

        @block.gpsimd
        def _(pool):
            pool.memset(mhalf[:], -0.5).then_inc(consts, 1)
            pool.memset(qa[:, :, :, 3, :], 0.0).then_inc(consts, 1)
            pool.memset(ka[:, :, :, 3, :], 0.0).then_inc(consts, 1)
            pool.memset(qT[:], 0.0).then_inc(consts, 1)
            pool.wait_ge(consts, 4)
            pool.wait_ge(c_in, 16 * 9)

            with pool.Fori(0, BATCH) as i:
                for g in range(G2):
                    wait_apart(pool, passed, m["mvd"], i * G2 + (g + 1))
                    pool.tensor_scalar(var[:], mv[:, :, 1], EPS, None, ALU.add).then_inc(m["va"], 1)
                    pool.wait_ge(m["va"], i * G2 + (g + 1))
                    pool.tensor_tensor(rstd[:], var[:], mhalf[:, 0:GT], ALU.pow).then_inc(m["rs"], 1)
                for s_ in range(T + LAST + 1):
                    t = parts(s_, 8)
                    if t is not None:
                        after(pool, i, "sum2_done", t)
                        if t >= 2:
                            after(pool, i, "scaled", t - 2)
                        pool.sem_inc(passed, 1)
                        pool.tensor_scalar(hvar[:, t % 2], hsq[:, t % 2], 1.0 / HD, EPS, ALU.mult, ALU.add).then_inc(m["hvar_done"], 1)
                        after(pool, i, "hvar_done", t)
                        pool.tensor_tensor(hvar[:, t % 2], hvar[:, t % 2], mhalf[:, 0:H], ALU.pow).then_inc(m["hrs_done"], 1)
                    t = parts(s_, 9)
                    if t is not None:
                        after(pool, i, "scaled", t)
                        part = r[:, t % 4].rearrange("p h f -> p (h f)")
                        pool.tensor_tensor(part, part, gnp[:, 0, :], ALU.mult).then_inc(m["gam_done"], 1)
                        after(pool, i, "gam_done", t)
                        pool.tensor_tensor(part, part, gnp[:, 1, :], ALU.add).then_inc(m["bet_done"], 1)
                    t = parts(s_, 2)
                    if t is not None:
                        after(pool, i, "rope_done", t)
                        if t >= 3:
                            after(pool, i, "qd_turned", t - 3)
                            after(pool, i, "kdlo_done", t - 3)
                        pool.tensor_tensor(qd[:, t % 3], qk[:, t % 4, 0:H, :], dq[:].unsqueeze(2).to_broadcast([P, H, HD]), ALU.mult).then_inc(m["qd_done"], 1)
                        pool.tensor_tensor(kd[:, t % 3], qk[:, t % 4, H:HK, :], dk[:].unsqueeze(2).to_broadcast([P, H, HD]), ALU.mult).then_inc(m["kd_done"], 1)
                        after(pool, i, "vhi_done", t)
                        pool.tensor_tensor(vlo[:, t % 8, :], v[:, t % 3, :], vhi[:, t % 8, :], ALU.subtract).then_inc(m["vlo_done"], 1)
                    t = parts(s_, 3)
                    if t is not None:
                        after(pool, i, "kdhi_done", t)
                        pool.tensor_tensor(kdlo[:, t % 6, :], kd[:, t % 3].rearrange("p h f -> p (h f)"), kdhi[:, t % 6, :], ALU.subtract).then_inc(m["kdlo_done"], 1)

        @block.scalar
        def _(act):
            for n in range(NW):
                act.wait_ge(w_turned, n + 1)
                act.activation(wT[:, WQ:WO].rearrange("p (c o) -> p c o", c=KD)[:, :, n * P:(n + 1) * P],
                               bank[n % 2][:, 0:KD * P].rearrange("p (c o) -> p c o", c=KD), ACT.Copy).then_inc(w_copied, 1)
            act.wait_ge(w_copied, NW)
            act.wait_ge(wo_in, 16)
            act.activation(wThi[:], wT[:], ACT.Copy, scale=WS).then_inc(w_ready, 1)
            act.wait_ge(consts, 4)

            with act.Fori(0, BATCH) as i:
                for g in range(G2):
                    act.wait_ge(m["turned"], i * G2 + (g + 1))
                    for c in range(KD):
                        ins = act.activation(xhi[:, c, g * GN:(g + 1) * GN], bank[c], ACT.Copy)
                    ins.then_inc(m["xhi_done"], 1)
                for s_ in range(T + LAST + 1):
                    t = parts(s_, 4)
                    if t is not None:
                        after(act, i, "ka_turned", t)
                        if t >= 2:
                            after(act, i, "sc_done", t - 2, SR)
                        act.activation(kT[:, t % 2], bank16[KA].rearrange("p (h t) -> p h t", h=PAIRS), ACT.Copy).then_inc(m["kT_done"], 1)
                        after(act, i, "qd_turned", t)
                        act.activation(qdhi[:, t % 4], bank[QD][:, 0:OCT * P].rearrange("p (c t) -> p c t", c=OCT), ACT.Copy).then_inc(m["qdhi_done"], 1)
                    t = parts(s_, 10)
                    if t is not None:
                        after(act, i, "r_turned", t)
                        if t >= 2:
                            after(act, i, "y_done", t - 2)
                        act.activation(rhi[:, t % 2], bank[QK][:, 0:D].rearrange("p (c t) -> p c t", c=OCT), ACT.Copy).then_inc(m["rhi_done"], 1)
                    t = parts(s_, 6)
                    if t is not None:
                        after(act, i, "out_done", t)
                        act.activation(r[:, t % 4], bank[RO][:, 0:D].rearrange("p (h f) -> p h f", h=H), ACT.Copy).then_inc(m["r_copied"], 1)
                        after(act, i, "s2", t)
                        act.activation(sthi[:], st[:], ACT.Copy).then_inc(m["sthi_done"], 1)
                    t = parts(s_, 2)
                    if t is not None:
                        after(act, i, "rope_done", t)
                        if t >= 2:
                            after(act, i, "ka_turned", t - 2)
                            after(act, i, "qa_turned", t - 2)
                        for n in (0, 2):
                            act.activation(qa[:, t % 2, :, n, :], qk[:, t % 4, 0:H, :], ACT.Copy)
                        for n in (0, 1):
                            ins = act.activation(ka[:, t % 2, :, n, :], qk[:, t % 4, H:HK, :], ACT.Copy)
                        ins.then_inc(m["hi_done"], 1)
                    t = parts(s_, 3)
                    if t is not None:
                        after(act, i, "kd_done", t)
                        act.activation(kdhi[:, t % 6, :], kd[:, t % 3].rearrange("p h f -> p (h f)"), ACT.Copy).then_inc(m["kdhi_done"], 1)
                    t = parts(s_, 7)
                    if t is not None:
                        after(act, i, "cen_done", t)
                        act.activation(rsq[:, t % 2], r[:, t % 4], ACT.Square).then_inc(m["sq_done"], 1)
                    t = parts(s_, 0)
                    if t is not None:
                        after(act, i, "qkv_done", t)
                        if t >= 4:
                            after(act, i, "lo_done", t - 4)
                            after(act, i, "kd_done", t - 4)
                        act.activation(qk[:, t % 4], bank[QK].rearrange("p (h f) -> p h f", h=HK), ACT.Copy, scale=1.0 / WS).then_inc(m["qk_copied"], 1)
                        if t >= 3:
                            after(act, i, "vlo_done", t - 3)
                        act.activation(v[:, t % 3, :], bank[VY][:, 0:D], ACT.Copy, scale=1.0 / WS).then_inc(m["v_copied"], 1)
                        after(act, i, "v_copied", t)
                        act.activation(vhi[:, t % 8, :], v[:, t % 3, :], ACT.Copy).then_inc(m["vhi_done"], 1)
                    t = parts(s_, 4)
                    if t is not None:
                        for n in range(SR):
                            h = slice(n * H // SR, (n + 1) * H // SR)
                            after(act, i, "am_done", t, SR, n + 1)
                            act.activation(ahi[:, t % 3, h, :], am[:, h, :], ACT.Copy).then_inc(m["ahi_done"], 1)

        @block.vector
        def _(dve):
            dve.wait_ge(w_ready, 1)
            dve.scalar_tensor_tensor(out=wTlo[:], in0=wT[:], scalar=WS, in1=wThi[:], op0=ALU.mult, op1=ALU.subtract).then_inc(w_ready, 1)
            dve.wait_ge(consts, 4)
            dve.wait_ge(c_in, 16 * 9)
            with dve.Fori(0, BATCH) as i:
                for g in range(G2):
                    def xt(t):
                        return X[:, bass.ds(i * T + (g * GT + t), 1), :]
                    for t in range(GT):
                        ins = dve.bn_stats(stats[:, t, :], xt(t))
                    ins.then_inc(m["stx"], 1)
                    wait_apart(dve, passed, m["stx"], i * G2 + (g + 1))
                    for t in range(GT):
                        ins = dve.bn_aggr(mv[:, t, :], stats[:, t, :])
                    ins.then_inc(m["mvd"], 1)
                    dve.wait_ge(m["rs"], i * G2 + (g + 1))
                    if g:
                        dve.wait_ge(m["turned"], i * G2 + g)
                    for t in range(GT):
                        ins = dve.tensor_scalar(xn[:, t, :], xt(t), mv[:, t, 0:1], rstd[:, t:t + 1], ALU.subtract, ALU.mult)
                    ins.then_inc(m["xn_done"], 1)
                    dve.wait_ge(m["xhi_done"], i * G2 + (g + 1))
                    for c in range(KD):
                        ins = dve.tensor_tensor(xlo[:, c, g * GN:(g + 1) * GN], bank[c], xhi[:, c, g * GN:(g + 1) * GN], ALU.subtract)
                    ins.then_inc(m["xlo_done"], 1)
                for s_ in range(T + LAST + 1):
                    t = parts(s_, 11)
                    if t is not None:
                        after(dve, i, "y_done", t)
                        x = X[:, bass.ds(i * T + t, 1), :].rearrange("p o d -> p (o d)")
                        dve.scalar_tensor_tensor(out=x, in0=bank[VY][:, 0:D], scalar=1.0 / WS, in1=x, op0=ALU.mult, op1=ALU.add).then_inc(m["y_added"], 1)
                    t = parts(s_, 4)
                    if t is not None:
                        after(dve, i, "qa_turned", t)
                        if t >= 2:
                            after(dve, i, "sc_done", t - 2, SR)
                        for h in range(2):
                            rows = slice(h * AW, (h + 1) * AW)
                            ins = dve.tensor_copy(qT[rows, t % 2, h::2, :], bank16[QA][rows, :].rearrange("p (h t) -> p h t", h=PAIRS))
                        ins.then_inc(m["qT_done"], 1)
                        after(dve, i, "qdhi_done", t)
                        dve.tensor_tensor(qdlo[:, t % 4], bank[QD][:, 0:OCT * P].rearrange("p (c t) -> p c t", c=OCT), qdhi[:, t % 4], ALU.subtract).then_inc(m["qdlo_done"], 1)
                    t = parts(s_, 5)
                    if t is not None:
                        after(dve, i, "ahi_done", t, SR)
                        dve.tensor_tensor(alo[:, t % 3], am[:], ahi[:, t % 3], ALU.subtract).then_inc(m["alo_done"], 1)
                    t = parts(s_, 10)
                    if t is not None:
                        after(dve, i, "rhi_done", t)
                        dve.tensor_tensor(rlo[:, t % 2], bank[QK][:, 0:D].rearrange("p (c t) -> p c t", c=OCT), rhi[:, t % 2], ALU.subtract).then_inc(m["rlo_done"], 1)
                    t = parts(s_, 6)
                    if t is not None:
                        after(dve, i, "out_done", t)
                        dve.tensor_tensor(stx[:], bank[QD][:, D:2 * D].rearrange("p (c f) -> p c f", c=OCT),
                                          blocks[:].unsqueeze(1).to_broadcast([P, OCT, P]), ALU.mult).then_inc(m["s1"], 1)
                        after(dve, i, "s1", t)
                        if t == 0:
                            dve.tensor_copy(st[:], stx[:]).then_inc(m["s2"], 1)
                        else:
                            for c in range(OCT):
                                ins = dve.scalar_tensor_tensor(out=st[:, c, :], in0=st[:, c, :], scalar=dstate[:, c:c + 1], in1=stx[:, c, :],
                                                               op0=ALU.mult, op1=ALU.add)
                            ins.then_inc(m["s2"], 1)
                        after(dve, i, "sthi_done", t)
                        dve.tensor_tensor(stlo[:], st[:], sthi[:], ALU.subtract).then_inc(m["stlo_done"], 1)
                    t = parts(s_, 9)
                    if t is not None:
                        after(dve, i, "hrs_done", t)
                        dve.tensor_tensor(r[:, t % 4], r[:, t % 4], hvar[:, t % 2].unsqueeze(2).to_broadcast([P, H, HD]), ALU.mult).then_inc(m["scaled"], 1)
                    t = parts(s_, 8)
                    if t is not None:
                        after(dve, i, "sq_done", t)
                        if t >= 2:
                            after(dve, i, "hvar_done", t - 2)
                        dve.tensor_reduce(hsq[:, t % 2], rsq[:, t % 2], AX.X, ALU.add).then_inc(m["sum2_done"], 1)
                    t = parts(s_, 7)
                    if t is not None:
                        after(dve, i, "r_copied", t)
                        dve.tensor_reduce(hsum[:, t % 2], r[:, t % 4], AX.X, ALU.add).then_inc(m["sum_done"], 1)
                        after(dve, i, "sum_done", t)
                        dve.tensor_scalar(hsum[:, t % 2], hsum[:, t % 2], 1.0 / HD, None, ALU.mult).then_inc(m["mean_done"], 1)
                        after(dve, i, "mean_done", t)
                        dve.tensor_tensor(r[:, t % 4], r[:, t % 4], hsum[:, t % 2].unsqueeze(2).to_broadcast([P, H, HD]), ALU.subtract).then_inc(m["cen_done"], 1)
                    t = parts(s_, 3)
                    if t is not None:
                        after(dve, i, "hi_done", t)
                        dve.tensor_tensor(qa[:, t % 2, :, 1, :], qk[:, t % 4, 0:H, :], qa[:, t % 2, :, 0, :], ALU.subtract)
                        dve.tensor_tensor(ka[:, t % 2, :, 2, :], qk[:, t % 4, H:HK, :], ka[:, t % 2, :, 0, :], ALU.subtract).then_inc(m["lo_done"], 1)
                    t = parts(s_, 1)
                    if t is not None:
                        after(dve, i, "qk_copied", t)
                        if t:
                            after(dve, i, "rope_done", t - 1)
                        q = qk[:, t % 4].rearrange("p h (f two) -> p h f two", two=2)
                        ro = rot[:].rearrange("p h (f two) -> p h f two", two=2)
                        sn = sin[:, t, :].rearrange("p (f two) -> p f two", two=2)
                        for n in range(2):
                            ins = dve.tensor_tensor(ro[:, :, :, n], q[:, :, :, 1 - n], sn[:, :, n].unsqueeze(1).to_broadcast([P, HK, HD // 2]), ALU.mult)
                        ins.then_inc(m["rot_done"], 1)
                        after(dve, i, "rot_done", t)
                        dve.tensor_tensor(qk[:, t % 4], qk[:, t % 4], cos[:, t, :].unsqueeze(1).to_broadcast([P, HK, HD]), ALU.mult).then_inc(m["cos_done"], 1)
                        after(dve, i, "cos_done", t)
                        dve.tensor_tensor(qk[:, t % 4], qk[:, t % 4], rot[:], ALU.add).then_inc(m["rope_done"], 1)
                    t = parts(s_, 4)
                    if t is not None:
                        for n in range(SR):
                            h = slice(n * H // SR, (n + 1) * H // SR)
                            after(dve, i, "sc_done", t, SR, n + 1)
                            if n == 0 and t:
                                after(dve, i, "alo_done", t - 1)
                            dve.tensor_tensor(am[:, h, :], bank[SC + n % 2].rearrange("p (h t) -> p h t", h=H // SR), dmask[:, h, :], ALU.mult).then_inc(m["am_done"], 1)

        @block.tensor
        def _(pe):
            pe.wait_ge(w_in, 48)
            for n in range(NW):
                if n >= 2:
                    pe.wait_ge(w_copied, n - 1)
                for c in range(KD):
                    ins = pe.transpose(bank[n % 2][:, c * P:(c + 1) * P], w_raw[:, n, c * P:(c + 1) * P], ident[:])
                ins.then_inc(w_turned, 1)
            pe.wait_ge(consts, 4)
            pe.wait_ge(w_ready, 2)
            wq_h, wq_l = (w[:, WQ:WO].rearrange("p (c o) -> p c o", c=KD) for w in (wThi, wTlo))
            wo_h, wo_l = (w[:, WO:WE].rearrange("p (c o) -> p c o", c=KD) for w in (wThi, wTlo))

            def three(out, hi, lo, w_hi, w_lo, start, stop):
                pe.matmul(out, hi, w_hi, start=start, stop=False, skip_group_check=True)
                pe.matmul(out, hi, w_lo, start=False, stop=False, skip_group_check=True)
                return pe.matmul(out, lo, w_hi, start=False, stop=stop, skip_group_check=True)

            with pe.Fori(0, BATCH) as i:
                for g in range(G2):
                    pe.wait_ge(m["xn_done"], i * G2 + (g + 1))
                    if g:
                        pe.wait_ge(m["xlo_done"], i * G2 + g)
                    for c in range(KD):
                        for t in range(GT):
                            ins = pe.transpose(bank[c][:, t * P:(t + 1) * P], xn[:, t, c * P:(c + 1) * P], ident[:])
                    ins.then_inc(m["turned"], 1)
                pe.wait_ge(m["xlo_done"], i * G2 + G2)
                for s_ in range(T + LAST + 1):
                    t = parts(s_, 6)
                    if t is not None:
                        for n in ("alo_done", "vlo_done", "kdlo_done"):
                            after(pe, i, n, t)
                        if t:
                            after(pe, i, "stlo_done", t - 1)
                            after(pe, i, "r_copied", t - 1)
                        after(pe, i, "qdlo_done", min(t + 2, T - 1))
                        out = bank[RO][:, 0:D]
                        if t:
                            for c in range(OCT):
                                three(out[:, c * P:(c + 1) * P], qdhi[:, t % 4, c, :], qdlo[:, t % 4, c, :], sthi[:, c, :], stlo[:, c, :], c == 0, False)
                        for h in range(H):
                            cols = slice(h * HD, (h + 1) * HD)
                            three(out[:, cols], ahi[:, t % 3, h, :], alo[:, t % 3, h, :], vhi[:, t % 8, cols], vlo[:, t % 8, cols],
                                  t == 0 and h == 0, h == H - 1)
                        for c in range(OCT):
                            cols = slice(c * P, (c + 1) * P)
                            ins = three(bank[QD][:, D + c * P:D + (c + 1) * P], kdhi[:, t % 6, cols], kdlo[:, t % 6, cols],
                                        vhi[:, t % 8, cols], vlo[:, t % 8, cols], c == 0, c == OCT - 1)
                        ins.then_inc(m["out_done"], 1)
                    t = parts(s_, 10)
                    if t is not None:
                        after(pe, i, "rlo_done", t)
                        if t < T - 2:
                            pass
                        for c in range(OCT):
                            ins = three(bank[VY][:, 0:D], rhi[:, t % 2, c, :], rlo[:, t % 2, c, :], wo_h[:, c, :], wo_l[:, c, :], c == 0, c == OCT - 1)
                        ins.then_inc(m["y_done"], 1)
                    t = parts(s_, 9)
                    if t is not None:
                        after(pe, i, "bet_done", t)
                        if t:
                            after(pe, i, "rlo_done", t - 1)
                        for c in range(OCT):
                            ins = pe.transpose(bank[QK][:, c * P:(c + 1) * P], r[:, t % 4].rearrange("p h f -> p (h f)")[:, c * P:(c + 1) * P], ident[:])
                        ins.then_inc(m["r_turned"], 1)
                    t = parts(s_, 0)
                    if t is not None:
                        tok = slice(t * P, (t + 1) * P)
                        if t:
                            after(pe, i, "qk_copied", t - 1)
                        for c in range(KD):
                            three(bank[QK], xhi[:, c, tok], xlo[:, c, tok], wq_h[:, c, 0:2 * D], wq_l[:, c, 0:2 * D], c == 0, c == KD - 1)
                        if t:
                            after(pe, i, "v_copied", t - 1)
                        for c in range(KD):
                            ins = three(bank[VY][:, 0:D], xhi[:, c, tok], xlo[:, c, tok], wq_h[:, c, 2 * D:], wq_l[:, c, 2 * D:], c == 0, c == KD - 1)
                        ins.then_inc(m["qkv_done"], 1)
                    t = parts(s_, 4)
                    if t is not None:
                        after(pe, i, "kT_done", t)
                        after(pe, i, "qT_done", t)
                        for n in range(SR):
                            if n >= 2:
                                after(pe, i, "am_done", t, SR, n - 1)
                            elif t:
                                after(pe, i, "am_done", t - 1, SR, SR)
                            for p in range(2 * n, 2 * n + 2):
                                at = (p % 2) * 2 * P
                                ins = pe.matmul(bank[SC + n % 2][:, at:at + 2 * P], kT[:, t % 2, p, :], qT[:, t % 2, 2 * p:2 * p + 2, :].rearrange("p h t -> p (h t)"),
                                                start=True, stop=True)
                            ins.then_inc(m["sc_done"], 1)
                    t = parts(s_, 3)
                    if t is not None:
                        after(pe, i, "lo_done", t)
                        after(pe, i, "qd_done", t)
                        if t:
                            after(pe, i, "kT_done", t - 1)
                            after(pe, i, "qT_done", t - 1)
                            after(pe, i, "qdlo_done", t - 1)
                        for src, b, name in ((ka[:, t % 2], KA, "ka_turned"), (qa[:, t % 2], QA, "qa_turned")):
                            for p in range(PAIRS):
                                ins = pe.transpose(bank16[b][:, p * P:(p + 1) * P], src[:, 2 * p:2 * p + 2, :, :].rearrange("p h a f -> p (h a f)"), ident16[:])
                            ins.then_inc(m[name], 1)
                        if t >= 3:
                            after(pe, i, "s1", t - 3)
                        for c in range(OCT):
                            ins = pe.transpose(bank[QD][:, c * P:(c + 1) * P], qd[:, t % 3].rearrange("p h f -> p (h f)")[:, c * P:(c + 1) * P], ident[:])
                        ins.then_inc(m["qd_turned"], 1)


def constants():
    f = np.float32
    t = np.arange(SEQ, dtype=f)[:, None]
    inv = (f(1.0) / np.power(f(10000.0), np.arange(8, dtype=f) / f(8))).astype(f)
    ang = (t * inv[None]).astype(f)
    c, s = np.cos(ang).astype(f), np.sin(ang).astype(f)
    inv1 = np.power(f(10.0), f(-4.0) * (np.arange(0, 16, 2, dtype=f) / f(16))).astype(f)
    ang1 = (t * inv1[None]).astype(f)
    c1, s1 = np.cos(ang1).astype(f), np.sin(ang1).astype(f)
    decay = 1.0 - 2.0 ** (-5.0 - np.arange(16.0))
    j, i = np.arange(P)[:, None], np.arange(P)[None, :]
    dmask = np.where(i >= j, decay[:, None, None] ** np.maximum(i - j, 0), 0.0).transpose(1, 0, 2)
    head = np.arange(P) // 16
    return {
        "c_cos1": np.repeat(c1, 2, 1),
        "c_sin1": np.stack([-s1, s1], -1).reshape(SEQ, 16),
        "c_dmask": dmask.astype(f),
        "c_dq": (decay[None] ** (np.arange(P)[:, None] + 1)).astype(f),
        "c_dk": (decay[None] ** (P - 1 - np.arange(P)[:, None])).astype(f),
        "c_dstate": np.stack([decay[head], decay[head + 8]], 1).astype(np.float64).__pow__(P).astype(f),
        "c_blocks": (head[:, None] == head[None]).astype(f),
        "c_ident": np.eye(P, dtype=f),
        "c_iota": np.arange(16, dtype=f),
        "c_cos0": np.concatenate([c, c], 1),
        "c_sin0": np.concatenate([-s, s], 1),
    }


def tower(nc, a, out):
    with ExitStack() as ctx:
        s = Store(nc, ctx, "")
        X = s.sb("X", [P, NT, D])
        ident = s.sb("ident", [P, P])
        ident16 = s.sb("ident16", [P, P], F16)
        ident_in, ident16_done, x_out = s.sem("ident_in"), s.sem("ident16_done"), s.sem("x_out")
        with nc.Block() as block:
            @block.sync
            def _(sp):
                sp.dma_start(ident[:], a["c_ident"]).then_inc(ident_in, 16)

            @block.vector
            def _(dve):
                dve.wait_ge(ident_in, 16)
                dve.tensor_copy(ident16[:], ident[:]).then_inc(ident16_done, 1)
                dve.wait_ge(ident16_done, 1)
        embed(nc, a, X)
        trunk(nc, a, X, ident)
        rotary_attention(nc, a, X, ident, ident16)
        experts(nc, a, X, ident, L1=False)
        retention(nc, a, X, ident, ident16)
        experts(nc, a, X, ident, L1=True)
        with nc.Block() as block:
            @block.sync
            def _(sp):
                sp.dma_start(out.rearrange("b (t p) d -> p (b t) d", p=P), X[:]).then_inc(x_out, 16)
                sp.wait_ge(x_out, 16)


_INS = ["x"] + ["L0_tok_" + n for n in "emb pos_emb A_diag B C D w1 b1 w2 b2 ln1_s ln1_b ln2_s ln2_b lnf_s lnf_b".split()] \
    + ["L0_attn_" + n for n in "w_qkv w_proj b_proj q_gamma q_beta k_gamma k_beta".split()] \
    + ["L0_ffn_" + n for n in "w_gate w_gate_proj w_up_proj w_down_proj".split()] \
    + ["L1_attn_" + n for n in "WQ WK WV WO gamma beta".split()] \
    + ["L1_ffn_" + n for n in "Wg bg W1 b1 W2 b2".split()]


def kernel(**inputs):
    import concourse.bacc as bacc
    from concourse.bass_utils import run_bass_kernel_spmd

    nc = bacc.Bacc("TRN2", target_bir_lowering=False, num_devices=1)
    arrays = {name: np.ascontiguousarray(inputs[name]) for name in _INS}
    arrays.update(constants())
    args = {name: nc.dram_tensor(f"in_{name}", v.shape, mybir.dt.from_np(v.dtype), kind="ExternalInput").ap()
            for name, v in arrays.items()}
    out = nc.dram_tensor("out_h", (BATCH, SEQ, D), F32, kind="ExternalOutput").ap()
    tower(nc, args, out)
    r = run_bass_kernel_spmd(nc, [{f"in_{name}": v for name, v in arrays.items()}], core_ids=[0])
    return r.results[0]["out_h"]
```

```python
from contextlib import ExitStack

import numpy as np
import concourse.bass as bass
from concourse import mybir

F32 = mybir.dt.float32
F16 = mybir.dt.float16
I32 = mybir.dt.int32
U32 = mybir.dt.uint32
ACT = mybir.ActivationFunctionType
ALU = mybir.AluOpType
AX = mybir.AxisListType

P = 128
BATCH, SEQ, D = 2, 1024, 256
N = BATCH * SEQ
NT = N // P
KD = D // P
GT = 4
GN = GT * P
NG = N // GN
SLOTS = 256
WS = 64.0


class Store:

    def __init__(self, nc, ctx, phase):
        self.nc, self.ctx, self.phase, self.sems = nc, ctx, phase, []
        ctx.callback(self.close)

    def sb(self, name, shape, dt=F32):
        return self.ctx.enter_context(self.nc.sbuf_tensor(self.phase + name, shape, dt))

    def ps(self, name, shape, dt=F32):
        return self.ctx.enter_context(self.nc.psum_tensor(self.phase + name, shape, dt))

    def sem(self, name):
        self.sems.append(self.nc.alloc_semaphore(self.phase + name))
        return self.sems[-1]

    def close(self):
        self.nc.clear_and_free_semaphores(self.sems)
        self.nc.all_engine_barrier()


def wait_apart(eng, passed, sem, value):
    eng.wait_ge(sem, value)
    eng.sem_inc(passed, 1)


def layer_stats(dve, passed, x, stats, mv, stats_done, before):
    for t in range(GT):
        ins = dve.bn_stats(stats[:, t, :], x[:, t, :])
    ins.then_inc(stats_done, 1)
    wait_apart(dve, passed, stats_done, before + 1)
    for t in range(GT):
        ins = dve.bn_aggr(mv[:, t, :], stats[:, t, :])
    return ins


def embed(nc, a, X):
    V = a["L0_tok_emb"].shape[0]
    with ExitStack() as ctx:
        s = Store(nc, ctx, "emb_")
        tok = s.sb("tok", [P, NT], I32)
        tokf = s.sb("tokf", [P, NT])
        wrap = s.sb("wrap", [P, NT])
        idx = s.sb("idx", [P, NT], U32)
        pos = s.sb("pos", [P, SEQ // P, D])
        tok_in, pos_in, rows_in = s.sem("tok_in"), s.sem("pos_in"), s.sem("rows_in")
        idx_step = s.sem("idx_step")
        added = s.sem("pos_added")
        passed = s.sem("passed")
        block = ctx.enter_context(nc.Block())

        @block.sync
        def _(sp):
            with nc.allow_non_contiguous_dma(reason="2048 token ids"):
                sp.dma_start(tok[:], a["x"].rearrange("b (t p) -> p (b t)", p=P)).then_inc(tok_in, 16)
            sp.dma_start(pos[:], a["L0_tok_pos_emb"][0:SEQ, :].rearrange("(t p) d -> p t d", p=P)).then_inc(pos_in, 16)

        @block.gpsimd
        def _(pool):
            pool.wait_ge(idx_step, 5)
            for t in range(NT):
                pool.indirect_dma_start(X[:, t, :], None, a["L0_tok_emb"],
                                        bass.IndirectOffsetOnAxis(idx[:, t:t + 1], 0)).then_inc(rows_in, 16)

        @block.vector
        def _(dve):
            dve.wait_ge(tok_in, 16)
            dve.tensor_copy(tokf[:], tok[:]).then_inc(idx_step, 1)
            dve.wait_ge(idx_step, 1)
            dve.tensor_scalar(wrap[:], tokf[:], 0.0, float(V), ALU.is_lt, ALU.mult).then_inc(idx_step, 1)
            dve.wait_ge(idx_step, 2)
            dve.tensor_tensor(tokf[:], tokf[:], wrap[:], ALU.add).then_inc(idx_step, 1)
            dve.wait_ge(idx_step, 3)
            dve.tensor_scalar(tokf[:], tokf[:], 0.0, float(V - 1), ALU.max, ALU.min).then_inc(idx_step, 1)
            dve.wait_ge(idx_step, 4)
            dve.tensor_copy(idx[:], tokf[:]).then_inc(idx_step, 1)
            dve.wait_ge(pos_in, 16)
            dve.wait_ge(rows_in, 16 * NT)
            for b in range(BATCH):
                xb = X[:, b * NT // BATCH:(b + 1) * NT // BATCH, :]
                dve.tensor_tensor(xb, xb, pos[:], ALU.add).then_inc(added, 1)
            dve.wait_ge(added, BATCH)


def trunk(nc, a, X, ident, rows_x):
    L, S = a["L0_tok_A_diag"].shape
    F = a["L0_tok_w1"].shape[2]
    FT = F // P
    SS = 8.0
    assert SS * SS == WS
    K = 2 * NG
    EPS = 1e-5
    W1, W2, WD, WB, WC, WB2, WE = np.cumsum([0, KD * F, FT * D, KD * D, KD * S, D, D]).tolist()
    Q = 4
    with ExitStack() as ctx:
        s = Store(nc, ctx, "trunk_")
        raw = s.sb("w_raw", [P, WE])
        whi = [s.sb(f"w_hi{j}", [P, WE], F16) for j in range(2)]
        wlo = [s.sb(f"w_lo{j}", [P, WE], F16) for j in range(2)]
        b1 = [s.sb(f"b1_{j}", [P, FT]) for j in range(2)]
        aff = [s.sb(f"aff{j}", [P, 2, 2, KD]) for j in range(2)]
        a_raw = s.sb("a_raw", [S, L])
        a_e = s.sb("a_e", [S, L])
        a_sig = s.sb("a_sig", [S, L])
        a_row = [s.sb(f"a_row{j}", [S, GN]) for j in range(2)]
        ones32 = s.sb("ones32", [S, GN])
        sel = s.sb("sel", [P, P], F16)
        mhalf = s.sb("mhalf", [P, GT])
        stats = s.sb("stats", [P, 2, GT, 6])
        mv = s.sb("mv", [P, 2, GT, 2])
        var = s.sb("var", [P, 2, GT])
        rstd = s.sb("rstd", [P, 2, GT])
        xn = s.sb("xn", [P, 2, GT, D])
        xT = s.sb("xT", [P, 2, KD, GN])
        xhi = s.sb("xhi", [P, 2, KD, GN], F16)
        xlo = s.sb("xlo", [P, 2, KD, GN], F16)
        hst = s.sb("hst", [S, 2, GN])
        hst_hi = s.sb("hst_hi", [P, GN], F16)
        hst_lo = s.sb("hst_lo", [P, GN], F16)
        NH = 3
        hf = s.sb("hf", [P, NH, GN])
        hhi = s.sb("hhi", [P, FT, GN], F16)
        hlo = s.sb("hlo", [P, FT, GN], F16)
        pT = [s.ps(f"pT{j}", [P, KD, GN]) for j in range(2)]
        pH = s.ps("pH", [P, 2, GN])
        pY = s.ps("pY", [P, GT, D])
        pU = pT[0][0:S, 0, :]

        w_in, small_in, a_in = s.sem("w_in"), [s.sem(f"small_in{j}") for j in range(2)], s.sem("a_in")
        whi_done, w_ready = s.sem("whi_done"), s.sem("w_ready")
        layer_free = s.sem("layer_free")
        consts = s.sem("consts")
        a_step = s.sem("a_step")
        ZT = 8
        zeros = s.sb("zeros", [P, ZT, D])
        zeros_set, zeros_out = s.sem("zeros_set"), s.sem("zeros_out")
        arow_ready = s.sem("arow_ready")
        st_done = [s.sem(f"st_done{j}") for j in range(2)]
        mv_done = [s.sem(f"mv_done{j}") for j in range(2)]
        var_done = [s.sem(f"var_done{j}") for j in range(2)]
        rstd_done = [s.sem(f"rstd_done{j}") for j in range(2)]
        xn_done = [s.sem(f"xn_done{j}") for j in range(2)]
        turned = [s.sem(f"turned{j}") for j in range(2)]
        xT_done = [s.sem(f"xT_done{j}") for j in range(2)]
        xhi_done = [s.sem(f"xhi_done{j}") for j in range(2)]
        xlo_done = [s.sem(f"xlo_done{j}") for j in range(2)]
        u_done, scan_done, hsthi_done, hstlo_done = (s.sem(n) for n in ("u_done", "scan_done", "hsthi_done", "hstlo_done"))
        ys_done, ys_added = s.sem("ys_done"), s.sem("ys_added")
        h_done, gelu_done, hhi_done, hlo_done = (s.sem(n) for n in ("h_done", "gelu_done", "hhi_done", "hlo_done"))
        yf_done, yf_added = s.sem("yf_done"), s.sem("yf_added")
        passed, sp_passed = s.sem("passed"), s.sem("sp_passed")
        block = ctx.enter_context(nc.Block())

        def w1v(w, c, f):
            return w[:, W1 + c * F + f * P:W1 + c * F + (f + 1) * P]

        def w2v(w, f):
            return w[:, W2 + f * D:W2 + (f + 1) * D]

        def wdv(w, c):
            return w[:, WD + c * D:WD + (c + 1) * D]

        def wbv(w, c):
            return w[:, WB + c * S:WB + (c + 1) * S]

        def seen(i, k, each, plus=0):
            return i * (K * each) + (k * each + plus)

        @block.sync
        def _(sp):
            with nc.allow_non_contiguous_dma(reason="small parameters"):
                sp.dma_start(a_raw[:], a["L0_tok_A_diag"].rearrange("l s -> s l")).then_inc(a_in, 16)
            sp.wait_ge(consts, 6)

            def load(j, l, n):
                def row(name):
                    return a[name][bass.ds(l, 1)]
                for dst, src in (
                    (raw[:, W1:W2].rearrange("p (c f) -> p c f", c=KD), row("L0_tok_w1").rearrange("o (c p) f -> p (o c) f", p=P)),
                    (raw[:, W2:WD].rearrange("p (c d) -> p c d", c=FT), row("L0_tok_w2").rearrange("o (c p) d -> p (o c) d", p=P)),
                    (raw[:, WD:WB].rearrange("p (c d) -> p c d", c=KD), row("L0_tok_D").rearrange("o (c p) d -> p (o c) d", p=P)),
                    (raw[:, WB:WC].rearrange("p (c d) -> p c d", c=KD), row("L0_tok_B").rearrange("o (c p) d -> p (o c) d", p=P)),
                    (raw[0:S, WC:WB2], row("L0_tok_C").rearrange("o s d -> (o s) d")),
                    (raw[0:1, WB2:WE], row("L0_tok_b2")),
                ):
                    sp.dma_start(dst, src).then_inc(w_in, 16)
                wait_apart(sp, sp_passed, layer_free, n + 1)
                with nc.allow_non_contiguous_dma(reason="small parameters"):
                    sp.dma_start(b1[j][:], row("L0_tok_b1").rearrange("o (c p) -> p (o c)", p=P)).then_inc(small_in[j], 16)
                    for m, name in enumerate(("ln1_s", "ln1_b", "ln2_s", "ln2_b")):
                        sp.dma_start(aff[j][:, m // 2, m % 2, :],
                                     row("L0_tok_" + name).rearrange("o (c p) -> p (o c)", p=P)).then_inc(small_in[j], 16)

            load(0, 0, 0)
            with sp.Fori(0, L // 2) as i:
                for j in (1, 2):
                    wait_apart(sp, sp_passed, w_ready, i * (2 * Q) + j * Q)
                    load(j % 2, (i * 2 + j) % L, i * 2 + j)
            sp.wait_ge(zeros_set, 1)
            for part in rows_x.rearrange("(n t p) d -> n p t d", t=ZT, p=P):
                sp.dma_start(part, zeros[:]).then_inc(zeros_out, 16)
            sp.wait_ge(zeros_out, rows_x.shape[0] // (ZT * P) * 16)

        NWD, NSD = 6, 5

        def parts(q):
            w = WB // Q
            return [(slice(q * w, (q + 1) * w), WS)] + ([(slice(WB, WB2), SS), (slice(WB2, WE), WS)] if q == Q - 1 else [])

        def quarters(i, k):
            return {1: [(1, 1, 0)], 2: [(1, 1, 1)], 3: [(1, 1, 2), (1, 1, 3)],
                    5: [(0, 2, 0)], 6: [(0, 2, 1)], 7: [(0, 2, 2)], 8: [(0, 2, 3)]}.get(k, [])

        @block.gpsimd
        def _(pool):
            pool.memset(ones32[:], 1.0).then_inc(consts, 1)
            pool.memset(sel[:], 0.0).then_inc(consts, 1)
            pool.memset(mhalf[:], -0.5).then_inc(consts, 1)
            pool.memset(raw[:, WC:WE], 0.0).then_inc(consts, 1)
            pool.memset(hst_hi[:], 0.0)
            pool.memset(hst_lo[:], 0.0).then_inc(consts, 1)
            pool.wait_ge(consts, 5)
            pool.memset(sel[0:1, :], 1.0).then_inc(consts, 1)

            def rsqrt(i, k, j):
                wait_apart(pool, passed, mv_done[j], seen(i, k, 1, 1))
                pool.tensor_scalar(var[:, j, :], mv[:, j, :, 1], EPS, None, ALU.add).then_inc(var_done[j], 1)
                pool.wait_ge(var_done[j], seen(i, k, 1, 1))
                pool.tensor_tensor(rstd[:, j, :], var[:, j, :], mhalf[:], ALU.pow).then_inc(rstd_done[j], 1)

            pool.memset(zeros[:], 0.0).then_inc(zeros_set, 1)
            pool.wait_ge(consts, 6)
            with pool.Fori(0, L // 2) as i:
                rsqrt(i, 0, 0)
                for k in range(K):
                    if k + 1 < K:
                        rsqrt(i, k + 1, 0)
                    rsqrt(i, k, 1)

        @block.scalar
        def _(act):
            act.wait_ge(a_in, 16)
            act.activation(a_sig[:], a_raw[:], ACT.Sigmoid).then_inc(a_step, 1)

            def affine(i, k, j):
                lj = k // NG
                act.wait_ge(turned[j], seen(i, k, 1, 1))
                if k % NG == 0:
                    act.wait_ge(small_in[lj], i * (NSD * 16) + NSD * 16)
                for c in range(KD):
                    ins = act.activation(xT[:, j, c, :], pT[j][:, c, :], ACT.Identity,
                                         bias=aff[lj][:, j, 1, c:c + 1], scale=aff[lj][:, j, 0, c:c + 1])
                ins.then_inc(xT_done[j], 1)
                act.wait_ge(xT_done[j], seen(i, k, 1, 1))
                for c in range(KD):
                    ins = act.activation(xhi[:, j, c, :], xT[:, j, c, :], ACT.Copy)
                ins.then_inc(xhi_done[j], 1)

            def gelu(i, k, f):
                lj = k // NG
                act.wait_ge(h_done, seen(i, k, FT, f + 1))
                act.activation(hf[:, f % NH, :], pH[:, f % 2, :], ACT.Gelu, bias=b1[lj][:, f:f + 1],
                               scale=1.0 / WS).then_inc(gelu_done, 1)
                act.wait_ge(gelu_done, seen(i, k, FT, f + 1))
                act.activation(hhi[:, f, :], hf[:, f % NH, :], ACT.Copy).then_inc(hhi_done, 1)

            def split_hi(j, i, l, q):
                if q == 0:
                    act.wait_ge(w_in, i * (2 * NWD * 16) + (l + 1) * NWD * 16)
                for c, scale in parts(q):
                    ins = act.activation(whi[j][:, c], raw[:, c], ACT.Copy, scale=scale)
                ins.then_inc(whi_done, 1)

            act.wait_ge(consts, 6)
            for q in range(Q):
                split_hi(0, 0, 0, q)
            with act.Fori(0, L // 2) as i:
                affine(i, 0, 0)
                for k in range(K + 1):
                    if k:
                        if k > 1:
                            act.wait_ge(yf_done, seen(i, k - 1, 2))
                            act.wait_ge(hlo_done, seen(i, k - 1, FT))
                        for f in range(FT // 2):
                            if f >= NH:
                                act.wait_ge(hlo_done, seen(i, k - 1, FT, f - NH + 1))
                            gelu(i, k - 1, f)
                    if k < K:
                        act.wait_ge(scan_done, seen(i, k, 1, 1))
                        act.activation(hst_hi[0:S], hst[:, k % 2, :], ACT.Copy).then_inc(hsthi_done, 1)
                    if k:
                        for f in range(FT // 2, FT):
                            act.wait_ge(hlo_done, seen(i, k - 1, FT, f - NH + 1))
                            gelu(i, k - 1, f)
                    if k < K:
                        affine(i, k, 1)
                    if k + 1 < K:
                        affine(i, k + 1, 0)
                    for j, l, q in quarters(i, k):
                        split_hi(j, i, l, q)
                act.wait_ge(yf_done, seen(i, K, 2))

        @block.vector
        def _(dve):
            def decay_row(i, j):
                dve.tensor_scalar(a_row[j][:], ones32[:], a_sig[:, bass.ds(i * 2 + j, 1)], None, ALU.mult).then_inc(arow_ready, 1)
                dve.wait_ge(arow_ready, i * 2 + (j + 1))

            def norm_stats(i, k, j):
                g = k % NG
                if j == 0:
                    if k >= NG:
                        dve.wait_ge(yf_added, seen(i, k - NG, 2, 2))
                else:
                    dve.wait_ge(ys_added, seen(i, k, 2, 2))
                layer_stats(dve, passed, X[:, g * GT:(g + 1) * GT, :], stats[:, j], mv[:, j], st_done[j],
                            seen(i, k, 1)).then_inc(mv_done[j], 1)

            def norm(i, k, j):
                g = k % NG
                dve.wait_ge(rstd_done[j], seen(i, k, 1, 1))
                if k:
                    dve.wait_ge(turned[j], seen(i, k, 1))
                for t in range(GT):
                    ins = dve.tensor_scalar(xn[:, j, t, :], X[:, g * GT + t, :], mv[:, j, t, 0:1],
                                            rstd[:, j, t:t + 1], ALU.subtract, ALU.mult)
                ins.then_inc(xn_done[j], 1)

            def low(i, k, j):
                dve.wait_ge(xhi_done[j], seen(i, k, 1, 1))
                for c in range(KD):
                    ins = dve.tensor_tensor(xlo[:, j, c, :], xT[:, j, c, :], xhi[:, j, c, :], ALU.subtract)
                ins.then_inc(xlo_done[j], 1)

            def h_low(i, k, f):
                dve.wait_ge(hhi_done, seen(i, k, FT, f + 1))
                dve.tensor_tensor(hlo[:, f, :], hf[:, f % NH, :], hhi[:, f, :], ALU.subtract).then_inc(hlo_done, 1)

            def add(i, k, half, done, added):
                g = k % NG
                dve.wait_ge(done, seen(i, k, 2, half + 1))
                x = X[:, g * GT + 2 * half:g * GT + 2 * half + 2, :]
                dve.scalar_tensor_tensor(out=x, in0=pY[:, 2 * half:2 * half + 2, :], scalar=1.0 / WS, in1=x,
                                         op0=ALU.mult, op1=ALU.add).then_inc(added, 1)

            def scan(i, k):
                dve.wait_ge(u_done, seen(i, k, 1, 1))
                if k >= 1:
                    dve.wait_ge(scan_done, seen(i, k, 1))
                start = 0.0 if k % 2 == 0 else hst[:, (k - 1) % 2, GN - 1:GN]
                dve.tensor_tensor_scan(hst[:, k % 2, :], a_row[k // NG][:], pU, start, ALU.mult, ALU.add).then_inc(scan_done, 1)
                dve.wait_ge(hsthi_done, seen(i, k, 1, 1))
                dve.tensor_tensor(hst_lo[0:S], hst[:, k % 2, :], hst_hi[0:S], ALU.subtract).then_inc(hstlo_done, 1)

            def split_lo(j, i, l, q):
                dve.wait_ge(whi_done, i * (2 * Q) + (l * Q + q + 1))
                for c, scale in parts(q):
                    ins = dve.scalar_tensor_tensor(out=wlo[j][:, c], in0=raw[:, c], scalar=scale, in1=whi[j][:, c], op0=ALU.mult, op1=ALU.subtract)
                ins.then_inc(w_ready, 1)

            dve.sem_inc(layer_free, 2)
            dve.wait_ge(a_step, 1)
            dve.wait_ge(consts, 6)
            for q in range(Q):
                split_lo(0, 0, 0, q)
            with dve.Fori(0, L // 2) as i:
                decay_row(i, 0)
                decay_row(i, 1)
                norm_stats(i, 0, 0)
                norm(i, 0, 0)
                low(i, 0, 0)
                for k in range(K + 1):
                    if k + 1 < K:
                        norm_stats(i, k + 1, 0)
                        norm(i, k + 1, 0)
                    if k:
                        for f in range(FT // 2):
                            h_low(i, k - 1, f)
                    if k < K:
                        scan(i, k)
                    if k:
                        for f in range(FT // 2, FT):
                            h_low(i, k - 1, f)
                    if k < K:
                        add(i, k, 0, ys_done, ys_added)
                        add(i, k, 1, ys_done, ys_added)
                        norm_stats(i, k, 1)
                        norm(i, k, 1)
                    if k:
                        add(i, k - 1, 0, yf_done, yf_added)
                    if k < K:
                        low(i, k, 1)
                    if k + 1 < K:
                        low(i, k + 1, 0)
                    if k:
                        add(i, k - 1, 1, yf_done, yf_added)
                    for j, l, q in quarters(i, k):
                        split_lo(j, i, l, q)
                    if k == NG or k == K:
                        dve.wait_ge(yf_added, seen(i, k, 2))
                        dve.sem_inc(layer_free, 1)
                for j in range(2):
                    dve.wait_ge(turned[j], seen(i, K, 1))

        @block.tensor
        def _(pe):
            def turn(i, k, j):
                pe.wait_ge(xn_done[j], seen(i, k, 1, 1))
                if k:
                    pe.wait_ge(xhi_done[j], seen(i, k, 1))
                    if j == 0:
                        pe.wait_ge(scan_done, seen(i, k, 1))
                for c in range(KD):
                    for t in range(GT):
                        ins = pe.transpose(pT[j][:, c, t * P:(t + 1) * P], xn[:, j, t, c * P:(c + 1) * P], ident[:])
                ins.then_inc(turned[j], 1)

            def three(out, hi, lo, whi_, wlo_, start, stop):
                pe.matmul(out, hi, whi_, start=start, stop=False)
                pe.matmul(out, hi, wlo_, start=False, stop=False)
                return pe.matmul(out, lo, whi_, start=False, stop=stop)

            def hidden(i, k, f):
                lj = k // NG
                if f >= 2:
                    pe.wait_ge(gelu_done, seen(i, k, FT, f - 1))
                for c in range(KD):
                    x_hi, x_lo = xhi[:, 1, c, :], xlo[:, 1, c, :]
                    pe.matmul(pH[:, f % 2, :], w1v(whi[lj], c, f), x_hi, start=(c == 0), stop=False)
                    pe.matmul(pH[:, f % 2, :], w1v(whi[lj], c, f), x_lo, start=False, stop=False)
                    ins = pe.matmul(pH[:, f % 2, :], w1v(wlo[lj], c, f), x_hi, start=False, stop=(c == KD - 1))
                ins.then_inc(h_done, 1)

            def u(i, k):
                lj = k // NG
                pe.wait_ge(xlo_done[0], seen(i, k, 1, 1))
                for c in range(KD):
                    x_hi, x_lo = xhi[:, 0, c, :], xlo[:, 0, c, :]
                    pe.matmul(pU, wbv(whi[lj], c), x_hi, start=(c == 0), stop=False)
                    pe.matmul(pU, wbv(whi[lj], c), x_lo, start=False, stop=False)
                    ins = pe.matmul(pU, wbv(wlo[lj], c), x_hi, start=False, stop=(c == KD - 1))
                ins.then_inc(u_done, 1)

            def y_state(i, k):
                lj = k // NG
                pe.wait_ge(hstlo_done, seen(i, k, 1, 1))
                for t in range(GT):
                    tok = slice(t * P, (t + 1) * P)
                    if t % 2 == 0 and k >= 2:
                        pe.wait_ge(yf_added, seen(i, k - 2, 2, t // 2 + 1))
                    for c in range(KD):
                        three(pY[:, t, :], xhi[:, 0, c, tok], xlo[:, 0, c, tok], wdv(whi[lj], c), wdv(wlo[lj], c), c == 0, False)
                    ins = three(pY[:, t, :], hst_hi[:, tok], hst_lo[:, tok], whi[lj][:, WC:WB2], wlo[lj][:, WC:WB2], False, True)
                    if t % 2 == 1:
                        ins.then_inc(ys_done, 1)

            def y_ff(i, k, t):
                lj = k // NG
                tok = slice(t * P, (t + 1) * P)
                if t == 0:
                    pe.wait_ge(hlo_done, seen(i, k, FT, FT))
                if t % 2 == 0:
                    pe.wait_ge(ys_added, seen(i, min(k + 1, K - 1), 2, t // 2 + 1))
                pe.matmul(pY[:, t, :], sel[:], whi[lj][:, WB2:WE], start=True, stop=False)
                pe.matmul(pY[:, t, :], sel[:], wlo[lj][:, WB2:WE], start=False, stop=False)
                for f in range(FT):
                    ins = three(pY[:, t, :], hhi[:, f, tok], hlo[:, f, tok], w2v(whi[lj], f), w2v(wlo[lj], f), False, f == FT - 1)
                if t % 2 == 1:
                    ins.then_inc(yf_done, 1)

            pe.wait_ge(consts, 6)
            with pe.Fori(0, L // 2) as i:
                turn(i, 0, 0)
                for k in range(K + 1):
                    if k % NG == 0 and k < K:
                        pe.wait_ge(w_ready, i * (2 * Q) + (k // NG + 1) * Q)
                    if k:
                        pe.wait_ge(xlo_done[1], seen(i, k, 1))
                        for f in range(FT // 2):
                            hidden(i, k - 1, f)
                    if k < K:
                        u(i, k)
                    if k:
                        for f in range(FT // 2, FT):
                            hidden(i, k - 1, f)
                    if k < K:
                        y_state(i, k)
                    if k:
                        for t in range(GT - 1):
                            y_ff(i, k - 1, t)
                    if k < K:
                        turn(i, k, 1)
                    if k + 1 < K:
                        turn(i, k + 1, 0)
                    if k:
                        y_ff(i, k - 1, GT - 1)
                for j in range(2):
                    pe.wait_ge(xhi_done[j], seen(i, K, 1))
                pe.wait_ge(scan_done, seen(i, K, 1))
                pe.wait_ge(yf_added, seen(i, K, 2))


def norm_group(dve, x, mv, rstd, out):
    for t in range(GT):
        ins = dve.tensor_scalar(out[:, t, :], x[:, t, :], mv[:, t, 0:1], rstd[:, t:t + 1], ALU.subtract, ALU.mult)
    return ins


def rotary_attention(nc, a, X, ident, ident16):
    H, HD = 16, D // 16
    PAIRS = H // 2
    T = SEQ // P
    FOUR = 4
    QUADS = H // FOUR
    MU = T * FOUR
    EU = 2 * FOUR * T
    G2 = T // GT
    QH = SEQ // GN
    E1, E2, E3 = 1e-5, 1e-5, 1e-6
    AW = 4 * HD
    MX = 3 * HD
    HK = 2 * H
    UNITS = QUADS * EU
    WHOLE = (1, 4, 7)
    SPLIT = tuple(t for t in range(T) if t not in WHOLE)

    def split(n):
        return n % T in SPLIT

    def splits(n):
        return n // T * len(SPLIT) + sum(t < n % T for t in SPLIT)

    LAG = 4
    LO_LAG = 2
    M_END = 3 * MU // 2
    TURN = (M_END + 4, M_END + 9)
    OUT = LAG + 2
    with ExitStack() as ctx:
        s = Store(nc, ctx, "attn_")
        w_raw = s.sb("w_raw", [P, 3 * D // P + KD, D])
        wq_raw, wp_raw = w_raw[:, 0:3 * D // P, :], w_raw[:, 3 * D // P:, :]
        WQ, WPJ, WBI, WE = np.cumsum([0, KD * 3 * D, KD * D, D]).tolist()
        bias = s.sb("bias", [1, D])
        wThi = s.sb("wThi", [P, WE], F16)
        wTlo = s.sb("wTlo", [P, WE], F16)
        lnf = s.sb("lnf", [P, 2, D])
        gb = s.sb("gb", [P, 2, 2, HD])
        cos = s.sb("cos", [P, T, HD])
        sin = s.sb("sin", [P, T, HD])
        ones16 = s.sb("ones16", [1, P], F16)
        mhalf = s.sb("mhalf", [P, HK])
        stats = s.sb("stats", [P, T, 6])
        mv = s.sb("mv", [P, T, 2])
        var = s.sb("var", [P, T])
        rstd = s.sb("rstd", [P, T])
        xhi = s.sb("xhi", [P, KD, SEQ], F16)
        xlo = s.sb("xlo", [P, KD, SEQ], F16)
        R = 5
        NP = LAG + 2
        arena = s.sb("arena", [P, NP * 2 * GN])
        QKE, WKE, KAE, RTE = np.cumsum([R * HK * HD, 2 * HK * HD, 2 * HK * HD, HK * HD]).tolist()
        xn = arena[:, 0:T * D].rearrange("p (t d) -> p t d", t=T)
        qk = arena[:, 0:QKE].rearrange("p (r h f) -> p r h f", r=R, h=HK)
        work = arena[:, QKE:WKE].rearrange("p (r h f) -> p r h f", r=2, h=HK)
        ka = arena[:, WKE:KAE].bitcast(F16).rearrange("p (r h a f) -> p r h a f", r=2, h=H, a=4)
        rot = arena[:, KAE:RTE].rearrange("p (h f) -> p h f", h=HK)
        prob = arena[:, 0:NP * GN].rearrange("p (n q) -> p n q", n=NP)
        phi, plo = (arena[:, (2 + n) * NP * GN // 2:(3 + n) * NP * GN // 2].bitcast(F16).rearrange("p (n q) -> p n q", n=NP) for n in range(2))
        hsum = s.sb("hsum", [P, R, HK])
        hrs = s.sb("hrs", [P, R, HK])
        qa = s.sb("qa", [P, T, H, 4, HD], F16)
        vhi = s.sb("vhi", [P, len(SPLIT), H, P], F16)
        vlo = s.sb("vlo", [P, len(SPLIT), H, P], F16)
        v32 = s.sb("v32", [P, len(WHOLE), H, P])
        qT = s.sb("qT", [P, H, SEQ], F16)
        kT = s.sb("kT", [P, PAIRS, SEQ], F16)
        mx = s.sb("mx", [P, 2, T, FOUR])
        out_val, out_sum = s.sb("out_val", [P, GN]), s.sb("out_sum", [P, GN])
        attn = w_raw[:].rearrange("p w d -> p (w d)").rearrange("p (c t) -> p c t", c=KD)
        pairs = [s.ps(f"pair{n}", [P, 2, GN]) for n in range(2)]
        bank = [pairs[n // 2][:, n % 2, :] for n in range(4)] + [s.ps(f"bank{n}", [P, GN])[:] for n in range(4, 8)]
        bank16 = [b.bitcast(F16) for b in bank]

        w_in, c_in = s.sem("w_in"), s.sem("c_in")
        consts, w_turned, whi_done, w_ready = (s.sem(n) for n in ("consts", "w_turned", "whi_done", "w_ready"))
        names = ("st1 mv1 va1 rs1 n1 af1 st2 mv2 va2 rs2 xn_done turned xhi_done xlo_done qkv_done qk_copied "
                 "v_copied vlo_done sum_done cen_done sq_done sum2_done hvar_done hrs_done scaled gam_done bet_done rope1 rope_done hi_done "
                 "lo_done turn2 kT_done qT_done m_done mx_done qmx_done mturn mq_done sT_done ka_set exp_done phi_done plo_done av_done out_copied rd_done o_done "
                 "ahi_done alo_done y_done y_added").split()
        m = {n: s.sem(n) for n in names}
        passed = s.sem("passed")
        block = ctx.enter_context(nc.Block())

        def v_view(to, at, tiles, parity, ones):
            half = 64 * (parity ^ ones)
            w = H * P
            return bass.AP(to, at * w + parity * FOUR * P + half, [[tiles * w, P], [2 * FOUR * P, 2], [P + HD, FOUR], [1, HD]])

        def v_high(t, parity, ones):
            if t in SPLIT:
                return v_view(vhi, SPLIT.index(t), len(SPLIT), parity, ones)
            return v_view(v32, WHOLE.index(t), len(WHOLE), parity, ones)

        def seen(i, each, n):
            return i * each + n

        NW = 3 * D // P + KD

        def w_place(w, n):
            to = (w[:, WQ:WPJ] if n < NW - KD else w[:, WPJ:WBI]).rearrange("p (c o) -> p c o", c=KD)
            at = (n if n < NW - KD else n - (NW - KD)) * P
            return to[:, :, at:at + P]

        @block.sync
        def _(sp):
            sp.dma_start(wq_raw, a["L0_attn_w_qkv"].rearrange("(t p) c -> p t c", p=P)).then_inc(w_in, 16)
            sp.dma_start(wp_raw, a["L0_attn_w_proj"].rearrange("(t p) c -> p t c", p=P)).then_inc(w_in, 16)
            sp.dma_start(bias[:], a["L0_attn_b_proj"].rearrange("(o d) -> o d", o=1)).then_inc(w_in, 16)
            sp.dma_start(lnf[:, 0, :], a["L0_tok_lnf_s"].partition_broadcast(P)).then_inc(c_in, 16)
            sp.dma_start(lnf[:, 1, :], a["L0_tok_lnf_b"].partition_broadcast(P)).then_inc(c_in, 16)
            for n, name in enumerate(("q_gamma", "q_beta", "k_gamma", "k_beta")):
                sp.dma_start(gb[:, n % 2, n // 2, :], a["L0_attn_" + name].partition_broadcast(P)).then_inc(c_in, 16)
            sp.dma_start(cos[:], a["c_cos0"].rearrange("(t p) f -> p t f", p=P)).then_inc(c_in, 16)
            sp.dma_start(sin[:], a["c_sin0"].rearrange("(t p) f -> p t f", p=P)).then_inc(c_in, 16)

        @block.gpsimd
        def _(pool):
            pool.memset(ones16[:], 1.0).then_inc(consts, 1)
            pool.memset(mhalf[:], -0.5).then_inc(consts, 1)
            pool.memset(v32[:], 0.0)
            pool.memset(qT[:].rearrange("p h t -> p (h t)").bitcast(F32), 0.0).then_inc(consts, 1)
            pool.wait_ge(consts, 5)
            for t in range(T):
                for parity in range(2):
                    ins = pool.memset(v_high(t, parity, 1), 1.0)
            ins.then_inc(consts, 1)
            pool.memset(qa[:, :, :, 3, :], 0.0).then_inc(consts, 1)
            wait_apart(pool, passed, c_in, 16 * 8)
            pool.tensor_scalar(gb[:, :, 0, :], gb[:, :, 0, :], float(HD) ** -0.5, None, ALU.mult).then_inc(consts, 1)
            pool.wait_ge(consts, 8)

            def rsqrt(i, eps, mv_done, va, rs):
                wait_apart(pool, passed, m[mv_done], seen(i, 1, 1))
                pool.tensor_scalar(var[:], mv[:, :, 1], eps, None, ALU.add).then_inc(m[va], 1)
                pool.wait_ge(m[va], seen(i, 1, 1))
                pool.tensor_tensor(rstd[:], var[:], mhalf[:, 0:T], ALU.pow).then_inc(m[rs], 1)

            with pool.Fori(0, BATCH) as i:
                pool.memset(ka[:, :, :, 3, :], 0.0).then_inc(m["ka_set"], 1)
                wait_apart(pool, passed, m["ka_set"], seen(i, 2, 1))
                pool.memset(ka[:, :, :, 3, 0:1], 1.0).then_inc(m["ka_set"], 1)
                rsqrt(i, E1, "mv1", "va1", "rs1")
                rsqrt(i, E2, "mv2", "va2", "rs2")
                for st in range(T + 3):
                    if 1 <= st < T + 1:
                        t = st - 1
                        wait_apart(pool, passed, m["sum2_done"], seen(i, T, t + 1))
                        pool.tensor_scalar(hsum[:, t % R, :], hsum[:, t % R, :], 1.0 / HD, E3, ALU.mult, ALU.add).then_inc(m["hvar_done"], 1)
                        pool.wait_ge(m["hvar_done"], seen(i, T, t + 1))
                        pool.tensor_tensor(hrs[:, t % R, :], hsum[:, t % R, :], mhalf[:], ALU.pow).then_inc(m["hrs_done"], 1)
                    if 2 <= st < T + 2:
                        t = st - 2
                        pool.wait_ge(m["scaled"], seen(i, T, t + 1))
                        for n, step in enumerate(("gam_done", "bet_done")):
                            for j in range(2):
                                part = qk[:, t % R, j * H:(j + 1) * H, :]
                                by = gb[:, n, j, :].unsqueeze(1).to_broadcast([P, H, HD])
                                pool.tensor_tensor(part, part, by, ALU.add if n else ALU.mult).then_inc(m[step], 1)
                            pool.wait_ge(m[step], seen(i, 2 * T, 2 * t + 2))
                wait_apart(pool, passed, m["o_done"], seen(i, 2 * QUADS, 2 * QUADS))

        @block.scalar
        def _(act):
            for n in range(NW):
                act.wait_ge(w_turned, n + 1)
                act.activation(w_place(wThi, n), bank[n % 2][:, 0:KD * P].rearrange("p (c o) -> p c o", c=KD),
                               ACT.Copy, scale=WS).then_inc(whi_done, 1)
            act.wait_ge(w_in, 48)
            act.activation(wThi[0:1, WBI:WE], bias[:], ACT.Copy, scale=WS).then_inc(whi_done, 1)

            def exp(i, n):
                act.wait_ge(m["sT_done"], seen(i, UNITS, n + 1))
                if n >= NP:
                    act.wait_ge(m["av_done"], seen(i, UNITS, n - NP + 1))
                act.activation(prob[:, n % NP, :], bank[4 + n % 2][:], ACT.Exp).then_inc(m["exp_done"], 1)

            def prob_hi(i, n):
                act.wait_ge(m["exp_done"], seen(i, UNITS, n + 1))
                act.activation(phi[:, n % NP, :], prob[:, n % NP, :], ACT.Copy).then_inc(m["phi_done"], 1)

            def turned_q(i, p):
                act.wait_ge(m["mturn"], seen(i, PAIRS, p + 1))
                for h in range(2):
                    r = slice(h * AW, (h + 1) * AW)
                    ins = act.activation(qT[r, 2 * p + h, :], bank16[0][r, :], ACT.Copy)
                ins.then_inc(m["mq_done"], 1)

            def copy_out(i, n):
                d = n // 2
                val, den = slice(64 * (d % 2), 64 * (d % 2) + 64), slice(64 * (1 - d % 2), 64 * (1 - d % 2) + 64)
                act.wait_ge(m["av_done"], seen(i, UNITS, (n + 1) * EU // 2))
                if n:
                    act.wait_ge(m["o_done"], seen(i, 2 * QUADS, n))
                act.activation(out_val[val, :], bank[6 + n % 2][val, :], ACT.Copy)
                act.activation(out_sum[val, :], bank[6 + n % 2][den, :], ACT.Copy).then_inc(m["out_copied"], 1)

            act.wait_ge(consts, 8)
            with act.Fori(0, BATCH) as i:
                act.wait_ge(m["turned"], seen(i, 1, 1))
                for c in range(KD):
                    ins = act.activation(xhi[:, c, :], pairs[c][:].rearrange("p g t -> p (g t)"), ACT.Copy)
                ins.then_inc(m["xhi_done"], 1)
                for st in range(T + 5):
                    if st < T:
                        t = st
                        act.wait_ge(m["qkv_done"], seen(i, T, t + 1))
                        if t >= R:
                            act.wait_ge(m["lo_done"], seen(i, T, t - R + 1))
                        act.activation(qk[:, t % R, :, :], bank[2 + t % 2][:].rearrange("p (h f) -> p h f", h=HK), ACT.Copy,
                                       scale=1.0 / WS).then_inc(m["qk_copied"], 1)
                        for parity in range(2):
                            src = bank[4][:, 0:D].rearrange("p (a b j f) -> p b a j f", a=2, b=2, j=FOUR)[:, parity]
                            ins = act.activation(v_high(t, parity, 0), src, ACT.Copy, scale=1.0 / WS)
                        ins.then_inc(m["v_copied"], 1)
                    if 1 <= st < T + 1:
                        t = st - 1
                        act.wait_ge(m["cen_done"], seen(i, T, t + 1))
                        act.activation(work[:, t % 2], qk[:, t % R], ACT.Square).then_inc(m["sq_done"], 1)
                    if 3 <= st < T + 3:
                        t = st - 3
                        act.wait_ge(m["rope_done"], seen(i, T, t + 1))
                        if t >= 2:
                            act.wait_ge(m["turn2"], seen(i, 2 * T, 2 * (t - 1)))
                        else:
                            act.wait_ge(m["ka_set"], seen(i, 2, 2))
                        for n in (0, 2):
                            act.activation(qa[:, t, :, n, :], qk[:, t % R, 0:H, :], ACT.Copy)
                        for n in (0, 1):
                            ins = act.activation(ka[:, t % 2, :, n, :], qk[:, t % R, H:HK, :], ACT.Copy)
                        ins.then_inc(m["hi_done"], 1)
                    if 5 <= st < T + 5:
                        t = st - 5
                        act.wait_ge(m["turn2"], seen(i, 2 * T, 2 * t + 1))
                        act.activation(kT[:, :, t * P:(t + 1) * P], bank16[5].rearrange("p (h t) -> p h t", h=PAIRS),
                                       ACT.Copy).then_inc(m["kT_done"], 1)
                turned_q(i, 0)
                turned_q(i, 1)
                for n in range(UNITS + OUT):
                    v = n % EU
                    if n < UNITS:
                        exp(i, n)
                    if 1 <= n < UNITS + 1 and split(n - 1):
                        prob_hi(i, n - 1)
                    if n < UNITS - EU and v - 2 in TURN:
                        turned_q(i, 2 * (n // EU + 1) + TURN.index(v - 2))
                    if n >= EU // 2 and (n - OUT + 1) % (EU // 2) == 0:
                        copy_out(i, (n - OUT + 1) // (EU // 2) - 1)
                for g in range(G2):
                    act.wait_ge(m["o_done"], seen(i, 2 * QUADS, 2 * QUADS))
                    for c in range(KD):
                        ins = act.activation(xhi[:, c, g * GN:(g + 1) * GN], attn[:, c, g * GN:(g + 1) * GN], ACT.Copy)
                    ins.then_inc(m["ahi_done"], 1)
                act.wait_ge(m["y_done"], seen(i, 2 * G2, 2 * G2))

        @block.vector
        def _(dve):
            def query_max(i, d, n):
                dve.wait_ge(m["m_done"], seen(i, QUADS * MU, d * MU + n + 1))
                dve.tensor_reduce(mx[:, d % 2, n // FOUR, n % FOUR:n % FOUR + 1], pairs[n % 2][:], AX.XY, ALU.max).then_inc(m["mx_done"], 1)

            for v in (vhi, vlo):
                dve.memset(v[:].rearrange("p t h c -> p (t h c)").bitcast(F32), 0.0).then_inc(consts, 1)
            for n in range(NW):
                dve.wait_ge(whi_done, n + 1)
                dve.scalar_tensor_tensor(out=w_place(wTlo, n), in0=bank[n % 2][:, 0:KD * P].rearrange("p (c o) -> p c o", c=KD), scalar=WS,
                                         in1=w_place(wThi, n), op0=ALU.mult, op1=ALU.subtract).then_inc(w_ready, 1)
            dve.wait_ge(whi_done, NW + 1)
            dve.scalar_tensor_tensor(out=wTlo[0:1, WBI:WE], in0=bias[:], scalar=WS, in1=wThi[0:1, WBI:WE],
                                     op0=ALU.mult, op1=ALU.subtract).then_inc(w_ready, 1)
            dve.wait_ge(consts, 8)
            dve.wait_ge(c_in, 16 * 8)
            with dve.Fori(0, BATCH) as i:
                xg = X[:, bass.ds(i * T, T), :]

                def xt(t):
                    return X[:, bass.ds(i * T + t, 1), :]

                def stats_of(st, n):
                    for t in range(T):
                        ins = dve.bn_stats(stats[:, t, :], xt(t))
                    ins.then_inc(m[st], 1)
                    wait_apart(dve, passed, m[st], seen(i, 1, 1))
                    for t in range(T):
                        ins = dve.bn_aggr(mv[:, t, :], stats[:, t, :])
                    ins.then_inc(m[n], 1)

                stats_of("st1", "mv1")
                dve.wait_ge(m["rs1"], seen(i, 1, 1))
                for t in range(T):
                    ins = dve.tensor_scalar(xt(t), xt(t), mv[:, t, 0:1], rstd[:, t:t + 1], ALU.subtract, ALU.mult)
                ins.then_inc(m["n1"], 1)
                dve.wait_ge(m["n1"], seen(i, 1, 1))
                for n, op in ((0, ALU.mult), (1, ALU.add)):
                    dve.tensor_tensor(xg, xg, lnf[:, n, :].unsqueeze(1).to_broadcast([P, T, D]), op).then_inc(m["af1"], 1)
                    wait_apart(dve, passed, m["af1"], seen(i, 2, n + 1))
                stats_of("st2", "mv2")
                dve.wait_ge(m["rs2"], seen(i, 1, 1))
                for t in range(T):
                    ins = dve.tensor_scalar(xn[:, t, :], xt(t), mv[:, t, 0:1], rstd[:, t:t + 1], ALU.subtract, ALU.mult)
                ins.then_inc(m["xn_done"], 1)
                dve.wait_ge(m["xhi_done"], seen(i, 1, 1))
                for c in range(KD):
                    ins = dve.tensor_tensor(xlo[:, c, :], pairs[c][:].rearrange("p g t -> p (g t)"), xhi[:, c, :], ALU.subtract)
                ins.then_inc(m["xlo_done"], 1)
                for st in range(T + 5):
                    if st < T:
                        t = st
                        q = qk[:, t % R]
                        dve.wait_ge(m["qk_copied"], seen(i, T, t + 1))
                        dve.tensor_reduce(hsum[:, t % R, :], q, AX.X, ALU.add).then_inc(m["sum_done"], 1)
                        for parity in range(2) if t in SPLIT else ():
                            dve.wait_ge(m["v_copied"], seen(i, T, t + 1))
                            src = bank[4][:, 0:D].rearrange("p (a b j f) -> p b a j f", a=2, b=2, j=FOUR)[:, parity]
                            hi, lo = v_high(t, parity, 0), v_view(vlo, SPLIT.index(t), len(SPLIT), parity, 0)
                            for n in range(2):
                                ins = dve.scalar_tensor_tensor(out=lo[:, n], in0=src[:, n], scalar=1.0 / WS, in1=hi[:, n],
                                                               op0=ALU.mult, op1=ALU.subtract)
                        if t in SPLIT:
                            ins.then_inc(m["vlo_done"], 1)
                        dve.wait_ge(m["sum_done"], seen(i, 2 * T, 2 * t + 1))
                        dve.tensor_scalar(hsum[:, t % R, :], hsum[:, t % R, :], 1.0 / HD, None, ALU.mult).then_inc(m["sum_done"], 1)
                        dve.wait_ge(m["sum_done"], seen(i, 2 * T, 2 * t + 2))
                        dve.tensor_tensor(q, q, hsum[:, t % R, :].unsqueeze(2).to_broadcast([P, HK, HD]), ALU.subtract).then_inc(m["cen_done"], 1)
                    if 1 <= st < T + 1:
                        t = st - 1
                        dve.wait_ge(m["sq_done"], seen(i, T, t + 1))
                        dve.tensor_reduce(hsum[:, t % R, :], work[:, t % 2], AX.X, ALU.add).then_inc(m["sum2_done"], 1)
                    if 2 <= st < T + 2:
                        t = st - 2
                        q = qk[:, t % R]
                        dve.wait_ge(m["hrs_done"], seen(i, T, t + 1))
                        dve.tensor_tensor(q, q, hrs[:, t % R, :].unsqueeze(2).to_broadcast([P, HK, HD]), ALU.mult).then_inc(m["scaled"], 1)
                    if 3 <= st < T + 3:
                        t = st - 3
                        q = qk[:, t % R]
                        dve.wait_ge(m["bet_done"], seen(i, 2 * T, 2 * t + 2))
                        if t:
                            dve.wait_ge(m["rope_done"], seen(i, T, t))
                        half = HD // 2
                        for n in range(2):
                            to, frm = slice(n * half, (n + 1) * half), slice((1 - n) * half, (2 - n) * half)
                            ins = dve.tensor_tensor(rot[:, :, to], q[:, :, frm], sin[:, t, to].unsqueeze(1).to_broadcast([P, HK, half]), ALU.mult)
                        ins.then_inc(m["rope1"], 1)
                        dve.wait_ge(m["rope1"], seen(i, 2 * T, 2 * t + 1))
                        dve.tensor_tensor(q, q, cos[:, t, :].unsqueeze(1).to_broadcast([P, HK, HD]), ALU.mult).then_inc(m["rope1"], 1)
                        dve.wait_ge(m["rope1"], seen(i, 2 * T, 2 * t + 2))
                        dve.tensor_tensor(q, q, rot[:], ALU.add).then_inc(m["rope_done"], 1)
                    if 4 <= st < T + 4:
                        t = st - 4
                        dve.wait_ge(m["hi_done"], seen(i, T, t + 1))
                        dve.tensor_tensor(qa[:, t, :, 1, :], qk[:, t % R, 0:H, :], qa[:, t, :, 0, :], ALU.subtract)
                        dve.tensor_tensor(ka[:, t % 2, :, 2, :], qk[:, t % R, H:HK, :], ka[:, t % 2, :, 0, :], ALU.subtract).then_inc(m["lo_done"], 1)
                    if 5 <= st < T + 5:
                        t = st - 5
                        dve.wait_ge(m["turn2"], seen(i, 2 * T, 2 * t + 2))
                        for h in range(2):
                            r = slice(h * AW, (h + 1) * AW)
                            ins = dve.tensor_copy(qT[r, h::2, t * P:(t + 1) * P], bank16[6][r, :].rearrange("p (h t) -> p h t", h=PAIRS))
                        ins.then_inc(m["qT_done"], 1)

                def new_rows(d):
                    dve.wait_ge(m["mx_done"], seen(i, QUADS * MU, (d + 1) * MU))
                    dve.tensor_scalar(qa[:, :, FOUR * d:FOUR * (d + 1), 3, 0], mx[:, d % 2], -1.0, None, ALU.mult).then_inc(m["qmx_done"], 1)

                for n in range(MU):
                    query_max(i, 0, n)
                new_rows(0)
                for n in range(UNITS + OUT + 1):
                    d, v = n // EU, n % EU
                    if n >= EU // 2 and (n - OUT) % (EU // 2) == 0:
                        at = (n - OUT) // (EU // 2) - 1
                        val = slice(64 * (at // 2 % 2), 64 * (at // 2 % 2) + 64)
                        dve.wait_ge(m["out_copied"], seen(i, 2 * QUADS, at + 1))
                        dve.reciprocal(out_sum[val, :], out_sum[val, :]).then_inc(m["rd_done"], 1)
                        dve.wait_ge(m["rd_done"], seen(i, 2 * QUADS, at + 1))
                        dve.tensor_tensor(attn[val, at // 4, at % 2 * GN:(at % 2 + 1) * GN], out_val[val, :], out_sum[val, :],
                                          ALU.mult).then_inc(m["o_done"], 1)
                    if LO_LAG <= n < UNITS + LO_LAG and split(n - LO_LAG):
                        u = n - LO_LAG
                        dve.wait_ge(m["phi_done"], seen(i, splits(UNITS), splits(u + 1)))
                        dve.tensor_tensor(plo[:, u % NP, :], prob[:, u % NP, :], phi[:, u % NP, :], ALU.subtract).then_inc(m["plo_done"], 1)
                    if d + 1 < QUADS and v < M_END and v % 3 != 2:
                        query_max(i, d + 1, v - (v + 1) // 3)
                    if d + 1 < QUADS and v == M_END:
                        new_rows(d + 1)
                for g in range(G2):
                    dve.wait_ge(m["ahi_done"], seen(i, G2, g + 1))
                    for c in range(KD):
                        t = slice(g * GN, (g + 1) * GN)
                        ins = dve.tensor_tensor(xlo[:, c, t], attn[:, c, t], xhi[:, c, t], ALU.subtract)
                    ins.then_inc(m["alo_done"], 1)
                    for half in range(2):
                        dve.wait_ge(m["y_done"], seen(i, 2 * G2, 2 * g + half + 1))
                        x = X[:, bass.ds(i * T + (g * GT + 2 * half), 2), :]
                        dve.scalar_tensor_tensor(out=x, in0=bank[2 + half][:].rearrange("p (t d) -> p t d", t=2), scalar=1.0 / WS, in1=x,
                                                 op0=ALU.mult, op1=ALU.add).then_inc(m["y_added"], 1)

        @block.tensor
        def _(pe):
            pe.wait_ge(w_in, 48)
            for n in range(NW):
                src = wq_raw[:, n, :] if n < NW - KD else wp_raw[:, n - (NW - KD), :]
                if n >= 2:
                    pe.wait_ge(w_ready, n - 1)
                for c in range(KD):
                    ins = pe.transpose(bank[n % 2][:, c * P:(c + 1) * P], src[:, c * P:(c + 1) * P], ident[:])
                ins.then_inc(w_turned, 1)
            pe.wait_ge(consts, 8)
            pe.wait_ge(w_ready, NW + 1)
            wq_h = wThi[:, WQ:WPJ].rearrange("p (c o) -> p c o", c=KD)
            wq_l = wTlo[:, WQ:WPJ].rearrange("p (c o) -> p c o", c=KD)
            wp_h = wThi[:, WPJ:WBI].rearrange("p (c o) -> p c o", c=KD)
            wp_l = wTlo[:, WPJ:WBI].rearrange("p (c o) -> p c o", c=KD)

            def dense(out, tok, w_h, w_l, cols, start=True):
                for c in range(KD):
                    pe.matmul(out, xhi[:, c, tok], w_h[:, c, cols], start=start and c == 0, stop=False)
                    pe.matmul(out, xhi[:, c, tok], w_l[:, c, cols], start=False, stop=False)
                    ins = pe.matmul(out, xlo[:, c, tok], w_h[:, c, cols], start=False, stop=c == KD - 1)
                return ins

            def max_scores(i, d, n):
                t, h = n // FOUR, FOUR * d + n % FOUR
                if d or n >= 2:
                    pe.wait_ge(m["mx_done"], seen(i, QUADS * MU, d * MU + n - 1))
                if d and n == 0:
                    pe.wait_ge(m["mq_done"], seen(i, PAIRS, 2 * d))
                for half in range(2):
                    ins = pe.matmul(pairs[n % 2][:, half, :], qT[:, h, t * P:(t + 1) * P], kT[:, h // 2, half * GN:(half + 1) * GN],
                                    start=True, stop=True)
                ins.then_inc(m["m_done"], 1)

            def turn_q(i, p):
                pe.wait_ge(m["qmx_done"], seen(i, QUADS, p // 2 + 1))
                if p:
                    pe.wait_ge(m["mq_done"], seen(i, PAIRS, p))
                for t in range(T):
                    ins = pe.transpose(bank16[0][:, t * P:(t + 1) * P], qa[:, t, 2 * p:2 * p + 2, :, :].rearrange("p h a f -> p (h a f)"), ident16[:])
                ins.then_inc(m["mturn"], 1)

            def scores(i, n):
                d, half, h, kt = n // EU, n // (EU // 2) % 2, n // T % FOUR, n % T
                h += FOUR * d
                if n % EU == 0:
                    pe.wait_ge(m["mq_done"], seen(i, PAIRS, 2 * d + 2))
                if n >= 2:
                    pe.wait_ge(m["exp_done"], seen(i, UNITS, n - 1))
                pe.matmul(bank[4 + n % 2], kT[:, h // 2, kt * P:(kt + 1) * P], qT[:, h, half * GN:(half + 1) * GN],
                          start=True, stop=True).then_inc(m["sT_done"], 1)

            def values(i, n):
                d, h, kt = n // EU, n // T % FOUR, n % T
                first, last = n % (EU // 2) == 0, n % (EU // 2) == EU // 2 - 1
                at = n // (EU // 2)
                if first and at >= 2:
                    pe.wait_ge(m["out_copied"], seen(i, 2 * QUADS, at - 1))
                out, head = bank[6 + at % 2], FOUR * d + h
                if not split(n):
                    pe.wait_ge(m["exp_done"], seen(i, UNITS, n + 1))
                    pe.matmul(out, v32[:, WHOLE.index(kt), head, :], prob[:, n % NP, :], start=first, stop=last).then_inc(m["av_done"], 1)
                    return
                pe.wait_ge(m["plo_done"], seen(i, splits(UNITS), splits(n + 1)))
                v_h, v_l = vhi[:, SPLIT.index(kt), head, :], vlo[:, SPLIT.index(kt), head, :]
                pe.matmul(out, v_h, phi[:, n % NP, :], start=first, stop=False)
                pe.matmul(out, v_l, phi[:, n % NP, :], start=False, stop=False)
                pe.matmul(out, v_h, plo[:, n % NP, :], start=False, stop=last).then_inc(m["av_done"], 1)

            with pe.Fori(0, BATCH) as i:
                pe.wait_ge(m["xn_done"], seen(i, 1, 1))
                for c in range(KD):
                    for t in range(T):
                        ins = pe.transpose(pairs[c][:, t // GT, t % GT * P:(t % GT + 1) * P], xn[:, t, c * P:(c + 1) * P], ident[:])
                ins.then_inc(m["turned"], 1)
                pe.wait_ge(m["xlo_done"], seen(i, 1, 1))
                for st in range(T + 4):
                    if st < T:
                        t = st
                        if t >= 2:
                            pe.wait_ge(m["qk_copied"], seen(i, T, t - 1))
                        tok = slice(st * P, (st + 1) * P)
                        dense(bank[2 + t % 2], tok, wq_h, wq_l, slice(0, 2 * D))
                        if t:
                            pe.wait_ge(m["v_copied"], seen(i, T, t))
                            pe.wait_ge(m["vlo_done"], seen(i, len(SPLIT), splits(t)))
                        dense(bank[4][:, 0:D], tok, wq_h, wq_l, slice(2 * D, 3 * D)).then_inc(m["qkv_done"], 1)
                    if 4 <= st:
                        t = st - 4
                        pe.wait_ge(m["lo_done"], seen(i, T, t + 1))
                        if t:
                            pe.wait_ge(m["kT_done"], seen(i, T, t))
                            pe.wait_ge(m["qT_done"], seen(i, T, t))
                        for src, b in ((ka[:, t % 2], 5), (qa[:, t], 6)):
                            for p in range(PAIRS):
                                ins = pe.transpose(bank16[b][:, p * P:(p + 1) * P], src[:, 2 * p:2 * p + 2, :, :].rearrange("p h a f -> p (h a f)"), ident16[:])
                            ins.then_inc(m["turn2"], 1)
                pe.wait_ge(m["v_copied"], seen(i, T, T))
                pe.wait_ge(m["vlo_done"], seen(i, len(SPLIT), len(SPLIT)))
                pe.wait_ge(m["kT_done"], seen(i, T, T))
                pe.wait_ge(m["qT_done"], seen(i, T, T))
                for n in range(MU):
                    max_scores(i, 0, n)
                turn_q(i, 0)
                turn_q(i, 1)
                for n in range(UNITS + LAG):
                    d, v = n // EU, n % EU
                    if n < UNITS:
                        scores(i, n)
                    if d + 1 < QUADS:
                        if v < M_END and v % 3 != 2:
                            max_scores(i, d + 1, v - (v + 1) // 3)
                        if v in TURN:
                            turn_q(i, 2 * (d + 1) + TURN.index(v))
                    if n >= LAG:
                        values(i, n - LAG)
                for g in range(G2):
                    pe.wait_ge(m["alo_done"], seen(i, G2, g + 1))
                    for t in range(GT):
                        y = bank[2 + t // 2][:, (t % 2) * D:(t % 2 + 1) * D]
                        if g and t % 2 == 0:
                            pe.wait_ge(m["y_added"], seen(i, 2 * G2, 2 * (g - 1) + t // 2 + 1))
                        pe.matmul(y, ones16[:], wThi[0:1, WBI:WE], start=True, stop=False)
                        pe.matmul(y, ones16[:], wTlo[0:1, WBI:WE], start=False, stop=False)
                        ins = dense(y, slice((g * GT + t) * P, (g * GT + t + 1) * P), wp_h, wp_l, slice(0, D), start=False)
                        if t % 2:
                            ins.then_inc(m["y_done"], 1)
                pe.wait_ge(m["y_added"], seen(i, 2 * G2, 2 * G2))


def experts(nc, a, X, ident, L1):
    if L1:
        gate, E, F = a["L1_ffn_Wg"], a["L1_ffn_W1"].shape[0], a["L1_ffn_W1"].shape[2]
    else:
        gate, E, F = a["L0_ffn_w_gate"], a["L0_ffn_w_gate_proj"].shape[0], a["L0_ffn_w_gate_proj"].shape[2]
    FT = F // P
    UP = 1 if L1 else 2
    EPS = 1e-5
    WU, WDN, WE = np.cumsum([0, UP * KD * F, FT * D]).tolist()
    QC = WE // NG
    HALF = 2.0 ** -23
    out_scale = 1.0 / WS if L1 else 1.0 / WS / WS
    with ExitStack() as ctx:
        s = Store(nc, ctx, "moe1_" if L1 else "moe0_")
        raw = s.sb("e_raw", [P, WE])
        whi = [s.sb(f"e_hi{j}", [P, WE], F16) for j in range(2)]
        wlo = [s.sb(f"e_lo{j}", [P, WE], F16) for j in range(2)]
        g_raw = s.sb("g_raw", [P, KD, E])
        g_hi = s.sb("g_hi", [P, KD, E], F16)
        g_lo = s.sb("g_lo", [P, KD, E], F16)
        bg = s.sb("bg", [P, E])
        iota = s.sb("iota", [P, E])
        stats = s.sb("stats", [P, GT, 6])
        mv = s.sb("mv", [P, GT, 2])
        var = s.sb("var", [P, GT])
        rstd = s.sb("rstd", [P, GT])
        mhalf = s.sb("mhalf", [P, GT])
        xn = s.sb("xn", [P, 2, GT, D])
        xhi = s.sb("xhi", [P, KD, N], F16)
        xlo = s.sb("xlo", [P, KD, N], F16)
        logit = s.sb("logit", [P, NT, E])
        prob = s.sb("prob", [P, NT, E])
        red = s.sb("red", [P, NT])
        top = s.sb("top", [P, NT, 8])
        topi = s.sb("topi", [P, NT, 8], U32)
        topf = s.sb("topf", [P, NT, 2])
        we = s.sb("we", [P, NT, E])
        b1 = s.sb("b1", [P, E, FT])
        b2r = s.sb("b2r", [P, E, D])
        b2s = s.sb("b2s", [P, E, D], F16)
        sel = s.sb("sel", [P, P], F16)
        NH = 3
        act1 = s.sb("act1", [P, NH, GN])
        hf = s.sb("hf", [P, NH, GN])
        hhi = s.sb("hhi", [P, 2, FT, GN], F16)
        hlo = s.sb("hlo", [P, 2, FT, GN], F16)
        pH = s.ps("pH", [P, 2, UP, GN])
        pT = s.ps("pT", [P, KD, GN])
        pY = s.ps("pY", [P, GT, D])
        pL = pY[:, 0:2, :].rearrange("p t d -> p (t d)")[:, 0:NT * E].rearrange("p (t e) -> p t e", e=E)

        names = ("w_in c_in g_in consts st mvd va rs xn_done turned xhi_done xlo_done g_split logits pre_w steps asteps we_ready "
                 "whi_done wlo_done h_done a_done hf_done hhi_done hlo_done y_done y_added bias_done").split()
        m = {n: s.sem(n) for n in names}
        passed = s.sem("passed")
        block = ctx.enter_context(nc.Block())
        K = 2 * NG
        NWD = 2 if L1 else 3

        def seen(i, k, each, plus=0):
            return i * (K * each) + (k * each + plus)

        def loop(eng, body):
            with eng.Fori(0, E // 2 - 1) as i:
                body(i, False)
            body(E // 2 - 1, True)

        @block.sync
        def _(sp):
            def load(e):
                def row(name):
                    return a[name][bass.ds(e, 1)]
                if L1:
                    parts = ((WU, KD, F, "L1_ffn_W1"), (WDN, FT, D, "L1_ffn_W2"))
                else:
                    parts = ((WU, KD, F, "L0_ffn_w_gate_proj"), (WU + KD * F, KD, F, "L0_ffn_w_up_proj"), (WDN, FT, D, "L0_ffn_w_down_proj"))
                for at, c, f, name in parts:
                    sp.dma_start(raw[:, at:at + c * f].rearrange("p (c f) -> p c f", c=c),
                                 row(name).rearrange("o (c p) f -> p (o c) f", p=P)).then_inc(m["w_in"], 16)

            with nc.allow_non_contiguous_dma(reason="small parameters"):
                sp.dma_start(g_raw[:], gate.rearrange("(c p) e -> p c e", p=P)).then_inc(m["g_in"], 16)
                if L1:
                    sp.dma_start(bg[:], a["L1_ffn_bg"].partition_broadcast(P)).then_inc(m["c_in"], 16)
                    sp.dma_start(b1[:], a["L1_ffn_b1"].rearrange("e (c p) -> p e c", p=P)).then_inc(m["c_in"], 16)
                    for r in (0, 32):
                        sp.dma_start(b2r[r:r + 1], a["L1_ffn_b2"].rearrange("(o e) d -> o e d", o=1)).then_inc(m["c_in"], 16)
                else:
                    sp.dma_start(iota[:], a["c_iota"].partition_broadcast(P)).then_inc(m["c_in"], 16)
            load(0)
            sp.wait_ge(m["wlo_done"], NG)
            load(1)

            def body(i, last):
                for j in range(0 if last else 2):
                    sp.wait_ge(m["wlo_done"], i * (2 * NG) + (j + 2) * NG)
                    load(i * 2 + (j + 2))
            loop(sp, body)

        @block.gpsimd
        def _(pool):
            pool.memset(mhalf[:], -0.5).then_inc(m["consts"], 1)
            pool.memset(sel[:], 0.0).then_inc(m["consts"], 1)
            pool.memset(b2s[:], 0.0).then_inc(m["consts"], 1)
            pool.wait_ge(m["consts"], 3)
            for r in (0, 32):
                ins = pool.memset(sel[r:r + 1, :], 1.0)
            ins.then_inc(m["consts"], 1)
            pool.wait_ge(m["consts"], 4)
            for g in range(NG):
                wait_apart(pool, passed, m["mvd"], g + 1)
                pool.tensor_scalar(var[:], mv[:, :, 1], EPS, None, ALU.add).then_inc(m["va"], 1)
                pool.wait_ge(m["va"], g + 1)
                pool.tensor_tensor(rstd[:], var[:], mhalf[:], ALU.pow).then_inc(m["rs"], 1)

        @block.scalar
        def _(act):
            def split_hi(e_at, j, q):
                act.wait_ge(m["w_in"], e_at[0])
                act.activation(whi[j][:, q * QC:(q + 1) * QC], raw[:, q * QC:(q + 1) * QC], ACT.Copy, scale=WS).then_inc(m["whi_done"], 1)

            for q in range(NG):
                split_hi((16 * NWD,), 0, q)
            act.wait_ge(m["g_in"], 16)
            act.activation(g_hi[:], g_raw[:], ACT.Copy, scale=WS).then_inc(m["g_split"], 1)
            for g in range(NG):
                act.wait_ge(m["turned"], g + 1)
                for c in range(KD):
                    ins = act.activation(xhi[:, c, g * GN:(g + 1) * GN], pT[:, c, :], ACT.Copy)
                ins.then_inc(m["xhi_done"], 1)
            act.wait_ge(m["pre_w"], 1)
            act.activation(prob[:], logit[:], ACT.Sigmoid if L1 else ACT.Exp).then_inc(m["asteps"], 1)

            def body(i, last):
                for k in range(K):
                    e, g, n = k // NG, k % NG, k % 2
                    for f in range(FT):
                        act.wait_ge(m["h_done"], seen(i, k, FT, f + 1))
                        if L1:
                            if k or f >= NH:
                                wait_apart(act, passed, m["hlo_done"], seen(i, k, FT, max(f - NH + 1, 0)))
                            else:
                                act.sem_inc(passed, 1)
                            act.activation(hf[:, f % NH, :], pH[:, f % 2, 0, :], ACT.Relu, scale=1.0 / WS,
                                           bias=b1[:, bass.ds(i * 2 + e, 1), f]).then_inc(m["hf_done"], 1)
                        else:
                            if f >= NH:
                                act.wait_ge(m["hf_done"], seen(i, k, FT, f - NH + 1))
                            act.activation(act1[:, f % NH, :], pH[:, f % 2, 0, :], ACT.Silu, scale=1.0 / WS).then_inc(m["a_done"], 1)
                        if f == 0 and not (last and e):
                            split_hi((i * (2 * 16 * NWD) + (e + 2) * 16 * NWD,), (e + 1) % 2, g)
                        act.wait_ge(m["hf_done"], seen(i, k, FT, f + 1))
                        if f == 0:
                            if k >= 2:
                                act.wait_ge(m["y_done"], seen(i, k - 1, 2))
                        act.activation(hhi[:, n, f, :], hf[:, f % NH, :], ACT.Copy).then_inc(m["hhi_done"], 1)
                act.wait_ge(m["hlo_done"], seen(i, K, FT))
                act.wait_ge(m["y_done"], seen(i, K, 2))
            loop(act, body)

        @block.vector
        def _(dve):
            def split_lo(at, j, q):
                dve.wait_ge(m["whi_done"], at)
                c = slice(q * QC, (q + 1) * QC)
                dve.scalar_tensor_tensor(out=wlo[j][:, c], in0=raw[:, c], scalar=WS, in1=whi[j][:, c], op0=ALU.mult,
                                         op1=ALU.subtract).then_inc(m["wlo_done"], 1)

            dve.wait_ge(m["consts"], 4)
            for g in range(NG):
                layer_stats(dve, passed, X[:, g * GT:(g + 1) * GT, :], stats, mv, m["st"], g).then_inc(m["mvd"], 1)
                dve.wait_ge(m["rs"], g + 1)
                if g >= 2:
                    dve.wait_ge(m["turned"], g - 1)
                norm_group(dve, X[:, g * GT:(g + 1) * GT, :], mv, rstd, xn[:, g % 2]).then_inc(m["xn_done"], 1)
                dve.wait_ge(m["xhi_done"], g + 1)
                for c in range(KD):
                    t = slice(g * GN, (g + 1) * GN)
                    ins = dve.tensor_tensor(xlo[:, c, t], pT[:, c, :], xhi[:, c, t], ALU.subtract)
                ins.then_inc(m["xlo_done"], 1)
            for q in range(NG):
                split_lo(q + 1, 0, q)
            dve.wait_ge(m["g_split"], 1)
            dve.scalar_tensor_tensor(out=g_lo[:], in0=g_raw[:], scalar=WS, in1=g_hi[:], op0=ALU.mult,
                                     op1=ALU.subtract).then_inc(m["g_split"], 1)
            count = [0]

            def step(ins):
                count[0] += 1
                ins.then_inc(m["steps"], 1)
                dve.wait_ge(m["steps"], count[0])

            dve.wait_ge(m["logits"], 1)
            dve.wait_ge(m["c_in"], 64 if L1 else 16)
            step(dve.tensor_scalar(logit[:], pL, 1.0 / WS, None, ALU.mult))
            if L1:
                dve.tensor_tensor(logit[:], logit[:], bg[:].unsqueeze(1).to_broadcast([P, NT, E]), ALU.add).then_inc(m["pre_w"], 1)
                dve.wait_ge(m["asteps"], 1)
                step(dve.scalar_tensor_tensor(out=we[:], in0=logit[:], scalar=HALF, in1=prob[:], op0=ALU.is_gt, op1=ALU.mult))
                for r in (0, 32):
                    ins = dve.tensor_scalar(b2r[r:r + 1], b2r[r:r + 1], WS, None, ALU.mult)
                step(ins)
                for r in (0, 32):
                    ins = dve.tensor_copy(b2s[r:r + 1], b2r[r:r + 1])
                step(ins)
                dve.tensor_tensor(b2s[32:33], b2r[32:33], b2s[32:33], ALU.subtract).then_inc(m["bias_done"], 1)
            else:
                step(dve.tensor_reduce(red[:], logit[:], AX.X, ALU.max))
                dve.tensor_tensor(logit[:], logit[:], red[:].unsqueeze(2).to_broadcast([P, NT, E]), ALU.subtract).then_inc(m["pre_w"], 1)
                dve.wait_ge(m["asteps"], 1)
                step(dve.tensor_reduce(red[:], prob[:], AX.X, ALU.add))
                step(dve.reciprocal(red[:], red[:]))
                step(dve.tensor_tensor(prob[:], prob[:], red[:].unsqueeze(2).to_broadcast([P, NT, E]), ALU.mult))
                for t in range(NT):
                    ins = dve.max(top[:, t, :], prob[:, t, :])
                step(ins)
                for t in range(NT):
                    ins = dve.max_index(topi[:, t, :], top[:, t, :], prob[:, t, :])
                step(ins)
                step(dve.tensor_copy(topf[:], topi[:, :, 0:2]))
                step(dve.tensor_tensor(red[:], top[:, :, 0], top[:, :, 1], ALU.add))
                step(dve.reciprocal(red[:], red[:]))
                step(dve.tensor_tensor(top[:, :, 0:2], top[:, :, 0:2], red[:].unsqueeze(2).to_broadcast([P, NT, 2]), ALU.mult))
                for t in range(NT):
                    dve.tensor_scalar(we[:, t, :], iota[:], topf[:, t, 0:1], top[:, t, 0:1], ALU.is_equal, ALU.mult)
                    ins = dve.tensor_scalar(logit[:, t, :], iota[:], topf[:, t, 1:2], top[:, t, 1:2], ALU.is_equal, ALU.mult)
                step(ins)
                step(dve.tensor_tensor(we[:], we[:], logit[:], ALU.add))
            step(dve.tensor_scalar(we[:], we[:], out_scale, None, ALU.mult))

            def body(i, last):
                def add(k):
                    e, g = k // NG, k % NG
                    for t in range(GT):
                        if t % 2 == 0:
                            dve.wait_ge(m["y_done"], seen(i, k, 2, t // 2 + 1))
                        x = X[:, g * GT + t, :]
                        ins = dve.scalar_tensor_tensor(out=x, in0=pY[:, t, :], scalar=we[:, g * GT + t, bass.ds(i * 2 + e, 1)], in1=x,
                                                       op0=ALU.mult, op1=ALU.add)
                        if t % 2 == 1:
                            ins.then_inc(m["y_added"], 1)

                for k in range(K):
                    e, g, n = k // NG, k % NG, k % 2
                    for f in range(FT):
                        if not L1:
                            dve.wait_ge(m["a_done"], seen(i, k, FT, f + 1))
                            if k or f >= NH:
                                dve.wait_ge(m["hlo_done"], seen(i, k, FT, max(f - NH + 1, 0)))
                            dve.tensor_tensor(hf[:, f % NH, :], pH[:, f % 2, 1, :], act1[:, f % NH, :], ALU.mult).then_inc(m["hf_done"], 1)
                        if f == 0 and k:
                            add(k - 1)
                        if f == 1 and not (last and e):
                            split_lo(i * (2 * NG) + (e + 1) * NG + g + 1, (e + 1) % 2, g)
                        dve.wait_ge(m["hhi_done"], seen(i, k, FT, f + 1))
                        dve.tensor_tensor(hlo[:, n, f, :], hf[:, f % NH, :], hhi[:, n, f, :], ALU.subtract).then_inc(m["hlo_done"], 1)
                add(K - 1)
                dve.wait_ge(m["hlo_done"], seen(i, K, FT))
            loop(dve, body)

        @block.tensor
        def _(pe):
            pe.wait_ge(m["consts"], 4)
            for g in range(NG):
                pe.wait_ge(m["xn_done"], g + 1)
                if g:
                    pe.wait_ge(m["xlo_done"], g)
                for c in range(KD):
                    for t in range(GT):
                        ins = pe.transpose(pT[:, c, t * P:(t + 1) * P], xn[:, g % 2, t, c * P:(c + 1) * P], ident[:])
                ins.then_inc(m["turned"], 1)
            pe.wait_ge(m["xlo_done"], NG)
            pe.wait_ge(m["g_split"], 2)
            for t in range(NT):
                tok = slice(t * P, (t + 1) * P)
                for c in range(KD):
                    pe.matmul(pL[:, t, :], xhi[:, c, tok], g_hi[:, c, :], start=(c == 0), stop=False)
                    pe.matmul(pL[:, t, :], xhi[:, c, tok], g_lo[:, c, :], start=False, stop=False)
                    ins = pe.matmul(pL[:, t, :], xlo[:, c, tok], g_hi[:, c, :], start=False, stop=(c == KD - 1))
            ins.then_inc(m["logits"], 1)
            pe.wait_ge(m["pre_w"], 1)
            if L1:
                pe.wait_ge(m["bias_done"], 1)

            def body(i, last):
                for k in range(K):
                    e, g, n = k // NG, k % NG, k % 2
                    if g == 0:
                        pe.wait_ge(m["wlo_done"], i * (2 * NG) + (e + 1) * NG)
                    tok = slice(g * GN, (g + 1) * GN)
                    for f in range(FT):
                        if k or f >= 2:
                            pe.wait_ge(m["hf_done"], seen(i, k, FT, max(f - 1, 0)))
                        for u in range(UP):
                            out = pH[:, f % 2, u, :]
                            for c in range(KD):
                                at = WU + u * KD * F + c * F + f * P
                                w_h, w_l = whi[e][:, at:at + P], wlo[e][:, at:at + P]
                                pe.matmul(out, w_h, xhi[:, c, tok], start=(c == 0), stop=False)
                                pe.matmul(out, w_h, xlo[:, c, tok], start=False, stop=False)
                                ins = pe.matmul(out, w_l, xhi[:, c, tok], start=False, stop=(c == KD - 1))
                        ins.then_inc(m["h_done"], 1)
                    if k:
                        pe.wait_ge(m["y_added"], seen(i, k, 2))
                    if L1:
                        for t in range(GT):
                            pe.matmul(pY[:, t, :], sel[:], b2s[:, bass.ds(i * 2 + e, 1), :].rearrange("p o d -> p (o d)"),
                                      start=(t % 2 == 0), stop=False, skip_group_check=True)
                    for f in range(FT):
                        pe.wait_ge(m["hlo_done"], seen(i, k, FT, f + 1))
                        w = slice(WDN + f * D, WDN + (f + 1) * D)
                        for t in range(GT):
                            ts = slice(t * P, (t + 1) * P)
                            pe.matmul(pY[:, t, :], hhi[:, n, f, ts], whi[e][:, w], start=(f == 0 and t % 2 == 0 and not L1), stop=False,
                                      skip_group_check=True)
                            pe.matmul(pY[:, t, :], hhi[:, n, f, ts], wlo[e][:, w], start=False, stop=False, skip_group_check=True)
                            ins = pe.matmul(pY[:, t, :], hlo[:, n, f, ts], whi[e][:, w], start=False, stop=(f == FT - 1 and t % 2 == 1),
                                            skip_group_check=True)
                            if f == FT - 1 and t % 2 == 1:
                                ins.then_inc(m["y_done"], 1)
                pe.wait_ge(m["hf_done"], seen(i, K, FT))
                pe.wait_ge(m["y_added"], seen(i, K, 2))
            loop(pe, body)


def routed_experts(nc, a, X, ident, rows_x, rows_y, slots):
    gate, E, F = a["L0_ffn_w_gate"], a["L0_ffn_w_gate_proj"].shape[0], a["L0_ffn_w_gate_proj"].shape[2]
    FT = F // P
    FP = FT // 2
    EPS = 1e-5
    CH = 2
    ST = SLOTS // P
    NS = slots // SLOTS
    UPW = 2 * KD * F
    DNW = FT * D
    FULL = CH * N // SLOTS
    with ExitStack() as ctx:
        s = Store(nc, ctx, "moe0_")
        up_raw = [s.sb(f"up_raw{j}", [P, UPW]) for j in range(2)]
        up_hi = [s.sb(f"up_hi{j}", [P, UPW], F16) for j in range(2)]
        up_lo = [s.sb(f"up_lo{j}", [P, UPW], F16) for j in range(2)]
        dn_raw = [s.sb(f"dn_raw{j}", [P, DNW]) for j in range(2)]
        dn_hi = [s.sb(f"dn_hi{j}", [P, DNW], F16) for j in range(2)]
        dn_lo = [s.sb(f"dn_lo{j}", [P, DNW], F16) for j in range(2)]
        g_raw = s.sb("g_raw", [P, KD, E])
        g_hi = s.sb("g_hi", [P, KD, E], F16)
        g_lo = s.sb("g_lo", [P, KD, E], F16)
        iota = s.sb("iota", [P, NS])
        stats = s.sb("stats", [P, GT, 6])
        mv = s.sb("mv", [P, GT, 2])
        var = s.sb("var", [P, GT])
        rstd = s.sb("rstd", [P, GT])
        mhalf = s.sb("mhalf", [P, GT])
        xn = s.sb("xn", [P, NT, D])
        back = s.sb("back", [P, NT, D])
        xhi = s.sb("xhi", [P, KD, GN], F16)
        xlo = s.sb("xlo", [P, KD, GN], F16)
        logit = s.sb("logit", [P, NT, E])
        prob = s.sb("prob", [P, NT, E])
        red = s.sb("red", [P, NT])
        top = s.sb("top", [P, NT, 8])
        topi = s.sb("topi", [P, NT, 8], U32)
        topf = s.sb("topf", [P, NT, CH])
        tri = s.sb("tri", [P, P])
        tri16 = s.sb("tri16", [P, P], F16)
        ones16 = s.sb("ones16", [P, P], F16)
        chosen = [s.sb(f"chosen{n}", [P, NT, E]) for n in range(CH)]
        chosen16 = s.sb("chosen16", [P, NT, E], F16)
        rank = s.sb("rank", [P, NT, E])
        pre = [s.sb(f"pre{n}", [P, NT, E]) for n in range(2)]
        cmp = s.sb("cmp", [P, NS, E])
        lower = s.sb("lower", [P, E, E])
        iota_s = s.sb("iota_s", [P, FULL])
        tiles = s.sb("tiles", [P, E])
        first = s.sb("first", [P, E])
        base = s.sb("base", [P, E])
        slotf = s.sb("slotf", [P, NT, CH])
        slot = s.sb("slot", [P, CH, NT], U32)
        eidf = s.sb("eidf", [P, NS])
        eid = s.sb("eid", [P, NS], I32)
        xr = [s.sb(f"xr{j}", [P, ST, D]) for j in range(2)]
        thi = [s.sb(f"thi{j}", [P, KD, SLOTS], F16) for j in range(2)]
        tlo = [s.sb(f"tlo{j}", [P, KD, SLOTS], F16) for j in range(2)]
        act1 = [s.sb(f"act1{f}", [P, 2, SLOTS]) for f in range(FP)]
        hf = [s.sb(f"hf{f}", [P, 2, SLOTS]) for f in range(FP)]
        hhi = [s.sb(f"hhi{j}", [P, FT, SLOTS], F16) for j in range(2)]
        hlo = [s.sb(f"hlo{j}", [P, FT, SLOTS], F16) for j in range(2)]
        yo = [s.sb(f"yo{j}", [P, ST, D]) for j in range(2)]
        pH = [s.ps(f"pH{f}", [P, 2, 2, SLOTS]) for f in range(FP)]
        pT = s.ps("pT", [P, KD, GN])
        pY = [s.ps(f"pY{j}", [P, ST, D]) for j in range(2)]
        pL = pY[0][:].rearrange("p t d -> p (t d)")[:, 0:NT * E].rearrange("p (t e) -> p t e", e=E)
        pR = pY[1][:].rearrange("p t d -> p (t d)").rearrange("p (n t e) -> p n t e", n=2, e=E)
        pX = pT[:, 0, :].rearrange("p (c t) -> p c t", c=KD)

        names = ("g_in c_in consts st mvd va rs xn_done turned xhi_done xlo_done g_split logits pre_w steps asteps "
                 "tri_done chosen_done ranked slot_done eid_done sent x_turned thi_done tlo_done uph_done upl_done dnh_done dnl_done "
                 "h_done a_done hf_done hhi_done hlo_done y_done yo_done").split()
        m = {n: s.sem(n) for n in names}
        up_in, dn_in, x_in, y_sent, back_in = ([s.sem(f"{n}{j}") for j in range(2)] for n in ("up_in", "dn_in", "x_in", "y_sent", "back_in"))
        passed = [s.sem(f"passed{n}") for n in range(3)]
        block = ctx.enter_context(nc.Block())

        def upto(tile, each=1, plus=0):
            i, b = tile
            return i * (2 * each) + (b * each + plus)

        def upto_half(tile, each):
            i, b = tile
            return i * each + (b // 2 + 1) * each

        def plus(tile, n):
            return (tile[0], tile[1] + n)

        def steps_of(eng, step):
            step((0, 0))
            with eng.Fori(0, NS // 2 - 1) as i:
                step((i, 1))
                step((i, 2))
            step((0, NS - 1))

        @block.sync
        def _(sp):
            with nc.allow_non_contiguous_dma(reason="small parameters"):
                sp.dma_start(g_raw[:], gate.rearrange("(c p) e -> p c e", p=P)).then_inc(m["g_in"], 16)
                sp.dma_start(iota[:], a["c_iota"].partition_broadcast(P)).then_inc(m["c_in"], 16)
                sp.dma_start(tri[:], a["c_tri"]).then_inc(m["c_in"], 16)
            sp.wait_ge(m["eid_done"], 1)

            def load(tile):
                i, b = tile
                j = b % 2
                if b >= 2:
                    wait_apart(sp, passed[0], m["upl_done"], upto(tile, FP, -FP))
                e = sp.value_load(eid[0:1, bass.ds(i * 2 + b, 1)], min_val=0, max_val=E - 1)
                for n, name in enumerate(("gate", "up")):
                    sp.dma_start(up_raw[j][:, n * KD * F:(n + 1) * KD * F].rearrange("p (c f) -> p c f", c=KD),
                                 a[f"L0_ffn_w_{name}_proj"][bass.ds(e, 1)].rearrange("o (c p) f -> p (o c) f", p=P)).then_inc(up_in[j], 16)
                if b == 0:
                    sp.wait_ge(m["sent"], 16 * CH * NT)
                if b >= 2:
                    sp.wait_ge(m["x_turned"], upto(tile, 1, -1))
                sp.dma_start(xr[j][:], rows_x.rearrange("(n t p) d -> n p t d", t=ST, p=P)[bass.ds(i * 2 + b, 1)]
                             .rearrange("o p t d -> p (o t) d")).then_inc(x_in[j], 16)
                if b >= 2:
                    sp.wait_ge(m["dnl_done"], upto(tile, 1, -1))
                sp.dma_start(dn_raw[j][:].rearrange("p (c f) -> p c f", c=FT),
                             a["L0_ffn_w_down_proj"][bass.ds(e, 1)].rearrange("o (c p) f -> p (o c) f", p=P)).then_inc(dn_in[j], 16)

            load((0, 0))
            load((0, 1))
            with sp.Fori(0, NS // 2 - 1) as i:
                load((i, 2))
                load((i, 3))

        @block.gpsimd
        def _(pool):
            pool.memset(mhalf[:], -0.5).then_inc(m["consts"], 1)
            pool.memset(ones16[:], 1.0).then_inc(m["consts"], 1)
            pool.wait_ge(m["consts"], 2)
            for g in range(NG):
                wait_apart(pool, passed[1], m["mvd"], g + 1)
                pool.tensor_scalar(var[:], mv[:, :, 1], EPS, None, ALU.add).then_inc(m["va"], 1)
                pool.wait_ge(m["va"], g + 1)
                pool.tensor_tensor(rstd[:], var[:], mhalf[:], ALU.pow).then_inc(m["rs"], 1)
            pool.wait_ge(m["slot_done"], 1)
            for t in range(NT):
                for n in range(CH):
                    pool.indirect_dma_start(rows_x, bass.IndirectOffsetOnAxis(slot[:, n, t:t + 1], 0), xn[:, t, :], None).then_inc(m["sent"], 16)
            for j in range(2):
                pool.wait_ge(y_sent[j], 16 + 16 * NS // 2)
            for t in range(NT):
                for n, to in enumerate((xn, back)):
                    pool.indirect_dma_start(to[:, t, :], None, rows_y, bass.IndirectOffsetOnAxis(slot[:, n, t:t + 1], 0)).then_inc(back_in[t // (NT // 2)], 16)

        @block.scalar
        def _(act):
            act.sem_inc(m["yo_done"], 2)
            for j in range(2):
                act.sem_inc(y_sent[j], 16)
            act.wait_ge(m["g_in"], 16)
            act.activation(g_hi[:], g_raw[:], ACT.Copy, scale=WS).then_inc(m["g_split"], 1)
            for g in range(NG):
                act.wait_ge(m["turned"], g + 1)
                if g:
                    act.wait_ge(m["logits"], g)
                for c in range(KD):
                    ins = act.activation(xhi[:, c, :], pT[:, c, :], ACT.Copy)
                ins.then_inc(m["xhi_done"], 1)
            act.wait_ge(m["pre_w"], 1)
            act.activation(prob[:], logit[:], ACT.Exp).then_inc(m["asteps"], 1)

            def rows_hi(tile):
                j = tile[1] % 2
                act.wait_ge(m["x_turned"], upto(tile, 1, 1))
                act.activation(thi[j][:], pX, ACT.Copy).then_inc(m["thi_done"], 1)

            def up_split_hi(tile, f):
                j = tile[1] % 2
                c = slice(f * UPW // FP, (f + 1) * UPW // FP)
                if f == 0:
                    act.wait_ge(up_in[j], upto_half(tile, 32))
                act.activation(up_hi[j][:, c], up_raw[j][:, c], ACT.Copy, scale=WS).then_inc(m["uph_done"], 1)

            def down_split_hi(tile):
                j = tile[1] % 2
                act.wait_ge(dn_in[j], upto_half(tile, 16))
                act.activation(dn_hi[j][:], dn_raw[j][:], ACT.Copy, scale=WS).then_inc(m["dnh_done"], 1)

            def output(tile):
                j = tile[1] % 2
                act.wait_ge(m["y_done"], upto(tile, 1, 1))
                act.wait_ge(y_sent[j], upto_half(tile, 16))
                act.activation(yo[j][:], pY[j][:], ACT.Copy).then_inc(m["yo_done"], 1)
                act.wait_ge(m["yo_done"], upto(tile, 1, 3))
                act.dma_start(rows_y.rearrange("(n t p) d -> n p t d", t=ST, p=P)[bass.ds(tile[0] * 2 + tile[1], 1)]
                              .rearrange("o p t d -> p (o t) d"), yo[j][:]).then_inc(y_sent[j], 16)

            def silu(tile, f):
                act.wait_ge(m["h_done"], upto(tile, FP, f + 1))
                act.activation(act1[f][:], pH[f][:, :, 0, :], ACT.Silu, scale=1.0 / WS).then_inc(m["a_done"], 1)

            def hidden_hi(tile, f):
                j = tile[1] % 2
                act.wait_ge(m["hf_done"], upto(tile, FP, f + 1))
                act.activation(hhi[j][:, 2 * f:2 * f + 2, :], hf[f][:], ACT.Copy).then_inc(m["hhi_done"], 1)

            def step(tile):
                more = tile[1] + 1 < NS
                if more:
                    for f in range(FP):
                        up_split_hi(plus(tile, 1), f)
                silu(tile, 0)
                if more:
                    rows_hi(plus(tile, 1))
                down_split_hi(tile)
                hidden_hi(tile, 0)
                silu(tile, 1)
                hidden_hi(tile, 1)
                if tile[1]:
                    output(plus(tile, -1))

            for f in range(FP):
                up_split_hi((0, 0), f)
            rows_hi((0, 0))
            steps_of(act, step)
            output((0, NS - 1))

        @block.vector
        def _(dve):
            dve.wait_ge(m["consts"], 2)
            dve.wait_ge(m["g_split"], 1)
            dve.scalar_tensor_tensor(out=g_lo[:], in0=g_raw[:], scalar=WS, in1=g_hi[:], op0=ALU.mult,
                                     op1=ALU.subtract).then_inc(m["g_split"], 1)
            dve.wait_ge(m["c_in"], 32)
            dve.tensor_copy(tri16[:], tri[:]).then_inc(m["tri_done"], 1)
            for g in range(NG):
                layer_stats(dve, passed[2], X[:, g * GT:(g + 1) * GT, :], stats, mv, m["st"], g).then_inc(m["mvd"], 1)
                dve.wait_ge(m["rs"], g + 1)
                norm_group(dve, X[:, g * GT:(g + 1) * GT, :], mv, rstd, xn[:, g * GT:(g + 1) * GT]).then_inc(m["xn_done"], 1)
                dve.wait_ge(m["xhi_done"], g + 1)
                for c in range(KD):
                    ins = dve.tensor_tensor(xlo[:, c, :], pT[:, c, :], xhi[:, c, :], ALU.subtract)
                ins.then_inc(m["xlo_done"], 1)
            count = [0]

            def step_(ins):
                count[0] += 1
                ins.then_inc(m["steps"], 1)
                dve.wait_ge(m["steps"], count[0])

            def all_tokens(v):
                return v.unsqueeze(2).to_broadcast([P, NT, E])

            dve.wait_ge(m["logits"], NG)
            step_(dve.tensor_scalar(logit[:], pL, 1.0 / WS, None, ALU.mult))
            step_(dve.tensor_reduce(red[:], logit[:], AX.X, ALU.max))
            dve.tensor_tensor(logit[:], logit[:], all_tokens(red[:]), ALU.subtract).then_inc(m["pre_w"], 1)
            dve.tensor_scalar(iota_s[:], iota[:, 0:FULL], float(SLOTS), None, ALU.mult)
            step_(dve.tensor_tensor(lower[:], iota[:, 0:E].unsqueeze(1).to_broadcast([P, E, E]),
                                    iota[:, 0:E].unsqueeze(2).to_broadcast([P, E, E]), ALU.is_lt))
            dve.wait_ge(m["asteps"], 1)
            step_(dve.tensor_reduce(red[:], prob[:], AX.X, ALU.add))
            step_(dve.reciprocal(red[:], red[:]))
            step_(dve.tensor_tensor(prob[:], prob[:], all_tokens(red[:]), ALU.mult))
            for t in range(NT):
                ins = dve.max(top[:, t, :], prob[:, t, :])
            step_(ins)
            for t in range(NT):
                ins = dve.max_index(topi[:, t, :], top[:, t, :], prob[:, t, :])
            step_(ins)
            step_(dve.tensor_copy(topf[:], topi[:, :, 0:CH]))
            for n in range(CH):
                ins = dve.tensor_tensor(chosen[n][:], iota[:, 0:E].unsqueeze(1).to_broadcast([P, NT, E]), all_tokens(topf[:, :, n]), ALU.is_equal)
            step_(ins)
            dve.tensor_tensor(chosen16[:], chosen[0][:], chosen[1][:], ALU.add).then_inc(m["chosen_done"], 1)
            step_(dve.tensor_tensor(red[:], top[:, :, 0], top[:, :, 1], ALU.add))
            step_(dve.reciprocal(red[:], red[:]))
            step_(dve.scalar_tensor_tensor(out=top[:, :, 0:CH], in0=top[:, :, 0:CH], scalar=1.0 / WS / WS,
                                           in1=red[:].unsqueeze(2).to_broadcast([P, NT, CH]), op0=ALU.mult, op1=ALU.mult))
            dve.wait_ge(m["ranked"], 1)
            step_(dve.tensor_copy(pre[0][:], pR[:, 1]))
            step_(dve.tensor_tensor(rank[:], pR[:, 0], pre[0][:], ALU.subtract))
            n, w = 0, 1
            while w < NT:
                dve.tensor_copy(pre[1 - n][:, 0:w, :], pre[n][:, 0:w, :])
                step_(dve.tensor_tensor(pre[1 - n][:, w:, :], pre[n][:, w:, :], pre[n][:, 0:NT - w, :], ALU.add))
                n, w = 1 - n, 2 * w
            total = pre[n][:, NT - 1, :]
            dve.tensor_tensor(rank[:], rank[:], pre[n][:], ALU.add)
            step_(dve.tensor_tensor(cmp[:, 0:E, 0:FULL], total.unsqueeze(2).to_broadcast([P, E, FULL]),
                                    iota_s[:].unsqueeze(1).to_broadcast([P, E, FULL]), ALU.is_gt))
            step_(dve.tensor_reduce(tiles[:], cmp[:, 0:E, 0:FULL], AX.X, ALU.add))
            step_(dve.tensor_tensor(lower[:], lower[:], tiles[:].unsqueeze(1).to_broadcast([P, E, E]), ALU.mult))
            step_(dve.tensor_reduce(first[:], lower[:], AX.X, ALU.add))
            dve.tensor_scalar(base[:], first[:], float(SLOTS), None, ALU.mult)
            step_(dve.tensor_tensor(tiles[:], tiles[:], first[:], ALU.add))
            step_(dve.tensor_tensor(cmp[:], iota[:].unsqueeze(2).to_broadcast([P, NS, E]),
                                    tiles[:].unsqueeze(1).to_broadcast([P, NS, E]), ALU.is_ge))
            step_(dve.tensor_reduce(eidf[:], cmp[:], AX.X, ALU.add))
            step_(dve.tensor_scalar(eidf[:], eidf[:], float(E - 1), None, ALU.min))
            dve.tensor_copy(eid[:], eidf[:]).then_inc(m["eid_done"], 1)
            step_(dve.tensor_tensor(rank[:], rank[:], base[:].unsqueeze(1).to_broadcast([P, NT, E]), ALU.add))
            for n in range(CH):
                ins = dve.tensor_tensor(chosen[n][:], chosen[n][:], rank[:], ALU.mult)
            step_(ins)
            for n in range(CH):
                ins = dve.tensor_reduce(slotf[:, :, n], chosen[n][:], AX.X, ALU.add)
            step_(ins)
            dve.tensor_copy(slot[:].rearrange("p n t -> p t n"), slotf[:]).then_inc(m["slot_done"], 1)

            def rows_lo(tile):
                j = tile[1] % 2
                dve.wait_ge(m["thi_done"], upto(tile, 1, 1))
                dve.tensor_tensor(tlo[j][:], pX, thi[j][:], ALU.subtract).then_inc(m["tlo_done"], 1)

            def up_split_lo(tile, f):
                j = tile[1] % 2
                c = slice(f * UPW // FP, (f + 1) * UPW // FP)
                dve.wait_ge(m["uph_done"], upto(tile, FP, f + 1))
                dve.scalar_tensor_tensor(out=up_lo[j][:, c], in0=up_raw[j][:, c], scalar=WS, in1=up_hi[j][:, c], op0=ALU.mult,
                                         op1=ALU.subtract).then_inc(m["upl_done"], 1)

            def down_split_lo(tile):
                j = tile[1] % 2
                dve.wait_ge(m["dnh_done"], upto(tile, 1, 1))
                dve.scalar_tensor_tensor(out=dn_lo[j][:], in0=dn_raw[j][:], scalar=WS, in1=dn_hi[j][:], op0=ALU.mult,
                                         op1=ALU.subtract).then_inc(m["dnl_done"], 1)

            def hidden(tile, f):
                dve.wait_ge(m["a_done"], upto(tile, FP, f + 1))
                dve.tensor_tensor(hf[f][:], pH[f][:, :, 1, :], act1[f][:], ALU.mult).then_inc(m["hf_done"], 1)

            def hidden_lo(tile, f):
                j = tile[1] % 2
                dve.wait_ge(m["hhi_done"], upto(tile, FP, f + 1))
                dve.tensor_tensor(hlo[j][:, 2 * f:2 * f + 2, :], hf[f][:], hhi[j][:, 2 * f:2 * f + 2, :], ALU.subtract).then_inc(m["hlo_done"], 1)

            def step(tile):
                more = tile[1] + 1 < NS
                if more:
                    for f in range(FP):
                        up_split_lo(plus(tile, 1), f)
                hidden(tile, 0)
                if more:
                    rows_lo(plus(tile, 1))
                down_split_lo(tile)
                hidden_lo(tile, 0)
                hidden(tile, 1)
                hidden_lo(tile, 1)

            for f in range(FP):
                up_split_lo((0, 0), f)
            rows_lo((0, 0))
            steps_of(dve, step)
            for t in range(NT):
                if t % (NT // 2) == 0:
                    dve.wait_ge(back_in[t // (NT // 2)], 16 * CH * NT // 2)
                for n, rows in enumerate((xn, back)):
                    if t or n:
                        dve.wait_ge(m["steps"], count[0])
                    step_(dve.scalar_tensor_tensor(out=X[:, t, :], in0=rows[:, t, :], scalar=top[:, t, n:n + 1], in1=X[:, t, :],
                                                   op0=ALU.mult, op1=ALU.add))

        @block.tensor
        def _(pe):
            pe.wait_ge(m["consts"], 2)
            pe.wait_ge(m["g_split"], 2)
            for g in range(NG):
                pe.wait_ge(m["xn_done"], g + 1)
                if g:
                    pe.wait_ge(m["xlo_done"], g)
                for c in range(KD):
                    for t in range(GT):
                        ins = pe.transpose(pT[:, c, t * P:(t + 1) * P], xn[:, g * GT + t, c * P:(c + 1) * P], ident[:])
                ins.then_inc(m["turned"], 1)
                pe.wait_ge(m["xlo_done"], g + 1)
                for t in range(GT):
                    tok = slice(t * P, (t + 1) * P)
                    out = pL[:, g * GT + t, :]
                    for c in range(KD):
                        pe.matmul(out, xhi[:, c, tok], g_hi[:, c, :], start=(c == 0), stop=False)
                        pe.matmul(out, xhi[:, c, tok], g_lo[:, c, :], start=False, stop=False)
                        ins = pe.matmul(out, xlo[:, c, tok], g_hi[:, c, :], start=False, stop=(c == KD - 1))
                ins.then_inc(m["logits"], 1)
            pe.wait_ge(m["tri_done"], 1)
            pe.wait_ge(m["chosen_done"], 1)
            flat = chosen16[:].rearrange("p t e -> p (t e)")
            for n, w in enumerate((tri16, ones16)):
                ins = pe.matmul(pR[:, n].rearrange("p t e -> p (t e)"), w[:], flat, start=True, stop=True)
            ins.then_inc(m["ranked"], 1)

            def turn(tile):
                i, b = tile
                j = b % 2
                pe.wait_ge(x_in[j], upto_half(tile, 16))
                if b:
                    pe.wait_ge(m["tlo_done"], upto(tile))
                for c in range(KD):
                    for t in range(ST):
                        ins = pe.transpose(pX[:, c, t * P:(t + 1) * P], xr[j][:, t, c * P:(c + 1) * P], ident[:])
                ins.then_inc(m["x_turned"], 1)

            def up(tile, f):
                i, b = tile
                j = b % 2
                if f == 0:
                    pe.wait_ge(m["upl_done"], upto(tile, FP, FP))
                    pe.wait_ge(m["tlo_done"], upto(tile, 1, 1))
                if b:
                    pe.wait_ge(m["hf_done"], upto(tile, FP, f + 1 - FP))
                for n in range(2):
                    for u in range(2):
                        for c in range(KD):
                            at = u * KD * F + c * F + (2 * f + n) * P
                            w_h, w_l = up_hi[j][:, at:at + P], up_lo[j][:, at:at + P]
                            out = pH[f][:, n, u, :]
                            pe.matmul(out, w_h, thi[j][:, c, :], start=(c == 0), stop=False)
                            pe.matmul(out, w_h, tlo[j][:, c, :], start=False, stop=False)
                            ins = pe.matmul(out, w_l, thi[j][:, c, :], start=False, stop=(c == KD - 1))
                ins.then_inc(m["h_done"], 1)

            def down(tile):
                i, b = tile
                j = b % 2
                pe.wait_ge(m["dnl_done"], upto(tile, 1, 1))
                pe.wait_ge(m["hlo_done"], upto(tile, FP, FP))
                pe.wait_ge(m["yo_done"], upto(tile, 1, 1))
                for t in range(ST):
                    ts = slice(t * P, (t + 1) * P)
                    for f in range(FT):
                        w = slice(f * D, (f + 1) * D)
                        pe.matmul(pY[j][:, t, :], hhi[j][:, f, ts], dn_hi[j][:, w], start=(f == 0), stop=False)
                        pe.matmul(pY[j][:, t, :], hhi[j][:, f, ts], dn_lo[j][:, w], start=False, stop=False)
                        ins = pe.matmul(pY[j][:, t, :], hlo[j][:, f, ts], dn_hi[j][:, w], start=False, stop=(f == FT - 1))
                ins.then_inc(m["y_done"], 1)

            def step(tile):
                up(tile, 0)
                if tile[1] + 1 < NS:
                    turn(plus(tile, 1))
                up(tile, 1)
                if tile[1]:
                    down(plus(tile, -1))

            turn((0, 0))
            steps_of(pe, step)
            down((0, NS - 1))


def retention(nc, a, X, ident, ident16):
    H, HD = 16, D // 16
    PAIRS = H // 2
    OCT = 2
    T = SEQ // P
    G2 = T // GT
    EPS = 1e-5
    AW = 4 * HD
    HK = 2 * H
    LAST = 11
    with ExitStack() as ctx:
        s = Store(nc, ctx, "ret_")
        w_raw = s.sb("w_raw", [P, 3 * KD, D])
        WQ, WO, WE = np.cumsum([0, KD * 3 * D, KD * D]).tolist()
        wT = s.sb("wT", [P, WE])
        wThi = s.sb("wThi", [P, WE], F16)
        wTlo = s.sb("wTlo", [P, WE], F16)
        gnp = s.sb("gnp", [P, 2, D])
        cos = s.sb("cos", [P, T, HD])
        sin = s.sb("sin", [P, T, HD])
        dmask = s.sb("dmask", [P, H, P])
        dq = s.sb("dq", [P, H])
        dk = s.sb("dk", [P, H])
        dstate = s.sb("dstate", [P, OCT])
        blocks = s.sb("blocks", [P, P])
        mhalf = s.sb("mhalf", [P, HK])
        stats = s.sb("stats", [P, GT, 6])
        mv = s.sb("mv", [P, GT, 2])
        var = s.sb("var", [P, GT])
        rstd = s.sb("rstd", [P, GT])
        xn = s.sb("xn", [P, GT, D])
        xhi = s.sb("xhi", [P, KD, SEQ], F16)
        xlo = s.sb("xlo", [P, KD, SEQ], F16)
        qk = s.sb("qk", [P, 4, HK, HD])
        rot = s.sb("rot", [P, HK, HD])
        v = s.sb("v", [P, 3, D])
        vhi = s.sb("vhi", [P, 8, D], F16)
        vlo = s.sb("vlo", [P, 8, D], F16)
        qd = s.sb("qd", [P, 3, H, HD])
        kd = s.sb("kd", [P, 3, H, HD])
        kdhi = s.sb("kdhi", [P, 6, D], F16)
        kdlo = s.sb("kdlo", [P, 6, D], F16)
        qa = s.sb("qa", [P, 2, H, 4, HD], F16)
        ka = s.sb("ka", [P, 2, H, 4, HD], F16)
        kT = s.sb("kT", [P, 2, PAIRS, P], F16)
        qT = s.sb("qT", [P, 2, H, P], F16)
        qdhi = s.sb("qdhi", [P, 4, OCT, P], F16)
        qdlo = s.sb("qdlo", [P, 4, OCT, P], F16)
        am = s.sb("am", [P, H, P])
        ahi = s.sb("ahi", [P, 3, H, P], F16)
        alo = s.sb("alo", [P, 3, H, P], F16)
        st = s.sb("st", [P, OCT, P])
        stx = s.sb("stx", [P, OCT, P])
        sthi = s.sb("sthi", [P, OCT, P], F16)
        stlo = s.sb("stlo", [P, OCT, P], F16)
        r = s.sb("r", [P, 4, H, HD])
        rsq = s.sb("rsq", [P, 2, H, HD])
        hsum = s.sb("hsum", [P, 2, H])
        hsq = s.sb("hsq", [P, 2, H])
        hvar = s.sb("hvar", [P, 2, H])
        rhi = s.sb("rhi", [P, 2, OCT, P], F16)
        rlo = s.sb("rlo", [P, 2, OCT, P], F16)
        bank = [s.ps(f"bank{n}", [P, GN])[:] for n in range(8)]
        bank16 = [b.bitcast(F16) for b in bank]
        QK, VY, KA, QA, SC, QD, RO = 0, 1, 2, 3, 4, 6, 7

        w_in, wo_in, c_in = s.sem("w_in"), s.sem("wo_in"), s.sem("c_in")
        consts, w_turned, w_copied, w_ready = (s.sem(n) for n in ("consts", "w_turned", "w_copied", "w_ready"))
        names = ("stx mvd va rs xn_done turned xhi_done xlo_done qkv_done qk_copied v_copied vhi_done vlo_done rot_done cos_done "
                 "rope_done qd_done kd_done hi_done kdhi_done kdlo_done lo_done ka_turned qa_turned qd_turned kT_done qT_done "
                 "qdhi_done qdlo_done sc_done am_done ahi_done alo_done out_done s1 s2 sthi_done stlo_done r_copied sum_done mean_done "
                 "cen_done sq_done sum2_done hvar_done hrs_done scaled gam_done bet_done r_turned rhi_done rlo_done y_done y_added").split()
        m = {n: s.sem(n) for n in names}
        passed = s.sem("passed")
        block = ctx.enter_context(nc.Block())
        NW = 3 * D // P
        SR = 4

        def after(eng, i, name, t, each=1, part=None):
            eng.wait_ge(m[name], i * (T * each) + (t * each + (each if part is None else part)))

        def parts(s_, lag):
            return s_ - lag if 0 <= s_ - lag < T else None

        @block.sync
        def _(sp):
            for n, name in enumerate(("WQ", "WK", "WV")):
                w = a["L1_attn_" + name].rearrange("h u d -> (h u) d")
                sp.dma_start(w_raw[:, n * KD:(n + 1) * KD, :], w.rearrange("(t p) c -> p t c", p=P)).then_inc(w_in, 16)
            sp.dma_start(wT[:, WO:WE].rearrange("p (c d) -> p c d", c=KD), a["L1_attn_WO"].rearrange("(c p) d -> p c d", p=P)).then_inc(wo_in, 16)
            sp.dma_start(gnp[:, 0, :], a["L1_attn_gamma"].partition_broadcast(P)).then_inc(c_in, 16)
            sp.dma_start(gnp[:, 1, :], a["L1_attn_beta"].partition_broadcast(P)).then_inc(c_in, 16)
            for dst, name in ((cos, "c_cos1"), (sin, "c_sin1")):
                sp.dma_start(dst[:], a[name].rearrange("(t p) f -> p t f", p=P)).then_inc(c_in, 16)
            for dst, name in ((dmask, "c_dmask"), (dq, "c_dq"), (dk, "c_dk"), (dstate, "c_dstate"), (blocks, "c_blocks")):
                sp.dma_start(dst[:], a[name]).then_inc(c_in, 16)

        @block.gpsimd
        def _(pool):
            pool.memset(mhalf[:], -0.5).then_inc(consts, 1)
            pool.memset(qa[:, :, :, 3, :], 0.0).then_inc(consts, 1)
            pool.memset(ka[:, :, :, 3, :], 0.0).then_inc(consts, 1)
            pool.memset(qT[:], 0.0).then_inc(consts, 1)
            pool.wait_ge(consts, 4)
            pool.wait_ge(c_in, 16 * 9)

            with pool.Fori(0, BATCH) as i:
                for g in range(G2):
                    wait_apart(pool, passed, m["mvd"], i * G2 + (g + 1))
                    pool.tensor_scalar(var[:], mv[:, :, 1], EPS, None, ALU.add).then_inc(m["va"], 1)
                    pool.wait_ge(m["va"], i * G2 + (g + 1))
                    pool.tensor_tensor(rstd[:], var[:], mhalf[:, 0:GT], ALU.pow).then_inc(m["rs"], 1)
                for s_ in range(T + LAST + 1):
                    t = parts(s_, 8)
                    if t is not None:
                        after(pool, i, "sum2_done", t)
                        if t >= 2:
                            after(pool, i, "scaled", t - 2)
                        pool.sem_inc(passed, 1)
                        pool.tensor_scalar(hvar[:, t % 2], hsq[:, t % 2], 1.0 / HD, EPS, ALU.mult, ALU.add).then_inc(m["hvar_done"], 1)
                        after(pool, i, "hvar_done", t)
                        pool.tensor_tensor(hvar[:, t % 2], hvar[:, t % 2], mhalf[:, 0:H], ALU.pow).then_inc(m["hrs_done"], 1)
                    t = parts(s_, 9)
                    if t is not None:
                        after(pool, i, "scaled", t)
                        part = r[:, t % 4].rearrange("p h f -> p (h f)")
                        pool.tensor_tensor(part, part, gnp[:, 0, :], ALU.mult).then_inc(m["gam_done"], 1)
                        after(pool, i, "gam_done", t)
                        pool.tensor_tensor(part, part, gnp[:, 1, :], ALU.add).then_inc(m["bet_done"], 1)
                    t = parts(s_, 2)
                    if t is not None:
                        after(pool, i, "rope_done", t)
                        if t >= 3:
                            after(pool, i, "qd_turned", t - 3)
                            after(pool, i, "kdlo_done", t - 3)
                        pool.tensor_tensor(qd[:, t % 3], qk[:, t % 4, 0:H, :], dq[:].unsqueeze(2).to_broadcast([P, H, HD]), ALU.mult).then_inc(m["qd_done"], 1)
                        pool.tensor_tensor(kd[:, t % 3], qk[:, t % 4, H:HK, :], dk[:].unsqueeze(2).to_broadcast([P, H, HD]), ALU.mult).then_inc(m["kd_done"], 1)
                        after(pool, i, "vhi_done", t)
                        pool.tensor_tensor(vlo[:, t % 8, :], v[:, t % 3, :], vhi[:, t % 8, :], ALU.subtract).then_inc(m["vlo_done"], 1)
                    t = parts(s_, 3)
                    if t is not None:
                        after(pool, i, "kdhi_done", t)
                        pool.tensor_tensor(kdlo[:, t % 6, :], kd[:, t % 3].rearrange("p h f -> p (h f)"), kdhi[:, t % 6, :], ALU.subtract).then_inc(m["kdlo_done"], 1)

        @block.scalar
        def _(act):
            for n in range(NW):
                act.wait_ge(w_turned, n + 1)
                act.activation(wT[:, WQ:WO].rearrange("p (c o) -> p c o", c=KD)[:, :, n * P:(n + 1) * P],
                               bank[n % 2][:, 0:KD * P].rearrange("p (c o) -> p c o", c=KD), ACT.Copy).then_inc(w_copied, 1)
            act.wait_ge(w_copied, NW)
            act.wait_ge(wo_in, 16)
            act.activation(wThi[:], wT[:], ACT.Copy, scale=WS).then_inc(w_ready, 1)
            act.wait_ge(consts, 4)

            with act.Fori(0, BATCH) as i:
                for g in range(G2):
                    act.wait_ge(m["turned"], i * G2 + (g + 1))
                    for c in range(KD):
                        ins = act.activation(xhi[:, c, g * GN:(g + 1) * GN], bank[c], ACT.Copy)
                    ins.then_inc(m["xhi_done"], 1)
                for s_ in range(T + LAST + 1):
                    t = parts(s_, 4)
                    if t is not None:
                        after(act, i, "ka_turned", t)
                        if t >= 2:
                            after(act, i, "sc_done", t - 2, SR)
                        act.activation(kT[:, t % 2], bank16[KA].rearrange("p (h t) -> p h t", h=PAIRS), ACT.Copy).then_inc(m["kT_done"], 1)
                        after(act, i, "qd_turned", t)
                        act.activation(qdhi[:, t % 4], bank[QD][:, 0:OCT * P].rearrange("p (c t) -> p c t", c=OCT), ACT.Copy).then_inc(m["qdhi_done"], 1)
                    t = parts(s_, 10)
                    if t is not None:
                        after(act, i, "r_turned", t)
                        if t >= 2:
                            after(act, i, "y_done", t - 2)
                        act.activation(rhi[:, t % 2], bank[QK][:, 0:D].rearrange("p (c t) -> p c t", c=OCT), ACT.Copy).then_inc(m["rhi_done"], 1)
                    t = parts(s_, 6)
                    if t is not None:
                        after(act, i, "out_done", t)
                        act.activation(r[:, t % 4], bank[RO][:, 0:D].rearrange("p (h f) -> p h f", h=H), ACT.Copy).then_inc(m["r_copied"], 1)
                        after(act, i, "s2", t)
                        act.activation(sthi[:], st[:], ACT.Copy).then_inc(m["sthi_done"], 1)
                    t = parts(s_, 2)
                    if t is not None:
                        after(act, i, "rope_done", t)
                        if t >= 2:
                            after(act, i, "ka_turned", t - 2)
                            after(act, i, "qa_turned", t - 2)
                        for n in (0, 2):
                            act.activation(qa[:, t % 2, :, n, :], qk[:, t % 4, 0:H, :], ACT.Copy)
                        for n in (0, 1):
                            ins = act.activation(ka[:, t % 2, :, n, :], qk[:, t % 4, H:HK, :], ACT.Copy)
                        ins.then_inc(m["hi_done"], 1)
                    t = parts(s_, 3)
                    if t is not None:
                        after(act, i, "kd_done", t)
                        act.activation(kdhi[:, t % 6, :], kd[:, t % 3].rearrange("p h f -> p (h f)"), ACT.Copy).then_inc(m["kdhi_done"], 1)
                    t = parts(s_, 7)
                    if t is not None:
                        after(act, i, "cen_done", t)
                        act.activation(rsq[:, t % 2], r[:, t % 4], ACT.Square).then_inc(m["sq_done"], 1)
                    t = parts(s_, 0)
                    if t is not None:
                        after(act, i, "qkv_done", t)
                        if t >= 4:
                            after(act, i, "lo_done", t - 4)
                            after(act, i, "kd_done", t - 4)
                        act.activation(qk[:, t % 4], bank[QK].rearrange("p (h f) -> p h f", h=HK), ACT.Copy, scale=1.0 / WS).then_inc(m["qk_copied"], 1)
                        if t >= 3:
                            after(act, i, "vlo_done", t - 3)
                        act.activation(v[:, t % 3, :], bank[VY][:, 0:D], ACT.Copy, scale=1.0 / WS).then_inc(m["v_copied"], 1)
                        after(act, i, "v_copied", t)
                        act.activation(vhi[:, t % 8, :], v[:, t % 3, :], ACT.Copy).then_inc(m["vhi_done"], 1)
                    t = parts(s_, 4)
                    if t is not None:
                        for n in range(SR):
                            h = slice(n * H // SR, (n + 1) * H // SR)
                            after(act, i, "am_done", t, SR, n + 1)
                            act.activation(ahi[:, t % 3, h, :], am[:, h, :], ACT.Copy).then_inc(m["ahi_done"], 1)

        @block.vector
        def _(dve):
            dve.wait_ge(w_ready, 1)
            dve.scalar_tensor_tensor(out=wTlo[:], in0=wT[:], scalar=WS, in1=wThi[:], op0=ALU.mult, op1=ALU.subtract).then_inc(w_ready, 1)
            dve.wait_ge(consts, 4)
            dve.wait_ge(c_in, 16 * 9)
            with dve.Fori(0, BATCH) as i:
                for g in range(G2):
                    def xt(t):
                        return X[:, bass.ds(i * T + (g * GT + t), 1), :]
                    for t in range(GT):
                        ins = dve.bn_stats(stats[:, t, :], xt(t))
                    ins.then_inc(m["stx"], 1)
                    wait_apart(dve, passed, m["stx"], i * G2 + (g + 1))
                    for t in range(GT):
                        ins = dve.bn_aggr(mv[:, t, :], stats[:, t, :])
                    ins.then_inc(m["mvd"], 1)
                    dve.wait_ge(m["rs"], i * G2 + (g + 1))
                    if g:
                        dve.wait_ge(m["turned"], i * G2 + g)
                    for t in range(GT):
                        ins = dve.tensor_scalar(xn[:, t, :], xt(t), mv[:, t, 0:1], rstd[:, t:t + 1], ALU.subtract, ALU.mult)
                    ins.then_inc(m["xn_done"], 1)
                    dve.wait_ge(m["xhi_done"], i * G2 + (g + 1))
                    for c in range(KD):
                        ins = dve.tensor_tensor(xlo[:, c, g * GN:(g + 1) * GN], bank[c], xhi[:, c, g * GN:(g + 1) * GN], ALU.subtract)
                    ins.then_inc(m["xlo_done"], 1)
                for s_ in range(T + LAST + 1):
                    t = parts(s_, 11)
                    if t is not None:
                        after(dve, i, "y_done", t)
                        x = X[:, bass.ds(i * T + t, 1), :].rearrange("p o d -> p (o d)")
                        dve.scalar_tensor_tensor(out=x, in0=bank[VY][:, 0:D], scalar=1.0 / WS, in1=x, op0=ALU.mult, op1=ALU.add).then_inc(m["y_added"], 1)
                    t = parts(s_, 4)
                    if t is not None:
                        after(dve, i, "qa_turned", t)
                        if t >= 2:
                            after(dve, i, "sc_done", t - 2, SR)
                        for h in range(2):
                            rows = slice(h * AW, (h + 1) * AW)
                            ins = dve.tensor_copy(qT[rows, t % 2, h::2, :], bank16[QA][rows, :].rearrange("p (h t) -> p h t", h=PAIRS))
                        ins.then_inc(m["qT_done"], 1)
                        after(dve, i, "qdhi_done", t)
                        dve.tensor_tensor(qdlo[:, t % 4], bank[QD][:, 0:OCT * P].rearrange("p (c t) -> p c t", c=OCT), qdhi[:, t % 4], ALU.subtract).then_inc(m["qdlo_done"], 1)
                    t = parts(s_, 5)
                    if t is not None:
                        after(dve, i, "ahi_done", t, SR)
                        dve.tensor_tensor(alo[:, t % 3], am[:], ahi[:, t % 3], ALU.subtract).then_inc(m["alo_done"], 1)
                    t = parts(s_, 10)
                    if t is not None:
                        after(dve, i, "rhi_done", t)
                        dve.tensor_tensor(rlo[:, t % 2], bank[QK][:, 0:D].rearrange("p (c t) -> p c t", c=OCT), rhi[:, t % 2], ALU.subtract).then_inc(m["rlo_done"], 1)
                    t = parts(s_, 6)
                    if t is not None:
                        after(dve, i, "out_done", t)
                        dve.tensor_tensor(stx[:], bank[QD][:, D:2 * D].rearrange("p (c f) -> p c f", c=OCT),
                                          blocks[:].unsqueeze(1).to_broadcast([P, OCT, P]), ALU.mult).then_inc(m["s1"], 1)
                        after(dve, i, "s1", t)
                        if t == 0:
                            dve.tensor_copy(st[:], stx[:]).then_inc(m["s2"], 1)
                        else:
                            for c in range(OCT):
                                ins = dve.scalar_tensor_tensor(out=st[:, c, :], in0=st[:, c, :], scalar=dstate[:, c:c + 1], in1=stx[:, c, :],
                                                               op0=ALU.mult, op1=ALU.add)
                            ins.then_inc(m["s2"], 1)
                        after(dve, i, "sthi_done", t)
                        dve.tensor_tensor(stlo[:], st[:], sthi[:], ALU.subtract).then_inc(m["stlo_done"], 1)
                    t = parts(s_, 9)
                    if t is not None:
                        after(dve, i, "hrs_done", t)
                        dve.tensor_tensor(r[:, t % 4], r[:, t % 4], hvar[:, t % 2].unsqueeze(2).to_broadcast([P, H, HD]), ALU.mult).then_inc(m["scaled"], 1)
                    t = parts(s_, 8)
                    if t is not None:
                        after(dve, i, "sq_done", t)
                        if t >= 2:
                            after(dve, i, "hvar_done", t - 2)
                        dve.tensor_reduce(hsq[:, t % 2], rsq[:, t % 2], AX.X, ALU.add).then_inc(m["sum2_done"], 1)
                    t = parts(s_, 7)
                    if t is not None:
                        after(dve, i, "r_copied", t)
                        dve.tensor_reduce(hsum[:, t % 2], r[:, t % 4], AX.X, ALU.add).then_inc(m["sum_done"], 1)
                        after(dve, i, "sum_done", t)
                        dve.tensor_scalar(hsum[:, t % 2], hsum[:, t % 2], 1.0 / HD, None, ALU.mult).then_inc(m["mean_done"], 1)
                        after(dve, i, "mean_done", t)
                        dve.tensor_tensor(r[:, t % 4], r[:, t % 4], hsum[:, t % 2].unsqueeze(2).to_broadcast([P, H, HD]), ALU.subtract).then_inc(m["cen_done"], 1)
                    t = parts(s_, 3)
                    if t is not None:
                        after(dve, i, "hi_done", t)
                        dve.tensor_tensor(qa[:, t % 2, :, 1, :], qk[:, t % 4, 0:H, :], qa[:, t % 2, :, 0, :], ALU.subtract)
                        dve.tensor_tensor(ka[:, t % 2, :, 2, :], qk[:, t % 4, H:HK, :], ka[:, t % 2, :, 0, :], ALU.subtract).then_inc(m["lo_done"], 1)
                    t = parts(s_, 1)
                    if t is not None:
                        after(dve, i, "qk_copied", t)
                        if t:
                            after(dve, i, "rope_done", t - 1)
                        q = qk[:, t % 4].rearrange("p h (f two) -> p h f two", two=2)
                        ro = rot[:].rearrange("p h (f two) -> p h f two", two=2)
                        sn = sin[:, t, :].rearrange("p (f two) -> p f two", two=2)
                        for n in range(2):
                            ins = dve.tensor_tensor(ro[:, :, :, n], q[:, :, :, 1 - n], sn[:, :, n].unsqueeze(1).to_broadcast([P, HK, HD // 2]), ALU.mult)
                        ins.then_inc(m["rot_done"], 1)
                        after(dve, i, "rot_done", t)
                        dve.tensor_tensor(qk[:, t % 4], qk[:, t % 4], cos[:, t, :].unsqueeze(1).to_broadcast([P, HK, HD]), ALU.mult).then_inc(m["cos_done"], 1)
                        after(dve, i, "cos_done", t)
                        dve.tensor_tensor(qk[:, t % 4], qk[:, t % 4], rot[:], ALU.add).then_inc(m["rope_done"], 1)
                    t = parts(s_, 4)
                    if t is not None:
                        for n in range(SR):
                            h = slice(n * H // SR, (n + 1) * H // SR)
                            after(dve, i, "sc_done", t, SR, n + 1)
                            if n == 0 and t:
                                after(dve, i, "alo_done", t - 1)
                            dve.tensor_tensor(am[:, h, :], bank[SC + n % 2].rearrange("p (h t) -> p h t", h=H // SR), dmask[:, h, :], ALU.mult).then_inc(m["am_done"], 1)

        @block.tensor
        def _(pe):
            pe.wait_ge(w_in, 48)
            for n in range(NW):
                if n >= 2:
                    pe.wait_ge(w_copied, n - 1)
                for c in range(KD):
                    ins = pe.transpose(bank[n % 2][:, c * P:(c + 1) * P], w_raw[:, n, c * P:(c + 1) * P], ident[:])
                ins.then_inc(w_turned, 1)
            pe.wait_ge(consts, 4)
            pe.wait_ge(w_ready, 2)
            wq_h, wq_l = (w[:, WQ:WO].rearrange("p (c o) -> p c o", c=KD) for w in (wThi, wTlo))
            wo_h, wo_l = (w[:, WO:WE].rearrange("p (c o) -> p c o", c=KD) for w in (wThi, wTlo))

            def three(out, hi, lo, w_hi, w_lo, start, stop):
                pe.matmul(out, hi, w_hi, start=start, stop=False, skip_group_check=True)
                pe.matmul(out, hi, w_lo, start=False, stop=False, skip_group_check=True)
                return pe.matmul(out, lo, w_hi, start=False, stop=stop, skip_group_check=True)

            with pe.Fori(0, BATCH) as i:
                for g in range(G2):
                    pe.wait_ge(m["xn_done"], i * G2 + (g + 1))
                    if g:
                        pe.wait_ge(m["xlo_done"], i * G2 + g)
                    for c in range(KD):
                        for t in range(GT):
                            ins = pe.transpose(bank[c][:, t * P:(t + 1) * P], xn[:, t, c * P:(c + 1) * P], ident[:])
                    ins.then_inc(m["turned"], 1)
                pe.wait_ge(m["xlo_done"], i * G2 + G2)
                for s_ in range(T + LAST + 1):
                    t = parts(s_, 6)
                    if t is not None:
                        for n in ("alo_done", "vlo_done", "kdlo_done"):
                            after(pe, i, n, t)
                        if t:
                            after(pe, i, "stlo_done", t - 1)
                            after(pe, i, "r_copied", t - 1)
                        after(pe, i, "qdlo_done", min(t + 2, T - 1))
                        out = bank[RO][:, 0:D]
                        if t:
                            for c in range(OCT):
                                three(out[:, c * P:(c + 1) * P], qdhi[:, t % 4, c, :], qdlo[:, t % 4, c, :], sthi[:, c, :], stlo[:, c, :], c == 0, False)
                        for h in range(H):
                            cols = slice(h * HD, (h + 1) * HD)
                            three(out[:, cols], ahi[:, t % 3, h, :], alo[:, t % 3, h, :], vhi[:, t % 8, cols], vlo[:, t % 8, cols],
                                  t == 0 and h == 0, h == H - 1)
                        for c in range(OCT):
                            cols = slice(c * P, (c + 1) * P)
                            ins = three(bank[QD][:, D + c * P:D + (c + 1) * P], kdhi[:, t % 6, cols], kdlo[:, t % 6, cols],
                                        vhi[:, t % 8, cols], vlo[:, t % 8, cols], c == 0, c == OCT - 1)
                        ins.then_inc(m["out_done"], 1)
                    t = parts(s_, 10)
                    if t is not None:
                        after(pe, i, "rlo_done", t)
                        if t < T - 2:
                            pass
                        for c in range(OCT):
                            ins = three(bank[VY][:, 0:D], rhi[:, t % 2, c, :], rlo[:, t % 2, c, :], wo_h[:, c, :], wo_l[:, c, :], c == 0, c == OCT - 1)
                        ins.then_inc(m["y_done"], 1)
                    t = parts(s_, 9)
                    if t is not None:
                        after(pe, i, "bet_done", t)
                        if t:
                            after(pe, i, "rlo_done", t - 1)
                        for c in range(OCT):
                            ins = pe.transpose(bank[QK][:, c * P:(c + 1) * P], r[:, t % 4].rearrange("p h f -> p (h f)")[:, c * P:(c + 1) * P], ident[:])
                        ins.then_inc(m["r_turned"], 1)
                    t = parts(s_, 0)
                    if t is not None:
                        tok = slice(t * P, (t + 1) * P)
                        if t:
                            after(pe, i, "qk_copied", t - 1)
                        for c in range(KD):
                            three(bank[QK], xhi[:, c, tok], xlo[:, c, tok], wq_h[:, c, 0:2 * D], wq_l[:, c, 0:2 * D], c == 0, c == KD - 1)
                        if t:
                            after(pe, i, "v_copied", t - 1)
                        for c in range(KD):
                            ins = three(bank[VY][:, 0:D], xhi[:, c, tok], xlo[:, c, tok], wq_h[:, c, 2 * D:], wq_l[:, c, 2 * D:], c == 0, c == KD - 1)
                        ins.then_inc(m["qkv_done"], 1)
                    t = parts(s_, 4)
                    if t is not None:
                        after(pe, i, "kT_done", t)
                        after(pe, i, "qT_done", t)
                        for n in range(SR):
                            if n >= 2:
                                after(pe, i, "am_done", t, SR, n - 1)
                            elif t:
                                after(pe, i, "am_done", t - 1, SR, SR)
                            for p in range(2 * n, 2 * n + 2):
                                at = (p % 2) * 2 * P
                                ins = pe.matmul(bank[SC + n % 2][:, at:at + 2 * P], kT[:, t % 2, p, :], qT[:, t % 2, 2 * p:2 * p + 2, :].rearrange("p h t -> p (h t)"),
                                                start=True, stop=True)
                            ins.then_inc(m["sc_done"], 1)
                    t = parts(s_, 3)
                    if t is not None:
                        after(pe, i, "lo_done", t)
                        after(pe, i, "qd_done", t)
                        if t:
                            after(pe, i, "kT_done", t - 1)
                            after(pe, i, "qT_done", t - 1)
                            after(pe, i, "qdlo_done", t - 1)
                        for src, b, name in ((ka[:, t % 2], KA, "ka_turned"), (qa[:, t % 2], QA, "qa_turned")):
                            for p in range(PAIRS):
                                ins = pe.transpose(bank16[b][:, p * P:(p + 1) * P], src[:, 2 * p:2 * p + 2, :, :].rearrange("p h a f -> p (h a f)"), ident16[:])
                            ins.then_inc(m[name], 1)
                        if t >= 3:
                            after(pe, i, "s1", t - 3)
                        for c in range(OCT):
                            ins = pe.transpose(bank[QD][:, c * P:(c + 1) * P], qd[:, t % 3].rearrange("p h f -> p (h f)")[:, c * P:(c + 1) * P], ident[:])
                        ins.then_inc(m["qd_turned"], 1)


def constants():
    f = np.float32
    t = np.arange(SEQ, dtype=f)[:, None]
    inv = (f(1.0) / np.power(f(10000.0), np.arange(8, dtype=f) / f(8))).astype(f)
    ang = (t * inv[None]).astype(f)
    c, s = np.cos(ang).astype(f), np.sin(ang).astype(f)
    inv1 = np.power(f(10.0), f(-4.0) * (np.arange(0, 16, 2, dtype=f) / f(16))).astype(f)
    ang1 = (t * inv1[None]).astype(f)
    c1, s1 = np.cos(ang1).astype(f), np.sin(ang1).astype(f)
    decay = 1.0 - 2.0 ** (-5.0 - np.arange(16.0))
    j, i = np.arange(P)[:, None], np.arange(P)[None, :]
    dmask = np.where(i >= j, decay[:, None, None] ** np.maximum(i - j, 0), 0.0).transpose(1, 0, 2)
    head = np.arange(P) // 16
    return {
        "c_cos1": np.repeat(c1, 2, 1),
        "c_sin1": np.stack([-s1, s1], -1).reshape(SEQ, 16),
        "c_dmask": dmask.astype(f),
        "c_dq": (decay[None] ** (np.arange(P)[:, None] + 1)).astype(f),
        "c_dk": (decay[None] ** (P - 1 - np.arange(P)[:, None])).astype(f),
        "c_dstate": np.stack([decay[head], decay[head + 8]], 1).astype(np.float64).__pow__(P).astype(f),
        "c_blocks": (head[:, None] == head[None]).astype(f),
        "c_ident": np.eye(P, dtype=f),
        "c_iota": np.arange(32, dtype=f),
        "c_tri": (j < i).astype(f),
        "c_cos0": np.concatenate([c, c], 1),
        "c_sin0": np.concatenate([-s, s], 1),
    }


def tower(nc, a, out):
    with ExitStack() as ctx:
        s = Store(nc, ctx, "")
        X = s.sb("X", [P, NT, D])
        ident = s.sb("ident", [P, P])
        ident16 = s.sb("ident16", [P, P], F16)
        ident_in, ident16_done, x_out = s.sem("ident_in"), s.sem("ident16_done"), s.sem("x_out")
        with nc.Block() as block:
            @block.sync
            def _(sp):
                sp.dma_start(ident[:], a["c_ident"]).then_inc(ident_in, 16)

            @block.vector
            def _(dve):
                dve.wait_ge(ident_in, 16)
                dve.tensor_copy(ident16[:], ident[:]).then_inc(ident16_done, 1)
                dve.wait_ge(ident16_done, 1)
        slots = (16 + 2 * N // SLOTS) * SLOTS
        rows_x = nc.dram_tensor("rows_x", (slots, D), F32, kind="Internal").ap()
        rows_y = nc.dram_tensor("rows_y", (slots, D), F32, kind="Internal").ap()
        embed(nc, a, X)
        trunk(nc, a, X, ident, rows_x)
        rotary_attention(nc, a, X, ident, ident16)
        routed_experts(nc, a, X, ident, rows_x, rows_y, slots)
        retention(nc, a, X, ident, ident16)
        experts(nc, a, X, ident, L1=True)
        with nc.Block() as block:
            @block.sync
            def _(sp):
                sp.dma_start(out.rearrange("b (t p) d -> p (b t) d", p=P), X[:]).then_inc(x_out, 16)
                sp.wait_ge(x_out, 16)


_INS = ["x"] + ["L0_tok_" + n for n in "emb pos_emb A_diag B C D w1 b1 w2 b2 ln1_s ln1_b ln2_s ln2_b lnf_s lnf_b".split()] \
    + ["L0_attn_" + n for n in "w_qkv w_proj b_proj q_gamma q_beta k_gamma k_beta".split()] \
    + ["L0_ffn_" + n for n in "w_gate w_gate_proj w_up_proj w_down_proj".split()] \
    + ["L1_attn_" + n for n in "WQ WK WV WO gamma beta".split()] \
    + ["L1_ffn_" + n for n in "Wg bg W1 b1 W2 b2".split()]


def kernel(**inputs):
    import concourse.bacc as bacc
    from concourse.bass_utils import run_bass_kernel_spmd

    nc = bacc.Bacc("TRN2", target_bir_lowering=False, num_devices=1)
    arrays = {name: np.ascontiguousarray(inputs[name]) for name in _INS}
    arrays.update(constants())
    args = {name: nc.dram_tensor(f"in_{name}", v.shape, mybir.dt.from_np(v.dtype), kind="ExternalInput").ap()
            for name, v in arrays.items()}
    out = nc.dram_tensor("out_h", (BATCH, SEQ, D), F32, kind="ExternalOutput").ap()
    tower(nc, args, out)
    r = run_bass_kernel_spmd(nc, [{f"in_{name}": v for name, v in arrays.items()}], core_ids=[0])
    return r.results[0]["out_h"]
```

```python
from contextlib import ExitStack

import numpy as np
import concourse.bass as bass
from concourse import mybir

F32 = mybir.dt.float32
F16 = mybir.dt.float16
I32 = mybir.dt.int32
U32 = mybir.dt.uint32
ACT = mybir.ActivationFunctionType
ALU = mybir.AluOpType
AX = mybir.AxisListType

P = 128
BATCH, SEQ, D = 2, 1024, 256
N = BATCH * SEQ
NT = N // P
KD = D // P
GT = 4
GN = GT * P
NG = N // GN
SLOTS = 256
WS = 64.0


class Store:

    def __init__(self, nc, ctx, phase):
        self.nc, self.ctx, self.phase, self.sems = nc, ctx, phase, []
        ctx.callback(self.close)

    def sb(self, name, shape, dt=F32):
        return self.ctx.enter_context(self.nc.sbuf_tensor(self.phase + name, shape, dt))

    def ps(self, name, shape, dt=F32):
        return self.ctx.enter_context(self.nc.psum_tensor(self.phase + name, shape, dt))

    def sem(self, name):
        self.sems.append(self.nc.alloc_semaphore(self.phase + name))
        return self.sems[-1]

    def close(self):
        self.nc.clear_and_free_semaphores(self.sems)
        self.nc.all_engine_barrier()


def wait_apart(eng, passed, sem, value):
    eng.wait_ge(sem, value)
    eng.sem_inc(passed, 1)


def layer_stats(dve, passed, x, stats, mv, stats_done, before):
    for t in range(GT):
        ins = dve.bn_stats(stats[:, t, :], x[:, t, :])
    ins.then_inc(stats_done, 1)
    wait_apart(dve, passed, stats_done, before + 1)
    for t in range(GT):
        ins = dve.bn_aggr(mv[:, t, :], stats[:, t, :])
    return ins


def trunk(nc, a, X, ident, rows_x):
    L, S = a["L0_tok_A_diag"].shape
    F = a["L0_tok_w1"].shape[2]
    FT = F // P
    SS = 8.0
    assert SS * SS == WS
    K = 2 * NG
    EPS = 1e-5
    W1, W2, WD, WB, WC, WB2, WE = np.cumsum([0, KD * F, FT * D, KD * D, KD * S, D, D]).tolist()
    Q = 4
    with ExitStack() as ctx:
        s = Store(nc, ctx, "trunk_")
        raw = s.sb("w_raw", [P, WE])
        whi = [s.sb(f"w_hi{j}", [P, WE], F16) for j in range(2)]
        wlo = [s.sb(f"w_lo{j}", [P, WE], F16) for j in range(2)]
        b1 = [s.sb(f"b1_{j}", [P, FT]) for j in range(2)]
        aff = [s.sb(f"aff{j}", [P, 2, 2, KD]) for j in range(2)]
        a_raw = s.sb("a_raw", [S, L])
        a_sig = s.sb("a_sig", [S, L])
        a_row = [s.sb(f"a_row{j}", [S, GN]) for j in range(2)]
        ones32 = s.sb("ones32", [S, GN])
        sel = s.sb("sel", [P, P], F16)
        mhalf = s.sb("mhalf", [P, GT])
        stats = s.sb("stats", [P, 2, GT, 6])
        mv = s.sb("mv", [P, 2, GT, 2])
        var = s.sb("var", [P, 2, GT])
        rstd = s.sb("rstd", [P, 2, GT])
        xn = s.sb("xn", [P, 2, GT, D])
        xT = s.sb("xT", [P, 2, KD, GN])
        xhi = s.sb("xhi", [P, 2, KD, GN], F16)
        xlo = s.sb("xlo", [P, 2, KD, GN], F16)
        hst = s.sb("hst", [S, 2, GN])
        hst_hi = s.sb("hst_hi", [P, GN], F16)
        hst_lo = s.sb("hst_lo", [P, GN], F16)
        NH = 3
        hf = s.sb("hf", [P, NH, GN])
        hhi = s.sb("hhi", [P, FT, GN], F16)
        hlo = s.sb("hlo", [P, FT, GN], F16)
        pT = [s.ps(f"pT{j}", [P, KD, GN]) for j in range(2)]
        pH = s.ps("pH", [P, 2, GN])
        pY = s.ps("pY", [P, GT, D])
        pU = pT[0][0:S, 0, :]

        w_in, small_in, a_in = s.sem("w_in"), [s.sem(f"small_in{j}") for j in range(2)], s.sem("a_in")
        whi_done, w_ready = s.sem("whi_done"), s.sem("w_ready")
        layer_free = s.sem("layer_free")
        consts = s.sem("consts")
        a_step = s.sem("a_step")
        V = a["L0_tok_emb"].shape[0]
        tok = s.sb("tok", [P, NT], I32)
        tokf = s.sb("tokf", [P, NT])
        wrap = s.sb("wrap", [P, NT])
        idx = s.sb("idx", [P, NT], U32)
        PT = SEQ // P
        pos = s.sb("pos", [P, PT, D])
        tok_in, pos_in, idx_step, added = (s.sem(n) for n in ("tok_in", "pos_in", "idx_step", "pos_added"))
        rows_in = [s.sem(f"rows_in{g}") for g in range(NG)]
        ZT = 8
        zeros = s.sb("zeros", [P, ZT, D])
        zeros_set, zeros_out = s.sem("zeros_set"), s.sem("zeros_out")
        arow_ready = s.sem("arow_ready")
        st_done = [s.sem(f"st_done{j}") for j in range(2)]
        mv_done = [s.sem(f"mv_done{j}") for j in range(2)]
        var_done = [s.sem(f"var_done{j}") for j in range(2)]
        rstd_done = [s.sem(f"rstd_done{j}") for j in range(2)]
        xn_done = [s.sem(f"xn_done{j}") for j in range(2)]
        turned = [s.sem(f"turned{j}") for j in range(2)]
        xT_done = [s.sem(f"xT_done{j}") for j in range(2)]
        xhi_done = [s.sem(f"xhi_done{j}") for j in range(2)]
        xlo_done = [s.sem(f"xlo_done{j}") for j in range(2)]
        u_done, scan_done, hsthi_done, hstlo_done = (s.sem(n) for n in ("u_done", "scan_done", "hsthi_done", "hstlo_done"))
        ys_done, ys_added = s.sem("ys_done"), s.sem("ys_added")
        h_done, gelu_done, hhi_done, hlo_done = (s.sem(n) for n in ("h_done", "gelu_done", "hhi_done", "hlo_done"))
        yf_done, yf_added = s.sem("yf_done"), s.sem("yf_added")
        passed, sp_passed = s.sem("passed"), s.sem("sp_passed")
        block = ctx.enter_context(nc.Block())

        def w1v(w, c, f):
            return w[:, W1 + c * F + f * P:W1 + c * F + (f + 1) * P]

        def w2v(w, f):
            return w[:, W2 + f * D:W2 + (f + 1) * D]

        def wdv(w, c):
            return w[:, WD + c * D:WD + (c + 1) * D]

        def wbv(w, c):
            return w[:, WB + c * S:WB + (c + 1) * S]

        def seen(i, k, each, plus=0):
            return i * (K * each) + (k * each + plus)

        @block.sync
        def _(sp):
            with nc.allow_non_contiguous_dma(reason="2048 token ids"):
                sp.dma_start(tok[:], a["x"].rearrange("b (t p) -> p (b t)", p=P)).then_inc(tok_in, 16)
            sp.dma_start(pos[:], a["L0_tok_pos_emb"][0:SEQ, :].rearrange("(t p) d -> p t d", p=P)).then_inc(pos_in, 16)
            with nc.allow_non_contiguous_dma(reason="small parameters"):
                sp.dma_start(a_raw[:], a["L0_tok_A_diag"].rearrange("l s -> s l")).then_inc(a_in, 16)
            sp.wait_ge(consts, 6)

            def load(j, l, n):
                def row(name):
                    return a[name][bass.ds(l, 1)]
                for dst, src in (
                    (raw[:, W1:W2].rearrange("p (c f) -> p c f", c=KD), row("L0_tok_w1").rearrange("o (c p) f -> p (o c) f", p=P)),
                    (raw[:, W2:WD].rearrange("p (c d) -> p c d", c=FT), row("L0_tok_w2").rearrange("o (c p) d -> p (o c) d", p=P)),
                    (raw[:, WD:WB].rearrange("p (c d) -> p c d", c=KD), row("L0_tok_D").rearrange("o (c p) d -> p (o c) d", p=P)),
                    (raw[:, WB:WC].rearrange("p (c d) -> p c d", c=KD), row("L0_tok_B").rearrange("o (c p) d -> p (o c) d", p=P)),
                    (raw[0:S, WC:WB2], row("L0_tok_C").rearrange("o s d -> (o s) d")),
                    (raw[0:1, WB2:WE], row("L0_tok_b2")),
                ):
                    sp.dma_start(dst, src).then_inc(w_in, 16)
                wait_apart(sp, sp_passed, layer_free, n + 1)
                with nc.allow_non_contiguous_dma(reason="small parameters"):
                    sp.dma_start(b1[j][:], row("L0_tok_b1").rearrange("o (c p) -> p (o c)", p=P)).then_inc(small_in[j], 16)
                    for m, name in enumerate(("ln1_s", "ln1_b", "ln2_s", "ln2_b")):
                        sp.dma_start(aff[j][:, m // 2, m % 2, :],
                                     row("L0_tok_" + name).rearrange("o (c p) -> p (o c)", p=P)).then_inc(small_in[j], 16)

            load(0, 0, 0)
            with sp.Fori(0, L // 2) as i:
                for j in (1, 2):
                    wait_apart(sp, sp_passed, w_ready, i * (2 * Q) + j * Q)
                    load(j % 2, (i * 2 + j) % L, i * 2 + j)
            sp.wait_ge(zeros_set, 1)
            for part in rows_x.rearrange("(n t p) d -> n p t d", t=ZT, p=P):
                sp.dma_start(part, zeros[:]).then_inc(zeros_out, 16)
            sp.wait_ge(zeros_out, rows_x.shape[0] // (ZT * P) * 16)

        NWD, NSD = 6, 5

        def parts(q):
            w = WB // Q
            return [(slice(q * w, (q + 1) * w), WS)] + ([(slice(WB, WB2), SS), (slice(WB2, WE), WS)] if q == Q - 1 else [])

        def quarters(k):
            return {1: [(1, 1, 0)], 2: [(1, 1, 1), (1, 1, 2)], 3: [(1, 1, 3)],
                    5: [(0, 2, 0)], 6: [(0, 2, 1), (0, 2, 2)], 7: [(0, 2, 3)]}.get(k, [])

        @block.gpsimd
        def _(pool):
            pool.memset(ones32[:], 1.0).then_inc(consts, 1)
            pool.memset(sel[:], 0.0).then_inc(consts, 1)
            pool.memset(mhalf[:], -0.5).then_inc(consts, 1)
            pool.memset(raw[:, WC:WE], 0.0).then_inc(consts, 1)
            pool.memset(hst_hi[:], 0.0)
            pool.memset(hst_lo[:], 0.0).then_inc(consts, 1)
            pool.wait_ge(consts, 5)
            pool.memset(sel[0:1, :], 1.0).then_inc(consts, 1)

            def gather(t):
                pool.indirect_dma_start(X[:, t, :], None, a["L0_tok_emb"],
                                        bass.IndirectOffsetOnAxis(idx[:, t:t + 1], 0)).then_inc(rows_in[t // GT], 16)

            pool.wait_ge(idx_step, 5)
            for t in range(NT // 2):
                gather(t)

            def rsqrt(i, k, j):
                wait_apart(pool, passed, mv_done[j], seen(i, k, 1, 1))
                pool.tensor_scalar(var[:, j, :], mv[:, j, :, 1], EPS, None, ALU.add).then_inc(var_done[j], 1)
                pool.wait_ge(var_done[j], seen(i, k, 1, 1))
                pool.tensor_tensor(rstd[:, j, :], var[:, j, :], mhalf[:], ALU.pow).then_inc(rstd_done[j], 1)

            pool.wait_ge(consts, 6)
            rsqrt(0, 0, 0)
            for t in range(NT // 2, NT):
                gather(t)
            pool.memset(zeros[:], 0.0).then_inc(zeros_set, 1)
            with pool.Fori(0, L // 2) as i:
                for k in range(K):
                    if k < K:
                        rsqrt(i, k + 1, 0)
                    rsqrt(i, k, 1)

        @block.scalar
        def _(act):
            act.wait_ge(a_in, 16)
            act.activation(a_sig[:], a_raw[:], ACT.Sigmoid).then_inc(a_step, 1)

            def affine(i, k, j):
                lj = k // NG % 2
                act.wait_ge(turned[j], seen(i, k, 1, 1))
                if k % NG == 0:
                    act.wait_ge(small_in[lj], i * (NSD * 16) + (k // K + 1) * NSD * 16)
                for c in range(KD):
                    ins = act.activation(xT[:, j, c, :], pT[j][:, c, :], ACT.Identity,
                                         bias=aff[lj][:, j, 1, c:c + 1], scale=aff[lj][:, j, 0, c:c + 1])
                ins.then_inc(xT_done[j], 1)
                act.wait_ge(xT_done[j], seen(i, k, 1, 1))
                for c in range(KD):
                    ins = act.activation(xhi[:, j, c, :], xT[:, j, c, :], ACT.Copy)
                ins.then_inc(xhi_done[j], 1)

            def gelu(i, k, f):
                lj = k // NG
                act.wait_ge(h_done, seen(i, k, FT, f + 1))
                act.activation(hf[:, f % NH, :], pH[:, f % 2, :], ACT.Gelu, bias=b1[lj][:, f:f + 1],
                               scale=1.0 / WS).then_inc(gelu_done, 1)
                act.wait_ge(gelu_done, seen(i, k, FT, f + 1))
                act.activation(hhi[:, f, :], hf[:, f % NH, :], ACT.Copy).then_inc(hhi_done, 1)

            def split_hi(j, i, l, q):
                if q == 0:
                    act.wait_ge(w_in, i * (2 * NWD * 16) + (l + 1) * NWD * 16)
                for c, scale in parts(q):
                    ins = act.activation(whi[j][:, c], raw[:, c], ACT.Copy, scale=scale)
                ins.then_inc(whi_done, 1)

            act.wait_ge(consts, 6)
            for q in range(Q):
                split_hi(0, 0, 0, q)
            affine(0, 0, 0)
            with act.Fori(0, L // 2) as i:
                for k in range(K + 1):
                    if k:
                        if k > 1:
                            act.wait_ge(yf_done, seen(i, k - 1, 2))
                            act.wait_ge(hlo_done, seen(i, k - 1, FT))
                        for f in range(FT // 2):
                            if f >= NH:
                                act.wait_ge(hlo_done, seen(i, k - 1, FT, f - NH + 1))
                            gelu(i, k - 1, f)
                    if k < K:
                        act.wait_ge(scan_done, seen(i, k, 1, 1))
                        act.activation(hst_hi[0:S], hst[:, k % 2, :], ACT.Copy).then_inc(hsthi_done, 1)
                    if k:
                        for f in range(FT // 2, FT):
                            act.wait_ge(hlo_done, seen(i, k - 1, FT, f - NH + 1))
                            gelu(i, k - 1, f)
                    for j, l, q in quarters(k):
                        split_hi(j, i, l, q)
                    if k < K:
                        affine(i, k, 1)
                        affine(i, k + 1, 0)
                act.wait_ge(yf_done, seen(i, K, 2))

        @block.vector
        def _(dve):
            def decay_row(i, j):
                dve.tensor_scalar(a_row[j][:], ones32[:], a_sig[:, bass.ds(i * 2 + j, 1)], None, ALU.mult).then_inc(arow_ready, 1)
                dve.wait_ge(arow_ready, i * 2 + (j + 1))

            def norm_stats(i, k, j):
                g = k % NG
                if j == 0:
                    if k >= NG:
                        dve.wait_ge(yf_added, seen(i, k - NG, 2, 2))
                else:
                    dve.wait_ge(ys_added, seen(i, k, 2, 2))
                layer_stats(dve, passed, X[:, g * GT:(g + 1) * GT, :], stats[:, j], mv[:, j], st_done[j],
                            seen(i, k, 1)).then_inc(mv_done[j], 1)

            def norm(i, k, j):
                g = k % NG
                dve.wait_ge(rstd_done[j], seen(i, k, 1, 1))
                if k:
                    dve.wait_ge(turned[j], seen(i, k, 1))
                for t in range(GT):
                    ins = dve.tensor_scalar(xn[:, j, t, :], X[:, g * GT + t, :], mv[:, j, t, 0:1],
                                            rstd[:, j, t:t + 1], ALU.subtract, ALU.mult)
                ins.then_inc(xn_done[j], 1)

            def low(i, k, j):
                dve.wait_ge(xhi_done[j], seen(i, k, 1, 1))
                for c in range(KD):
                    ins = dve.tensor_tensor(xlo[:, j, c, :], xT[:, j, c, :], xhi[:, j, c, :], ALU.subtract)
                ins.then_inc(xlo_done[j], 1)

            def h_low(i, k, f):
                dve.wait_ge(hhi_done, seen(i, k, FT, f + 1))
                dve.tensor_tensor(hlo[:, f, :], hf[:, f % NH, :], hhi[:, f, :], ALU.subtract).then_inc(hlo_done, 1)

            def add(i, k, half, done, added):
                g = k % NG
                dve.wait_ge(done, seen(i, k, 2, half + 1))
                x = X[:, g * GT + 2 * half:g * GT + 2 * half + 2, :]
                dve.scalar_tensor_tensor(out=x, in0=pY[:, 2 * half:2 * half + 2, :], scalar=1.0 / WS, in1=x,
                                         op0=ALU.mult, op1=ALU.add).then_inc(added, 1)

            def scan(i, k):
                dve.wait_ge(u_done, seen(i, k, 1, 1))
                if k >= 1:
                    dve.wait_ge(scan_done, seen(i, k, 1))
                start = 0.0 if k % 2 == 0 else hst[:, (k - 1) % 2, GN - 1:GN]
                dve.tensor_tensor_scan(hst[:, k % 2, :], a_row[k // NG][:], pU, start, ALU.mult, ALU.add).then_inc(scan_done, 1)
                dve.wait_ge(hsthi_done, seen(i, k, 1, 1))
                dve.tensor_tensor(hst_lo[0:S], hst[:, k % 2, :], hst_hi[0:S], ALU.subtract).then_inc(hstlo_done, 1)

            def split_lo(j, i, l, q):
                dve.wait_ge(whi_done, i * (2 * Q) + (l * Q + q + 1))
                for c, scale in parts(q):
                    ins = dve.scalar_tensor_tensor(out=wlo[j][:, c], in0=raw[:, c], scalar=scale, in1=whi[j][:, c], op0=ALU.mult, op1=ALU.subtract)
                ins.then_inc(w_ready, 1)

            dve.sem_inc(layer_free, 2)
            dve.wait_ge(tok_in, 16)
            dve.tensor_copy(tokf[:], tok[:]).then_inc(idx_step, 1)
            dve.wait_ge(idx_step, 1)
            dve.tensor_scalar(wrap[:], tokf[:], 0.0, float(V), ALU.is_lt, ALU.mult).then_inc(idx_step, 1)
            dve.wait_ge(idx_step, 2)
            dve.tensor_tensor(tokf[:], tokf[:], wrap[:], ALU.add).then_inc(idx_step, 1)
            dve.wait_ge(idx_step, 3)
            dve.tensor_scalar(tokf[:], tokf[:], 0.0, float(V - 1), ALU.max, ALU.min).then_inc(idx_step, 1)
            dve.wait_ge(idx_step, 4)
            dve.tensor_copy(idx[:], tokf[:]).then_inc(idx_step, 1)
            dve.wait_ge(a_step, 1)
            dve.wait_ge(consts, 6)
            dve.wait_ge(pos_in, 16)

            def add_position(g):
                dve.wait_ge(rows_in[g], 16 * GT)
                xg, at = X[:, g * GT:(g + 1) * GT, :], g * GT % PT
                dve.tensor_tensor(xg, xg, pos[:, at:at + GT, :], ALU.add).then_inc(added, 1)

            add_position(0)
            dve.wait_ge(added, 1)
            norm_stats(0, 0, 0)
            norm(0, 0, 0)
            for q in range(Q):
                split_lo(0, 0, 0, q)
            low(0, 0, 0)
            for g in range(1, NG):
                add_position(g)
            dve.wait_ge(added, NG)
            with dve.Fori(0, L // 2) as i:
                decay_row(i, 0)
                decay_row(i, 1)
                for k in range(K + 1):
                    if k < K:
                        norm_stats(i, k + 1, 0)
                        norm(i, k + 1, 0)
                    if k:
                        for f in range(FT // 2):
                            h_low(i, k - 1, f)
                    if k < K:
                        scan(i, k)
                    if k:
                        for f in range(FT // 2, FT):
                            h_low(i, k - 1, f)
                    if k < K:
                        add(i, k, 0, ys_done, ys_added)
                        add(i, k, 1, ys_done, ys_added)
                        norm_stats(i, k, 1)
                        norm(i, k, 1)
                    for j, l, q in quarters(k):
                        split_lo(j, i, l, q)
                    if k:
                        add(i, k - 1, 0, yf_done, yf_added)
                    if k < K:
                        low(i, k, 1)
                        low(i, k + 1, 0)
                    if k:
                        add(i, k - 1, 1, yf_done, yf_added)
                    if k == NG or k == K:
                        dve.wait_ge(yf_added, seen(i, k, 2))
                        dve.sem_inc(layer_free, 1)
                for j in range(2):
                    dve.wait_ge(turned[j], seen(i, K, 1))

        @block.tensor
        def _(pe):
            def turn(i, k, j):
                pe.wait_ge(xn_done[j], seen(i, k, 1, 1))
                if k:
                    pe.wait_ge(xhi_done[j], seen(i, k, 1))
                    if j == 0:
                        pe.wait_ge(scan_done, seen(i, k, 1))
                for c in range(KD):
                    for t in range(GT):
                        ins = pe.transpose(pT[j][:, c, t * P:(t + 1) * P], xn[:, j, t, c * P:(c + 1) * P], ident[:])
                ins.then_inc(turned[j], 1)

            def three(out, hi, lo, whi_, wlo_, start, stop):
                pe.matmul(out, hi, whi_, start=start, stop=False)
                pe.matmul(out, hi, wlo_, start=False, stop=False)
                return pe.matmul(out, lo, whi_, start=False, stop=stop)

            def hidden(i, k, f):
                lj = k // NG
                if f >= 2:
                    pe.wait_ge(gelu_done, seen(i, k, FT, f - 1))
                for c in range(KD):
                    x_hi, x_lo = xhi[:, 1, c, :], xlo[:, 1, c, :]
                    pe.matmul(pH[:, f % 2, :], w1v(whi[lj], c, f), x_hi, start=(c == 0), stop=False)
                    pe.matmul(pH[:, f % 2, :], w1v(whi[lj], c, f), x_lo, start=False, stop=False)
                    ins = pe.matmul(pH[:, f % 2, :], w1v(wlo[lj], c, f), x_hi, start=False, stop=(c == KD - 1))
                ins.then_inc(h_done, 1)

            def u(i, k):
                lj = k // NG
                pe.wait_ge(xlo_done[0], seen(i, k, 1, 1))
                for c in range(KD):
                    x_hi, x_lo = xhi[:, 0, c, :], xlo[:, 0, c, :]
                    pe.matmul(pU, wbv(whi[lj], c), x_hi, start=(c == 0), stop=False)
                    pe.matmul(pU, wbv(whi[lj], c), x_lo, start=False, stop=False)
                    ins = pe.matmul(pU, wbv(wlo[lj], c), x_hi, start=False, stop=(c == KD - 1))
                ins.then_inc(u_done, 1)

            def y_state(i, k):
                lj = k // NG
                pe.wait_ge(hstlo_done, seen(i, k, 1, 1))
                for t in range(GT):
                    tok = slice(t * P, (t + 1) * P)
                    if t % 2 == 0 and k >= 2:
                        pe.wait_ge(yf_added, seen(i, k - 2, 2, t // 2 + 1))
                    for c in range(KD):
                        three(pY[:, t, :], xhi[:, 0, c, tok], xlo[:, 0, c, tok], wdv(whi[lj], c), wdv(wlo[lj], c), c == 0, False)
                    ins = three(pY[:, t, :], hst_hi[:, tok], hst_lo[:, tok], whi[lj][:, WC:WB2], wlo[lj][:, WC:WB2], False, True)
                    if t % 2 == 1:
                        ins.then_inc(ys_done, 1)

            def y_ff(i, k, t):
                lj = k // NG
                tok = slice(t * P, (t + 1) * P)
                if t == 0:
                    pe.wait_ge(hlo_done, seen(i, k, FT, FT))
                if t % 2 == 0:
                    pe.wait_ge(ys_added, seen(i, min(k + 1, K - 1), 2, t // 2 + 1))
                pe.matmul(pY[:, t, :], sel[:], whi[lj][:, WB2:WE], start=True, stop=False)
                pe.matmul(pY[:, t, :], sel[:], wlo[lj][:, WB2:WE], start=False, stop=False)
                for f in range(FT):
                    ins = three(pY[:, t, :], hhi[:, f, tok], hlo[:, f, tok], w2v(whi[lj], f), w2v(wlo[lj], f), False, f == FT - 1)
                if t % 2 == 1:
                    ins.then_inc(yf_done, 1)

            pe.wait_ge(consts, 6)
            turn(0, 0, 0)
            with pe.Fori(0, L // 2) as i:
                for k in range(K + 1):
                    if k % NG == 0 and k < K:
                        pe.wait_ge(w_ready, i * (2 * Q) + (k // NG + 1) * Q)
                    if k:
                        pe.wait_ge(xlo_done[1], seen(i, k, 1))
                        for f in range(FT // 2):
                            hidden(i, k - 1, f)
                    if k < K:
                        u(i, k)
                    if k:
                        for f in range(FT // 2, FT):
                            hidden(i, k - 1, f)
                    if k < K:
                        y_state(i, k)
                    if k:
                        for t in range(GT - 1):
                            y_ff(i, k - 1, t)
                    if k < K:
                        turn(i, k, 1)
                        turn(i, k + 1, 0)
                    if k:
                        y_ff(i, k - 1, GT - 1)
                for j in range(2):
                    pe.wait_ge(xhi_done[j], seen(i, K, 1))
                pe.wait_ge(scan_done, seen(i, K, 1))
                pe.wait_ge(yf_added, seen(i, K, 2))


def norm_group(dve, x, mv, rstd, out):
    for t in range(GT):
        ins = dve.tensor_scalar(out[:, t, :], x[:, t, :], mv[:, t, 0:1], rstd[:, t:t + 1], ALU.subtract, ALU.mult)
    return ins


def rotary_attention(nc, a, X, ident, ident16):
    H, HD = 16, D // 16
    PAIRS = H // 2
    T = SEQ // P
    FOUR = 4
    QUADS = H // FOUR
    MU = T * FOUR
    EU = 2 * FOUR * T
    G2 = T // GT
    QH = SEQ // GN
    E1, E2, E3 = 1e-5, 1e-5, 1e-6
    AW = 4 * HD
    MX = 3 * HD
    HK = 2 * H
    UNITS = QUADS * EU
    PARTS = 4
    WHOLE = (1, 4, 7)
    SPLIT = tuple(t for t in range(T) if t not in WHOLE)

    def split(n):
        return n % T in SPLIT

    def splits(n):
        return n // T * len(SPLIT) + sum(t < n % T for t in SPLIT)

    LAG = 4
    LO_LAG = 2
    M_END = 3 * MU // 2
    TURN = (M_END + 4, M_END + 9)
    OUT = LAG + 2
    with ExitStack() as ctx:
        s = Store(nc, ctx, "attn_")
        w_raw = s.sb("w_raw", [P, 3 * D // P + KD, D])
        wq_raw, wp_raw = w_raw[:, 0:3 * D // P, :], w_raw[:, 3 * D // P:, :]
        WQ, WPJ, WBI, WE = np.cumsum([0, KD * 3 * D, KD * D, D]).tolist()
        bias = s.sb("bias", [1, D])
        wThi = s.sb("wThi", [P, WE], F16)
        wTlo = s.sb("wTlo", [P, WE], F16)
        lnf = s.sb("lnf", [P, 2, D])
        gb = s.sb("gb", [P, 2, 2, HD])
        cos = s.sb("cos", [P, T, HD])
        sin = s.sb("sin", [P, T, HD])
        ones16 = s.sb("ones16", [1, P], F16)
        mhalf = s.sb("mhalf", [P, T])
        eps = s.sb("eps", [P, 1])
        stats = s.sb("stats", [P, T, 6])
        mv = s.sb("mv", [P, T, 2])
        var = s.sb("var", [P, T])
        rstd = s.sb("rstd", [P, T])
        xhi = s.sb("xhi", [P, KD, SEQ], F16)
        xlo = s.sb("xlo", [P, KD, SEQ], F16)
        R = 5
        NP = LAG + 2
        arena = s.sb("arena", [P, NP * 2 * GN])
        QKE, WKE, KAE, RTE = np.cumsum([R * HK * HD, 2 * HK * HD, 2 * HK * HD, HK * HD]).tolist()
        xn = arena[:, 0:T * D].rearrange("p (t d) -> p t d", t=T)
        qk = arena[:, 0:QKE].rearrange("p (r h f) -> p r h f", r=R, h=HK)
        work = arena[:, QKE:WKE].rearrange("p (r h f) -> p r h f", r=2, h=HK)
        ka = arena[:, WKE:KAE].bitcast(F16).rearrange("p (r h a f) -> p r h a f", r=2, h=H, a=4)
        rot = arena[:, KAE:RTE].rearrange("p (h f) -> p h f", h=HK)
        prob = arena[:, 0:NP * GN].rearrange("p (n q) -> p n q", n=NP)
        phi, plo = (arena[:, (2 + n) * NP * GN // 2:(3 + n) * NP * GN // 2].bitcast(F16).rearrange("p (n q) -> p n q", n=NP) for n in range(2))
        hsum = s.sb("hsum", [P, R, HK])
        hrs = s.sb("hrs", [P, R, HK])
        qa = s.sb("qa", [P, T, H, 4, HD], F16)
        vhi = s.sb("vhi", [P, len(SPLIT), H, P], F16)
        vlo = s.sb("vlo", [P, len(SPLIT), H, P], F16)
        v32 = s.sb("v32", [P, len(WHOLE), H, P])
        qT = s.sb("qT", [P, H, SEQ], F16)
        kT = s.sb("kT", [P, PAIRS, SEQ], F16)
        mx = s.sb("mx", [P, 2, T, FOUR])
        out_val, out_sum = s.sb("out_val", [P, GN]), s.sb("out_sum", [P, GN])
        attn = w_raw[:].rearrange("p w d -> p (w d)").rearrange("p (c t) -> p c t", c=KD)
        pairs = [s.ps(f"pair{n}", [P, 2, GN]) for n in range(2)]
        bank = [pairs[n // 2][:, n % 2, :] for n in range(4)] + [s.ps(f"bank{n}", [P, GN])[:] for n in range(4, 8)]
        bank16 = [b.bitcast(F16) for b in bank]

        w_in, c_in = s.sem("w_in"), s.sem("c_in")
        consts, w_turned, whi_done, w_ready = (s.sem(n) for n in ("consts", "w_turned", "whi_done", "w_ready"))
        names = ("st1 mv1 va1 rs1 n1 af1 st2 mv2 va2 rs2 xn_done turned xhi_done xlo_done qkv_done qk_copied "
                 "v_copied vlo_done sum_done cen_done sq_done sum2_done hdev_done hrs_done scaled gam_done bet_done rope1 rope_done hi_done "
                 "lo_done turn2 kT_done qT_done m_done mx_done qmx_done mturn mq_done sT_done ka_set exp_done phi_done plo_done av_done out_copied rd_done o_done "
                 "ahi_done alo_done y_done y_added").split()
        m = {n: s.sem(n) for n in names}
        passed = s.sem("passed")
        block = ctx.enter_context(nc.Block())

        def v_view(to, at, tiles, parity, ones):
            half = 64 * (parity ^ ones)
            w = H * P
            return bass.AP(to, at * w + parity * FOUR * P + half, [[tiles * w, P], [2 * FOUR * P, 2], [P + HD, FOUR], [1, HD]])

        def v_high(t, parity, ones):
            if t in SPLIT:
                return v_view(vhi, SPLIT.index(t), len(SPLIT), parity, ones)
            return v_view(v32, WHOLE.index(t), len(WHOLE), parity, ones)

        def seen(i, each, n):
            return i * each + n

        NW = 3 * D // P + KD

        def w_place(w, n):
            to = (w[:, WQ:WPJ] if n < NW - KD else w[:, WPJ:WBI]).rearrange("p (c o) -> p c o", c=KD)
            at = (n if n < NW - KD else n - (NW - KD)) * P
            return to[:, :, at:at + P]

        @block.sync
        def _(sp):
            sp.dma_start(wq_raw, a["L0_attn_w_qkv"].rearrange("(t p) c -> p t c", p=P)).then_inc(w_in, 16)
            sp.dma_start(wp_raw, a["L0_attn_w_proj"].rearrange("(t p) c -> p t c", p=P)).then_inc(w_in, 16)
            sp.dma_start(bias[:], a["L0_attn_b_proj"].rearrange("(o d) -> o d", o=1)).then_inc(w_in, 16)
            sp.dma_start(lnf[:, 0, :], a["L0_tok_lnf_s"].partition_broadcast(P)).then_inc(c_in, 16)
            sp.dma_start(lnf[:, 1, :], a["L0_tok_lnf_b"].partition_broadcast(P)).then_inc(c_in, 16)
            for n, name in enumerate(("q_gamma", "q_beta", "k_gamma", "k_beta")):
                sp.dma_start(gb[:, n % 2, n // 2, :], a["L0_attn_" + name].partition_broadcast(P)).then_inc(c_in, 16)
            sp.dma_start(cos[:], a["c_cos0"].rearrange("(t p) f -> p t f", p=P)).then_inc(c_in, 16)
            sp.dma_start(sin[:], a["c_sin0"].rearrange("(t p) f -> p t f", p=P)).then_inc(c_in, 16)

        @block.gpsimd
        def _(pool):
            pool.memset(ones16[:], 1.0).then_inc(consts, 1)
            pool.memset(eps[:], E3)
            pool.memset(mhalf[:], -0.5).then_inc(consts, 1)
            pool.memset(v32[:], 0.0)
            pool.memset(qT[:].rearrange("p h t -> p (h t)").bitcast(F32), 0.0).then_inc(consts, 1)
            pool.wait_ge(consts, 5)
            for t in range(T):
                for parity in range(2):
                    ins = pool.memset(v_high(t, parity, 1), 1.0)
            ins.then_inc(consts, 1)
            pool.memset(qa[:, :, :, 3, :], 0.0).then_inc(consts, 1)
            wait_apart(pool, passed, c_in, 16 * 8)
            pool.tensor_scalar(gb[:, :, 0, :], gb[:, :, 0, :], float(HD) ** -0.5, None, ALU.mult).then_inc(consts, 1)
            pool.wait_ge(consts, 8)

            def rsqrt(i, eps, mv_done, va, rs):
                wait_apart(pool, passed, m[mv_done], seen(i, 1, 1))
                pool.tensor_scalar(var[:], mv[:, :, 1], eps, None, ALU.add).then_inc(m[va], 1)
                pool.wait_ge(m[va], seen(i, 1, 1))
                pool.tensor_tensor(rstd[:], var[:], mhalf[:], ALU.pow).then_inc(m[rs], 1)

            with pool.Fori(0, BATCH) as i:
                pool.memset(ka[:, :, :, 3, :], 0.0).then_inc(m["ka_set"], 1)
                wait_apart(pool, passed, m["ka_set"], seen(i, 2, 1))
                pool.memset(ka[:, :, :, 3, 0:1], 1.0).then_inc(m["ka_set"], 1)
                rsqrt(i, E1, "mv1", "va1", "rs1")
                rsqrt(i, E2, "mv2", "va2", "rs2")
                for st in range(T + 3):
                    if 2 <= st < T + 2:
                        t = st - 2
                        pool.wait_ge(m["scaled"], seen(i, T, t + 1))
                        for n, step in enumerate(("gam_done", "bet_done")):
                            for j in range(2):
                                part = qk[:, t % R, j * H:(j + 1) * H, :]
                                by = gb[:, n, j, :].unsqueeze(1).to_broadcast([P, H, HD])
                                pool.tensor_tensor(part, part, by, ALU.add if n else ALU.mult).then_inc(m[step], 1)
                            pool.wait_ge(m[step], seen(i, 2 * T, 2 * t + 2))
                wait_apart(pool, passed, m["o_done"], seen(i, 2 * QUADS, 2 * QUADS))

        @block.scalar
        def _(act):
            for n in range(NW):
                act.wait_ge(w_turned, n + 1)
                act.activation(w_place(wThi, n), bank[n % 2][:, 0:KD * P].rearrange("p (c o) -> p c o", c=KD),
                               ACT.Copy, scale=WS).then_inc(whi_done, 1)
            act.wait_ge(w_in, 48)
            act.activation(wThi[0:1, WBI:WE], bias[:], ACT.Copy, scale=WS).then_inc(whi_done, 1)

            def exp(i, n):
                act.wait_ge(m["sT_done"], seen(i, UNITS, n + 1))
                if n >= NP:
                    act.wait_ge(m["av_done"], seen(i, UNITS, n - NP + 1))
                act.activation(prob[:, n % NP, :], bank[4 + n % 2][:], ACT.Exp).then_inc(m["exp_done"], 1)

            def prob_hi(i, n):
                act.wait_ge(m["exp_done"], seen(i, UNITS, n + 1))
                act.activation(phi[:, n % NP, :], prob[:, n % NP, :], ACT.Copy).then_inc(m["phi_done"], 1)

            def turned_q(i, p):
                act.wait_ge(m["mturn"], seen(i, PAIRS, p + 1))
                for h in range(2):
                    r = slice(h * AW, (h + 1) * AW)
                    ins = act.activation(qT[r, 2 * p + h, :], bank16[0][r, :], ACT.Copy)
                ins.then_inc(m["mq_done"], 1)

            def copy_out(i, n):
                d = n // 2
                val, den = slice(64 * (d % 2), 64 * (d % 2) + 64), slice(64 * (1 - d % 2), 64 * (1 - d % 2) + 64)
                act.wait_ge(m["av_done"], seen(i, UNITS, (n + 1) * EU // 2))
                if n:
                    act.wait_ge(m["o_done"], seen(i, 2 * QUADS, n))
                act.activation(out_val[val, :], bank[6 + n % 2][val, :], ACT.Copy)
                act.activation(out_sum[val, :], bank[6 + n % 2][den, :], ACT.Copy).then_inc(m["out_copied"], 1)

            act.wait_ge(consts, 8)
            with act.Fori(0, BATCH) as i:
                act.wait_ge(m["turned"], seen(i, 1, 1))
                for c in range(KD):
                    ins = act.activation(xhi[:, c, :], pairs[c][:].rearrange("p g t -> p (g t)"), ACT.Copy)
                ins.then_inc(m["xhi_done"], 1)
                for st in range(T + 5):
                    if 2 <= st < T + 2:
                        t = st - 2
                        act.wait_ge(m["sum2_done"], seen(i, T, t + 1))
                        act.activation(hsum[:, t % R, :], hsum[:, t % R, :], ACT.Sqrt, scale=1.0 / HD, bias=eps[:]).then_inc(m["hdev_done"], 1)
                    if st < T:
                        t = st
                        act.wait_ge(m["qkv_done"], seen(i, T, t + 1))
                        if t >= R:
                            act.wait_ge(m["lo_done"], seen(i, T, t - R + 1))
                        act.activation(qk[:, t % R, :, :], bank[2 + t % 2][:].rearrange("p (h f) -> p h f", h=HK), ACT.Copy,
                                       scale=1.0 / WS).then_inc(m["qk_copied"], 1)
                        for parity in range(2):
                            src = bank[4][:, 0:D].rearrange("p (a b j f) -> p b a j f", a=2, b=2, j=FOUR)[:, parity]
                            ins = act.activation(v_high(t, parity, 0), src, ACT.Copy, scale=1.0 / WS)
                        ins.then_inc(m["v_copied"], 1)
                    if 1 <= st < T + 1:
                        t = st - 1
                        act.wait_ge(m["cen_done"], seen(i, T, t + 1))
                        act.activation(work[:, t % 2], qk[:, t % R], ACT.Square).then_inc(m["sq_done"], 1)
                    if 3 <= st < T + 3:
                        t = st - 3
                        act.wait_ge(m["rope_done"], seen(i, T, t + 1))
                        if t >= 2:
                            act.wait_ge(m["turn2"], seen(i, 2 * T, 2 * (t - 1)))
                        else:
                            act.wait_ge(m["ka_set"], seen(i, 2, 2))
                        for n in (0, 2):
                            act.activation(qa[:, t, :, n, :], qk[:, t % R, 0:H, :], ACT.Copy)
                        for n in (0, 1):
                            ins = act.activation(ka[:, t % 2, :, n, :], qk[:, t % R, H:HK, :], ACT.Copy)
                        ins.then_inc(m["hi_done"], 1)
                    if 5 <= st < T + 5:
                        t = st - 5
                        act.wait_ge(m["turn2"], seen(i, 2 * T, 2 * t + 1))
                        act.activation(kT[:, :, t * P:(t + 1) * P], bank16[5].rearrange("p (h t) -> p h t", h=PAIRS),
                                       ACT.Copy).then_inc(m["kT_done"], 1)
                        act.wait_ge(m["turn2"], seen(i, 2 * T, 2 * t + 2))
                        for h in range(2):
                            rows = slice(h * AW, (h + 1) * AW)
                            ins = act.activation(qT[rows, h::2, t * P:(t + 1) * P], bank16[6][rows, :].rearrange("p (h t) -> p h t", h=PAIRS), ACT.Copy)
                        ins.then_inc(m["qT_done"], 1)
                turned_q(i, 0)
                turned_q(i, 1)
                for n in range(UNITS + OUT):
                    v = n % EU
                    if n < UNITS:
                        exp(i, n)
                    if 1 <= n < UNITS + 1 and split(n - 1):
                        prob_hi(i, n - 1)
                    if n < UNITS - EU and v - 2 in TURN:
                        turned_q(i, 2 * (n // EU + 1) + TURN.index(v - 2))
                    if n >= EU // 2 and (n - OUT + 1) % (EU // 2) == 0:
                        copy_out(i, (n - OUT + 1) // (EU // 2) - 1)
                for g in range(G2):
                    act.wait_ge(m["o_done"], seen(i, 2 * QUADS, 2 * QUADS))
                    for c in range(KD):
                        ins = act.activation(xhi[:, c, g * GN:(g + 1) * GN], attn[:, c, g * GN:(g + 1) * GN], ACT.Copy)
                    ins.then_inc(m["ahi_done"], 1)
                act.wait_ge(m["y_done"], seen(i, 2 * G2, 2 * G2))

        @block.vector
        def _(dve):
            def query_max(i, d, n):
                dve.wait_ge(m["m_done"], seen(i, QUADS * MU, d * MU + n + 1))
                dve.tensor_reduce(mx[:, d % 2, n // FOUR, n % FOUR:n % FOUR + 1], pairs[n % 2][:], AX.XY, ALU.max).then_inc(m["mx_done"], 1)

            for v in (vhi, vlo):
                dve.memset(v[:].rearrange("p t h c -> p (t h c)").bitcast(F32), 0.0).then_inc(consts, 1)
            for n in range(NW):
                dve.wait_ge(whi_done, n + 1)
                dve.scalar_tensor_tensor(out=w_place(wTlo, n), in0=bank[n % 2][:, 0:KD * P].rearrange("p (c o) -> p c o", c=KD), scalar=WS,
                                         in1=w_place(wThi, n), op0=ALU.mult, op1=ALU.subtract).then_inc(w_ready, 1)
            dve.wait_ge(whi_done, NW + 1)
            dve.scalar_tensor_tensor(out=wTlo[0:1, WBI:WE], in0=bias[:], scalar=WS, in1=wThi[0:1, WBI:WE],
                                     op0=ALU.mult, op1=ALU.subtract).then_inc(w_ready, 1)
            dve.wait_ge(consts, 8)
            dve.wait_ge(c_in, 16 * 8)
            with dve.Fori(0, BATCH) as i:
                xg = X[:, bass.ds(i * T, T), :]

                def xt(t):
                    return X[:, bass.ds(i * T + t, 1), :]

                def stats_of(st, n):
                    for t in range(T):
                        ins = dve.bn_stats(stats[:, t, :], xt(t))
                    ins.then_inc(m[st], 1)
                    wait_apart(dve, passed, m[st], seen(i, 1, 1))
                    for t in range(T):
                        ins = dve.bn_aggr(mv[:, t, :], stats[:, t, :])
                    ins.then_inc(m[n], 1)

                stats_of("st1", "mv1")
                dve.wait_ge(m["rs1"], seen(i, 1, 1))
                for t in range(T):
                    ins = dve.tensor_scalar(xt(t), xt(t), mv[:, t, 0:1], rstd[:, t:t + 1], ALU.subtract, ALU.mult)
                ins.then_inc(m["n1"], 1)
                dve.wait_ge(m["n1"], seen(i, 1, 1))
                for n, op in ((0, ALU.mult), (1, ALU.add)):
                    dve.tensor_tensor(xg, xg, lnf[:, n, :].unsqueeze(1).to_broadcast([P, T, D]), op).then_inc(m["af1"], 1)
                    wait_apart(dve, passed, m["af1"], seen(i, 2, n + 1))
                stats_of("st2", "mv2")
                dve.wait_ge(m["rs2"], seen(i, 1, 1))
                for t in range(T):
                    ins = dve.tensor_scalar(xn[:, t, :], xt(t), mv[:, t, 0:1], rstd[:, t:t + 1], ALU.subtract, ALU.mult)
                ins.then_inc(m["xn_done"], 1)
                dve.wait_ge(m["xhi_done"], seen(i, 1, 1))
                for c in range(KD):
                    ins = dve.tensor_tensor(xlo[:, c, :], pairs[c][:].rearrange("p g t -> p (g t)"), xhi[:, c, :], ALU.subtract)
                ins.then_inc(m["xlo_done"], 1)
                for st in range(T + 5):
                    if st < T:
                        t = st
                        q = qk[:, t % R]
                        dve.wait_ge(m["qk_copied"], seen(i, T, t + 1))
                        dve.tensor_reduce(hsum[:, t % R, :], q, AX.X, ALU.add).then_inc(m["sum_done"], 1)
                        for parity in range(2) if t in SPLIT else ():
                            dve.wait_ge(m["v_copied"], seen(i, T, t + 1))
                            src = bank[4][:, 0:D].rearrange("p (a b j f) -> p b a j f", a=2, b=2, j=FOUR)[:, parity]
                            hi, lo = v_high(t, parity, 0), v_view(vlo, SPLIT.index(t), len(SPLIT), parity, 0)
                            for n in range(2):
                                ins = dve.scalar_tensor_tensor(out=lo[:, n], in0=src[:, n], scalar=1.0 / WS, in1=hi[:, n],
                                                               op0=ALU.mult, op1=ALU.subtract)
                        if t in SPLIT:
                            ins.then_inc(m["vlo_done"], 1)
                        dve.wait_ge(m["sum_done"], seen(i, T, t + 1))
                        dve.scalar_tensor_tensor(out=q, in0=hsum[:, t % R, :].unsqueeze(2).to_broadcast([P, HK, HD]), scalar=-1.0 / HD, in1=q,
                                                 op0=ALU.mult, op1=ALU.add).then_inc(m["cen_done"], 1)
                    if 1 <= st < T + 1:
                        t = st - 1
                        dve.wait_ge(m["sq_done"], seen(i, T, t + 1))
                        dve.tensor_reduce(hsum[:, t % R, :], work[:, t % 2], AX.X, ALU.add).then_inc(m["sum2_done"], 1)
                    if 2 <= st < T + 2:
                        t = st - 2
                        q = qk[:, t % R]
                        dve.wait_ge(m["hdev_done"], seen(i, T, t + 1))
                        dve.reciprocal(hrs[:, t % R, :], hsum[:, t % R, :]).then_inc(m["hrs_done"], 1)
                        dve.wait_ge(m["hrs_done"], seen(i, T, t + 1))
                        dve.tensor_tensor(q, q, hrs[:, t % R, :].unsqueeze(2).to_broadcast([P, HK, HD]), ALU.mult).then_inc(m["scaled"], 1)
                    if 3 <= st < T + 3:
                        t = st - 3
                        q = qk[:, t % R]
                        dve.wait_ge(m["bet_done"], seen(i, 2 * T, 2 * t + 2))
                        if t:
                            dve.wait_ge(m["rope_done"], seen(i, T, t))
                        half = HD // 2
                        for n in range(2):
                            to, frm = slice(n * half, (n + 1) * half), slice((1 - n) * half, (2 - n) * half)
                            ins = dve.tensor_tensor(rot[:, :, to], q[:, :, frm], sin[:, t, to].unsqueeze(1).to_broadcast([P, HK, half]), ALU.mult)
                        ins.then_inc(m["rope1"], 1)
                        dve.wait_ge(m["rope1"], seen(i, 2 * T, 2 * t + 1))
                        dve.tensor_tensor(q, q, cos[:, t, :].unsqueeze(1).to_broadcast([P, HK, HD]), ALU.mult).then_inc(m["rope1"], 1)
                        dve.wait_ge(m["rope1"], seen(i, 2 * T, 2 * t + 2))
                        dve.tensor_tensor(q, q, rot[:], ALU.add).then_inc(m["rope_done"], 1)
                    if 4 <= st < T + 4:
                        t = st - 4
                        dve.wait_ge(m["hi_done"], seen(i, T, t + 1))
                        dve.tensor_tensor(qa[:, t, :, 1, :], qk[:, t % R, 0:H, :], qa[:, t, :, 0, :], ALU.subtract)
                        dve.tensor_tensor(ka[:, t % 2, :, 2, :], qk[:, t % R, H:HK, :], ka[:, t % 2, :, 0, :], ALU.subtract).then_inc(m["lo_done"], 1)

                def new_rows(d):
                    dve.wait_ge(m["mx_done"], seen(i, QUADS * MU, (d + 1) * MU))
                    dve.tensor_scalar(qa[:, :, FOUR * d:FOUR * (d + 1), 3, 0], mx[:, d % 2], -1.0, None, ALU.mult).then_inc(m["qmx_done"], 1)

                for n in range(MU):
                    query_max(i, 0, n)
                new_rows(0)
                for n in range(UNITS + OUT + PARTS + 1):
                    d, v = n // EU, n % EU
                    at, part = (n - OUT) // (EU // 2) - 1, (n - OUT) % (EU // 2)
                    if at >= 0 and part <= PARTS:
                        val = slice(64 * (at // 2 % 2), 64 * (at // 2 % 2) + 64)
                        if part < PARTS:
                            dve.wait_ge(m["out_copied"], seen(i, 2 * QUADS, at + 1))
                            c = slice(part * GN // PARTS, (part + 1) * GN // PARTS)
                            dve.reciprocal(out_sum[val, c], out_sum[val, c]).then_inc(m["rd_done"], 1)
                        else:
                            dve.wait_ge(m["rd_done"], seen(i, 2 * QUADS * PARTS, (at + 1) * PARTS))
                            dve.tensor_tensor(attn[val, at // 4, at % 2 * GN:(at % 2 + 1) * GN], out_val[val, :], out_sum[val, :],
                                              ALU.mult).then_inc(m["o_done"], 1)
                    if LO_LAG <= n < UNITS + LO_LAG and split(n - LO_LAG):
                        u = n - LO_LAG
                        dve.wait_ge(m["phi_done"], seen(i, splits(UNITS), splits(u + 1)))
                        dve.tensor_tensor(plo[:, u % NP, :], prob[:, u % NP, :], phi[:, u % NP, :], ALU.subtract).then_inc(m["plo_done"], 1)
                    if d + 1 < QUADS and v < M_END and v % 3 != 2:
                        query_max(i, d + 1, v - (v + 1) // 3)
                    if d + 1 < QUADS and v == M_END:
                        new_rows(d + 1)
                for g in range(G2):
                    dve.wait_ge(m["ahi_done"], seen(i, G2, g + 1))
                    for c in range(KD):
                        t = slice(g * GN, (g + 1) * GN)
                        ins = dve.tensor_tensor(xlo[:, c, t], attn[:, c, t], xhi[:, c, t], ALU.subtract)
                    ins.then_inc(m["alo_done"], 1)
                    for half in range(2):
                        dve.wait_ge(m["y_done"], seen(i, 2 * G2, 2 * g + half + 1))
                        x = X[:, bass.ds(i * T + (g * GT + 2 * half), 2), :]
                        dve.scalar_tensor_tensor(out=x, in0=bank[2 + half][:].rearrange("p (t d) -> p t d", t=2), scalar=1.0 / WS, in1=x,
                                                 op0=ALU.mult, op1=ALU.add).then_inc(m["y_added"], 1)

        @block.tensor
        def _(pe):
            pe.wait_ge(w_in, 48)
            for n in range(NW):
                src = wq_raw[:, n, :] if n < NW - KD else wp_raw[:, n - (NW - KD), :]
                if n >= 2:
                    pe.wait_ge(w_ready, n - 1)
                for c in range(KD):
                    ins = pe.transpose(bank[n % 2][:, c * P:(c + 1) * P], src[:, c * P:(c + 1) * P], ident[:])
                ins.then_inc(w_turned, 1)
            pe.wait_ge(consts, 8)
            pe.wait_ge(w_ready, NW + 1)
            wq_h = wThi[:, WQ:WPJ].rearrange("p (c o) -> p c o", c=KD)
            wq_l = wTlo[:, WQ:WPJ].rearrange("p (c o) -> p c o", c=KD)
            wp_h = wThi[:, WPJ:WBI].rearrange("p (c o) -> p c o", c=KD)
            wp_l = wTlo[:, WPJ:WBI].rearrange("p (c o) -> p c o", c=KD)

            def dense(out, tok, w_h, w_l, cols, start=True):
                for c in range(KD):
                    pe.matmul(out, xhi[:, c, tok], w_h[:, c, cols], start=start and c == 0, stop=False)
                    pe.matmul(out, xhi[:, c, tok], w_l[:, c, cols], start=False, stop=False)
                    ins = pe.matmul(out, xlo[:, c, tok], w_h[:, c, cols], start=False, stop=c == KD - 1)
                return ins

            def max_scores(i, d, n):
                t, h = n // FOUR, FOUR * d + n % FOUR
                if d or n >= 2:
                    pe.wait_ge(m["mx_done"], seen(i, QUADS * MU, d * MU + n - 1))
                if d and n == 0:
                    pe.wait_ge(m["mq_done"], seen(i, PAIRS, 2 * d))
                for half in range(2):
                    ins = pe.matmul(pairs[n % 2][:, half, :], qT[:, h, t * P:(t + 1) * P], kT[:, h // 2, half * GN:(half + 1) * GN],
                                    start=True, stop=True)
                ins.then_inc(m["m_done"], 1)

            def turn_q(i, p):
                pe.wait_ge(m["qmx_done"], seen(i, QUADS, p // 2 + 1))
                if p:
                    pe.wait_ge(m["mq_done"], seen(i, PAIRS, p))
                for t in range(T):
                    ins = pe.transpose(bank16[0][:, t * P:(t + 1) * P], qa[:, t, 2 * p:2 * p + 2, :, :].rearrange("p h a f -> p (h a f)"), ident16[:])
                ins.then_inc(m["mturn"], 1)

            def scores(i, n):
                d, half, h, kt = n // EU, n // (EU // 2) % 2, n // T % FOUR, n % T
                h += FOUR * d
                if n % EU == 0:
                    pe.wait_ge(m["mq_done"], seen(i, PAIRS, 2 * d + 2))
                if n >= 2:
                    pe.wait_ge(m["exp_done"], seen(i, UNITS, n - 1))
                pe.matmul(bank[4 + n % 2], kT[:, h // 2, kt * P:(kt + 1) * P], qT[:, h, half * GN:(half + 1) * GN],
                          start=True, stop=True).then_inc(m["sT_done"], 1)

            def values(i, n):
                d, h, kt = n // EU, n // T % FOUR, n % T
                first, last = n % (EU // 2) == 0, n % (EU // 2) == EU // 2 - 1
                at = n // (EU // 2)
                if first and at >= 2:
                    pe.wait_ge(m["out_copied"], seen(i, 2 * QUADS, at - 1))
                out, head = bank[6 + at % 2], FOUR * d + h
                if not split(n):
                    pe.wait_ge(m["exp_done"], seen(i, UNITS, n + 1))
                    pe.matmul(out, v32[:, WHOLE.index(kt), head, :], prob[:, n % NP, :], start=first, stop=last).then_inc(m["av_done"], 1)
                    return
                pe.wait_ge(m["plo_done"], seen(i, splits(UNITS), splits(n + 1)))
                v_h, v_l = vhi[:, SPLIT.index(kt), head, :], vlo[:, SPLIT.index(kt), head, :]
                pe.matmul(out, v_h, phi[:, n % NP, :], start=first, stop=False)
                pe.matmul(out, v_l, phi[:, n % NP, :], start=False, stop=False)
                pe.matmul(out, v_h, plo[:, n % NP, :], start=False, stop=last).then_inc(m["av_done"], 1)

            with pe.Fori(0, BATCH) as i:
                pe.wait_ge(m["xn_done"], seen(i, 1, 1))
                for c in range(KD):
                    for t in range(T):
                        ins = pe.transpose(pairs[c][:, t // GT, t % GT * P:(t % GT + 1) * P], xn[:, t, c * P:(c + 1) * P], ident[:])
                ins.then_inc(m["turned"], 1)
                pe.wait_ge(m["xlo_done"], seen(i, 1, 1))
                for st in range(T + 5):
                    if st < T:
                        t = st
                        if t >= 2:
                            pe.wait_ge(m["qk_copied"], seen(i, T, t - 1))
                        tok = slice(st * P, (st + 1) * P)
                        dense(bank[2 + t % 2], tok, wq_h, wq_l, slice(0, 2 * D))
                        if t:
                            pe.wait_ge(m["v_copied"], seen(i, T, t))
                            pe.wait_ge(m["vlo_done"], seen(i, len(SPLIT), splits(t)))
                        dense(bank[4][:, 0:D], tok, wq_h, wq_l, slice(2 * D, 3 * D)).then_inc(m["qkv_done"], 1)
                    if 5 <= st:
                        t = st - 5
                        pe.wait_ge(m["lo_done"], seen(i, T, t + 1))
                        if t:
                            pe.wait_ge(m["kT_done"], seen(i, T, t))
                            pe.wait_ge(m["qT_done"], seen(i, T, t))
                        for src, b in ((ka[:, t % 2], 5), (qa[:, t], 6)):
                            for p in range(PAIRS):
                                ins = pe.transpose(bank16[b][:, p * P:(p + 1) * P], src[:, 2 * p:2 * p + 2, :, :].rearrange("p h a f -> p (h a f)"), ident16[:])
                            ins.then_inc(m["turn2"], 1)
                pe.wait_ge(m["v_copied"], seen(i, T, T))
                pe.wait_ge(m["vlo_done"], seen(i, len(SPLIT), len(SPLIT)))
                pe.wait_ge(m["kT_done"], seen(i, T, T))
                pe.wait_ge(m["qT_done"], seen(i, T, T))
                for n in range(MU):
                    max_scores(i, 0, n)
                turn_q(i, 0)
                turn_q(i, 1)
                for n in range(UNITS + LAG):
                    d, v = n // EU, n % EU
                    if n < UNITS:
                        scores(i, n)
                    if d + 1 < QUADS:
                        if v < M_END and v % 3 != 2:
                            max_scores(i, d + 1, v - (v + 1) // 3)
                        if v in TURN:
                            turn_q(i, 2 * (d + 1) + TURN.index(v))
                    if n >= LAG:
                        values(i, n - LAG)
                for g in range(G2):
                    pe.wait_ge(m["alo_done"], seen(i, G2, g + 1))
                    for t in range(GT):
                        y = bank[2 + t // 2][:, (t % 2) * D:(t % 2 + 1) * D]
                        if g and t % 2 == 0:
                            pe.wait_ge(m["y_added"], seen(i, 2 * G2, 2 * (g - 1) + t // 2 + 1))
                        pe.matmul(y, ones16[:], wThi[0:1, WBI:WE], start=True, stop=False)
                        pe.matmul(y, ones16[:], wTlo[0:1, WBI:WE], start=False, stop=False)
                        ins = dense(y, slice((g * GT + t) * P, (g * GT + t + 1) * P), wp_h, wp_l, slice(0, D), start=False)
                        if t % 2:
                            ins.then_inc(m["y_done"], 1)
                pe.wait_ge(m["y_added"], seen(i, 2 * G2, 2 * G2))


def gated_experts(nc, a, X, ident):
    gate, E, F = a["L1_ffn_Wg"], a["L1_ffn_W1"].shape[0], a["L1_ffn_W1"].shape[2]
    FT = F // P
    EPS = 1e-5
    WU, WDN, WE = np.cumsum([0, KD * F, FT * D]).tolist()
    QC = WE // NG
    HALF = 2.0 ** -23
    with ExitStack() as ctx:
        s = Store(nc, ctx, "moe1_")
        raw = s.sb("e_raw", [P, WE])
        whi = [s.sb(f"e_hi{j}", [P, WE], F16) for j in range(2)]
        wlo = [s.sb(f"e_lo{j}", [P, WE], F16) for j in range(2)]
        g_raw = s.sb("g_raw", [P, KD, E])
        g_hi = s.sb("g_hi", [P, KD, E], F16)
        g_lo = s.sb("g_lo", [P, KD, E], F16)
        bg = s.sb("bg", [P, E])
        stats = s.sb("stats", [P, GT, 6])
        mv = s.sb("mv", [P, GT, 2])
        var = s.sb("var", [P, GT])
        rstd = s.sb("rstd", [P, GT])
        mhalf = s.sb("mhalf", [P, GT])
        xn = s.sb("xn", [P, 2, GT, D])
        xhi = s.sb("xhi", [P, KD, N], F16)
        xlo = s.sb("xlo", [P, KD, N], F16)
        logit = s.sb("logit", [P, NT, E])
        prob = s.sb("prob", [P, NT, E])
        we = s.sb("we", [P, NT, E])
        b1 = s.sb("b1", [P, E, FT])
        b2r = s.sb("b2r", [P, E, D])
        b2s = s.sb("b2s", [P, E, D], F16)
        sel = s.sb("sel", [P, P], F16)
        NH = 3
        hf = s.sb("hf", [P, NH, GN])
        hhi = s.sb("hhi", [P, 2, FT, GN], F16)
        hlo = s.sb("hlo", [P, 2, FT, GN], F16)
        pH = s.ps("pH", [P, 2, GN])
        pT = [s.ps(f"pT{j}", [P, KD, GN]) for j in range(2)]
        pY = s.ps("pY", [P, GT, D])
        pL = pY[:, 0:2, :].rearrange("p t d -> p (t d)")[:, 0:NT * E].rearrange("p (t e) -> p t e", e=E)

        names = ("w_in c_in g_in consts st mvd va rs xn_done turned xhi_done xlo_done g_split logits pre_w steps asteps we_ready "
                 "whi_done wlo_done h_done hf_done hhi_done hlo_done y_done y_added bias_done").split()
        m = {n: s.sem(n) for n in names}
        passed = s.sem("passed")
        block = ctx.enter_context(nc.Block())
        K = 2 * NG
        NWD = 2

        def seen(i, k, each, plus=0):
            return i * (K * each) + (k * each + plus)

        def loop(eng, body):
            with eng.Fori(0, E // 2 - 1) as i:
                body(i, False)
            body(E // 2 - 1, True)

        @block.sync
        def _(sp):
            def load(e):
                def row(name):
                    return a[name][bass.ds(e, 1)]
                for at, c, f, name in ((WU, KD, F, "L1_ffn_W1"), (WDN, FT, D, "L1_ffn_W2")):
                    sp.dma_start(raw[:, at:at + c * f].rearrange("p (c f) -> p c f", c=c),
                                 row(name).rearrange("o (c p) f -> p (o c) f", p=P)).then_inc(m["w_in"], 16)

            with nc.allow_non_contiguous_dma(reason="small parameters"):
                sp.dma_start(g_raw[:], gate.rearrange("(c p) e -> p c e", p=P)).then_inc(m["g_in"], 16)
                sp.dma_start(bg[:], a["L1_ffn_bg"].partition_broadcast(P)).then_inc(m["c_in"], 16)
                sp.dma_start(b1[:], a["L1_ffn_b1"].rearrange("e (c p) -> p e c", p=P)).then_inc(m["c_in"], 16)
                for r in (0, 32):
                    sp.dma_start(b2r[r:r + 1], a["L1_ffn_b2"].rearrange("(o e) d -> o e d", o=1)).then_inc(m["c_in"], 16)
            load(0)
            sp.wait_ge(m["wlo_done"], NG)
            load(1)

            def body(i, last):
                for j in range(0 if last else 2):
                    sp.wait_ge(m["wlo_done"], i * (2 * NG) + (j + 2) * NG)
                    load(i * 2 + (j + 2))
            loop(sp, body)

        @block.gpsimd
        def _(pool):
            pool.memset(mhalf[:], -0.5).then_inc(m["consts"], 1)
            pool.memset(sel[:], 0.0).then_inc(m["consts"], 1)
            pool.memset(b2s[:], 0.0).then_inc(m["consts"], 1)
            pool.wait_ge(m["consts"], 3)
            for r in (0, 32):
                ins = pool.memset(sel[r:r + 1, :], 1.0)
            ins.then_inc(m["consts"], 1)
            pool.wait_ge(m["consts"], 4)
            for g in range(NG):
                wait_apart(pool, passed, m["mvd"], g + 1)
                pool.tensor_scalar(var[:], mv[:, :, 1], EPS, None, ALU.add).then_inc(m["va"], 1)
                pool.wait_ge(m["va"], g + 1)
                pool.tensor_tensor(rstd[:], var[:], mhalf[:], ALU.pow).then_inc(m["rs"], 1)

        @block.scalar
        def _(act):
            def split_hi(e_at, j, q):
                act.wait_ge(m["w_in"], e_at[0])
                act.activation(whi[j][:, q * QC:(q + 1) * QC], raw[:, q * QC:(q + 1) * QC], ACT.Copy, scale=WS).then_inc(m["whi_done"], 1)

            for q in range(NG):
                split_hi((16 * NWD,), 0, q)
            act.wait_ge(m["g_in"], 16)
            act.activation(g_hi[:], g_raw[:], ACT.Copy, scale=WS).then_inc(m["g_split"], 1)
            for g in range(NG):
                act.wait_ge(m["turned"], g + 1)
                for c in range(KD):
                    ins = act.activation(xhi[:, c, g * GN:(g + 1) * GN], pT[g % len(pT)][:, c, :], ACT.Copy)
                ins.then_inc(m["xhi_done"], 1)
            act.wait_ge(m["pre_w"], 1)
            act.activation(prob[:], logit[:], ACT.Sigmoid).then_inc(m["asteps"], 1)

            def body(i, last):
                for k in range(K):
                    e, g, n = k // NG, k % NG, k % 2
                    for f in range(FT):
                        act.wait_ge(m["h_done"], seen(i, k, FT, f + 1))
                        if k or f >= NH:
                            wait_apart(act, passed, m["hlo_done"], seen(i, k, FT, max(f - NH + 1, 0)))
                        else:
                            act.sem_inc(passed, 1)
                        act.activation(hf[:, f % NH, :], pH[:, f % 2, :], ACT.Relu, scale=1.0 / WS,
                                       bias=b1[:, bass.ds(i * 2 + e, 1), f]).then_inc(m["hf_done"], 1)
                        if f == 0 and not (last and e):
                            split_hi((i * (2 * 16 * NWD) + (e + 2) * 16 * NWD,), (e + 1) % 2, g)
                        act.wait_ge(m["hf_done"], seen(i, k, FT, f + 1))
                        if f == 0:
                            if k >= 2:
                                act.wait_ge(m["y_done"], seen(i, k - 1, 2))
                        act.activation(hhi[:, n, f, :], hf[:, f % NH, :], ACT.Copy).then_inc(m["hhi_done"], 1)
                act.wait_ge(m["hlo_done"], seen(i, K, FT))
                act.wait_ge(m["y_done"], seen(i, K, 2))
            loop(act, body)

        @block.vector
        def _(dve):
            def split_lo(at, j, q):
                dve.wait_ge(m["whi_done"], at)
                c = slice(q * QC, (q + 1) * QC)
                dve.scalar_tensor_tensor(out=wlo[j][:, c], in0=raw[:, c], scalar=WS, in1=whi[j][:, c], op0=ALU.mult,
                                         op1=ALU.subtract).then_inc(m["wlo_done"], 1)

            dve.wait_ge(m["consts"], 4)
            for g in range(NG + 1):
                if g < NG:
                    layer_stats(dve, passed, X[:, g * GT:(g + 1) * GT, :], stats, mv, m["st"], g).then_inc(m["mvd"], 1)
                    dve.wait_ge(m["rs"], g + 1)
                    if g >= 2:
                        dve.wait_ge(m["turned"], g - 1)
                    norm_group(dve, X[:, g * GT:(g + 1) * GT, :], mv, rstd, xn[:, g % 2]).then_inc(m["xn_done"], 1)
                if g:
                    dve.wait_ge(m["xhi_done"], g)
                    for c in range(KD):
                        t = slice((g - 1) * GN, g * GN)
                        ins = dve.tensor_tensor(xlo[:, c, t], pT[(g - 1) % len(pT)][:, c, :], xhi[:, c, t], ALU.subtract)
                    ins.then_inc(m["xlo_done"], 1)
            for q in range(NG):
                split_lo(q + 1, 0, q)
            dve.wait_ge(m["g_split"], 1)
            dve.scalar_tensor_tensor(out=g_lo[:], in0=g_raw[:], scalar=WS, in1=g_hi[:], op0=ALU.mult,
                                     op1=ALU.subtract).then_inc(m["g_split"], 1)
            count = [0]

            def step(ins):
                count[0] += 1
                ins.then_inc(m["steps"], 1)
                dve.wait_ge(m["steps"], count[0])

            dve.wait_ge(m["logits"], 1)
            dve.wait_ge(m["c_in"], 64)
            step(dve.tensor_scalar(logit[:], pL, 1.0 / WS, None, ALU.mult))
            dve.tensor_tensor(logit[:], logit[:], bg[:].unsqueeze(1).to_broadcast([P, NT, E]), ALU.add).then_inc(m["pre_w"], 1)
            dve.wait_ge(m["asteps"], 1)
            step(dve.scalar_tensor_tensor(out=we[:], in0=logit[:], scalar=HALF, in1=prob[:], op0=ALU.is_gt, op1=ALU.mult))
            for r in (0, 32):
                ins = dve.tensor_scalar(b2r[r:r + 1], b2r[r:r + 1], WS, None, ALU.mult)
            step(ins)
            for r in (0, 32):
                ins = dve.tensor_copy(b2s[r:r + 1], b2r[r:r + 1])
            step(ins)
            dve.tensor_tensor(b2s[32:33], b2r[32:33], b2s[32:33], ALU.subtract).then_inc(m["bias_done"], 1)
            step(dve.tensor_scalar(we[:], we[:], 1.0 / WS, None, ALU.mult))

            def body(i, last):
                def add(k):
                    e, g = k // NG, k % NG
                    for t in range(GT):
                        if t % 2 == 0:
                            dve.wait_ge(m["y_done"], seen(i, k, 2, t // 2 + 1))
                        x = X[:, g * GT + t, :]
                        ins = dve.scalar_tensor_tensor(out=x, in0=pY[:, t, :], scalar=we[:, g * GT + t, bass.ds(i * 2 + e, 1)], in1=x,
                                                       op0=ALU.mult, op1=ALU.add)
                        if t % 2 == 1:
                            ins.then_inc(m["y_added"], 1)

                for k in range(K):
                    e, g, n = k // NG, k % NG, k % 2
                    for f in range(FT):
                        if f == 0 and k:
                            add(k - 1)
                        if f == 1 and not (last and e):
                            split_lo(i * (2 * NG) + (e + 1) * NG + g + 1, (e + 1) % 2, g)
                        dve.wait_ge(m["hhi_done"], seen(i, k, FT, f + 1))
                        dve.tensor_tensor(hlo[:, n, f, :], hf[:, f % NH, :], hhi[:, n, f, :], ALU.subtract).then_inc(m["hlo_done"], 1)
                add(K - 1)
                dve.wait_ge(m["hlo_done"], seen(i, K, FT))
            loop(dve, body)

        @block.tensor
        def _(pe):
            pe.wait_ge(m["consts"], 4)
            for g in range(NG):
                pe.wait_ge(m["xn_done"], g + 1)
                if g >= len(pT):
                    pe.wait_ge(m["xlo_done"], g + 1 - len(pT))
                for c in range(KD):
                    for t in range(GT):
                        ins = pe.transpose(pT[g % len(pT)][:, c, t * P:(t + 1) * P], xn[:, g % 2, t, c * P:(c + 1) * P], ident[:])
                ins.then_inc(m["turned"], 1)
            pe.wait_ge(m["xlo_done"], NG)
            pe.wait_ge(m["g_split"], 2)
            for t in range(NT):
                tok = slice(t * P, (t + 1) * P)
                for c in range(KD):
                    pe.matmul(pL[:, t, :], xhi[:, c, tok], g_hi[:, c, :], start=(c == 0), stop=False)
                    pe.matmul(pL[:, t, :], xhi[:, c, tok], g_lo[:, c, :], start=False, stop=False)
                    ins = pe.matmul(pL[:, t, :], xlo[:, c, tok], g_hi[:, c, :], start=False, stop=(c == KD - 1))
            ins.then_inc(m["logits"], 1)
            pe.wait_ge(m["pre_w"], 1)
            pe.wait_ge(m["bias_done"], 1)

            def body(i, last):
                for k in range(K):
                    e, g, n = k // NG, k % NG, k % 2
                    if g == 0:
                        pe.wait_ge(m["wlo_done"], i * (2 * NG) + (e + 1) * NG)
                    tok = slice(g * GN, (g + 1) * GN)
                    for f in range(FT):
                        if k or f >= 2:
                            pe.wait_ge(m["hf_done"], seen(i, k, FT, max(f - 1, 0)))
                        out = pH[:, f % 2, :]
                        for c in range(KD):
                            at = WU + c * F + f * P
                            w_h, w_l = whi[e][:, at:at + P], wlo[e][:, at:at + P]
                            pe.matmul(out, w_h, xhi[:, c, tok], start=(c == 0), stop=False)
                            pe.matmul(out, w_h, xlo[:, c, tok], start=False, stop=False)
                            ins = pe.matmul(out, w_l, xhi[:, c, tok], start=False, stop=(c == KD - 1))
                        ins.then_inc(m["h_done"], 1)
                    if k:
                        pe.wait_ge(m["y_added"], seen(i, k, 2))
                    for t in range(GT):
                        pe.matmul(pY[:, t, :], sel[:], b2s[:, bass.ds(i * 2 + e, 1), :].rearrange("p o d -> p (o d)"),
                                  start=(t % 2 == 0), stop=False, skip_group_check=True)
                    for f in range(FT):
                        pe.wait_ge(m["hlo_done"], seen(i, k, FT, f + 1))
                        w = slice(WDN + f * D, WDN + (f + 1) * D)
                        for t in range(GT):
                            ts = slice(t * P, (t + 1) * P)
                            pe.matmul(pY[:, t, :], hhi[:, n, f, ts], whi[e][:, w], start=False, stop=False,
                                      skip_group_check=True)
                            pe.matmul(pY[:, t, :], hhi[:, n, f, ts], wlo[e][:, w], start=False, stop=False, skip_group_check=True)
                            ins = pe.matmul(pY[:, t, :], hlo[:, n, f, ts], whi[e][:, w], start=False, stop=(f == FT - 1 and t % 2 == 1),
                                            skip_group_check=True)
                            if f == FT - 1 and t % 2 == 1:
                                ins.then_inc(m["y_done"], 1)
                pe.wait_ge(m["hf_done"], seen(i, K, FT))
                pe.wait_ge(m["y_added"], seen(i, K, 2))
            loop(pe, body)


def routed_experts(nc, a, X, ident, rows_x, rows_y, slots):
    gate, E, F = a["L0_ffn_w_gate"], a["L0_ffn_w_gate_proj"].shape[0], a["L0_ffn_w_gate_proj"].shape[2]
    FT = F // P
    FP = FT // 2
    EPS = 1e-5
    CH = 2
    ST = SLOTS // P
    NS = slots // SLOTS
    UPW = 2 * KD * F
    DNW = FT * D
    FULL = CH * N // SLOTS
    with ExitStack() as ctx:
        s = Store(nc, ctx, "moe0_")
        up_raw = [s.sb(f"up_raw{j}", [P, UPW]) for j in range(2)]
        up_hi = [s.sb(f"up_hi{j}", [P, UPW], F16) for j in range(2)]
        up_lo = [s.sb(f"up_lo{j}", [P, UPW], F16) for j in range(2)]
        dn_raw = [s.sb(f"dn_raw{j}", [P, DNW]) for j in range(2)]
        dn_hi = [s.sb(f"dn_hi{j}", [P, DNW], F16) for j in range(2)]
        dn_lo = [s.sb(f"dn_lo{j}", [P, DNW], F16) for j in range(2)]
        g_raw = s.sb("g_raw", [P, KD, E])
        g_hi = s.sb("g_hi", [P, KD, E], F16)
        g_lo = s.sb("g_lo", [P, KD, E], F16)
        iota = s.sb("iota", [P, NS])
        stats = s.sb("stats", [P, GT, 6])
        mv = s.sb("mv", [P, GT, 2])
        var = s.sb("var", [P, GT])
        rstd = s.sb("rstd", [P, GT])
        mhalf = s.sb("mhalf", [P, GT])
        xn = s.sb("xn", [P, NT, D])
        back = s.sb("back", [P, NT, D])
        xhi = s.sb("xhi", [P, KD, GN], F16)
        xlo = s.sb("xlo", [P, KD, GN], F16)
        logit = s.sb("logit", [P, NT, E])
        prob = s.sb("prob", [P, NT, E])
        red = s.sb("red", [P, NT])
        top = s.sb("top", [P, NT, 8])
        topi = s.sb("topi", [P, NT, 8], U32)
        topf = s.sb("topf", [P, NT, CH])
        tri = s.sb("tri", [P, P])
        tri16 = s.sb("tri16", [P, P], F16)
        ones16 = s.sb("ones16", [P, P], F16)
        chosen = [s.sb(f"chosen{n}", [P, NT, E]) for n in range(CH)]
        chosen16 = s.sb("chosen16", [P, NT, E], F16)
        rank = s.sb("rank", [P, NT, E])
        pre = [s.sb(f"pre{n}", [P, NT, E]) for n in range(2)]
        cmp = s.sb("cmp", [P, NS, E])
        lower = s.sb("lower", [P, E, E])
        iota_s = s.sb("iota_s", [P, FULL])
        tiles = s.sb("tiles", [P, E])
        first = s.sb("first", [P, E])
        base = s.sb("base", [P, E])
        slotf = s.sb("slotf", [P, NT, CH])
        slot = s.sb("slot", [P, CH, NT], U32)
        eidf = s.sb("eidf", [P, NS])
        eid = s.sb("eid", [P, NS], I32)
        xr = [s.sb(f"xr{j}", [P, ST, D]) for j in range(2)]
        thi = [s.sb(f"thi{j}", [P, KD, SLOTS], F16) for j in range(2)]
        tlo = [s.sb(f"tlo{j}", [P, KD, SLOTS], F16) for j in range(2)]
        act1 = [s.sb(f"act1{f}", [P, 2, SLOTS]) for f in range(FP)]
        hf = [s.sb(f"hf{f}", [P, 2, SLOTS]) for f in range(FP)]
        hhi = [s.sb(f"hhi{j}", [P, FT, SLOTS], F16) for j in range(2)]
        hlo = [s.sb(f"hlo{j}", [P, FT, SLOTS], F16) for j in range(2)]
        yo = [s.sb(f"yo{j}", [P, ST, D]) for j in range(2)]
        pH = [s.ps(f"pH{f}", [P, 2, 2, SLOTS]) for f in range(FP)]
        pT = s.ps("pT", [P, KD, GN])
        pY = [s.ps(f"pY{j}", [P, ST, D]) for j in range(2)]
        pL = pY[0][:].rearrange("p t d -> p (t d)")[:, 0:NT * E].rearrange("p (t e) -> p t e", e=E)
        pR = pY[1][:].rearrange("p t d -> p (t d)").rearrange("p (n t e) -> p n t e", n=2, e=E)
        pX = pT[:, 0, :].rearrange("p (c t) -> p c t", c=KD)

        names = ("g_in c_in consts st mvd va rs xn_done turned xhi_done xlo_done g_split logits pre_w steps asteps "
                 "tri_done chosen_done ranked slot_done eid_done sent x_turned thi_done tlo_done uph_done upl_done dnh_done dnl_done "
                 "h_done a_done hf_done hhi_done hlo_done y_done yo_done").split()
        m = {n: s.sem(n) for n in names}
        up_in, dn_in, x_in, y_sent = ([s.sem(f"{n}{j}") for j in range(2)] for n in ("up_in", "dn_in", "x_in", "y_sent"))
        back_in = [s.sem(f"back_in{g}") for g in range(NG)]
        passed = [s.sem(f"passed{n}") for n in range(3)]
        block = ctx.enter_context(nc.Block())

        def upto(tile, each=1, plus=0):
            i, b = tile
            return i * (2 * each) + (b * each + plus)

        def upto_half(tile, each):
            i, b = tile
            return i * each + (b // 2 + 1) * each

        def plus(tile, n):
            return (tile[0], tile[1] + n)

        def steps_of(eng, step):
            step((0, 0))
            with eng.Fori(0, NS // 2 - 1) as i:
                step((i, 1))
                step((i, 2))
            step((0, NS - 1))

        @block.sync
        def _(sp):
            with nc.allow_non_contiguous_dma(reason="small parameters"):
                sp.dma_start(g_raw[:], gate.rearrange("(c p) e -> p c e", p=P)).then_inc(m["g_in"], 16)
                sp.dma_start(iota[:], a["c_iota"].partition_broadcast(P)).then_inc(m["c_in"], 16)
                sp.dma_start(tri[:], a["c_tri"]).then_inc(m["c_in"], 16)
            sp.wait_ge(m["eid_done"], 1)

            def load(tile):
                i, b = tile
                j = b % 2
                if b >= 2:
                    wait_apart(sp, passed[0], m["upl_done"], upto(tile, FP, -FP))
                e = sp.value_load(eid[0:1, bass.ds(i * 2 + b, 1)], min_val=0, max_val=E - 1)
                for n, name in enumerate(("gate", "up")):
                    sp.dma_start(up_raw[j][:, n * KD * F:(n + 1) * KD * F].rearrange("p (c f) -> p c f", c=KD),
                                 a[f"L0_ffn_w_{name}_proj"][bass.ds(e, 1)].rearrange("o (c p) f -> p (o c) f", p=P)).then_inc(up_in[j], 16)
                if b == 0:
                    sp.wait_ge(m["sent"], 16 * CH * NT)
                if b >= 2:
                    sp.wait_ge(m["x_turned"], upto(tile, 1, -1))
                sp.dma_start(xr[j][:], rows_x.rearrange("(n t p) d -> n p t d", t=ST, p=P)[bass.ds(i * 2 + b, 1)]
                             .rearrange("o p t d -> p (o t) d")).then_inc(x_in[j], 16)
                if b >= 2:
                    sp.wait_ge(m["dnl_done"], upto(tile, 1, -1))
                sp.dma_start(dn_raw[j][:].rearrange("p (c f) -> p c f", c=FT),
                             a["L0_ffn_w_down_proj"][bass.ds(e, 1)].rearrange("o (c p) f -> p (o c) f", p=P)).then_inc(dn_in[j], 16)

            load((0, 0))
            load((0, 1))
            with sp.Fori(0, NS // 2 - 1) as i:
                load((i, 2))
                load((i, 3))

        @block.gpsimd
        def _(pool):
            pool.memset(mhalf[:], -0.5).then_inc(m["consts"], 1)
            pool.memset(ones16[:], 1.0).then_inc(m["consts"], 1)
            pool.wait_ge(m["consts"], 2)
            for g in range(NG):
                wait_apart(pool, passed[1], m["mvd"], g + 1)
                pool.tensor_scalar(var[:], mv[:, :, 1], EPS, None, ALU.add).then_inc(m["va"], 1)
                pool.wait_ge(m["va"], g + 1)
                pool.tensor_tensor(rstd[:], var[:], mhalf[:], ALU.pow).then_inc(m["rs"], 1)
            pool.wait_ge(m["slot_done"], 1)
            for t in range(NT):
                for n in range(CH):
                    pool.indirect_dma_start(rows_x, bass.IndirectOffsetOnAxis(slot[:, n, t:t + 1], 0), xn[:, t, :], None).then_inc(m["sent"], 16)
            for j in range(2):
                pool.wait_ge(y_sent[j], 16 + 16 * NS // 2)
            for t in range(NT):
                for n, to in enumerate((xn, back)):
                    pool.indirect_dma_start(to[:, t, :], None, rows_y, bass.IndirectOffsetOnAxis(slot[:, n, t:t + 1], 0)).then_inc(back_in[t // GT], 16)

        @block.scalar
        def _(act):
            act.sem_inc(m["yo_done"], 2)
            for j in range(2):
                act.sem_inc(y_sent[j], 16)
            act.wait_ge(m["g_in"], 16)
            act.activation(g_hi[:], g_raw[:], ACT.Copy, scale=WS).then_inc(m["g_split"], 1)
            for g in range(NG):
                act.wait_ge(m["turned"], g + 1)
                if g:
                    act.wait_ge(m["logits"], g)
                for c in range(KD):
                    ins = act.activation(xhi[:, c, :], pT[:, c, :], ACT.Copy)
                ins.then_inc(m["xhi_done"], 1)
            act.wait_ge(m["pre_w"], 1)
            act.activation(prob[:], logit[:], ACT.Exp).then_inc(m["asteps"], 1)

            def rows_hi(tile):
                j = tile[1] % 2
                act.wait_ge(m["x_turned"], upto(tile, 1, 1))
                act.activation(thi[j][:], pX, ACT.Copy).then_inc(m["thi_done"], 1)

            def up_split_hi(tile, f):
                j = tile[1] % 2
                c = slice(f * UPW // FP, (f + 1) * UPW // FP)
                if f == 0:
                    act.wait_ge(up_in[j], upto_half(tile, 32))
                act.activation(up_hi[j][:, c], up_raw[j][:, c], ACT.Copy, scale=WS).then_inc(m["uph_done"], 1)

            def down_split_hi(tile):
                j = tile[1] % 2
                act.wait_ge(dn_in[j], upto_half(tile, 16))
                act.activation(dn_hi[j][:], dn_raw[j][:], ACT.Copy, scale=WS).then_inc(m["dnh_done"], 1)

            def output(tile):
                j = tile[1] % 2
                act.wait_ge(m["y_done"], upto(tile, 1, 1))
                act.wait_ge(y_sent[j], upto_half(tile, 16))
                act.activation(yo[j][:], pY[j][:], ACT.Copy).then_inc(m["yo_done"], 1)
                act.wait_ge(m["yo_done"], upto(tile, 1, 3))
                act.dma_start(rows_y.rearrange("(n t p) d -> n p t d", t=ST, p=P)[bass.ds(tile[0] * 2 + tile[1], 1)]
                              .rearrange("o p t d -> p (o t) d"), yo[j][:]).then_inc(y_sent[j], 16)

            def silu(tile, f):
                act.wait_ge(m["h_done"], upto(tile, FP, f + 1))
                act.activation(act1[f][:], pH[f][:, :, 0, :], ACT.Silu, scale=1.0 / WS).then_inc(m["a_done"], 1)

            def hidden_hi(tile, f):
                j = tile[1] % 2
                act.wait_ge(m["hf_done"], upto(tile, FP, f + 1))
                act.activation(hhi[j][:, 2 * f:2 * f + 2, :], hf[f][:], ACT.Copy).then_inc(m["hhi_done"], 1)

            def step(tile):
                more = tile[1] + 1 < NS
                if more:
                    for f in range(FP):
                        up_split_hi(plus(tile, 1), f)
                silu(tile, 0)
                if more:
                    rows_hi(plus(tile, 1))
                down_split_hi(tile)
                hidden_hi(tile, 0)
                silu(tile, 1)
                hidden_hi(tile, 1)
                if tile[1]:
                    output(plus(tile, -1))

            for f in range(FP):
                up_split_hi((0, 0), f)
            rows_hi((0, 0))
            steps_of(act, step)
            output((0, NS - 1))

        @block.vector
        def _(dve):
            dve.wait_ge(m["consts"], 2)
            dve.wait_ge(m["g_split"], 1)
            dve.scalar_tensor_tensor(out=g_lo[:], in0=g_raw[:], scalar=WS, in1=g_hi[:], op0=ALU.mult,
                                     op1=ALU.subtract).then_inc(m["g_split"], 1)
            dve.wait_ge(m["c_in"], 32)
            dve.tensor_copy(tri16[:], tri[:]).then_inc(m["tri_done"], 1)
            for g in range(NG + 1):
                if g < NG:
                    layer_stats(dve, passed[2], X[:, g * GT:(g + 1) * GT, :], stats, mv, m["st"], g).then_inc(m["mvd"], 1)
                    dve.wait_ge(m["rs"], g + 1)
                    norm_group(dve, X[:, g * GT:(g + 1) * GT, :], mv, rstd, xn[:, g * GT:(g + 1) * GT]).then_inc(m["xn_done"], 1)
                if g:
                    dve.wait_ge(m["xhi_done"], g)
                    for c in range(KD):
                        ins = dve.tensor_tensor(xlo[:, c, :], pT[:, c, :], xhi[:, c, :], ALU.subtract)
                    ins.then_inc(m["xlo_done"], 1)
            count = [0]

            def step_(ins):
                count[0] += 1
                ins.then_inc(m["steps"], 1)
                dve.wait_ge(m["steps"], count[0])

            def all_tokens(v):
                return v.unsqueeze(2).to_broadcast([P, NT, E])

            dve.wait_ge(m["logits"], NG)
            step_(dve.tensor_scalar(logit[:], pL, 1.0 / WS, None, ALU.mult))
            step_(dve.tensor_reduce(red[:], logit[:], AX.X, ALU.max))
            dve.tensor_tensor(logit[:], logit[:], all_tokens(red[:]), ALU.subtract).then_inc(m["pre_w"], 1)
            dve.tensor_scalar(iota_s[:], iota[:, 0:FULL], float(SLOTS), None, ALU.mult)
            step_(dve.tensor_tensor(lower[:], iota[:, 0:E].unsqueeze(1).to_broadcast([P, E, E]),
                                    iota[:, 0:E].unsqueeze(2).to_broadcast([P, E, E]), ALU.is_lt))
            dve.wait_ge(m["asteps"], 1)
            step_(dve.tensor_reduce(red[:], prob[:], AX.X, ALU.add))
            step_(dve.reciprocal(red[:], red[:]))
            step_(dve.tensor_tensor(prob[:], prob[:], all_tokens(red[:]), ALU.mult))
            for t in range(NT):
                ins = dve.max(top[:, t, :], prob[:, t, :])
            step_(ins)
            for t in range(NT):
                ins = dve.max_index(topi[:, t, :], top[:, t, :], prob[:, t, :])
            step_(ins)
            step_(dve.tensor_copy(topf[:], topi[:, :, 0:CH]))
            for n in range(CH):
                ins = dve.tensor_tensor(chosen[n][:], iota[:, 0:E].unsqueeze(1).to_broadcast([P, NT, E]), all_tokens(topf[:, :, n]), ALU.is_equal)
            step_(ins)
            dve.tensor_tensor(chosen16[:], chosen[0][:], chosen[1][:], ALU.add).then_inc(m["chosen_done"], 1)
            step_(dve.tensor_tensor(red[:], top[:, :, 0], top[:, :, 1], ALU.add))
            step_(dve.reciprocal(red[:], red[:]))
            step_(dve.scalar_tensor_tensor(out=top[:, :, 0:CH], in0=top[:, :, 0:CH], scalar=1.0 / WS / WS,
                                           in1=red[:].unsqueeze(2).to_broadcast([P, NT, CH]), op0=ALU.mult, op1=ALU.mult))
            dve.wait_ge(m["ranked"], 1)
            step_(dve.tensor_copy(pre[0][:], pR[:, 1]))
            step_(dve.tensor_tensor(rank[:], pR[:, 0], pre[0][:], ALU.subtract))
            n, w = 0, 1
            while w < NT:
                dve.tensor_copy(pre[1 - n][:, 0:w, :], pre[n][:, 0:w, :])
                step_(dve.tensor_tensor(pre[1 - n][:, w:, :], pre[n][:, w:, :], pre[n][:, 0:NT - w, :], ALU.add))
                n, w = 1 - n, 2 * w
            total = pre[n][:, NT - 1, :]
            dve.tensor_tensor(rank[:], rank[:], pre[n][:], ALU.add)
            step_(dve.tensor_tensor(cmp[:, 0:E, 0:FULL], total.unsqueeze(2).to_broadcast([P, E, FULL]),
                                    iota_s[:].unsqueeze(1).to_broadcast([P, E, FULL]), ALU.is_gt))
            step_(dve.tensor_reduce(tiles[:], cmp[:, 0:E, 0:FULL], AX.X, ALU.add))
            step_(dve.tensor_tensor(lower[:], lower[:], tiles[:].unsqueeze(1).to_broadcast([P, E, E]), ALU.mult))
            step_(dve.tensor_reduce(first[:], lower[:], AX.X, ALU.add))
            dve.tensor_scalar(base[:], first[:], float(SLOTS), None, ALU.mult)
            step_(dve.tensor_tensor(tiles[:], tiles[:], first[:], ALU.add))
            step_(dve.tensor_tensor(cmp[:], iota[:].unsqueeze(2).to_broadcast([P, NS, E]),
                                    tiles[:].unsqueeze(1).to_broadcast([P, NS, E]), ALU.is_ge))
            step_(dve.tensor_reduce(eidf[:], cmp[:], AX.X, ALU.add))
            step_(dve.tensor_scalar(eidf[:], eidf[:], float(E - 1), None, ALU.min))
            dve.tensor_copy(eid[:], eidf[:]).then_inc(m["eid_done"], 1)
            step_(dve.tensor_tensor(rank[:], rank[:], base[:].unsqueeze(1).to_broadcast([P, NT, E]), ALU.add))
            for n in range(CH):
                ins = dve.tensor_tensor(chosen[n][:], chosen[n][:], rank[:], ALU.mult)
            step_(ins)
            for n in range(CH):
                ins = dve.tensor_reduce(slotf[:, :, n], chosen[n][:], AX.X, ALU.add)
            step_(ins)
            dve.tensor_copy(slot[:].rearrange("p n t -> p t n"), slotf[:]).then_inc(m["slot_done"], 1)

            def rows_lo(tile):
                j = tile[1] % 2
                dve.wait_ge(m["thi_done"], upto(tile, 1, 1))
                dve.tensor_tensor(tlo[j][:], pX, thi[j][:], ALU.subtract).then_inc(m["tlo_done"], 1)

            def up_split_lo(tile, f):
                j = tile[1] % 2
                c = slice(f * UPW // FP, (f + 1) * UPW // FP)
                dve.wait_ge(m["uph_done"], upto(tile, FP, f + 1))
                dve.scalar_tensor_tensor(out=up_lo[j][:, c], in0=up_raw[j][:, c], scalar=WS, in1=up_hi[j][:, c], op0=ALU.mult,
                                         op1=ALU.subtract).then_inc(m["upl_done"], 1)

            def down_split_lo(tile):
                j = tile[1] % 2
                dve.wait_ge(m["dnh_done"], upto(tile, 1, 1))
                dve.scalar_tensor_tensor(out=dn_lo[j][:], in0=dn_raw[j][:], scalar=WS, in1=dn_hi[j][:], op0=ALU.mult,
                                         op1=ALU.subtract).then_inc(m["dnl_done"], 1)

            def hidden(tile, f):
                dve.wait_ge(m["a_done"], upto(tile, FP, f + 1))
                dve.tensor_tensor(hf[f][:], pH[f][:, :, 1, :], act1[f][:], ALU.mult).then_inc(m["hf_done"], 1)

            def hidden_lo(tile, f):
                j = tile[1] % 2
                dve.wait_ge(m["hhi_done"], upto(tile, FP, f + 1))
                dve.tensor_tensor(hlo[j][:, 2 * f:2 * f + 2, :], hf[f][:], hhi[j][:, 2 * f:2 * f + 2, :], ALU.subtract).then_inc(m["hlo_done"], 1)

            def step(tile):
                more = tile[1] + 1 < NS
                if more:
                    for f in range(FP):
                        up_split_lo(plus(tile, 1), f)
                hidden(tile, 0)
                if more:
                    rows_lo(plus(tile, 1))
                down_split_lo(tile)
                hidden_lo(tile, 0)
                hidden(tile, 1)
                hidden_lo(tile, 1)

            for f in range(FP):
                up_split_lo((0, 0), f)
            rows_lo((0, 0))
            steps_of(dve, step)
            for t in range(NT):
                if t % GT == 0:
                    dve.wait_ge(back_in[t // GT], 16 * CH * GT)
                for n, rows in enumerate((xn, back)):
                    if t or n:
                        dve.wait_ge(m["steps"], count[0])
                    step_(dve.scalar_tensor_tensor(out=X[:, t, :], in0=rows[:, t, :], scalar=top[:, t, n:n + 1], in1=X[:, t, :],
                                                   op0=ALU.mult, op1=ALU.add))

        @block.tensor
        def _(pe):
            pe.wait_ge(m["consts"], 2)
            pe.wait_ge(m["g_split"], 2)
            for g in range(NG):
                pe.wait_ge(m["xn_done"], g + 1)
                if g:
                    pe.wait_ge(m["xlo_done"], g)
                for c in range(KD):
                    for t in range(GT):
                        ins = pe.transpose(pT[:, c, t * P:(t + 1) * P], xn[:, g * GT + t, c * P:(c + 1) * P], ident[:])
                ins.then_inc(m["turned"], 1)
                pe.wait_ge(m["xlo_done"], g + 1)
                for t in range(GT):
                    tok = slice(t * P, (t + 1) * P)
                    out = pL[:, g * GT + t, :]
                    for c in range(KD):
                        pe.matmul(out, xhi[:, c, tok], g_hi[:, c, :], start=(c == 0), stop=False)
                        pe.matmul(out, xhi[:, c, tok], g_lo[:, c, :], start=False, stop=False)
                        ins = pe.matmul(out, xlo[:, c, tok], g_hi[:, c, :], start=False, stop=(c == KD - 1))
                ins.then_inc(m["logits"], 1)
            pe.wait_ge(m["tri_done"], 1)
            pe.wait_ge(m["chosen_done"], 1)
            flat = chosen16[:].rearrange("p t e -> p (t e)")
            for n, w in enumerate((tri16, ones16)):
                ins = pe.matmul(pR[:, n].rearrange("p t e -> p (t e)"), w[:], flat, start=True, stop=True)
            ins.then_inc(m["ranked"], 1)

            def turn(tile):
                i, b = tile
                j = b % 2
                pe.wait_ge(x_in[j], upto_half(tile, 16))
                if b:
                    pe.wait_ge(m["tlo_done"], upto(tile))
                for c in range(KD):
                    for t in range(ST):
                        ins = pe.transpose(pX[:, c, t * P:(t + 1) * P], xr[j][:, t, c * P:(c + 1) * P], ident[:])
                ins.then_inc(m["x_turned"], 1)

            def up(tile, f):
                i, b = tile
                j = b % 2
                if f == 0:
                    pe.wait_ge(m["upl_done"], upto(tile, FP, FP))
                    pe.wait_ge(m["tlo_done"], upto(tile, 1, 1))
                if b:
                    pe.wait_ge(m["hf_done"], upto(tile, FP, f + 1 - FP))
                for n in range(2):
                    for u in range(2):
                        for c in range(KD):
                            at = u * KD * F + c * F + (2 * f + n) * P
                            w_h, w_l = up_hi[j][:, at:at + P], up_lo[j][:, at:at + P]
                            out = pH[f][:, n, u, :]
                            pe.matmul(out, w_h, thi[j][:, c, :], start=(c == 0), stop=False)
                            pe.matmul(out, w_h, tlo[j][:, c, :], start=False, stop=False)
                            ins = pe.matmul(out, w_l, thi[j][:, c, :], start=False, stop=(c == KD - 1))
                ins.then_inc(m["h_done"], 1)

            def down(tile):
                i, b = tile
                j = b % 2
                pe.wait_ge(m["dnl_done"], upto(tile, 1, 1))
                pe.wait_ge(m["hlo_done"], upto(tile, FP, FP))
                pe.wait_ge(m["yo_done"], upto(tile, 1, 1))
                for t in range(ST):
                    ts = slice(t * P, (t + 1) * P)
                    for f in range(FT):
                        w = slice(f * D, (f + 1) * D)
                        pe.matmul(pY[j][:, t, :], hhi[j][:, f, ts], dn_hi[j][:, w], start=(f == 0), stop=False)
                        pe.matmul(pY[j][:, t, :], hhi[j][:, f, ts], dn_lo[j][:, w], start=False, stop=False)
                        ins = pe.matmul(pY[j][:, t, :], hlo[j][:, f, ts], dn_hi[j][:, w], start=False, stop=(f == FT - 1))
                ins.then_inc(m["y_done"], 1)

            def step(tile):
                up(tile, 0)
                if tile[1] + 1 < NS:
                    turn(plus(tile, 1))
                up(tile, 1)
                if tile[1]:
                    down(plus(tile, -1))

            turn((0, 0))
            steps_of(pe, step)
            down((0, NS - 1))


def retention(nc, a, X, ident, ident16):
    H, HD = 16, D // 16
    PAIRS = H // 2
    OCT = 2
    TS = SEQ // P
    T = NT
    EPS = 1e-5
    AW = 4 * HD
    HK = 2 * H
    LAST = 11
    with ExitStack() as ctx:
        s = Store(nc, ctx, "ret_")
        w_raw = s.sb("w_raw", [P, 3 * KD, D])
        WQ, WO, WE = np.cumsum([0, KD * 3 * D, KD * D]).tolist()
        wT = s.sb("wT", [P, WE])
        wThi = s.sb("wThi", [P, WE], F16)
        wTlo = s.sb("wTlo", [P, WE], F16)
        gnp = s.sb("gnp", [P, 2, D])
        cos = s.sb("cos", [P, TS, HD])
        sin = s.sb("sin", [P, TS, HD])
        dmask = s.sb("dmask", [P, H, P])
        dq = s.sb("dq", [P, H])
        dk = s.sb("dk", [P, H])
        dstate = s.sb("dstate", [P, OCT])
        blocks = s.sb("blocks", [P, P])
        mhalf = s.sb("mhalf", [P, HK])
        stats = s.sb("stats", [P, GT, 6])
        mv = s.sb("mv", [P, GT, 2])
        var = s.sb("var", [P, GT])
        rstd = s.sb("rstd", [P, GT])
        xn = s.sb("xn", [P, 2, GT, D])
        xhi = s.sb("xhi", [P, KD, N], F16)
        xlo = s.sb("xlo", [P, KD, N], F16)
        qk = s.sb("qk", [P, 4, HK, HD])
        rot = s.sb("rot", [P, HK, HD])
        v = s.sb("v", [P, 3, D])
        vhi = s.sb("vhi", [P, 8, D], F16)
        vlo = s.sb("vlo", [P, 8, D], F16)
        qd = s.sb("qd", [P, 3, H, HD])
        kd = s.sb("kd", [P, 3, H, HD])
        kdhi = s.sb("kdhi", [P, 6, D], F16)
        kdlo = s.sb("kdlo", [P, 6, D], F16)
        qa = s.sb("qa", [P, 2, H, 4, HD], F16)
        ka = s.sb("ka", [P, 2, H, 4, HD], F16)
        kT = s.sb("kT", [P, 2, PAIRS, P], F16)
        qT = s.sb("qT", [P, 2, H, P], F16)
        qdhi = s.sb("qdhi", [P, 4, OCT, P], F16)
        qdlo = s.sb("qdlo", [P, 4, OCT, P], F16)
        am = s.sb("am", [P, H, P])
        ahi = s.sb("ahi", [P, 3, H, P], F16)
        alo = s.sb("alo", [P, 3, H, P], F16)
        st = s.sb("st", [P, OCT, P])
        stx = s.sb("stx", [P, OCT, P])
        sthi = s.sb("sthi", [P, OCT, P], F16)
        stlo = s.sb("stlo", [P, OCT, P], F16)
        r = s.sb("r", [P, 4, H, HD])
        rsq = s.sb("rsq", [P, 2, H, HD])
        hsum = s.sb("hsum", [P, 2, H])
        hsq = s.sb("hsq", [P, 2, H])
        hvar = s.sb("hvar", [P, 2, H])
        rhi = s.sb("rhi", [P, 2, OCT, P], F16)
        rlo = s.sb("rlo", [P, 2, OCT, P], F16)
        bank = [s.ps(f"bank{n}", [P, GN])[:] for n in range(8)]
        bank16 = [b.bitcast(F16) for b in bank]
        QK, VY, KA, QA, SC, QD, RO = 0, 1, 2, 3, 4, 6, 7

        w_in, wo_in, c_in = s.sem("w_in"), s.sem("wo_in"), s.sem("c_in")
        consts, w_turned, w_copied, w_ready = (s.sem(n) for n in ("consts", "w_turned", "w_copied", "w_ready"))
        names = ("stx mvd va rs xn_done turned xhi_done xlo_done qkv_done qk_copied v_copied vhi_done vlo_done rot_done cos_done "
                 "rope_done qd_done kd_done hi_done kdhi_done kdlo_done lo_done ka_turned qa_turned qd_turned kT_done qT_done "
                 "qdhi_done qdlo_done sc_done am_done ahi_done alo_done out_done s1 s2 sthi_done stlo_done r_copied sum_done "
                 "cen_done sq_done sum2_done hvar_done hrs_done scaled gam_done bet_done r_turned rhi_done rlo_done y_done y_added").split()
        m = {n: s.sem(n) for n in names}
        passed = s.sem("passed")
        block = ctx.enter_context(nc.Block())
        NW = 3 * D // P
        SR = 4

        def after(eng, name, t, each=1, part=None):
            eng.wait_ge(m[name], t * each + (each if part is None else part))

        def parts(s_, lag):
            return s_ - lag if 0 <= s_ - lag < T else None

        @block.sync
        def _(sp):
            for n, name in enumerate(("WQ", "WK", "WV")):
                w = a["L1_attn_" + name].rearrange("h u d -> (h u) d")
                sp.dma_start(w_raw[:, n * KD:(n + 1) * KD, :], w.rearrange("(t p) c -> p t c", p=P)).then_inc(w_in, 16)
            sp.dma_start(wT[:, WO:WE].rearrange("p (c d) -> p c d", c=KD), a["L1_attn_WO"].rearrange("(c p) d -> p c d", p=P)).then_inc(wo_in, 16)
            sp.dma_start(gnp[:, 0, :], a["L1_attn_gamma"].partition_broadcast(P)).then_inc(c_in, 16)
            sp.dma_start(gnp[:, 1, :], a["L1_attn_beta"].partition_broadcast(P)).then_inc(c_in, 16)
            for dst, name in ((cos, "c_cos1"), (sin, "c_sin1")):
                sp.dma_start(dst[:], a[name].rearrange("(t p) f -> p t f", p=P)).then_inc(c_in, 16)
            for dst, name in ((dmask, "c_dmask"), (dq, "c_dq"), (dk, "c_dk"), (dstate, "c_dstate"), (blocks, "c_blocks")):
                sp.dma_start(dst[:], a[name]).then_inc(c_in, 16)

        @block.gpsimd
        def _(pool):
            pool.memset(mhalf[:], -0.5).then_inc(consts, 1)
            pool.memset(qa[:, :, :, 3, :], 0.0).then_inc(consts, 1)
            pool.memset(ka[:, :, :, 3, :], 0.0).then_inc(consts, 1)
            pool.memset(qT[:], 0.0).then_inc(consts, 1)
            pool.wait_ge(consts, 4)
            pool.wait_ge(c_in, 16 * 9)

            for g in range(NG):
                wait_apart(pool, passed, m["mvd"], g + 1)
                pool.tensor_scalar(var[:], mv[:, :, 1], EPS, None, ALU.add).then_inc(m["va"], 1)
                pool.wait_ge(m["va"], g + 1)
                pool.tensor_tensor(rstd[:], var[:], mhalf[:, 0:GT], ALU.pow).then_inc(m["rs"], 1)
            for s_ in range(T + LAST + 1):
                t = parts(s_, 8)
                if t is not None:
                    after(pool, "sum2_done", t)
                    if t >= 2:
                        after(pool, "scaled", t - 2)
                    pool.sem_inc(passed, 1)
                    pool.tensor_scalar(hvar[:, t % 2], hsq[:, t % 2], 1.0 / HD, EPS, ALU.mult, ALU.add).then_inc(m["hvar_done"], 1)
                    after(pool, "hvar_done", t)
                    pool.tensor_tensor(hvar[:, t % 2], hvar[:, t % 2], mhalf[:, 0:H], ALU.pow).then_inc(m["hrs_done"], 1)
                t = parts(s_, 9)
                if t is not None:
                    after(pool, "scaled", t)
                    part = r[:, t % 4].rearrange("p h f -> p (h f)")
                    pool.tensor_tensor(part, part, gnp[:, 0, :], ALU.mult).then_inc(m["gam_done"], 1)
                    after(pool, "gam_done", t)
                    pool.tensor_tensor(part, part, gnp[:, 1, :], ALU.add).then_inc(m["bet_done"], 1)
                t = parts(s_, 2)
                if t is not None:
                    after(pool, "rope_done", t)
                    if t >= 3:
                        after(pool, "qd_turned", t - 3)
                        after(pool, "kdlo_done", t - 3)
                    pool.tensor_tensor(qd[:, t % 3], qk[:, t % 4, 0:H, :], dq[:].unsqueeze(2).to_broadcast([P, H, HD]), ALU.mult).then_inc(m["qd_done"], 1)
                    pool.tensor_tensor(kd[:, t % 3], qk[:, t % 4, H:HK, :], dk[:].unsqueeze(2).to_broadcast([P, H, HD]), ALU.mult).then_inc(m["kd_done"], 1)
                    after(pool, "vhi_done", t)
                    pool.tensor_tensor(vlo[:, t % 8, :], v[:, t % 3, :], vhi[:, t % 8, :], ALU.subtract).then_inc(m["vlo_done"], 1)
                t = parts(s_, 3)
                if t is not None:
                    after(pool, "kdhi_done", t)
                    pool.tensor_tensor(kdlo[:, t % 6, :], kd[:, t % 3].rearrange("p h f -> p (h f)"), kdhi[:, t % 6, :], ALU.subtract).then_inc(m["kdlo_done"], 1)

        @block.scalar
        def _(act):
            for n in range(NW):
                act.wait_ge(w_turned, n + 1)
                act.activation(wT[:, WQ:WO].rearrange("p (c o) -> p c o", c=KD)[:, :, n * P:(n + 1) * P],
                               bank[n % 2][:, 0:KD * P].rearrange("p (c o) -> p c o", c=KD), ACT.Copy).then_inc(w_copied, 1)
            act.wait_ge(w_copied, NW)
            act.wait_ge(wo_in, 16)
            act.activation(wThi[:], wT[:], ACT.Copy, scale=WS).then_inc(w_ready, 1)
            act.wait_ge(consts, 4)

            for g in range(NG):
                act.wait_ge(m["turned"], g + 1)
                for c in range(KD):
                    ins = act.activation(xhi[:, c, g * GN:(g + 1) * GN], bank[g % 2 * KD + c], ACT.Copy)
                ins.then_inc(m["xhi_done"], 1)
            for s_ in range(T + LAST + 1):
                t = parts(s_, 10)
                if t is not None:
                    after(act, "r_turned", t)
                    if t >= 2:
                        after(act, "y_done", t - 2)
                    act.activation(rhi[:, t % 2], bank[VY][:, D:2 * D].rearrange("p (c t) -> p c t", c=OCT), ACT.Copy).then_inc(m["rhi_done"], 1)
                t = parts(s_, 4)
                if t is not None:
                    after(act, "ka_turned", t)
                    if t >= 2:
                        after(act, "sc_done", t - 2, SR)
                    act.activation(kT[:, t % 2], bank16[KA].rearrange("p (h t) -> p h t", h=PAIRS), ACT.Copy).then_inc(m["kT_done"], 1)
                    after(act, "qd_turned", t)
                    act.activation(qdhi[:, t % 4], bank[QD][:, 0:OCT * P].rearrange("p (c t) -> p c t", c=OCT), ACT.Copy).then_inc(m["qdhi_done"], 1)
                t = parts(s_, 6)
                if t is not None:
                    after(act, "out_done", t)
                    act.activation(r[:, t % 4], bank[RO][:, 0:D].rearrange("p (h f) -> p h f", h=H), ACT.Copy).then_inc(m["r_copied"], 1)
                    after(act, "s2", t)
                    act.activation(sthi[:], st[:], ACT.Copy).then_inc(m["sthi_done"], 1)
                t = parts(s_, 2)
                if t is not None:
                    after(act, "rope_done", t)
                    if t >= 2:
                        after(act, "ka_turned", t - 2)
                        after(act, "qa_turned", t - 2)
                    for n in (0, 2):
                        act.activation(qa[:, t % 2, :, n, :], qk[:, t % 4, 0:H, :], ACT.Copy)
                    for n in (0, 1):
                        ins = act.activation(ka[:, t % 2, :, n, :], qk[:, t % 4, H:HK, :], ACT.Copy)
                    ins.then_inc(m["hi_done"], 1)
                t = parts(s_, 3)
                if t is not None:
                    after(act, "kd_done", t)
                    act.activation(kdhi[:, t % 6, :], kd[:, t % 3].rearrange("p h f -> p (h f)"), ACT.Copy).then_inc(m["kdhi_done"], 1)
                t = parts(s_, 7)
                if t is not None:
                    after(act, "cen_done", t)
                    act.activation(rsq[:, t % 2], r[:, t % 4], ACT.Square).then_inc(m["sq_done"], 1)
                t = parts(s_, 0)
                if t is not None:
                    after(act, "qkv_done", t)
                    if t >= 4:
                        after(act, "lo_done", t - 4)
                        after(act, "kd_done", t - 4)
                    act.activation(qk[:, t % 4], bank[QK].rearrange("p (h f) -> p h f", h=HK), ACT.Copy, scale=1.0 / WS).then_inc(m["qk_copied"], 1)
                    if t >= 3:
                        after(act, "vlo_done", t - 3)
                    act.activation(v[:, t % 3, :], bank[VY][:, 0:D], ACT.Copy, scale=1.0 / WS).then_inc(m["v_copied"], 1)
                    after(act, "v_copied", t)
                    act.activation(vhi[:, t % 8, :], v[:, t % 3, :], ACT.Copy).then_inc(m["vhi_done"], 1)
                t = parts(s_, 4)
                if t is not None:
                    for n in range(SR):
                        h = slice(n * H // SR, (n + 1) * H // SR)
                        after(act, "am_done", t, SR, n + 1)
                        act.activation(ahi[:, t % 3, h, :], am[:, h, :], ACT.Copy).then_inc(m["ahi_done"], 1)

        @block.vector
        def _(dve):
            dve.wait_ge(w_ready, 1)
            dve.scalar_tensor_tensor(out=wTlo[:], in0=wT[:], scalar=WS, in1=wThi[:], op0=ALU.mult, op1=ALU.subtract).then_inc(w_ready, 1)
            dve.wait_ge(consts, 4)
            dve.wait_ge(c_in, 16 * 9)
            for g in range(NG + 1):
                if g < NG:
                    xg = X[:, g * GT:(g + 1) * GT, :]
                    layer_stats(dve, passed, xg, stats, mv, m["stx"], g).then_inc(m["mvd"], 1)
                    dve.wait_ge(m["rs"], g + 1)
                    if g >= 2:
                        dve.wait_ge(m["turned"], g - 1)
                    norm_group(dve, xg, mv, rstd, xn[:, g % 2]).then_inc(m["xn_done"], 1)
                if g:
                    dve.wait_ge(m["xhi_done"], g)
                    for c in range(KD):
                        t = slice((g - 1) * GN, g * GN)
                        ins = dve.tensor_tensor(xlo[:, c, t], bank[(g - 1) % 2 * KD + c], xhi[:, c, t], ALU.subtract)
                    ins.then_inc(m["xlo_done"], 1)
            for s_ in range(T + LAST + 1):
                t = parts(s_, 11)
                if t is not None:
                    after(dve, "y_done", t)
                    if t + 1 < T:
                        after(dve, "rhi_done", t + 1)
                    x = X[:, t, :]
                    dve.scalar_tensor_tensor(out=x, in0=bank[VY][:, 0:D], scalar=1.0 / WS, in1=x, op0=ALU.mult, op1=ALU.add).then_inc(m["y_added"], 1)
                t = parts(s_, 10)
                if t is not None:
                    after(dve, "rhi_done", t)
                    dve.tensor_tensor(rlo[:, t % 2], bank[VY][:, D:2 * D].rearrange("p (c t) -> p c t", c=OCT), rhi[:, t % 2], ALU.subtract).then_inc(m["rlo_done"], 1)
                t = parts(s_, 4)
                if t is not None:
                    after(dve, "qa_turned", t)
                    if t >= 2:
                        after(dve, "sc_done", t - 2, SR)
                    for h in range(2):
                        rows = slice(h * AW, (h + 1) * AW)
                        ins = dve.tensor_copy(qT[rows, t % 2, h::2, :], bank16[QA][rows, :].rearrange("p (h t) -> p h t", h=PAIRS))
                    ins.then_inc(m["qT_done"], 1)
                    after(dve, "qdhi_done", t)
                    dve.tensor_tensor(qdlo[:, t % 4], bank[QD][:, 0:OCT * P].rearrange("p (c t) -> p c t", c=OCT), qdhi[:, t % 4], ALU.subtract).then_inc(m["qdlo_done"], 1)
                t = parts(s_, 5)
                if t is not None:
                    after(dve, "ahi_done", t, SR)
                    dve.tensor_tensor(alo[:, t % 3], am[:], ahi[:, t % 3], ALU.subtract).then_inc(m["alo_done"], 1)
                t = parts(s_, 6)
                if t is not None:
                    after(dve, "out_done", t)
                    dve.tensor_tensor(stx[:], bank[QD][:, D:2 * D].rearrange("p (c f) -> p c f", c=OCT),
                                      blocks[:].unsqueeze(1).to_broadcast([P, OCT, P]), ALU.mult).then_inc(m["s1"], 1)
                    after(dve, "s1", t)
                    if t % TS == 0:
                        dve.tensor_copy(st[:], stx[:]).then_inc(m["s2"], 1)
                    else:
                        for c in range(OCT):
                            ins = dve.scalar_tensor_tensor(out=st[:, c, :], in0=st[:, c, :], scalar=dstate[:, c:c + 1], in1=stx[:, c, :],
                                                           op0=ALU.mult, op1=ALU.add)
                        ins.then_inc(m["s2"], 1)
                    after(dve, "sthi_done", t)
                    dve.tensor_tensor(stlo[:], st[:], sthi[:], ALU.subtract).then_inc(m["stlo_done"], 1)
                t = parts(s_, 9)
                if t is not None:
                    after(dve, "hrs_done", t)
                    dve.tensor_tensor(r[:, t % 4], r[:, t % 4], hvar[:, t % 2].unsqueeze(2).to_broadcast([P, H, HD]), ALU.mult).then_inc(m["scaled"], 1)
                t = parts(s_, 8)
                if t is not None:
                    after(dve, "sq_done", t)
                    if t >= 2:
                        after(dve, "hvar_done", t - 2)
                    dve.tensor_reduce(hsq[:, t % 2], rsq[:, t % 2], AX.X, ALU.add).then_inc(m["sum2_done"], 1)
                t = parts(s_, 7)
                if t is not None:
                    after(dve, "r_copied", t)
                    dve.tensor_reduce(hsum[:, t % 2], r[:, t % 4], AX.X, ALU.add).then_inc(m["sum_done"], 1)
                    after(dve, "sum_done", t)
                    dve.scalar_tensor_tensor(out=r[:, t % 4], in0=hsum[:, t % 2].unsqueeze(2).to_broadcast([P, H, HD]), scalar=-1.0 / HD,
                                             in1=r[:, t % 4], op0=ALU.mult, op1=ALU.add).then_inc(m["cen_done"], 1)
                t = parts(s_, 3)
                if t is not None:
                    after(dve, "hi_done", t)
                    dve.tensor_tensor(qa[:, t % 2, :, 1, :], qk[:, t % 4, 0:H, :], qa[:, t % 2, :, 0, :], ALU.subtract)
                    dve.tensor_tensor(ka[:, t % 2, :, 2, :], qk[:, t % 4, H:HK, :], ka[:, t % 2, :, 0, :], ALU.subtract).then_inc(m["lo_done"], 1)
                t = parts(s_, 1)
                if t is not None:
                    after(dve, "qk_copied", t)
                    if t:
                        after(dve, "rope_done", t - 1)
                    q = qk[:, t % 4].rearrange("p h (f two) -> p h f two", two=2)
                    ro = rot[:].rearrange("p h (f two) -> p h f two", two=2)
                    sn = sin[:, t % TS, :].rearrange("p (f two) -> p f two", two=2)
                    for n in range(2):
                        ins = dve.tensor_tensor(ro[:, :, :, n], q[:, :, :, 1 - n], sn[:, :, n].unsqueeze(1).to_broadcast([P, HK, HD // 2]), ALU.mult)
                    ins.then_inc(m["rot_done"], 1)
                    after(dve, "rot_done", t)
                    dve.tensor_tensor(qk[:, t % 4], qk[:, t % 4], cos[:, t % TS, :].unsqueeze(1).to_broadcast([P, HK, HD]), ALU.mult).then_inc(m["cos_done"], 1)
                    after(dve, "cos_done", t)
                    dve.tensor_tensor(qk[:, t % 4], qk[:, t % 4], rot[:], ALU.add).then_inc(m["rope_done"], 1)
                t = parts(s_, 4)
                if t is not None:
                    for n in range(SR):
                        h = slice(n * H // SR, (n + 1) * H // SR)
                        after(dve, "sc_done", t, SR, n + 1)
                        if n == 0 and t:
                            after(dve, "alo_done", t - 1)
                        dve.tensor_tensor(am[:, h, :], bank[SC + n % 2].rearrange("p (h t) -> p h t", h=H // SR), dmask[:, h, :], ALU.mult).then_inc(m["am_done"], 1)

        @block.tensor
        def _(pe):
            pe.wait_ge(w_in, 48)
            for n in range(NW):
                if n >= 2:
                    pe.wait_ge(w_copied, n - 1)
                for c in range(KD):
                    ins = pe.transpose(bank[n % 2][:, c * P:(c + 1) * P], w_raw[:, n, c * P:(c + 1) * P], ident[:])
                ins.then_inc(w_turned, 1)
            pe.wait_ge(consts, 4)
            pe.wait_ge(w_ready, 2)
            wq_h, wq_l = (w[:, WQ:WO].rearrange("p (c o) -> p c o", c=KD) for w in (wThi, wTlo))
            wo_h, wo_l = (w[:, WO:WE].rearrange("p (c o) -> p c o", c=KD) for w in (wThi, wTlo))

            def three(out, hi, lo, w_hi, w_lo, start, stop):
                pe.matmul(out, hi, w_hi, start=start, stop=False, skip_group_check=True)
                pe.matmul(out, hi, w_lo, start=False, stop=False, skip_group_check=True)
                return pe.matmul(out, lo, w_hi, start=False, stop=stop, skip_group_check=True)

            for g in range(NG):
                pe.wait_ge(m["xn_done"], g + 1)
                if g >= 2:
                    pe.wait_ge(m["xlo_done"], g - 1)
                for c in range(KD):
                    for t in range(GT):
                        ins = pe.transpose(bank[g % 2 * KD + c][:, t * P:(t + 1) * P], xn[:, g % 2, t, c * P:(c + 1) * P], ident[:])
                ins.then_inc(m["turned"], 1)
            pe.wait_ge(m["xlo_done"], NG)
            for s_ in range(T + LAST + 1):
                t = parts(s_, 6)
                if t is not None:
                    for n in ("alo_done", "vlo_done", "kdlo_done"):
                        after(pe, n, t)
                    if t:
                        after(pe, "stlo_done", t - 1)
                        after(pe, "r_copied", t - 1)
                    after(pe, "qdlo_done", min(t + 2, T - 1))
                    out = bank[RO][:, 0:D]
                    if t % TS:
                        for c in range(OCT):
                            three(out[:, c * P:(c + 1) * P], qdhi[:, t % 4, c, :], qdlo[:, t % 4, c, :], sthi[:, c, :], stlo[:, c, :], c == 0, False)
                    for h in range(H):
                        cols = slice(h * HD, (h + 1) * HD)
                        three(out[:, cols], ahi[:, t % 3, h, :], alo[:, t % 3, h, :], vhi[:, t % 8, cols], vlo[:, t % 8, cols],
                              t % TS == 0 and h == 0, h == H - 1)
                    for c in range(OCT):
                        cols = slice(c * P, (c + 1) * P)
                        ins = three(bank[QD][:, D + c * P:D + (c + 1) * P], kdhi[:, t % 6, cols], kdlo[:, t % 6, cols],
                                    vhi[:, t % 8, cols], vlo[:, t % 8, cols], c == 0, c == OCT - 1)
                    ins.then_inc(m["out_done"], 1)
                t = parts(s_, 0)
                if t is not None:
                    tok = slice(t * P, (t + 1) * P)
                    if t:
                        after(pe, "qk_copied", t - 1)
                    for c in range(KD):
                        three(bank[QK], xhi[:, c, tok], xlo[:, c, tok], wq_h[:, c, 0:2 * D], wq_l[:, c, 0:2 * D], c == 0, c == KD - 1)
                    if t:
                        after(pe, "v_copied", t - 1)
                    if t >= 11:
                        after(pe, "y_added", t - 11)
                    if t >= 10:
                        after(pe, "rlo_done", t - 10)
                    for c in range(KD):
                        ins = three(bank[VY][:, 0:D], xhi[:, c, tok], xlo[:, c, tok], wq_h[:, c, 2 * D:], wq_l[:, c, 2 * D:], c == 0, c == KD - 1)
                    ins.then_inc(m["qkv_done"], 1)
                t = parts(s_, 4)
                if t is not None:
                    after(pe, "kT_done", t)
                    after(pe, "qT_done", t)
                    for n in range(SR):
                        if n >= 2:
                            after(pe, "am_done", t, SR, n - 1)
                        elif t:
                            after(pe, "am_done", t - 1, SR, SR)
                        for p in range(2 * n, 2 * n + 2):
                            at = (p % 2) * 2 * P
                            ins = pe.matmul(bank[SC + n % 2][:, at:at + 2 * P], kT[:, t % 2, p, :], qT[:, t % 2, 2 * p:2 * p + 2, :].rearrange("p h t -> p (h t)"),
                                            start=True, stop=True)
                        ins.then_inc(m["sc_done"], 1)
                t = parts(s_, 3)
                if t is not None:
                    after(pe, "lo_done", t)
                    after(pe, "qd_done", t)
                    if t:
                        after(pe, "kT_done", t - 1)
                        after(pe, "qT_done", t - 1)
                        after(pe, "qdlo_done", t - 1)
                    for src, b, name in ((ka[:, t % 2], KA, "ka_turned"), (qa[:, t % 2], QA, "qa_turned")):
                        for p in range(PAIRS):
                            ins = pe.transpose(bank16[b][:, p * P:(p + 1) * P], src[:, 2 * p:2 * p + 2, :, :].rearrange("p h a f -> p (h a f)"), ident16[:])
                        ins.then_inc(m[name], 1)
                    if t >= 3:
                        after(pe, "s1", t - 3)
                    for c in range(OCT):
                        ins = pe.transpose(bank[QD][:, c * P:(c + 1) * P], qd[:, t % 3].rearrange("p h f -> p (h f)")[:, c * P:(c + 1) * P], ident[:])
                    ins.then_inc(m["qd_turned"], 1)
                if 8 <= s_ < T:
                    after(pe, "v_copied", s_)
                t = parts(s_, 10)
                if t is not None:
                    after(pe, "rlo_done", t)
                    for c in range(OCT):
                        ins = three(bank[VY][:, 0:D], rhi[:, t % 2, c, :], rlo[:, t % 2, c, :], wo_h[:, c, :], wo_l[:, c, :], c == 0, c == OCT - 1)
                    ins.then_inc(m["y_done"], 1)
                t = parts(s_, 9)
                if t is not None:
                    after(pe, "bet_done", t)
                    if t:
                        after(pe, "rlo_done", t - 1)
                    for c in range(OCT):
                        ins = pe.transpose(bank[VY][:, D + c * P:D + (c + 1) * P], r[:, t % 4].rearrange("p h f -> p (h f)")[:, c * P:(c + 1) * P], ident[:])
                    ins.then_inc(m["r_turned"], 1)


def constants():
    f = np.float32
    t = np.arange(SEQ, dtype=f)[:, None]
    inv = (f(1.0) / np.power(f(10000.0), np.arange(8, dtype=f) / f(8))).astype(f)
    ang = (t * inv[None]).astype(f)
    c, s = np.cos(ang).astype(f), np.sin(ang).astype(f)
    inv1 = np.power(f(10.0), f(-4.0) * (np.arange(0, 16, 2, dtype=f) / f(16))).astype(f)
    ang1 = (t * inv1[None]).astype(f)
    c1, s1 = np.cos(ang1).astype(f), np.sin(ang1).astype(f)
    decay = 1.0 - 2.0 ** (-5.0 - np.arange(16.0))
    j, i = np.arange(P)[:, None], np.arange(P)[None, :]
    dmask = np.where(i >= j, decay[:, None, None] ** np.maximum(i - j, 0), 0.0).transpose(1, 0, 2)
    head = np.arange(P) // 16
    return {
        "c_cos1": np.repeat(c1, 2, 1),
        "c_sin1": np.stack([-s1, s1], -1).reshape(SEQ, 16),
        "c_dmask": dmask.astype(f),
        "c_dq": (decay[None] ** (np.arange(P)[:, None] + 1)).astype(f),
        "c_dk": (decay[None] ** (P - 1 - np.arange(P)[:, None])).astype(f),
        "c_dstate": np.stack([decay[head], decay[head + 8]], 1).astype(np.float64).__pow__(P).astype(f),
        "c_blocks": (head[:, None] == head[None]).astype(f),
        "c_ident": np.eye(P, dtype=f),
        "c_iota": np.arange(32, dtype=f),
        "c_tri": (j < i).astype(f),
        "c_cos0": np.concatenate([c, c], 1),
        "c_sin0": np.concatenate([-s, s], 1),
    }


def tower(nc, a, out):
    with ExitStack() as ctx:
        s = Store(nc, ctx, "")
        X = s.sb("X", [P, NT, D])
        ident = s.sb("ident", [P, P])
        ident16 = s.sb("ident16", [P, P], F16)
        ident_in, ident16_done, x_out = s.sem("ident_in"), s.sem("ident16_done"), s.sem("x_out")
        with nc.Block() as block:
            @block.sync
            def _(sp):
                sp.dma_start(ident[:], a["c_ident"]).then_inc(ident_in, 16)

            @block.vector
            def _(dve):
                dve.wait_ge(ident_in, 16)
                dve.tensor_copy(ident16[:], ident[:]).then_inc(ident16_done, 1)
                dve.wait_ge(ident16_done, 1)
        slots = (16 + 2 * N // SLOTS) * SLOTS
        rows_x = nc.dram_tensor("rows_x", (slots, D), F32, kind="Internal").ap()
        rows_y = nc.dram_tensor("rows_y", (slots, D), F32, kind="Internal").ap()
        trunk(nc, a, X, ident, rows_x)
        rotary_attention(nc, a, X, ident, ident16)
        routed_experts(nc, a, X, ident, rows_x, rows_y, slots)
        retention(nc, a, X, ident, ident16)
        gated_experts(nc, a, X, ident)
        with nc.Block() as block:
            @block.sync
            def _(sp):
                sp.dma_start(out.rearrange("b (t p) d -> p (b t) d", p=P), X[:]).then_inc(x_out, 16)
                sp.wait_ge(x_out, 16)


_INS = ["x"] + ["L0_tok_" + n for n in "emb pos_emb A_diag B C D w1 b1 w2 b2 ln1_s ln1_b ln2_s ln2_b lnf_s lnf_b".split()] \
    + ["L0_attn_" + n for n in "w_qkv w_proj b_proj q_gamma q_beta k_gamma k_beta".split()] \
    + ["L0_ffn_" + n for n in "w_gate w_gate_proj w_up_proj w_down_proj".split()] \
    + ["L1_attn_" + n for n in "WQ WK WV WO gamma beta".split()] \
    + ["L1_ffn_" + n for n in "Wg bg W1 b1 W2 b2".split()]


def kernel(**inputs):
    import concourse.bacc as bacc
    from concourse.bass_utils import run_bass_kernel_spmd

    nc = bacc.Bacc("TRN2", target_bir_lowering=False, num_devices=1)
    arrays = {name: np.ascontiguousarray(inputs[name]) for name in _INS}
    arrays.update(constants())
    args = {name: nc.dram_tensor(f"in_{name}", v.shape, mybir.dt.from_np(v.dtype), kind="ExternalInput").ap()
            for name, v in arrays.items()}
    out = nc.dram_tensor("out_h", (BATCH, SEQ, D), F32, kind="ExternalOutput").ap()
    tower(nc, args, out)
    r = run_bass_kernel_spmd(nc, [{f"in_{name}": v for name, v in arrays.items()}], core_ids=[0])
    return r.results[0]["out_h"]
```
